# Optimizing a Trainium2 kernel written in Bass

```python
import numpy as np
import jax
import jax.numpy as jnp

def _softmax(x, axis=-1):
    return jax.nn.softmax(x, axis=axis)

def _gelu(x):
    return jax.nn.gelu(x, approximate=True)

def _silu(x):
    return jax.nn.silu(x)

def _sigmoid(x):
    return jax.nn.sigmoid(x)

def _layernorm(x, axis=-1, eps=1e-05):
    m = jnp.mean(x, axis=axis, keepdims=True)
    v = jnp.var(x, axis=axis, keepdims=True)
    return (x - m) / jnp.sqrt(v + eps)

def _scatter_add(tgt, idx, src, axis=0):
    return tgt.at[idx].add(src)

def _segment_sum(src, seg, n):
    return jax.ops.segment_sum(src, seg, n)
kernel_name = 'mk_perceiver_d4_seqx_r4_919636'

def setup_inputs(seed: int=0):
    np.random.seed(seed)
    _w = jnp.asarray

    def _rec_inputs():
        import jax
        import jax.numpy as jnp
        _rk = jax.random.key(seed)
        x = -0.0002928 + 1 * jax.random.normal(jax.random.fold_in(_rk, 1), (1, 128, 256), jnp.float32)
        _lenS = 128 - jax.random.randint(jax.random.fold_in(_rk, 7), (1,), 0, max(1, 128 // 4) + 1, jnp.int32)
        _lenS2 = 12544 - jax.random.randint(jax.random.fold_in(_rk, 8), (1,), 0, max(1, 12544 // 4) + 1, jnp.int32)
        _ctx_1024P = jax.random.normal(jax.random.fold_in(_rk, 11), (1, 16, 256), jnp.float32)
        _ctx_1024c = jax.random.dirichlet(jax.random.fold_in(_rk, 511), 0.3 * jnp.ones((16,), jnp.float32), (1, 12544))
        _ctx_1024t = jnp.einsum('bsk,bkd->bsd', _ctx_1024c, _ctx_1024P)
        _ctx_1024t = _ctx_1024t * jax.lax.rsqrt(jnp.mean(jnp.square(_ctx_1024t)) + 1e-12) * 0.953939
        ctx_1024 = -1.39393e-06 + 0.999914 * (_ctx_1024t + 0.3 * jax.random.normal(jax.random.fold_in(_rk, 611), (1, 12544, 256), jnp.float32))
        _validS = jnp.arange(128)[None, :] < _lenS[:, None]
        _validS2 = jnp.arange(12544)[None, :] < _lenS2[:, None]
        _causal = jnp.tril(jnp.ones((128, 128), dtype=bool))
        mask_BxS2_bk1 = jnp.broadcast_to(_validS2[:, :], (1, 12544))
        mask_BxS2_ff1 = jnp.where(jnp.ones((1, 12544), dtype=bool), 1.0, 0.0).astype(jnp.float32)
        mask_BxSxS2_ik1 = jnp.where(jnp.broadcast_to(_validS2[:, None, :], (1, 128, 12544)), 1, 0).astype(jnp.int32)
        return (x, ctx_1024, mask_BxS2_bk1, mask_BxS2_ff1, mask_BxSxS2_ik1)
    x, ctx_1024, mask_BxS2_bk1, mask_BxS2_ff1, mask_BxSxS2_ik1 = _rec_inputs()

    def _L0_xattn_setup():
        import jax, jax.numpy as jnp
        import numpy as np
        DIM = 256
        HEADS = 16
        HEAD_DIM = 64
        INNER = HEADS * HEAD_DIM

        def _split_heads(t):
            b, n, _ = t.shape
            return t.reshape(b, n, HEADS, HEAD_DIM).transpose(0, 2, 1, 3)
        key = jax.random.key(seed)
        ks = jax.random.split(key, 7)
        b, n, m = (2, 512, 512)
        s = 0.02
        return {'x': jax.random.normal(ks[0], (b, n, DIM), dtype=jnp.float32), 'context': jax.random.normal(ks[1], (b, m, DIM), dtype=jnp.float32), 'w_kv': jax.random.normal(ks[2], (DIM, 2 * INNER), dtype=jnp.float32) * s, 'w_q': jax.random.normal(ks[3], (DIM, INNER), dtype=jnp.float32) * s, 'w_out1': jax.random.normal(ks[4], (INNER, DIM), dtype=jnp.float32) * s, 'w_out2': jax.random.normal(ks[5], (DIM, DIM), dtype=jnp.float32) * s, 'gamma': jnp.ones((DIM,), dtype=jnp.float32)}
    _L0_xattn_all = _L0_xattn_setup()
    _L0_xattn_in = {k: v for k, v in _L0_xattn_all.items() if k in ('w_kv', 'w_q', 'w_out1', 'w_out2', 'gamma')}
    del _L0_xattn_all

    def _L0_attn_setup():
        import jax, jax.numpy as jnp
        import numpy as np
        B, T, V = (4, 1024, 256)
        DECAY_INIT = 3.0
        key = jax.random.key(seed)
        k_x, = jax.random.split(key, 1)
        x = jax.random.normal(k_x, (B, T, V), dtype=jnp.float32)
        return {'x': x, 'decay_logit': jnp.asarray(DECAY_INIT, dtype=jnp.float32), 'out_scale': jnp.asarray(0.1, dtype=jnp.float32), 'q_scale': jnp.ones((V,), dtype=jnp.float32), 'k_scale': jnp.ones((V,), dtype=jnp.float32)}
    _L0_attn_all = _L0_attn_setup()
    _L0_attn_in = {k: v for k, v in _L0_attn_all.items() if k in ('decay_logit', 'out_scale', 'q_scale', 'k_scale')}
    del _L0_attn_all

    def _L0_ffn_setup():
        import jax, jax.numpy as jnp
        import numpy as np
        TOPK = 2
        EPS = 1e-06
        key = jax.random.key(seed)
        ks = jax.random.split(key, 8)
        b, t, d, h, n = (2, 256, 256, 512, 16)
        x = jax.random.normal(ks[0], (b, t, d), dtype=jnp.float32)
        router_w = jax.random.normal(ks[1], (n, d), dtype=jnp.float32) * (1.0 / np.sqrt(d))
        router_bias = jnp.zeros((n,), dtype=jnp.float32)
        bank_mag = jax.random.normal(ks[2], (n, d, h), dtype=jnp.float32) * (1.0 / np.sqrt(d))
        bank_freq = jax.random.uniform(ks[3], (n, d, h), dtype=jnp.float32, minval=0.5, maxval=2.0) * (1.0 / np.sqrt(d))
        bank_phase = jax.random.uniform(ks[4], (n, h), dtype=jnp.float32, minval=-0.3, maxval=0.3)
        bank_down = jax.random.normal(ks[5], (n, h, d), dtype=jnp.float32) * (1.0 / np.sqrt(h))
        norm_w = jnp.ones((d,), dtype=jnp.float32)
        return {'x': x, 'router_w': router_w, 'router_bias': router_bias, 'bank_mag': bank_mag, 'bank_freq': bank_freq, 'bank_phase': bank_phase, 'bank_down': bank_down, 'norm_w': norm_w}
    _L0_ffn_all = _L0_ffn_setup()
    _L0_ffn_in = {k: v for k, v in _L0_ffn_all.items() if k in ('router_w', 'router_bias', 'bank_mag', 'bank_freq', 'bank_phase', 'bank_down', 'norm_w')}
    del _L0_ffn_all

    def _L1_xattn_setup():
        import jax, jax.numpy as jnp
        import numpy as np
        DIM = 256
        DIM_HEAD = 64
        HEADS = 8
        INNER = DIM_HEAD * HEADS
        EPS = 1e-05

        def layernorm(x, g, b):
            mu = jnp.mean(x, axis=-1, keepdims=True)
            var = jnp.var(x, axis=-1, keepdims=True)
            return (x - mu) * jax.lax.rsqrt(var + EPS) * g + b
        key = jax.random.key(seed)
        ks = jax.random.split(key, 8)
        b, n, m = (8, 1024, 64)
        x = jax.random.normal(ks[0], (b, n, DIM), dtype=jnp.float32)
        latents = jax.random.normal(ks[1], (b, m, DIM), dtype=jnp.float32)
        mask = jax.random.bernoulli(ks[2], 0.9, (b, n))
        s = DIM ** (-0.5)
        Wq = jax.random.normal(ks[3], (DIM, INNER), dtype=jnp.float32) * s
        Wkv = jax.random.normal(ks[4], (DIM, 2 * INNER), dtype=jnp.float32) * s
        Wo = jax.random.normal(ks[5], (INNER, DIM), dtype=jnp.float32) * INNER ** (-0.5)
        ln_x_g = jnp.ones((DIM,), jnp.float32)
        ln_x_b = jnp.zeros((DIM,), jnp.float32)
        ln_l_g = jnp.ones((DIM,), jnp.float32)
        ln_l_b = jnp.zeros((DIM,), jnp.float32)
        ln_o_g = jnp.ones((DIM,), jnp.float32)
        ln_o_b = jnp.zeros((DIM,), jnp.float32)
        return {'x': x, 'latents': latents, 'mask': mask, 'Wq': Wq, 'Wkv': Wkv, 'Wo': Wo, 'ln_x_g': ln_x_g, 'ln_x_b': ln_x_b, 'ln_l_g': ln_l_g, 'ln_l_b': ln_l_b, 'ln_o_g': ln_o_g, 'ln_o_b': ln_o_b}
    _L1_xattn_all = _L1_xattn_setup()
    _L1_xattn_in = {k: v for k, v in _L1_xattn_all.items() if k in ('Wq', 'Wkv', 'Wo', 'ln_x_g', 'ln_x_b', 'ln_l_g', 'ln_l_b', 'ln_o_g', 'ln_o_b')}
    del _L1_xattn_all

    def _L1_attn_setup():
        import jax, jax.numpy as jnp
        import numpy as np
        B, S, D = (8, 256, 256)
        H, HD = (8, 64)
        HID = H * HD
        P = 2 * D
        K = 4
        EPS = 1e-06
        CAP = 15.0

        def _layernorm(x, g, b):
            mu = jnp.mean(x, -1, keepdims=True)
            var = jnp.var(x, -1, keepdims=True)
            return (x - mu) * jax.lax.rsqrt(var + EPS) * g + b

        def _soft_cap(v):
            return CAP * jnp.tanh(v / CAP)

        def _causal_conv_feat(x, w, b):
            L = x.shape[-1]
            xp = jnp.pad(x, ((0, 0), (0, 0), (K - 1, 0)))
            out = b
            for m in range(K):
                out = out + w[m] * xp[..., m:m + L]
            return out

        def _forward(x, ln_g, ln_b, mh_g, mh_b, W_up_l, b_up_l, W_up_r, b_up_r, W_down, b_down, conv_w, conv_b, W_skip, b_skip, W_i, b_i, W_f, b_f, W_o, b_o, W_q, b_q, W_k, b_k, W_v, b_v):
            Bs, Sl, _ = x.shape
            xn = _layernorm(x, ln_g, ln_b)
            x_t = xn @ W_up_l.T + b_up_l
            r_t = xn @ W_up_r.T + b_up_r
            x_c = jax.nn.silu(_causal_conv_feat(x_t, conv_w, conv_b))
            x_skip = x_c @ W_skip.T + b_skip
            q = (x_c @ W_q.T + b_q).reshape(Bs, Sl, H, HD)
            k = (x_c @ W_k.T + b_k).reshape(Bs, Sl, H, HD) / float(np.sqrt(HD))
            v = (x_t @ W_v.T + b_v).reshape(Bs, Sl, H, HD)
            i_pre = _soft_cap(x_c @ W_i.T + b_i)
            f_pre = _soft_cap(x_c @ W_f.T + b_f)
            o = jax.nn.sigmoid(x_t @ W_o.T + b_o)

            def step(carry, inp):
                c, n, m = carry
                qt, kt, vt, it, ft = inp
                m_t = jnp.maximum(ft + m, it)
                ie = jnp.exp(it - m_t)
                fe = jnp.exp(ft - m_t + m)
                c = fe[:, :, None, None] * c + ie[:, :, None, None] * jnp.einsum('bhd,bhe->bhde', vt, kt)
                n = fe[:, :, None] * n + ie[:, :, None] * kt
                num = jnp.einsum('bhde,bhe->bhd', c, qt)
                den = jnp.maximum(jnp.sum(n * qt, -1, keepdims=True), 1.0)
                return ((c, n, m_t), num / den)
            c0 = jnp.zeros((Bs, H, HD, HD), x.dtype)
            n0 = jnp.ones((Bs, H, HD), x.dtype)
            m0 = jnp.zeros((Bs, H), x.dtype)
            seq = tuple((jnp.moveaxis(a, 1, 0) for a in (q, k, v, i_pre, f_pre)))
            _, hs = jax.lax.scan(step, (c0, n0, m0), seq)
            h = o * jnp.moveaxis(hs, 0, 1).reshape(Bs, Sl, HID)
            hn = _layernorm(h.reshape(Bs, Sl, H, HD), mh_g, mh_b).reshape(Bs, Sl, HID)
            out = (hn + x_skip) * jax.nn.silu(r_t)
            return out @ W_down.T + b_down + x
        key = jax.random.key(seed)
        ks = jax.random.split(key, 16)

        def w(kk, shape):
            return jax.random.normal(kk, shape, jnp.float32) / np.sqrt(shape[-1]).astype(np.float32)
        return {'x': jax.random.normal(ks[0], (B, S, D), jnp.float32), 'ln_g': jnp.ones((D,), jnp.float32), 'ln_b': jnp.zeros((D,), jnp.float32), 'mh_g': jnp.ones((H, HD), jnp.float32), 'mh_b': jnp.zeros((H, HD), jnp.float32), 'W_up_l': w(ks[1], (P, D)), 'b_up_l': jnp.zeros((P,), jnp.float32), 'W_up_r': w(ks[2], (HID, D)), 'b_up_r': jnp.zeros((HID,), jnp.float32), 'W_down': w(ks[3], (D, HID)), 'b_down': jnp.zeros((D,), jnp.float32), 'conv_w': jax.random.normal(ks[4], (K,), jnp.float32) * 0.3, 'conv_b': jnp.zeros((), jnp.float32), 'W_skip': w(ks[5], (HID, P)), 'b_skip': jnp.zeros((HID,), jnp.float32), 'W_i': w(ks[6], (H, P)), 'b_i': jnp.zeros((H,), jnp.float32), 'W_f': w(ks[7], (H, P)), 'b_f': jnp.zeros((H,), jnp.float32), 'W_o': w(ks[8], (HID, P)), 'b_o': jnp.zeros((HID,), jnp.float32), 'W_q': w(ks[9], (HID, P)), 'b_q': jnp.zeros((HID,), jnp.float32), 'W_k': w(ks[10], (HID, P)), 'b_k': jnp.zeros((HID,), jnp.float32), 'W_v': w(ks[11], (HID, P)), 'b_v': jnp.zeros((HID,), jnp.float32)}
    _L1_attn_all = _L1_attn_setup()
    _L1_attn_in = {k: v for k, v in _L1_attn_all.items() if k in ('ln_g', 'ln_b', 'mh_g', 'mh_b', 'W_up_l', 'b_up_l', 'W_up_r', 'b_up_r', 'W_down', 'b_down', 'conv_w', 'conv_b', 'W_skip', 'b_skip', 'W_i', 'b_i', 'W_f', 'b_f', 'W_o', 'b_o', 'W_q', 'b_q', 'W_k', 'b_k', 'W_v', 'b_v')}
    del _L1_attn_all

    def _L1_ffn_setup():
        import jax, jax.numpy as jnp
        import numpy as np
        B, T, D, F, E = (4, 512, 256, 1024, 8)
        key = jax.random.key(seed)
        k = jax.random.split(key, 7)
        x = jax.random.normal(k[0], (B, T, D), dtype=jnp.float32)
        wr = jax.random.normal(k[1], (D,), dtype=jnp.float32)
        br = jnp.zeros((), dtype=jnp.float32)
        W1 = jax.random.normal(k[2], (E, D, F), dtype=jnp.float32) * 0.02
        b1 = jnp.zeros((E, F), dtype=jnp.float32)
        W2 = jax.random.normal(k[3], (E, F, D), dtype=jnp.float32) * 0.02
        b2 = jnp.zeros((E, D), dtype=jnp.float32)
        return {'x': x, 'wr': wr, 'br': br, 'W1': W1, 'b1': b1, 'W2': W2, 'b2': b2}
    _L1_ffn_all = _L1_ffn_setup()
    _L1_ffn_in = {k: v for k, v in _L1_ffn_all.items() if k in ('wr', 'br', 'W1', 'b1', 'W2', 'b2')}
    del _L1_ffn_all

    def _L2_xattn_setup():
        import jax, jax.numpy as jnp
        import numpy as np
        D_MODEL = 256
        HEADS = 16
        DEPTH = D_MODEL // HEADS
        B, S = (4, 1024)
        EPS_K = 1e-06
        EPS_LN = 1e-06

        def _layernorm(x, g, b):
            m = jnp.mean(x, axis=-1, keepdims=True)
            var = jnp.var(x, axis=-1, keepdims=True)
            return (x - m) * jax.lax.rsqrt(var + EPS_LN) * g + b

        def _split_heads(x):
            bsz, sl, _ = x.shape
            return x.reshape(bsz, sl, HEADS, DEPTH).transpose(0, 2, 1, 3)
        key = jax.random.key(seed)
        ks = jax.random.split(key, 8)
        lecun = 1.0 / np.sqrt(D_MODEL)
        glorot = np.sqrt(2.0 / (D_MODEL + D_MODEL))
        return {'q': jax.random.normal(ks[0], (B, S, D_MODEL), jnp.float32), 'k': jax.random.normal(ks[1], (B, S, D_MODEL), jnp.float32), 'v': jax.random.normal(ks[2], (B, S, D_MODEL), jnp.float32), 'mask': jnp.ones((B, S), jnp.float32), 'wq': jax.random.normal(ks[3], (D_MODEL, D_MODEL), jnp.float32) * lecun, 'wk': jax.random.normal(ks[4], (D_MODEL, D_MODEL), jnp.float32) * lecun, 'wv': jax.random.normal(ks[5], (D_MODEL, D_MODEL), jnp.float32) * lecun, 'ln_gamma': jnp.ones((D_MODEL,), jnp.float32), 'ln_beta': jnp.zeros((D_MODEL,), jnp.float32), 'dense_w': jax.random.normal(ks[6], (D_MODEL, D_MODEL), jnp.float32) * glorot, 'dense_b': jnp.zeros((D_MODEL,), jnp.float32)}
    _L2_xattn_all = _L2_xattn_setup()
    _L2_xattn_in = {k: v for k, v in _L2_xattn_all.items() if k in ('wq', 'wk', 'wv', 'ln_gamma', 'ln_beta', 'dense_w', 'dense_b')}
    del _L2_xattn_all

    def _L2_attn_setup():
        import jax, jax.numpy as jnp
        import numpy as np
        D = 256
        H = 16
        DK = D // H
        CHUNK = 64
        EPS = 1e-05

        def _layernorm_noaffine(k):
            mu = jnp.mean(k, axis=-1, keepdims=True)
            var = jnp.mean((k - mu) ** 2, axis=-1, keepdims=True)
            return (k - mu) / jnp.sqrt(var + EPS)

        def _linear_attn(x, W_qkv, W_o):
            B, L, Dm = x.shape
            qkv = (x @ W_qkv).reshape(B, L, 3, H, DK)
            q, k, v = (qkv[:, :, 0], qkv[:, :, 1], qkv[:, :, 2])
            k = _layernorm_noaffine(k)
            nC = L // CHUNK
            to_chunks = lambda t: t.reshape(B, nC, CHUNK, H, DK).transpose(1, 0, 2, 3, 4)
            qc, kc, vc = (to_chunks(q), to_chunks(k), to_chunks(v))
            causal = jnp.tril(jnp.ones((CHUNK, CHUNK), dtype=bool))

            def step(S, chunk):
                q_c, k_c, v_c = chunk
                inter = jnp.einsum('bhde,bthe->bthd', S, q_c)
                scores = jnp.einsum('bthd,bshd->bhts', q_c, k_c)
                scores = jnp.where(causal, scores, 0.0)
                intra = jnp.einsum('bhts,bshd->bthd', scores, v_c)
                S = S + jnp.einsum('bthd,bthe->bhde', v_c, k_c)
                return (S, inter + intra)
            S0 = jnp.zeros((B, H, DK, DK), dtype=x.dtype)
            _, ys = jax.lax.scan(step, S0, (qc, kc, vc))
            y = ys.transpose(1, 0, 2, 3, 4).reshape(B, L, Dm)
            return y @ W_o
        key = jax.random.key(seed)
        k1, k2, k3 = jax.random.split(key, 3)
        x = jax.random.normal(k1, (4, 1024, D), dtype=jnp.float32)
        W_qkv = jax.random.normal(k2, (D, 3 * D), dtype=jnp.float32) * 0.02
        W_o = jax.random.normal(k3, (D, D), dtype=jnp.float32) * 0.02
        return {'x': x, 'W_qkv': W_qkv, 'W_o': W_o}
    _L2_attn_all = _L2_attn_setup()
    _L2_attn_in = {k: v for k, v in _L2_attn_all.items() if k in ('W_qkv', 'W_o')}
    del _L2_attn_all

    def _L2_ffn_setup():
        import jax, jax.numpy as jnp
        import numpy as np
        E = 8
        K = 2
        D = 256
        H = 1024
        CAP_FACTOR = 1.0
        key = jax.random.key(seed)
        ks = jax.random.split(key, 5)
        x = jax.random.normal(ks[0], (4, 512, D), jnp.float32)
        gate_w = jax.random.normal(ks[1], (E, D), jnp.float32) * 0.02
        fc1_w = jax.random.normal(ks[2], (E, H, D), jnp.float32) * 0.02
        fc1_b = jnp.zeros((E, 1, H), jnp.float32)
        fc2_w = jax.random.normal(ks[3], (E, H, D), jnp.float32) * 0.02
        fc2_b = jnp.zeros((E, 1, D), jnp.float32)
        return {'x': x, 'gate_w': gate_w, 'fc1_w': fc1_w, 'fc1_b': fc1_b, 'fc2_w': fc2_w, 'fc2_b': fc2_b}
    _L2_ffn_all = _L2_ffn_setup()
    _L2_ffn_in = {k: v for k, v in _L2_ffn_all.items() if k in ('gate_w', 'fc1_w', 'fc1_b', 'fc2_w', 'fc2_b')}
    del _L2_ffn_all

    def _L3_xattn_setup():
        import jax, jax.numpy as jnp
        import numpy as np
        N_HEADS = 16
        NEG_BIAS = -1000000000.0

        def _split_heads(x):
            B, S, D = x.shape
            return x.reshape(B, S, N_HEADS, D // N_HEADS).transpose(0, 2, 1, 3)
        key = jax.random.key(seed)
        k1, k2, k3, k4 = jax.random.split(key, 4)
        B, S, D = (2, 512, 256)
        queries = jax.random.normal(k1, (B, S, D), dtype=jnp.float32)
        keys = jax.random.normal(k2, (B, S, D), dtype=jnp.float32)
        values = jax.random.normal(k3, (B, S, D), dtype=jnp.float32)
        mask = jax.random.randint(k4, (B, S, S), 0, 2, dtype=jnp.int32)
        return {'queries': queries, 'keys': keys, 'values': values, 'mask': mask}
    _L3_xattn_all = _L3_xattn_setup()
    _L3_xattn_in = {k: v for k, v in _L3_xattn_all.items() if k in ()}
    del _L3_xattn_all

    def _L3_attn_setup():
        import jax, jax.numpy as jnp
        import numpy as np
        DIM = 256
        HEADS = 16
        HEAD_DIM = DIM // HEADS
        B, N = (2, 512)
        SCALE = 1.0 / np.float32(np.sqrt(DIM))

        def _split_heads(t):
            b, n, _ = t.shape
            return jnp.moveaxis(t.reshape(b, n, HEADS, HEAD_DIM), 2, 0)
        key = jax.random.key(seed)
        ks = jax.random.split(key, 9)
        s = 0.02
        return {'x': jax.random.normal(ks[0], (B, N, DIM), dtype=jnp.float32), 'Wq': jax.random.normal(ks[1], (DIM, DIM), dtype=jnp.float32) * s, 'bq': jax.random.normal(ks[2], (DIM,), dtype=jnp.float32) * s, 'Wk': jax.random.normal(ks[3], (DIM, DIM), dtype=jnp.float32) * s, 'bk': jax.random.normal(ks[4], (DIM,), dtype=jnp.float32) * s, 'Wv': jax.random.normal(ks[5], (DIM, DIM), dtype=jnp.float32) * s, 'bv': jax.random.normal(ks[6], (DIM,), dtype=jnp.float32) * s, 'Wo': jax.random.normal(ks[7], (DIM, DIM), dtype=jnp.float32) * s, 'bo': jax.random.normal(ks[8], (DIM,), dtype=jnp.float32) * s}
    _L3_attn_all = _L3_attn_setup()
    _L3_attn_in = {k: v for k, v in _L3_attn_all.items() if k in ('Wq', 'bq', 'Wk', 'bk', 'Wv', 'bv', 'Wo', 'bo')}
    del _L3_attn_all

    def _L3_ffn_setup():
        import jax, jax.numpy as jnp
        import numpy as np
        B, N, C, H, REG = (1, 2309, 256, 16, 5)
        D = C // H
        key = jax.random.key(seed)
        k0, k1, k2, k3 = jax.random.split(key, 4)
        x = jax.random.normal(k0, (B, N, C), dtype=jnp.float32)
        g_info = jax.random.normal(k1, (12, 2, C), dtype=jnp.float32)
        W_qkv = jax.random.normal(k2, (C, 3 * C), dtype=jnp.float32) * 0.02
        W_proj = jax.random.normal(k3, (C, C), dtype=jnp.float32) * 0.02
        b_proj = jnp.zeros((C,), dtype=jnp.float32)
        return {'x': x, 'g_info': g_info, 'W_qkv': W_qkv, 'W_proj': W_proj, 'b_proj': b_proj}
    _L3_ffn_all = _L3_ffn_setup()
    _L3_ffn_in = {k: v for k, v in _L3_ffn_all.items() if k in ('g_info', 'W_qkv', 'W_proj', 'b_proj')}
    del _L3_ffn_all
    return {'x': x, 'ctx_1024': ctx_1024, 'mask_BxS2_bk1': mask_BxS2_bk1, 'mask_BxS2_ff1': mask_BxS2_ff1, 'mask_BxSxS2_ik1': mask_BxSxS2_ik1, 'L0_xattn_w_kv': _L0_xattn_in['w_kv'], 'L0_xattn_w_q': _L0_xattn_in['w_q'], 'L0_xattn_w_out1': _L0_xattn_in['w_out1'], 'L0_xattn_w_out2': _L0_xattn_in['w_out2'], 'L0_xattn_gamma': _L0_xattn_in['gamma'], 'L0_attn_decay_logit': _L0_attn_in['decay_logit'], 'L0_attn_out_scale': _L0_attn_in['out_scale'], 'L0_attn_q_scale': _L0_attn_in['q_scale'], 'L0_attn_k_scale': _L0_attn_in['k_scale'], 'L0_ffn_router_w': _L0_ffn_in['router_w'], 'L0_ffn_router_bias': _L0_ffn_in['router_bias'], 'L0_ffn_bank_mag': _L0_ffn_in['bank_mag'], 'L0_ffn_bank_freq': _L0_ffn_in['bank_freq'], 'L0_ffn_bank_phase': _L0_ffn_in['bank_phase'], 'L0_ffn_bank_down': _L0_ffn_in['bank_down'], 'L0_ffn_norm_w': _L0_ffn_in['norm_w'], 'L1_xattn_Wq': _L1_xattn_in['Wq'], 'L1_xattn_Wkv': _L1_xattn_in['Wkv'], 'L1_xattn_Wo': _L1_xattn_in['Wo'], 'L1_xattn_ln_x_g': _L1_xattn_in['ln_x_g'], 'L1_xattn_ln_x_b': _L1_xattn_in['ln_x_b'], 'L1_xattn_ln_l_g': _L1_xattn_in['ln_l_g'], 'L1_xattn_ln_l_b': _L1_xattn_in['ln_l_b'], 'L1_xattn_ln_o_g': _L1_xattn_in['ln_o_g'], 'L1_xattn_ln_o_b': _L1_xattn_in['ln_o_b'], 'L1_attn_ln_g': _L1_attn_in['ln_g'], 'L1_attn_ln_b': _L1_attn_in['ln_b'], 'L1_attn_mh_g': _L1_attn_in['mh_g'], 'L1_attn_mh_b': _L1_attn_in['mh_b'], 'L1_attn_W_up_l': _L1_attn_in['W_up_l'], 'L1_attn_b_up_l': _L1_attn_in['b_up_l'], 'L1_attn_W_up_r': _L1_attn_in['W_up_r'], 'L1_attn_b_up_r': _L1_attn_in['b_up_r'], 'L1_attn_W_down': _L1_attn_in['W_down'], 'L1_attn_b_down': _L1_attn_in['b_down'], 'L1_attn_conv_w': _L1_attn_in['conv_w'], 'L1_attn_conv_b': _L1_attn_in['conv_b'], 'L1_attn_W_skip': _L1_attn_in['W_skip'], 'L1_attn_b_skip': _L1_attn_in['b_skip'], 'L1_attn_W_i': _L1_attn_in['W_i'], 'L1_attn_b_i': _L1_attn_in['b_i'], 'L1_attn_W_f': _L1_attn_in['W_f'], 'L1_attn_b_f': _L1_attn_in['b_f'], 'L1_attn_W_o': _L1_attn_in['W_o'], 'L1_attn_b_o': _L1_attn_in['b_o'], 'L1_attn_W_q': _L1_attn_in['W_q'], 'L1_attn_b_q': _L1_attn_in['b_q'], 'L1_attn_W_k': _L1_attn_in['W_k'], 'L1_attn_b_k': _L1_attn_in['b_k'], 'L1_attn_W_v': _L1_attn_in['W_v'], 'L1_attn_b_v': _L1_attn_in['b_v'], 'L1_ffn_wr': _L1_ffn_in['wr'], 'L1_ffn_br': _L1_ffn_in['br'], 'L1_ffn_W1': _L1_ffn_in['W1'], 'L1_ffn_b1': _L1_ffn_in['b1'], 'L1_ffn_W2': _L1_ffn_in['W2'], 'L1_ffn_b2': _L1_ffn_in['b2'], 'L2_xattn_wq': _L2_xattn_in['wq'], 'L2_xattn_wk': _L2_xattn_in['wk'], 'L2_xattn_wv': _L2_xattn_in['wv'], 'L2_xattn_ln_gamma': _L2_xattn_in['ln_gamma'], 'L2_xattn_ln_beta': _L2_xattn_in['ln_beta'], 'L2_xattn_dense_w': _L2_xattn_in['dense_w'], 'L2_xattn_dense_b': _L2_xattn_in['dense_b'], 'L2_attn_W_qkv': _L2_attn_in['W_qkv'], 'L2_attn_W_o': _L2_attn_in['W_o'], 'L2_ffn_gate_w': _L2_ffn_in['gate_w'], 'L2_ffn_fc1_w': _L2_ffn_in['fc1_w'], 'L2_ffn_fc1_b': _L2_ffn_in['fc1_b'], 'L2_ffn_fc2_w': _L2_ffn_in['fc2_w'], 'L2_ffn_fc2_b': _L2_ffn_in['fc2_b'], 'L3_attn_Wq': _L3_attn_in['Wq'], 'L3_attn_bq': _L3_attn_in['bq'], 'L3_attn_Wk': _L3_attn_in['Wk'], 'L3_attn_bk': _L3_attn_in['bk'], 'L3_attn_Wv': _L3_attn_in['Wv'], 'L3_attn_bv': _L3_attn_in['bv'], 'L3_attn_Wo': _L3_attn_in['Wo'], 'L3_attn_bo': _L3_attn_in['bo'], 'L3_ffn_g_info': _L3_ffn_in['g_info'], 'L3_ffn_W_qkv': _L3_ffn_in['W_qkv'], 'L3_ffn_W_proj': _L3_ffn_in['W_proj'], 'L3_ffn_b_proj': _L3_ffn_in['b_proj']}

def reference(x, ctx_1024, mask_BxS2_bk1, mask_BxS2_ff1, mask_BxSxS2_ik1, L0_xattn_w_kv, L0_xattn_w_q, L0_xattn_w_out1, L0_xattn_w_out2, L0_xattn_gamma, L0_attn_decay_logit, L0_attn_out_scale, L0_attn_q_scale, L0_attn_k_scale, L0_ffn_router_w, L0_ffn_router_bias, L0_ffn_bank_mag, L0_ffn_bank_freq, L0_ffn_bank_phase, L0_ffn_bank_down, L0_ffn_norm_w, L1_xattn_Wq, L1_xattn_Wkv, L1_xattn_Wo, L1_xattn_ln_x_g, L1_xattn_ln_x_b, L1_xattn_ln_l_g, L1_xattn_ln_l_b, L1_xattn_ln_o_g, L1_xattn_ln_o_b, L1_attn_ln_g, L1_attn_ln_b, L1_attn_mh_g, L1_attn_mh_b, L1_attn_W_up_l, L1_attn_b_up_l, L1_attn_W_up_r, L1_attn_b_up_r, L1_attn_W_down, L1_attn_b_down, L1_attn_conv_w, L1_attn_conv_b, L1_attn_W_skip, L1_attn_b_skip, L1_attn_W_i, L1_attn_b_i, L1_attn_W_f, L1_attn_b_f, L1_attn_W_o, L1_attn_b_o, L1_attn_W_q, L1_attn_b_q, L1_attn_W_k, L1_attn_b_k, L1_attn_W_v, L1_attn_b_v, L1_ffn_wr, L1_ffn_br, L1_ffn_W1, L1_ffn_b1, L1_ffn_W2, L1_ffn_b2, L2_xattn_wq, L2_xattn_wk, L2_xattn_wv, L2_xattn_ln_gamma, L2_xattn_ln_beta, L2_xattn_dense_w, L2_xattn_dense_b, L2_attn_W_qkv, L2_attn_W_o, L2_ffn_gate_w, L2_ffn_fc1_w, L2_ffn_fc1_b, L2_ffn_fc2_w, L2_ffn_fc2_b, L3_attn_Wq, L3_attn_bq, L3_attn_Wk, L3_attn_bk, L3_attn_Wv, L3_attn_bv, L3_attn_Wo, L3_attn_bo, L3_ffn_g_info, L3_ffn_W_qkv, L3_ffn_W_proj, L3_ffn_b_proj):
    import jax
    import jax.numpy as jnp

    def _L0_xattn_ref(x, context, w_kv, w_q, w_out1, w_out2, gamma):
        import jax, jax.numpy as jnp
        import numpy as np
        DIM = 256
        HEADS = 16
        HEAD_DIM = 64
        INNER = HEADS * HEAD_DIM

        def _split_heads(t):
            b, n, _ = t.shape
            return t.reshape(b, n, HEADS, HEAD_DIM).transpose(0, 2, 1, 3)
        scale = HEAD_DIM ** (-0.5)
        kv = context @ w_kv
        k, v = jnp.split(kv, 2, axis=-1)
        q = _split_heads(x @ w_q)
        k = _split_heads(k)
        v = _split_heads(v)
        dots = jnp.einsum('bhid,bhjd->bhij', q, k) * scale
        attn = jax.nn.softmax(dots, axis=-1)
        out = jnp.einsum('bhij,bhjd->bhid', attn, v)
        b, h, n, d = out.shape
        out = out.transpose(0, 2, 1, 3).reshape(b, n, h * d)
        out = jax.nn.relu(out @ w_out1) @ w_out2
        mean = jnp.mean(out, axis=-1, keepdims=True)
        var = jnp.var(out, axis=-1, keepdims=True)
        return (out - mean) * jax.lax.rsqrt(var + 1e-05) * gamma

    def _L0_attn_ref(x, decay_logit, out_scale, q_scale, k_scale):
        import jax, jax.numpy as jnp
        import numpy as np
        B, T, V = (4, 1024, 256)
        DECAY_INIT = 3.0
        dtype = x.dtype
        Bx, Tx, Vx = x.shape
        queries = x * q_scale.astype(dtype)
        keys = x * k_scale.astype(dtype)
        scores = jnp.einsum('btv,bsv->bts', queries, keys)
        decay = jax.nn.sigmoid(decay_logit)
        pos = jnp.arange(Tx)
        diff = pos[None, :] - pos[:, None]
        causal = diff > 0
        weights = decay ** jnp.maximum(diff.astype(jnp.float32) - 1.0, 0.0) * causal
        scores = scores * weights.astype(dtype)[None]
        retrieved = jnp.einsum('bts,bsv->btv', scores, x)
        return retrieved * out_scale.astype(dtype)

    def _L0_ffn_ref(x, router_w, router_bias, bank_mag, bank_freq, bank_phase, bank_down, norm_w):
        import jax, jax.numpy as jnp
        import numpy as np
        TOPK = 2
        EPS = 1e-06
        b, t, d = x.shape
        scores = jnp.einsum('btd,nd->btn', x, router_w) + router_bias
        topv, topi = jax.lax.top_k(scores, TOPK)
        weights = jax.nn.softmax(topv, axis=-1)
        fx = x.reshape(b * t, d)
        mag = jnp.einsum('td,ndh->tnh', fx, bank_mag)
        freq = jnp.einsum('td,ndh->tnh', fx, bank_freq)
        hidden = jnp.tanh(mag) * jnp.cos(jax.nn.softplus(freq) + 0.1 + bank_phase[None, :, :])
        out_all = jnp.einsum('tnh,nhd->tnd', hidden, bank_down)
        ti = topi.reshape(b * t, TOPK)
        sel = jnp.take_along_axis(out_all, ti[:, :, None], axis=1)
        out = jnp.einsum('tkd,tk->td', sel, weights.reshape(b * t, TOPK)).reshape(b, t, d)
        out = out * jax.lax.rsqrt(jnp.mean(out * out, axis=-1, keepdims=True) + EPS) * norm_w
        return out

    def _L1_xattn_ref(x, latents, mask, Wq, Wkv, Wo, ln_x_g, ln_x_b, ln_l_g, ln_l_b, ln_o_g, ln_o_b):
        import jax, jax.numpy as jnp
        import numpy as np
        DIM = 256
        DIM_HEAD = 64
        HEADS = 8
        INNER = DIM_HEAD * HEADS
        EPS = 1e-05

        def layernorm(x, g, b):
            mu = jnp.mean(x, axis=-1, keepdims=True)
            var = jnp.var(x, axis=-1, keepdims=True)
            return (x - mu) * jax.lax.rsqrt(var + EPS) * g + b
        scale = DIM_HEAD ** (-0.5)
        b, m = (latents.shape[0], latents.shape[1])
        xn = layernorm(x, ln_x_g, ln_x_b)
        ln = layernorm(latents, ln_l_g, ln_l_b)
        q = ln @ Wq
        kv_in = jnp.concatenate([xn, ln], axis=1)
        kv = kv_in @ Wkv
        k, v = jnp.split(kv, 2, axis=-1)
        q = q.reshape(b, m, HEADS, DIM_HEAD).transpose(0, 2, 1, 3)
        k = k.reshape(b, k.shape[1], HEADS, DIM_HEAD).transpose(0, 2, 1, 3)
        v = v.reshape(b, v.shape[1], HEADS, DIM_HEAD).transpose(0, 2, 1, 3)
        sim = jnp.einsum('bhid,bhjd->bhij', q * scale, k) * scale
        full_mask = jnp.concatenate([mask, jnp.ones((b, m), dtype=bool)], axis=1)
        max_neg = -jnp.finfo(sim.dtype).max
        sim = jnp.where(full_mask[:, None, None, :], sim, max_neg)
        attn = jax.nn.softmax(sim.astype(jnp.float32), axis=-1).astype(sim.dtype)
        out = jnp.einsum('bhij,bhjd->bhid', attn, v)
        out = out.transpose(0, 2, 1, 3).reshape(b, m, INNER)
        out = out @ Wo
        return layernorm(out, ln_o_g, ln_o_b)

    def _L1_attn_ref(x, ln_g, ln_b, mh_g, mh_b, W_up_l, b_up_l, W_up_r, b_up_r, W_down, b_down, conv_w, conv_b, W_skip, b_skip, W_i, b_i, W_f, b_f, W_o, b_o, W_q, b_q, W_k, b_k, W_v, b_v):
        import jax, jax.numpy as jnp
        import numpy as np
        B, S, D = (8, 256, 256)
        H, HD = (8, 64)
        HID = H * HD
        P = 2 * D
        K = 4
        EPS = 1e-06
        CAP = 15.0

        def _layernorm(x, g, b):
            mu = jnp.mean(x, -1, keepdims=True)
            var = jnp.var(x, -1, keepdims=True)
            return (x - mu) * jax.lax.rsqrt(var + EPS) * g + b

        def _soft_cap(v):
            return CAP * jnp.tanh(v / CAP)

        def _causal_conv_feat(x, w, b):
            L = x.shape[-1]
            xp = jnp.pad(x, ((0, 0), (0, 0), (K - 1, 0)))
            out = b
            for m in range(K):
                out = out + w[m] * xp[..., m:m + L]
            return out

        def _forward(x, ln_g, ln_b, mh_g, mh_b, W_up_l, b_up_l, W_up_r, b_up_r, W_down, b_down, conv_w, conv_b, W_skip, b_skip, W_i, b_i, W_f, b_f, W_o, b_o, W_q, b_q, W_k, b_k, W_v, b_v):
            Bs, Sl, _ = x.shape
            xn = _layernorm(x, ln_g, ln_b)
            x_t = xn @ W_up_l.T + b_up_l
            r_t = xn @ W_up_r.T + b_up_r
            x_c = jax.nn.silu(_causal_conv_feat(x_t, conv_w, conv_b))
            x_skip = x_c @ W_skip.T + b_skip
            q = (x_c @ W_q.T + b_q).reshape(Bs, Sl, H, HD)
            k = (x_c @ W_k.T + b_k).reshape(Bs, Sl, H, HD) / float(np.sqrt(HD))
            v = (x_t @ W_v.T + b_v).reshape(Bs, Sl, H, HD)
            i_pre = _soft_cap(x_c @ W_i.T + b_i)
            f_pre = _soft_cap(x_c @ W_f.T + b_f)
            o = jax.nn.sigmoid(x_t @ W_o.T + b_o)

            def step(carry, inp):
                c, n, m = carry
                qt, kt, vt, it, ft = inp
                m_t = jnp.maximum(ft + m, it)
                ie = jnp.exp(it - m_t)
                fe = jnp.exp(ft - m_t + m)
                c = fe[:, :, None, None] * c + ie[:, :, None, None] * jnp.einsum('bhd,bhe->bhde', vt, kt)
                n = fe[:, :, None] * n + ie[:, :, None] * kt
                num = jnp.einsum('bhde,bhe->bhd', c, qt)
                den = jnp.maximum(jnp.sum(n * qt, -1, keepdims=True), 1.0)
                return ((c, n, m_t), num / den)
            c0 = jnp.zeros((Bs, H, HD, HD), x.dtype)
            n0 = jnp.ones((Bs, H, HD), x.dtype)
            m0 = jnp.zeros((Bs, H), x.dtype)
            seq = tuple((jnp.moveaxis(a, 1, 0) for a in (q, k, v, i_pre, f_pre)))
            _, hs = jax.lax.scan(step, (c0, n0, m0), seq)
            h = o * jnp.moveaxis(hs, 0, 1).reshape(Bs, Sl, HID)
            hn = _layernorm(h.reshape(Bs, Sl, H, HD), mh_g, mh_b).reshape(Bs, Sl, HID)
            out = (hn + x_skip) * jax.nn.silu(r_t)
            return out @ W_down.T + b_down + x
        return _forward(x, ln_g, ln_b, mh_g, mh_b, W_up_l, b_up_l, W_up_r, b_up_r, W_down, b_down, conv_w, conv_b, W_skip, b_skip, W_i, b_i, W_f, b_f, W_o, b_o, W_q, b_q, W_k, b_k, W_v, b_v)

    def _L1_ffn_ref(x, wr, br, W1, b1, W2, b2):
        import jax, jax.numpy as jnp
        import numpy as np
        B, T, D, F, E = (4, 512, 256, 1024, 8)
        keys = jnp.einsum('btd,d->bt', x, wr) + br
        expert_idx = jnp.mod(jnp.floor(keys).astype(jnp.int32), W1.shape[0])
        out = jnp.zeros_like(x)
        for e in range(W1.shape[0]):
            h = jax.nn.relu(jnp.einsum('btd,df->btf', x, W1[e]) + b1[e])
            y = jnp.einsum('btf,fd->btd', h, W2[e]) + b2[e]
            out = jnp.where((expert_idx == e)[..., None], y, out)
        return out

    def _L2_xattn_ref(q, k, v, mask, wq, wk, wv, ln_gamma, ln_beta, dense_w, dense_b):
        import jax, jax.numpy as jnp
        import numpy as np
        D_MODEL = 256
        HEADS = 16
        DEPTH = D_MODEL // HEADS
        B, S = (4, 1024)
        EPS_K = 1e-06
        EPS_LN = 1e-06

        def _layernorm(x, g, b):
            m = jnp.mean(x, axis=-1, keepdims=True)
            var = jnp.var(x, axis=-1, keepdims=True)
            return (x - m) * jax.lax.rsqrt(var + EPS_LN) * g + b

        def _split_heads(x):
            bsz, sl, _ = x.shape
            return x.reshape(bsz, sl, HEADS, DEPTH).transpose(0, 2, 1, 3)
        bsz = q.shape[0]
        em = mask[:, None, :, None]
        qh = _split_heads(_layernorm(q @ wq, ln_gamma, ln_beta))
        kh = _split_heads(_layernorm(k @ wk, ln_gamma, ln_beta))
        vh = _split_heads(_layernorm(v @ wv, ln_gamma, ln_beta))
        q_prime = jax.nn.relu(qh) + EPS_K
        k_prime = (jax.nn.relu(kh) + EPS_K) * em
        vh = vh * em
        kv = jnp.einsum('bhnd,bhne->bhde', k_prime, vh)
        z = 1.0 / (jnp.einsum('bhnd,bhd->bhn', q_prime, k_prime.sum(axis=-2)) + EPS_K)
        att = jnp.einsum('bhnd,bhde,bhn->bhne', q_prime, kv, z)
        att = att.reshape(bsz, -1, D_MODEL)
        out = att @ dense_w + dense_b
        return _layernorm(out, ln_gamma, ln_beta)

    def _L2_attn_ref(x, W_qkv, W_o):
        import jax, jax.numpy as jnp
        import numpy as np
        D = 256
        H = 16
        DK = D // H
        CHUNK = 64
        EPS = 1e-05

        def _layernorm_noaffine(k):
            mu = jnp.mean(k, axis=-1, keepdims=True)
            var = jnp.mean((k - mu) ** 2, axis=-1, keepdims=True)
            return (k - mu) / jnp.sqrt(var + EPS)

        def _linear_attn(x, W_qkv, W_o):
            B, L, Dm = x.shape
            qkv = (x @ W_qkv).reshape(B, L, 3, H, DK)
            q, k, v = (qkv[:, :, 0], qkv[:, :, 1], qkv[:, :, 2])
            k = _layernorm_noaffine(k)
            nC = L // CHUNK
            to_chunks = lambda t: t.reshape(B, nC, CHUNK, H, DK).transpose(1, 0, 2, 3, 4)
            qc, kc, vc = (to_chunks(q), to_chunks(k), to_chunks(v))
            causal = jnp.tril(jnp.ones((CHUNK, CHUNK), dtype=bool))

            def step(S, chunk):
                q_c, k_c, v_c = chunk
                inter = jnp.einsum('bhde,bthe->bthd', S, q_c)
                scores = jnp.einsum('bthd,bshd->bhts', q_c, k_c)
                scores = jnp.where(causal, scores, 0.0)
                intra = jnp.einsum('bhts,bshd->bthd', scores, v_c)
                S = S + jnp.einsum('bthd,bthe->bhde', v_c, k_c)
                return (S, inter + intra)
            S0 = jnp.zeros((B, H, DK, DK), dtype=x.dtype)
            _, ys = jax.lax.scan(step, S0, (qc, kc, vc))
            y = ys.transpose(1, 0, 2, 3, 4).reshape(B, L, Dm)
            return y @ W_o
        return _linear_attn(x, W_qkv, W_o)

    def _L2_ffn_ref(x, gate_w, fc1_w, fc1_b, fc2_w, fc2_b):
        import jax, jax.numpy as jnp
        import numpy as np
        E = 8
        K = 2
        D = 256
        H = 1024
        CAP_FACTOR = 1.0
        B, S, Dm = x.shape
        xf = x.reshape(-1, Dm)
        N = xf.shape[0]
        cap = int(K * CAP_FACTOR * ((N + E - 1) // E))
        logits = xf @ gate_w.T
        scores = jax.nn.softmax(logits, axis=-1)
        topv, topi = jax.lax.top_k(scores, K)
        gates = topv / jnp.sum(topv, axis=-1, keepdims=True)
        offset = jnp.zeros((E,), jnp.int32)
        locs = []
        for j in range(K):
            mask = jax.nn.one_hot(topi[:, j], E, dtype=jnp.int32)
            loc_in = jnp.cumsum(mask, axis=0) - 1 + offset[None, :]
            locs.append(jnp.take_along_axis(loc_in, topi[:, j:j + 1], axis=1)[:, 0])
            offset = offset + mask.sum(axis=0)
        loc = jnp.stack(locs, axis=1)
        valid = loc < cap
        flat_idx = jnp.where(valid, topi * cap + loc, 0)
        w = valid.astype(xf.dtype)
        disp = jnp.zeros((E * cap, Dm), xf.dtype)
        disp = disp.at[flat_idx.reshape(-1)].add((xf[:, None, :] * w[:, :, None]).reshape(-1, Dm))
        de = disp.reshape(E, cap, Dm)
        h = jax.nn.relu(jnp.einsum('ecd,ehd->ech', de, fc1_w) + fc1_b)
        eo = jnp.einsum('ech,ehd->ecd', h, fc2_w) + fc2_b
        gathered = eo.reshape(E * cap, Dm)[flat_idx]
        out = jnp.sum(gathered * (gates * w)[:, :, None], axis=1)
        return out.reshape(B, S, Dm)

    def _L3_xattn_ref(queries, keys, values, mask):
        import jax, jax.numpy as jnp
        import numpy as np
        N_HEADS = 16
        NEG_BIAS = -1000000000.0

        def _split_heads(x):
            B, S, D = x.shape
            return x.reshape(B, S, N_HEADS, D // N_HEADS).transpose(0, 2, 1, 3)
        q = _split_heads(queries)
        k = _split_heads(keys)
        v = _split_heads(values)
        d_head = q.shape[-1]
        sim = jnp.einsum('bhqd,bhkd->bhqk', q, k) / jnp.sqrt(jnp.float32(d_head))
        bias = NEG_BIAS * (1.0 - mask.astype(sim.dtype))[:, None]
        sim = sim + bias
        weights = jax.nn.softmax(sim, axis=-1)
        out = jnp.einsum('bhqk,bhkd->bhqd', weights, v)
        B, H, Sq, d = out.shape
        return out.transpose(0, 2, 1, 3).reshape(B, Sq, H * d)

    def _L3_attn_ref(x, Wq, bq, Wk, bk, Wv, bv, Wo, bo):
        import jax, jax.numpy as jnp
        import numpy as np
        DIM = 256
        HEADS = 16
        HEAD_DIM = DIM // HEADS
        B, N = (2, 512)
        SCALE = 1.0 / np.float32(np.sqrt(DIM))

        def _split_heads(t):
            b, n, _ = t.shape
            return jnp.moveaxis(t.reshape(b, n, HEADS, HEAD_DIM), 2, 0)
        q = _split_heads(x @ Wq.T + bq)
        k = _split_heads(x @ Wk.T + bk)
        v = _split_heads(x @ Wv.T + bv)
        scores = jnp.einsum('hbnd,hbmd->hbnm', k, q) * SCALE
        attn = jax.nn.softmax(scores, axis=-1)
        out = jnp.einsum('hbnm,hbmd->hbnd', attn, v)
        out = jnp.moveaxis(out, 0, 2).reshape(x.shape[0], x.shape[1], DIM)
        return out @ Wo.T + bo

    def _L3_ffn_ref(x, g_info, W_qkv, W_proj, b_proj):
        import jax, jax.numpy as jnp
        import numpy as np
        B, N, C, H, REG = (1, 2309, 256, 16, 5)
        D = C // H
        Bx, Nx, Cx = x.shape
        scale = D ** (-0.5)
        qkv = (x @ W_qkv).reshape(Bx, Nx, 3, H, D)
        q, k, v = (qkv[:, :, 0], qkv[:, :, 1], qkv[:, :, 2])
        g_layer = g_info[0].reshape(-1, H, D)
        q_g = g_layer[0]
        q_pure = q[:, REG:]
        q_n = q_pure / jnp.linalg.norm(q_pure, axis=-1, keepdims=True)
        qg_n = q_g / jnp.linalg.norm(q_g, axis=-1, keepdims=True)
        sim = (qg_n[None, None] * q_n).sum(-1).mean(-1)
        sim = (sim - sim.min()) / (sim.max() - sim.min())
        pos = sim > 0.9
        logits = jnp.einsum('bqhd,bkhd->bhqk', q * scale, k)

        def masked_attn(tok_mask):
            key_mask = jnp.concatenate([jnp.ones((Bx, REG), bool), tok_mask], axis=1)
            l = jnp.where(key_mask[:, None, None, :], logits, -jnp.inf)
            a = jax.nn.softmax(l, axis=-1)
            return jnp.einsum('bhqk,bkhd->bqhd', a, v)
        x_pos = masked_attn(pos)
        x_neg = masked_attn(~pos)
        reg_out = (x_pos[:, :REG] + x_neg[:, :REG]) * 0.5
        tok_out = jnp.where(pos[:, :, None, None], x_pos[:, REG:], x_neg[:, REG:])
        out = jnp.concatenate([reg_out, tok_out], axis=1).reshape(Bx, Nx, Cx)
        return out @ W_proj + b_proj
    x = x + _L0_xattn_ref(_layernorm(x, axis=-1), ctx_1024, L0_xattn_w_kv, L0_xattn_w_q, L0_xattn_w_out1, L0_xattn_w_out2, L0_xattn_gamma)
    x = x + _L0_attn_ref(_layernorm(x, axis=-1), L0_attn_decay_logit, L0_attn_out_scale, L0_attn_q_scale, L0_attn_k_scale)
    x = x + _L0_ffn_ref(_layernorm(x, axis=-1), L0_ffn_router_w, L0_ffn_router_bias, L0_ffn_bank_mag, L0_ffn_bank_freq, L0_ffn_bank_phase, L0_ffn_bank_down, L0_ffn_norm_w)
    x = x + _L1_xattn_ref(ctx_1024, _layernorm(x, axis=-1), mask_BxS2_bk1, L1_xattn_Wq, L1_xattn_Wkv, L1_xattn_Wo, L1_xattn_ln_x_g, L1_xattn_ln_x_b, L1_xattn_ln_l_g, L1_xattn_ln_l_b, L1_xattn_ln_o_g, L1_xattn_ln_o_b)
    x = x + _L1_attn_ref(_layernorm(x, axis=-1), L1_attn_ln_g, L1_attn_ln_b, L1_attn_mh_g, L1_attn_mh_b, L1_attn_W_up_l, L1_attn_b_up_l, L1_attn_W_up_r, L1_attn_b_up_r, L1_attn_W_down, L1_attn_b_down, L1_attn_conv_w, L1_attn_conv_b, L1_attn_W_skip, L1_attn_b_skip, L1_attn_W_i, L1_attn_b_i, L1_attn_W_f, L1_attn_b_f, L1_attn_W_o, L1_attn_b_o, L1_attn_W_q, L1_attn_b_q, L1_attn_W_k, L1_attn_b_k, L1_attn_W_v, L1_attn_b_v)
    x = x + _L1_ffn_ref(_layernorm(x, axis=-1), L1_ffn_wr, L1_ffn_br, L1_ffn_W1, L1_ffn_b1, L1_ffn_W2, L1_ffn_b2)
    x = x + _L2_xattn_ref(_layernorm(x, axis=-1), ctx_1024, ctx_1024, mask_BxS2_ff1, L2_xattn_wq, L2_xattn_wk, L2_xattn_wv, L2_xattn_ln_gamma, L2_xattn_ln_beta, L2_xattn_dense_w, L2_xattn_dense_b)
    x = x + _L2_attn_ref(_layernorm(x, axis=-1), L2_attn_W_qkv, L2_attn_W_o)
    x = x + _L2_ffn_ref(_layernorm(x, axis=-1), L2_ffn_gate_w, L2_ffn_fc1_w, L2_ffn_fc1_b, L2_ffn_fc2_w, L2_ffn_fc2_b)
    x = x + _L3_xattn_ref(_layernorm(x, axis=-1), ctx_1024, ctx_1024, mask_BxSxS2_ik1)
    x = x + _L3_attn_ref(_layernorm(x, axis=-1), L3_attn_Wq, L3_attn_bq, L3_attn_Wk, L3_attn_bk, L3_attn_Wv, L3_attn_bv, L3_attn_Wo, L3_attn_bo)
    x = x + _L3_ffn_ref(_layernorm(x, axis=-1), L3_ffn_g_info, L3_ffn_W_qkv, L3_ffn_W_proj, L3_ffn_b_proj)
    return x

_drawn_inputs = setup_inputs


def setup_inputs(seed=0):
    import zlib

    import numpy as np

    out = dict(_drawn_inputs(seed))
    spreads = {'L0_xattn_gamma': (1.0, 0.2),
     'L0_attn_q_scale': (1.0, 0.6),
     'L0_attn_k_scale': (1.0, 0.6),
     'L0_ffn_router_bias': (0.0, 2.0),
     'L0_ffn_norm_w': (1.0, 0.6),
     'L1_xattn_ln_x_g': (1.0, 0.6),
     'L1_xattn_ln_x_b': (0.0, 0.8),
     'L1_xattn_ln_l_g': (1.0, 0.6),
     'L1_xattn_ln_l_b': (0.0, 0.8),
     'L1_xattn_ln_o_g': (1.0, 0.6),
     'L1_xattn_ln_o_b': (0.0, 0.8),
     'L1_attn_ln_g': (1.0, 0.6),
     'L1_attn_ln_b': (0.0, 0.8),
     'L1_attn_mh_g': (1.0, 0.6),
     'L1_attn_mh_b': (0.0, 2.0),
     'L1_attn_b_up_l': (0.0, 0.8),
     'L1_attn_b_up_r': (0.0, 0.8),
     'L1_attn_b_down': (0.0, 2.0),
     'L1_attn_b_skip': (0.0, 2.0),
     'L1_attn_b_i': (0.0, 2.0),
     'L1_attn_b_f': (0.0, 2.0),
     'L1_attn_b_o': (0.0, 2.0),
     'L1_attn_b_q': (0.0, 2.0),
     'L1_attn_b_k': (0.0, 2.0),
     'L1_attn_b_v': (0.0, 2.0),
     'L1_ffn_b1': (0.0, 2.0),
     'L1_ffn_b2': (0.0, 2.0),
     'L2_xattn_ln_gamma': (1.0, 0.6),
     'L2_xattn_ln_beta': (0.0, 2.0),
     'L2_xattn_dense_b': (0.0, 2.0),
     'L2_ffn_fc1_b': (0.0, 2.0),
     'L2_ffn_fc2_b': (0.0, 2.0),
     'L3_ffn_b_proj': (0.0, 2.0)}
    factors = {'L0_xattn_w_q': 8.0,
     'L0_ffn_router_w': 7.899,
     'L0_ffn_bank_mag': 6.694,
     'L0_ffn_bank_freq': 8.0,
     'L0_ffn_bank_phase': 8.0,
     'L0_ffn_bank_down': 7.202,
     'L1_xattn_Wq': 8.0,
     'L1_xattn_Wkv': 8.0,
     'L1_xattn_Wo': 8.0,
     'L1_attn_W_up_l': 8.0,
     'L1_attn_W_up_r': 8.0,
     'L1_attn_W_down': 8.0,
     'L1_attn_conv_w': 8.0,
     'L1_attn_W_skip': 8.0,
     'L1_attn_W_i': 185.739,
     'L1_attn_W_f': 200.0,
     'L1_attn_W_o': 185.918,
     'L1_attn_W_q': 188.183,
     'L1_attn_W_k': 193.367,
     'L1_attn_W_v': 200.0,
     'L1_ffn_wr': 199.382,
     'L1_ffn_W1': 200.0,
     'L1_ffn_W2': 181.626,
     'L2_xattn_wq': 200.0,
     'L2_xattn_wk': 200.0,
     'L2_xattn_wv': 200.0,
     'L2_xattn_dense_w': 200.0,
     'L2_ffn_gate_w': 200.0,
     'L2_ffn_fc1_w': 200.0,
     'L2_ffn_fc2_w': 200.0,
     'L3_attn_Wq': 200.0,
     'L3_attn_bq': 200.0,
     'L3_attn_Wk': 200.0,
     'L3_attn_bk': 200.0,
     'L3_attn_Wv': 200.0,
     'L3_attn_bv': 200.0,
     'L3_attn_Wo': 200.0,
     'L3_attn_bo': 200.0,
     'L3_ffn_g_info': 200.0,
     'L3_ffn_W_qkv': 200.0,
     'L3_ffn_W_proj': 200.0,
     'L2_attn_W_qkv': 8.0,
     'L2_attn_W_o': 8.0}
    for name, (base, spread) in spreads.items():
        noise = np.random.default_rng([zlib.crc32(name.encode()), seed]).standard_normal(out[name].shape)
        drawn = base * np.exp(spread * noise) if base else spread * noise
        out[name] = jnp.asarray(drawn.astype(out[name].dtype))
    for name, factor in factors.items():
        out[name] = (out[name] * factor).astype(out[name].dtype)
    return out
```

```python
from contextlib import ExitStack

import concourse.bass as bass
from concourse import mybir

ALU = mybir.AluOpType
ACT = mybir.ActivationFunctionType
AX = mybir.AxisListType
F32 = mybir.dt.float32
I32 = mybir.dt.int32

T = 128
D = 256
DC = D // 128
S2 = 12544
CH = 896
CT = CH // 128
HALF = CH // 2
NCH = S2 // CH
ARENA = 51200
FAR = -1.0e30


class Stage:

    def __init__(self, nc, name):
        self.nc, self.name, self.ctx, self.sems = nc, name, ExitStack(), {}

    def __enter__(self):
        self.ctx.__enter__()
        self.arena = self.ctx.enter_context(self.nc.sbuf_tensor(f"{self.name}_sbuf", [128, ARENA], F32))
        self.psum = self.ctx.enter_context(self.nc.psum_tensor(f"{self.name}_psum", [128, 8, 512], F32))
        self.used = self.banks = 0
        return self

    def __exit__(self, *e):
        self.region.__exit__(*e)
        self.nc.clear_and_free_semaphores(list(self.sems.values()))
        self.nc.all_engine_barrier()
        return self.ctx.__exit__(*e)

    def sb(self, name, shape, dt=F32):
        n = 1
        for d in shape[1:]:
            n *= d
        assert self.used + n <= ARENA, f"{self.name}: no room for {name}"
        v = self.arena[0:shape[0], self.used:self.used + n]
        self.used += n
        if dt != F32:
            v = v.bitcast(dt)
        names = "abcd"[:len(shape) - 1]
        if len(names) > 1:
            v = v.rearrange(f"p ({' '.join(names)}) -> p {' '.join(names)}", **dict(zip(names, shape[1:])))
        return v

    def ps(self, name, banks=1):
        at = self.banks
        self.banks += banks
        assert self.banks <= 8, f"{self.name}: no bank for {name}"
        return self.psum[:, at, :] if banks == 1 else self.psum[:, at:at + banks, :]

    def sem(self, name):
        if name not in self.sems:
            self.sems[name] = self.nc.alloc_semaphore(f"{self.name}_{name}")
        return self.sems[name]

    def block(self):
        self.region = self.nc.Block()
        return self.region.__enter__()


def linker(eng, sem, base=0):
    count = [0]

    def link(ins):
        count[0] += 1
        ins.then_inc(sem, 1)
        eng.wait_ge(sem, base + count[0])

    link.count = count
    return link


def dve_moments(dve, link, src, st, mv, eps, done):
    link(dve.bn_stats(st, src))
    link(dve.bn_aggr(mv[:, 0:2], st))
    dve.tensor_scalar(mv[:, 1:2], mv[:, 1:2], eps, None, ALU.add).then_inc(done, 1)


def dve_rsqrt(dve, link, r, root, var):
    link(dve.reciprocal(r, root))
    link(dve.tensor_tensor(root, r, r, ALU.mult))
    link(dve.tensor_tensor(root, root, var, ALU.mult))
    link(dve.tensor_scalar(root, root, -0.5, 1.5, ALU.mult, ALU.add))
    link(dve.tensor_tensor(r, r, root, ALU.mult))


def dve_rescale(dve, link, dst, src, mv, done):
    dve_rsqrt(dve, link, mv[:, 3:4], mv[:, 2:3], mv[:, 1:2])
    dve.tensor_scalar(dst, src, mv[:, 0:1], mv[:, 3:4], ALU.subtract, ALU.mult).then_inc(done, 1)
    dve.wait_ge(done, 1)


class NormX:

    def __init__(self, s, x, ident, ps):
        self.s, self.x, self.ident, self.ps = s, x, ident, ps
        self.st, self.mv = s.sb("x_st", [128, 6]), s.sb("x_mv", [128, 4])
        self.xn, self.xnT = s.sb("xn", [128, D]), s.sb("xnT", [128, DC, T])

    def dve(self, dve, link):
        s = self.s
        dve_moments(dve, link, self.x[:, :], self.st[:, :], self.mv, 1e-5, s.sem("x_var"))
        dve.wait_ge(s.sem("x_std"), 1)
        dve_rescale(dve, link, self.xn[:, :], self.x[:, :], self.mv, s.sem("xn"))
        dve.wait_ge(s.sem("xnT_ps"), 1)
        dve.tensor_copy(self.xnT[:, :, :], self.ps[:, 0:D].rearrange("p (c t) -> p c t", c=DC)).then_inc(s.sem("xnT"), 1)

    def act(self, act):
        s = self.s
        act.wait_ge(s.sem("x_var"), 1)
        act.activation(self.mv[:, 2:3], self.mv[:, 1:2], ACT.Sqrt).then_inc(s.sem("x_std"), 1)

    def pe(self, pe):
        s = self.s
        pe.wait_ge(s.sem("xn"), 1)
        for c in range(DC):
            mm = pe.transpose(self.ps[:, c * 128:(c + 1) * 128], self.xn[:, c * 128:(c + 1) * 128], self.ident[:, :])
        mm.then_inc(s.sem("xnT_ps"), 1)


class ContextAttention:

    def __init__(self, s, heads, width, qt, values, kT_dram, v_dram, ident, mask=None, mask_dram=None,
                 bias_per_one=1.0e9, tail=None):
        self.s, self.H, self.W, self.qt, self.values = s, heads, width, qt, values
        self.kT_dram, self.v_dram, self.ident = kT_dram, v_dram, ident
        self.mask, self.mask_dram, self.bias_per_one, self.tail = mask, mask_dram, bias_per_one, tail
        self.U = 2 * heads
        self.kT = s.sb("ca_kT", [128, 2, DC, CH])
        self.v = s.sb("ca_v", [128, 2, CT, D])
        self.p = s.sb("ca_p", [128, 2, CH])
        self.pT = s.sb("ca_pT", [128, 2, CT, T])
        self.acc = s.sb("ca_acc", [128, heads, width])
        self.l = s.sb("ca_l", [128, heads])
        self.m = s.sb("ca_m", [128, 2, heads])
        self.mb = s.sb("ca_mb", [128, 2])
        self.negm = s.sb("ca_negm", [128, 4])
        self.alpha = s.sb("ca_alpha", [128, 4])
        self.rs = s.sb("ca_rs", [128, 4])
        if mask:
            self.raw = s.sb("ca_raw", [128, 2, CH], I32)
            self.bias = s.sb("ca_bias", [128, 2, CH])
            self.sm = s.sb("ca_sm", [128, 2, CH])
        self.ps_s = [s.ps(f"ca_s{i}", 2) for i in range(2)]
        self.ps_t = s.ps("ca_t", 2).rearrange("p b (t k) -> p (b t) k", k=T)
        self.ps_o = [s.ps(f"ca_o{i}") for i in range(2)]
        self.pre = heads if tail else 0

    def load(self, sp, j, chunk):
        s = self.s
        sp.dma_start(self.kT[:, j, :, :], self.kT_dram[:, :, bass.ds(chunk * CH, CH)]).then_inc(s.sem(f"kv_in{j}"), 16)
        sp.dma_start(self.v[:, j, :, :], self.v_dram[:, bass.ds(chunk * CT, CT), :]).then_inc(s.sem(f"kv_in{j}"), 16)
        if self.mask:
            sp.dma_start(self.raw[:, j, :], self.mask_dram[:, bass.ds(chunk * CH, CH)]).then_inc(s.sem(f"kv_in{j}"), 16)

    def sp(self, sp):
        s, H, U = self.s, self.H, self.U
        self.load(sp, 0, 0)
        self.load(sp, 1, 1)
        with sp.Fori(0, NCH // 2 - 1) as it:
            for j in range(2):
                sp.wait_ge(s.sem("pv"), it * U + (self.pre + H * (j + 1)))
                if self.mask:
                    sp.wait_ge(s.sem("bias"), it * 2 + (j + 1))
                self.load(sp, j, it * 2 + (2 + j))

    @property
    def per_chunk(self):
        return 48 if self.mask else 32

    def pe_scores(self, pe, base, u, h, j):
        s, b = self.s, u % 2
        if self.mask and j is not None:
            pe.wait_ge(s.sem("masked"), base - self.pre + max(0, u - 1))
        else:
            pe.wait_ge(s.sem("p"), base + max(0, u - 1))
        for i in range(2 if j is not None else 1):
            parts = self.qt(h)
            for n, (q, c) in enumerate(parts):
                if j is None:
                    rhs, out = self.tail[0][:, c, :], self.ps_s[b][:, 0, 0:T]
                else:
                    rhs, out = self.kT[:, j, c, i * HALF:(i + 1) * HALF], self.ps_s[b][:, i, 0:HALF]
                mm = pe.matmul(out, q, rhs, start=(n == 0), stop=(n == len(parts) - 1))
        mm.then_inc(s.sem("scores"), 1)

    def pe_transposes(self, pe, base, u, j):
        s = self.s
        pe.wait_ge(s.sem("p"), base + u + 1)
        pe.wait_ge(s.sem("pT"), base + u)
        for t in range(CT if j is not None else 1):
            mm = pe.transpose(self.ps_t[:, t, :], self.p[:, u % 2, t * 128:(t + 1) * 128], self.ident[:, :])
        mm.then_inc(s.sem("pT_ps"), 1)

    def pe_values(self, pe, base, u, h, j):
        s, b = self.s, u % 2
        pe.wait_ge(s.sem("pT"), base + u + 1)
        pe.wait_ge(s.sem("acc"), base + max(0, u - 1))
        lo, hi = self.values(h)
        n = CT if j is not None else 1
        for t in range(n):
            v = self.tail[1][:, lo:hi] if j is None else self.v[:, j, t, lo:hi]
            mm = pe.matmul(self.ps_o[b][:, 0:self.W], self.pT[:, b, t, :], v, start=(t == 0), stop=(t == n - 1))
        mm.then_inc(s.sem("pv"), 1)

    def pe_units(self, pe, base, units):
        n = len(units)
        for u in range(n + 2):
            if u < n:
                h, j, first = units[u]
                if first is not None:
                    pe.wait_ge(self.s.sem(f"kv_in{j}"), first)
                self.pe_scores(pe, base, u, h, j)
            if 1 <= u <= n:
                self.pe_transposes(pe, base, u - 1, units[u - 1][1])
            if u >= 2:
                self.pe_values(pe, base, u - 2, units[u - 2][0], units[u - 2][1])

    def units(self, it=None):
        if it is None:
            return [(h, None, None) for h in range(self.H)]
        return [(h, j, it * self.per_chunk + self.per_chunk if h == 0 else None) for j in range(2) for h in range(self.H)]

    def pe(self, pe):
        if self.tail:
            self.pe_units(pe, 0, self.units())
        with pe.Fori(0, NCH // 2) as it:
            self.pe_units(pe, it * self.U + self.pre, self.units(it))

    def act_units(self, act, base, units):
        s, n = self.s, len(units)
        for u in range(n + 1):
            if u < n:
                h, j, _ = units[u]
                b, q = u % 2, u % 4
                act.wait_ge(s.sem("negm"), base + u + 1)
                act.wait_ge(s.sem("sums"), base + max(0, u - 3))
                act.wait_ge(s.sem("acc"), base + max(0, u - 3))
                old = 1 if j is None else j
                act.activation(self.alpha[:, q:q + 1], self.m[:, old, h:h + 1], ACT.Exp,
                               bias=self.negm[:, q:q + 1]).then_inc(s.sem("alpha"), 1)
                act.wait_ge(s.sem("pT_ps"), base + max(0, u - 1))
                if j is None:
                    src, dst = self.ps_s[b][:, 0, 0:T], self.p[:, b, 0:T]
                elif self.mask:
                    src, dst = self.sm[:, b, :], self.p[:, b, :]
                else:
                    src = self.ps_s[b][:, :, 0:HALF]
                    dst = self.p[:, b, :].rearrange("p (i c) -> p i c", i=2)
                act.activation(dst, src, ACT.Exp, bias=self.negm[:, q:q + 1],
                               accum_out=self.rs[:, q:q + 1]).then_inc(s.sem("p"), 1)
            if u >= 1:
                w, j = u - 1, units[u - 1][1]
                k = CT if j is not None else 1
                act.wait_ge(s.sem("pT_ps"), base + w + 1)
                act.wait_ge(s.sem("pv"), base + max(0, w - 1))
                act.activation(self.pT[:, w % 2, 0:k, :], self.ps_t[:, 0:k, :], ACT.Copy).then_inc(s.sem("pT"), 1)

    def act(self, act):
        if self.tail:
            self.act_units(act, 0, self.units())
        with act.Fori(0, NCH // 2) as it:
            self.act_units(act, it * self.U + self.pre, self.units(it))

    def dve_units(self, dve, base, units, link, it=0):
        s, n = self.s, len(units)
        for u in range(n + 3):
            if u < n:
                h, j, first = units[u]
                b, q = u % 2, u % 4
                if self.mask and first is not None:
                    dve.wait_ge(s.sem(f"kv_in{j}"), first)
                    dve.tensor_scalar(self.bias[:, j, :], self.raw[:, j, :], 1.0, self.bias_per_one,
                                      ALU.subtract, ALU.mult).then_inc(s.sem("bias"), 1)
                    dve.wait_ge(s.sem("bias"), it * 2 + (j + 1))
                dve.wait_ge(s.sem("scores"), base + u + 1)
                if j is None:
                    src = self.ps_s[b][:, 0, 0:T]
                elif self.mask:
                    dve.wait_ge(s.sem("p"), base + max(0, u - 1))
                    src = self.sm[:, b, :]
                    dve.tensor_tensor(src.rearrange("p (i c) -> p i c", i=2), self.ps_s[b][:, :, 0:HALF],
                                      self.bias[:, j, :].rearrange("p (i c) -> p i c", i=2),
                                      ALU.add).then_inc(s.sem("masked"), 1)
                    dve.wait_ge(s.sem("masked"), base - self.pre + u + 1)
                else:
                    src = self.ps_s[b][:, :, 0:HALF]
                link(dve.tensor_reduce(self.mb[:, b:b + 1], src, AX.XY if len(src.shape) == 3 else AX.X, ALU.max))
                old, new = (1, 0) if j is None else (j, 1 - j)
                dve.wait_ge(s.sem("alpha"), base + max(0, u - self.H + 1))
                link(dve.tensor_tensor(self.m[:, new, h:h + 1], self.m[:, old, h:h + 1], self.mb[:, b:b + 1], ALU.max))
                dve.wait_ge(s.sem("p"), base + max(0, u - 3))
                dve.tensor_scalar(self.negm[:, q:q + 1], self.m[:, new, h:h + 1], -1.0, None,
                                  ALU.mult).then_inc(s.sem("negm"), 1)
            if u >= 3:
                w = u - 3
                h, q = units[w][0], w % 4
                dve.wait_ge(s.sem("pv"), base + w + 1)
                dve.wait_ge(s.sem("p"), base + w + 1)
                dve.wait_ge(s.sem("sums"), base + max(0, w - self.H + 1))
                dve.scalar_tensor_tensor(out=self.l[:, h:h + 1], in0=self.l[:, h:h + 1],
                                         scalar=self.alpha[:, q:q + 1], in1=self.rs[:, q:q + 1],
                                         op0=ALU.mult, op1=ALU.add).then_inc(s.sem("sums"), 1)
                dve.wait_ge(s.sem("acc"), base + max(0, w - self.H + 1))
                dve.scalar_tensor_tensor(out=self.acc[:, h, :], in0=self.acc[:, h, :],
                                         scalar=self.alpha[:, q:q + 1], in1=self.ps_o[w % 2][:, 0:self.W],
                                         op0=ALU.mult, op1=ALU.add).then_inc(s.sem("acc"), 1)

    def dve(self, dve):
        s = self.s
        link = linker(dve, s.sem("dve_init"))
        link(dve.memset(self.acc[:, :, :], 0.0))
        link(dve.memset(self.l[:, :], 0.0))
        link(dve.memset(self.m[:, :, :], FAR))
        if self.tail:
            self.dve_units(dve, 0, self.units(), linker(dve, s.sem("dve_pre")))
        U = self.U
        steps = 2 * U
        with dve.Fori(0, NCH // 2) as it:
            link = linker(dve, s.sem("dve_loop"), it * steps)
            self.dve_units(dve, it * U + self.pre, self.units(it), link, it)
            assert link.count[0] == steps
        dve.wait_ge(s.sem("sums"), NCH * self.H + self.pre)
        dve.wait_ge(s.sem("acc"), NCH * self.H + self.pre)
        link = linker(dve, s.sem("dve_end"))
        link(dve.reciprocal(self.l[:, :], self.l[:, :]))
        for h in range(self.H):
            dve.tensor_scalar(self.acc[:, h, :], self.acc[:, h, :], self.l[:, h:h + 1], None,
                              ALU.mult).then_inc(s.sem("attended"), 1)


def cols(ps, c=DC):
    return ps[:, 0:c * 128].rearrange("p (c t) -> p c t", c=c)


def finish(eng, ins, sem, n=1):
    ins.then_inc(sem, 1)
    eng.wait_ge(sem, n)


def pe_transposes(pe, ps, src, ident, n=DC):
    for c in range(n):
        mm = pe.transpose(ps[:, c * 128:(c + 1) * 128], src[:, c * 128:(c + 1) * 128], ident[:, :])
    return mm


def pe_dense(pe, out, lhsT, rhs, n=DC):
    for c in range(n):
        mm = pe.matmul(out, lhsT(c), rhs(c), start=(c == 0), stop=(c == n - 1))
    return mm


class WideHeads:

    HD = 64

    def __init__(self, s, H, A, prefix, ident, scale):
        self.s, self.H, self.A, self.prefix, self.ident, self.scale = s, H, A, prefix, ident, scale
        HD = self.HD
        self.wq, self.wkT = s.sb("wq", [128, DC, H * HD]), s.sb("wkT", [HD, H, D])
        self.wv, self.wo = s.sb("wv", [128, DC, H * HD]), s.sb("wo", [HD, H, D])
        self.qT = s.sb("qT", [HD, H, T])
        self.qk = s.sb("qk", [128, H, DC, T])
        self.aT, self.oT = s.sb("aT", [128, 2, DC, T]), s.sb("oT", [HD, 2, T])

    def qt(self, h):
        return [(self.qk[:, h, c, :], c) for c in range(DC)]

    def use(self, ca, nxT, nxT_sem):
        self.ca, self.nxT, self.nxT_sem = ca, nxT, nxT_sem
        self.banks = [ca.ps_o[1], ca.ps_o[0]]

    def sp(self, sp):
        for name, dst in (("wq", self.wq), ("wkT", self.wkT), ("wv", self.wv), ("wo", self.wo)):
            sp.dma_start(dst[:, :, :], self.A[self.prefix + name]).then_inc(self.s.sem(name + "_in"), 16)

    def pe_queries(self, pe):
        s, H, HD = self.s, self.H, self.HD
        pe.wait_ge(s.sem("wq_in"), 16)
        pe.wait_ge(self.nxT_sem, 1)
        for g in range(H // 4):
            if g >= 2:
                pe.wait_ge(s.sem("qT"), g - 1)
            for h in range(4 * g, 4 * g + 4):
                mm = pe_dense(pe, self.banks[g % 2][0:HD, (h % 4) * T:(h % 4 + 1) * T],
                              lambda c: self.wq[:, c, h * HD:(h + 1) * HD], lambda c: self.nxT[:, c, :])
            mm.then_inc(s.sem("qT_ps"), 1)
        pe.wait_ge(s.sem("wkT_in"), 16)
        pe.wait_ge(s.sem("qT"), H // 4)
        for g in range(H // 2):
            if g >= 2:
                pe.wait_ge(s.sem("qk"), g - 1)
            for h in range(2 * g, 2 * g + 2):
                for c in range(DC):
                    k = (h % 2) * DC + c
                    mm = pe.matmul(self.banks[g % 2][:, k * T:(k + 1) * T], self.wkT[:, h, c * 128:(c + 1) * 128],
                                   self.qT[:, h, :], start=True, stop=True)
            mm.then_inc(s.sem("qk_ps"), 1)
        pe.wait_ge(s.sem("qk"), H // 2)

    def dve_queries(self, dve):
        s, HD = self.s, self.HD
        for g in range(self.H // 4):
            dve.wait_ge(s.sem("qT_ps"), g + 1)
            dve.tensor_scalar(self.qT[:, 4 * g:4 * g + 4, :],
                              self.banks[g % 2][0:HD, :].rearrange("p (h t) -> p h t", h=4),
                              self.scale, None, ALU.mult).then_inc(s.sem("qT"), 1)

    def act_queries(self, act):
        s = self.s
        for g in range(self.H // 2):
            act.wait_ge(s.sem("qk_ps"), g + 1)
            act.activation(self.qk[:, 2 * g:2 * g + 2, :, :],
                           self.banks[g % 2][:, :].rearrange("p (h c t) -> p h c t", h=2, c=DC),
                           ACT.Copy).then_inc(s.sem("qk"), 1)

    def pe_outputs(self, pe, ps):
        s, H, HD, ca = self.s, self.H, self.HD, self.ca
        pe.wait_ge(s.sem("wv_in"), 16)
        pe.wait_ge(s.sem("wo_in"), 16)
        for h in range(H + 2):
            if h < H:
                pe.wait_ge(s.sem("attended"), h + 1)
                if h >= 2:
                    pe.wait_ge(s.sem("aT"), h - 1)
                pe_transposes(pe, ca.ps_s[h % 2][:, 0, :], ca.acc[:, h, :], self.ident).then_inc(s.sem("aT_ps"), 1)
            if 1 <= h <= H:
                g = h - 1
                pe.wait_ge(s.sem("aT"), g + 1)
                if g >= 2:
                    pe.wait_ge(s.sem("oT"), g - 1)
                pe_dense(pe, ca.ps_s[g % 2][0:HD, 1, 0:T], lambda c: self.wv[:, c, g * HD:(g + 1) * HD],
                         lambda c: self.aT[:, g % 2, c, :]).then_inc(s.sem("oT_ps"), 1)
            if h >= 2:
                g = h - 2
                pe.wait_ge(s.sem("oT"), g + 1)
                pe.matmul(ps[:, 0:D], self.oT[:, g % 2, :], self.wo[:, g, :], start=(g == 0),
                          stop=(g == H - 1)).then_inc(s.sem("out_ps"), 1)

    def dve_outputs(self, dve):
        s = self.s
        for h in range(self.H):
            dve.wait_ge(s.sem("aT_ps"), h + 1)
            if h >= 2:
                dve.wait_ge(s.sem("oT_ps"), h - 1)
            dve.tensor_copy(self.aT[:, h % 2, :, :], cols(self.ca.ps_s[h % 2][:, 0, :])).then_inc(s.sem("aT"), 1)

    def act_outputs(self, act):
        s = self.s
        for h in range(self.H):
            act.wait_ge(s.sem("oT_ps"), h + 1)
            if h >= 2:
                act.wait_ge(s.sem("out_ps"), h - 1)
            act.activation(self.oT[:, h % 2, :], self.ca.ps_s[h % 2][0:self.HD, 1, 0:T],
                           ACT.Copy).then_inc(s.sem("oT"), 1)


class RowNorm:

    def __init__(self, s, name, eps):
        self.s, self.name, self.eps = s, name, eps
        self.st, self.mv = s.sb(name + "_st", [128, 6]), s.sb(name + "_mv", [128, 4])

    def dve(self, dve, link, dst, src):
        s = self.s
        dve_moments(dve, link, src, self.st[:, :], self.mv, self.eps, s.sem(self.name + "_var"))
        dve.wait_ge(s.sem(self.name + "_std"), 1)
        dve_rescale(dve, link, dst, src, self.mv, s.sem(self.name))

    def act(self, act):
        act.wait_ge(self.s.sem(self.name + "_var"), 1)
        act.activation(self.mv[:, 2:3], self.mv[:, 1:2], ACT.Sqrt).then_inc(self.s.sem(self.name + "_std"), 1)


def load_rows(sp, s, A, rows):
    for name, dst, src in rows:
        sp.dma_start(dst[:, :], A[src].partition_broadcast(128)).then_inc(s.sem(name + "_in"), 16)


def stage_l0_xattn(nc, A, x, ident):
    H = 16
    with Stage(nc, "l0x") as s:
        heads = WideHeads(s, H, A, "L0_xattn_", ident, WideHeads.HD ** -0.5)
        ca = ContextAttention(s, H, D, heads.qt, lambda h: (0, D), A["ctxT"], A["ctx_rows"], ident)
        wo2, gam = s.sb("wo2", [128, DC, D]), s.sb("gamma", [128, D])
        h1, h1T, y = s.sb("h1", [128, D]), s.sb("h1T", [128, DC, T]), s.sb("y", [128, D])
        ps_a, ps_b = ca.ps_o[0], ca.ps_o[1]
        nx, ny = NormX(s, x, ident, ps_a), RowNorm(s, "y", 1e-5)
        heads.use(ca, nx.xnT, s.sem("xnT"))
        block = s.block()

        @block.sync
        def _(sp):
            heads.sp(sp)
            sp.dma_start(wo2[:, :, :], A["L0_xattn_w_out2"]).then_inc(s.sem("wo2_in"), 16)
            load_rows(sp, s, A, [("gamma", gam, "L0_xattn_gamma")])
            ca.sp(sp)

        @block.tensor
        def _(pe):
            nx.pe(pe)
            heads.pe_queries(pe)
            ca.pe(pe)
            heads.pe_outputs(pe, ps_a)
            pe.wait_ge(s.sem("h1"), 1)
            pe_transposes(pe, ps_b, h1, ident).then_inc(s.sem("h1T_ps"), 1)
            pe.wait_ge(s.sem("wo2_in"), 16)
            pe.wait_ge(s.sem("h1T"), 1)
            pe_dense(pe, ps_a[:, 0:D], lambda c: h1T[:, c, :], lambda c: wo2[:, c, :]).then_inc(s.sem("y_ps"), 1)

        @block.scalar
        def _(act):
            nx.act(act)
            heads.act_queries(act)
            ca.act(act)
            heads.act_outputs(act)
            ny.act(act)

        @block.vector
        def _(dve):
            link = linker(dve, s.sem("dve_steps"))
            nx.dve(dve, link)
            heads.dve_queries(dve)
            ca.dve(dve)
            heads.dve_outputs(dve)
            dve.wait_ge(s.sem("out_ps"), H)
            dve.tensor_scalar(h1[:, :], ps_a[:, 0:D], 0.0, None, ALU.max).then_inc(s.sem("h1"), 1)
            dve.wait_ge(s.sem("h1T_ps"), 1)
            dve.tensor_copy(h1T[:, :, :], cols(ps_b)).then_inc(s.sem("h1T"), 1)
            dve.wait_ge(s.sem("y_ps"), 1)
            ny.dve(dve, link, y[:, :], ps_a[:, 0:D])
            dve.wait_ge(s.sem("gamma_in"), 16)
            link(dve.tensor_tensor(y[:, :], y[:, :], gam[:, :], ALU.mult))
            link(dve.tensor_tensor(x[:, :], x[:, :], y[:, :], ALU.add))


def stage_prepare(nc, A, x, ident):
    NT = S2 // 128
    with Stage(nc, "prep") as s:
        rows, cT = s.sb("rows", [128, 2, D]), s.sb("cT", [128, 2, DC, 128])
        wkv = s.sb("wkv", [128, DC, 2 * D])
        g1, b1 = s.sb("g1", [128, D]), s.sb("b1", [128, D])
        g2, b2 = s.sb("g2", [128, D]), s.sb("b2", [128, D])
        mask = s.sb("mask", [128, NT])
        st, mv = s.sb("st", [128, 2, 3, 6]), s.sb("mv", [128, 2, 3, 2])
        std, rstd = s.sb("std", [128, 2, 3]), s.sb("rstd", [128, 2, 3])
        xh, xn, xnT = s.sb("xh", [128, 2, D]), s.sb("xn", [128, 2, D]), s.sb("xnT", [128, 2, DC, 128])
        kva = s.sb("kva", [128, 2, 2, D])
        kp, vp = s.sb("kp", [128, 2, D]), s.sb("vp", [128, 2, DC, 129])
        zero = s.sb("zero", [128, DC * 129])
        ps_kv = [s.ps(f"kv{j}") for j in range(2)]
        ps_t = [s.ps(f"t{j}") for j in range(2)]
        ps_sum = s.ps("sum")
        block = s.block()

        @block.sync
        def _(sp):
            def load(j, tile):
                sp.dma_start(rows[:, j, :], A["ctx_rows"][:, bass.ds(tile, 1), :]).then_inc(s.sem(f"ctx_in{j}"), 16)
                sp.dma_start(cT[:, j, :, :], A["ctxT"][:, :, bass.ds(tile * 128, 128)]).then_inc(s.sem(f"ctx_in{j}"), 16)

            load(0, 0)
            sp.dma_start(wkv[:, :, :], A["L2_xattn_wkv"]).then_inc(s.sem("wkv_in"), 16)
            load(1, 1)
            for name, dst, src in (("g1", g1, "L1_xattn_ln_x_g"), ("b1", b1, "L1_xattn_ln_x_b"),
                                   ("g2", g2, "L2_xattn_ln_gamma"), ("b2", b2, "L2_xattn_ln_beta")):
                sp.dma_start(dst[:, :], A[src].partition_broadcast(128)).then_inc(s.sem("gb_in"), 16)
            sp.dma_start(mask[:, :], A["mask_ff1"]).then_inc(s.sem("gb_in"), 16)
            with sp.Fori(0, NT // 2 - 1) as it:
                for j in range(2):
                    sp.wait_ge(s.sem("kv_ps"), it * 2 + (j + 1))
                    sp.wait_ge(s.sem("xhat"), it * 2 + (j + 1))
                    load(j, it * 2 + (2 + j))

        @block.tensor
        def _(pe):
            def project(j, n, seen):
                pe.wait_ge(s.sem(f"ctx_in{j}"), n)
                pe.wait_ge(s.sem("kv_read"), seen)
                pe_dense(pe, ps_kv[j][:, :], lambda c: cT[:, j, c, :], lambda c: wkv[:, c, :]).then_inc(s.sem("kv_ps"), 1)

            def collect(j, it):
                pe.wait_ge(s.sem("xn"), it * 2 + (j + 1))
                pe.wait_ge(s.sem("xnT"), it * 2)
                pe_transposes(pe, ps_t[j], xn[:, j, :], ident).then_inc(s.sem("xnT_ps"), 1)
                pe.wait_ge(s.sem("vp"), it * 2 + (j + 1))
                for c in range(DC):
                    mm = pe.matmul(ps_sum[:, c * 129:(c + 1) * 129], kp[:, j, c * 128:(c + 1) * 128],
                                   vp[:, j, c, :], start=False, stop=False, skip_group_check=True)
                mm.then_inc(s.sem("sum_ps"), 1)

            pe.wait_ge(s.sem("zero"), 1)
            pe.matmul(ps_sum[:, 0:DC * 129], zero[:, 0:128], zero[:, :], start=True, stop=False, skip_group_check=True)
            pe.wait_ge(s.sem("wkv_in"), 16)
            project(0, 32, 0)
            with pe.Fori(0, NT // 2 - 1) as it:
                project(1, it * 32 + 32, it * 2)
                collect(0, it)
                project(0, it * 32 + 64, it * 2 + 1)
                collect(1, it)
            project(1, NT // 2 * 32, NT - 2)
            collect(0, NT // 2 - 1)
            collect(1, NT // 2 - 1)
            pe.matmul(ps_sum[:, 0:DC * 129], zero[:, 0:128], zero[:, :], start=False, stop=True,
                      skip_group_check=True).then_inc(s.sem("all_ps"), 1)

        @block.scalar
        def _(act):
            with act.Fori(0, NT // 2) as it:
                for j in range(2):
                    n = it * 2 + j
                    m = mask[:, bass.ds(n, 1)]
                    act.wait_ge(s.sem("var"), n + 1)
                    act.activation(std[:, j, :], mv[:, j, :, 1], ACT.Sqrt).then_inc(s.sem("std"), 1)
                    act.wait_ge(s.sem("gb_in"), 5 * 16)
                    act.wait_ge(s.sem("v_affine"), n + 1)
                    act.wait_ge(s.sem("sum_ps"), it * 2)
                    act.activation(vp[:, j, :, 0:128], kva[:, j, 1, :].rearrange("p (c e) -> p c e", c=DC),
                                   ACT.Copy, scale=m).then_inc(s.sem("vp0"), 1)
                    act.wait_ge(s.sem("ones"), 1)
                    act.wait_ge(s.sem("k_pos"), n + 1)
                    act.activation(kp[:, j, :], kva[:, j, 0, :], ACT.Copy, scale=m).then_inc(s.sem("vp"), 1)
                    act.wait_ge(s.sem("xnT_ps"), n + 1)
                    act.wait_ge(s.sem(f"stored{j}"), it * 32)
                    act.activation(xnT[:, j, :, :], cols(ps_t[j]), ACT.Copy).then_inc(s.sem("xnT"), 1)
                    act.wait_ge(s.sem("xnT"), n + 1)
                    act.dma_start(A["xnT"][:, :, bass.ds(n * 128, 128)], xnT[:, j, :, :]).then_inc(s.sem(f"stored{j}"), 16)
                    act.dma_start(A["xn_rows"][:, bass.ds(n, 1), :], xn[:, j, :]).then_inc(s.sem(f"stored{j}"), 16)
            for j in range(2):
                act.wait_ge(s.sem(f"stored{j}"), NT // 2 * 32)

        @block.vector
        def _(dve):
            dve.memset(zero[:, :], 0.0).then_inc(s.sem("zero"), 1)
            dve.memset(vp[:, :, :, 128:129], 1.0).then_inc(s.sem("ones"), 1)
            dve.wait_ge(s.sem("gb_in"), 5 * 16)
            STEPS = 12
            with dve.Fori(0, NT // 2) as it:
                link = linker(dve, s.sem("dve_steps"), it * STEPS)
                for j in range(2):
                    n = it * 2 + j
                    dve.wait_ge(s.sem(f"ctx_in{j}"), it * 32 + 32)
                    dve.bn_stats(st[:, j, 0, :], rows[:, j, :]).then_inc(s.sem("stats"), 1)
                    dve.wait_ge(s.sem("kv_ps"), n + 1)
                    for i in range(2):
                        dve.bn_stats(st[:, j, 1 + i, :], ps_kv[j][:, i * D:(i + 1) * D]).then_inc(s.sem("stats"), 1)
                    dve.wait_ge(s.sem("stats"), n * 3 + 3)
                    dve.sem_inc(s.sem("stats_seen"), 1)
                    for i in range(3):
                        dve.bn_aggr(mv[:, j, i, :], st[:, j, i, :]).then_inc(s.sem("aggr"), 1)
                    dve.wait_ge(s.sem("aggr"), n * 3 + 3)
                    dve.tensor_scalar(mv[:, j, 0, 1:2], mv[:, j, 0, 1:2], 1e-5, None, ALU.add).then_inc(s.sem("eps"), 1)
                    dve.wait_ge(s.sem("eps"), n + 1)
                    dve.tensor_scalar(mv[:, j, 1:3, 1], mv[:, j, 1:3, 1], 1e-6, None, ALU.add).then_inc(s.sem("var"), 1)
                    dve.wait_ge(s.sem("vp"), it * 2)
                    for i in range(2):
                        last = dve.scalar_tensor_tensor(out=kva[:, j, i, :], in0=ps_kv[j][:, i * D:(i + 1) * D],
                                                        scalar=mv[:, j, 1 + i, 0:1], in1=g2[:, :],
                                                        op0=ALU.subtract, op1=ALU.mult)
                    last.then_inc(s.sem("kv_read"), 1)
                    dve.wait_ge(s.sem("std"), n + 1)
                    dve_rsqrt(dve, link, rstd[:, j, :], std[:, j, :], mv[:, j, :, 1])
                    dve.wait_ge(s.sem("xn"), it * 2)
                    dve.tensor_scalar(xh[:, j, :], rows[:, j, :], mv[:, j, 0, 0:1], rstd[:, j, 0:1],
                                      ALU.subtract, ALU.mult).then_inc(s.sem("xhat"), 1)
                    dve.wait_ge(s.sem("kv_read"), n + 1)
                    for i in (1, 0):
                        last = dve.scalar_tensor_tensor(out=kva[:, j, i, :], in0=kva[:, j, i, :],
                                                        scalar=rstd[:, j, 1 + i:2 + i], in1=b2[:, :],
                                                        op0=ALU.mult, op1=ALU.add)
                        if i == 1:
                            last.then_inc(s.sem("v_affine"), 1)
                        else:
                            link(last)
                    dve.tensor_scalar(kva[:, j, 0, :], kva[:, j, 0, :], 0.0, 1e-6, ALU.max, ALU.add).then_inc(s.sem("k_pos"), 1)
                assert link.count[0] == STEPS
            dve.wait_ge(s.sem("all_ps"), 1)
            finish(dve, dve.tensor_copy(A["kv_sum"][:, :, :], ps_sum[:, 0:DC * 129].rearrange("p (c e) -> p c e", c=DC)),
                   s.sem("kv_sum"))

        @block.gpsimd
        def _(pool):
            pool.wait_ge(s.sem("gb_in"), 5 * 16)
            with pool.Fori(0, NT // 2) as it:
                for j in range(2):
                    n = it * 2 + j
                    pool.wait_ge(s.sem("xhat"), n + 1)
                    pool.wait_ge(s.sem(f"stored{j}"), it * 32)
                    pool.tensor_tensor(xn[:, j, :], xh[:, j, :], g1[:, :], ALU.mult).then_inc(s.sem("xn_g"), 1)
                    pool.wait_ge(s.sem("xn_g"), n + 1)
                    pool.tensor_tensor(xn[:, j, :], xn[:, j, :], b1[:, :], ALU.add).then_inc(s.sem("xn"), 1)


def stage_l1_xattn(nc, A, x, ident):
    H = 8
    with Stage(nc, "l1x") as s:
        heads = WideHeads(s, H, A, "L1_xattn_", ident, WideHeads.HD ** -1.0)
        lat, latT = s.sb("lat", [128, D]), s.sb("latT", [128, DC, T])
        ca = ContextAttention(s, H, D, heads.qt, lambda h: (0, D), A["xnT"], A["xn_rows"], ident, mask="rows",
                              mask_dram=A["mask_bk1"].partition_broadcast(128), bias_per_one=-FAR, tail=(latT, lat))
        lg, lb, og, ob = (s.sb(n, [128, D]) for n in ("lg", "lb", "og", "ob"))
        y = s.sb("y", [128, D])
        ps_a, ps_b = ca.ps_o[0], ca.ps_o[1]
        n0, n1, ny = RowNorm(s, "n0", 1e-5), RowNorm(s, "n1", 1e-5), RowNorm(s, "y", 1e-5)
        heads.use(ca, latT, s.sem("latT"))
        block = s.block()

        @block.sync
        def _(sp):
            heads.sp(sp)
            load_rows(sp, s, A, [("lg", lg, "L1_xattn_ln_l_g"), ("lb", lb, "L1_xattn_ln_l_b"),
                                 ("og", og, "L1_xattn_ln_o_g"), ("ob", ob, "L1_xattn_ln_o_b")])
            ca.sp(sp)

        @block.tensor
        def _(pe):
            pe.wait_ge(s.sem("lat"), 1)
            pe_transposes(pe, ps_a, lat, ident).then_inc(s.sem("latT_ps"), 1)
            heads.pe_queries(pe)
            ca.pe(pe)
            heads.pe_outputs(pe, ps_a)

        @block.scalar
        def _(act):
            n0.act(act)
            n1.act(act)
            heads.act_queries(act)
            ca.act(act)
            heads.act_outputs(act)
            ny.act(act)

        @block.vector
        def _(dve):
            link = linker(dve, s.sem("dve_steps"))
            n0.dve(dve, link, lat[:, :], x[:, :])
            n1.dve(dve, link, lat[:, :], lat[:, :])
            dve.wait_ge(s.sem("lg_in"), 16)
            link(dve.tensor_tensor(lat[:, :], lat[:, :], lg[:, :], ALU.mult))
            dve.wait_ge(s.sem("lb_in"), 16)
            finish(dve, dve.tensor_tensor(lat[:, :], lat[:, :], lb[:, :], ALU.add), s.sem("lat"))
            dve.wait_ge(s.sem("latT_ps"), 1)
            dve.tensor_copy(latT[:, :, :], cols(ps_a)).then_inc(s.sem("latT"), 1)
            heads.dve_queries(dve)
            ca.dve(dve)
            heads.dve_outputs(dve)
            dve.wait_ge(s.sem("out_ps"), H)
            ny.dve(dve, link, y[:, :], ps_a[:, 0:D])
            dve.wait_ge(s.sem("og_in"), 16)
            link(dve.tensor_tensor(y[:, :], y[:, :], og[:, :], ALU.mult))
            dve.wait_ge(s.sem("ob_in"), 16)
            link(dve.tensor_tensor(y[:, :], y[:, :], ob[:, :], ALU.add))
            link(dve.tensor_tensor(x[:, :], x[:, :], y[:, :], ALU.add))


def stage_l2_xattn(nc, A, x, ident):
    with Stage(nc, "l2x") as s:
        wq, wd = s.sb("wq", [128, DC, D]), s.sb("wd", [128, DC, D])
        g, b, bd = s.sb("g", [128, D]), s.sb("b", [128, D]), s.sb("bd", [128, D])
        kvd = s.sb("kvd", [128, DC, 136])
        q, qT, den = s.sb("q", [128, D]), s.sb("qT", [128, DC, T]), s.sb("den", [128, DC, 8])
        att2 = s.sb("att2", [128, D])
        att, attT, y = s.sb("att", [128, D]), s.sb("attT", [128, DC, T]), s.sb("y", [128, D])
        ps_a, ps_b, ps_c = s.ps("ps_a"), s.ps("ps_b"), s.ps("ps_c")
        nx, nq, ny = NormX(s, x, ident, ps_a), RowNorm(s, "nq", 1e-6), RowNorm(s, "ny", 1e-6)
        hm, kv = A["head_mask"], A["kv_sum"]
        block = s.block()

        @block.sync
        def _(sp):
            sp.dma_start(wq[:, :, :], A["L2_xattn_wq"]).then_inc(s.sem("wq_in"), 16)
            sp.dma_start(wd[:, :, :], A["L2_xattn_dense_w"]).then_inc(s.sem("wd_in"), 16)
            load_rows(sp, s, A, [("g", g, "L2_xattn_ln_gamma"), ("b", b, "L2_xattn_ln_beta"), ("bd", bd, "L2_xattn_dense_b")])
            sp.wait_ge(s.sem("att"), DC)
            sp.dma_start(A["att_order"].rearrange("h n e -> n h e"),
                         att[:, :].rearrange("p (h e) -> p h e", h=16)).then_inc(s.sem("att_out"), 16)
            sp.wait_ge(s.sem("att_out"), 16)
            sp.dma_start(att2[:, :], A["att_order"].rearrange("h (a b) e -> (h a) (b e)", b=16)).then_inc(s.sem("att_in"), 16)

        @block.tensor
        def _(pe):
            nx.pe(pe)
            pe.wait_ge(s.sem("xnT"), 1)
            pe.wait_ge(s.sem("wq_in"), 16)
            pe_dense(pe, ps_b[:, 0:D], lambda c: nx.xnT[:, c, :], lambda c: wq[:, c, :]).then_inc(s.sem("q_ps"), 1)
            pe.wait_ge(s.sem("q"), 1)
            pe_transposes(pe, ps_a, q, ident).then_inc(s.sem("qT_ps"), 1)
            pe.wait_ge(s.sem("kvd"), 1)
            pe.wait_ge(s.sem("qT"), 1)
            for c in range(DC):
                mm = pe.matmul(ps_c[:, c * 136:(c + 1) * 136], qT[:, c, :], kvd[:, c, :], start=True, stop=True)
            mm.then_inc(s.sem("att_ps"), 1)
            pe.wait_ge(s.sem("att_in"), 16)
            pe_transposes(pe, ps_a, att2, ident).then_inc(s.sem("attT_ps"), 1)
            pe.wait_ge(s.sem("wd_in"), 16)
            pe.wait_ge(s.sem("attT"), 1)
            pe_dense(pe, ps_b[:, 0:D], lambda c: attT[:, c, :], lambda c: wd[:, c, :]).then_inc(s.sem("y_ps"), 1)

        @block.scalar
        def _(act):
            nx.act(act)
            nq.act(act)
            ny.act(act)

        @block.vector
        def _(dve):
            link = linker(dve, s.sem("dve_steps"))
            nx.dve(dve, link)
            link(dve.tensor_tensor(kvd[:, :, 0:128].rearrange("p c (h e) -> p c h e", h=8),
                                   kv[:, :, 0:128].rearrange("p c (h e) -> p c h e", h=8),
                                   hm[:, :].unsqueeze(1).unsqueeze(3).to_broadcast([128, DC, 8, 16]), ALU.mult))
            dve.tensor_tensor(kvd[:, :, 128:136], hm[:, :].unsqueeze(1).to_broadcast([128, DC, 8]),
                              kv[:, :, 128:129].to_broadcast([128, DC, 8]), ALU.mult).then_inc(s.sem("kvd"), 1)
            dve.wait_ge(s.sem("q_ps"), 1)
            nq.dve(dve, link, q[:, :], ps_b[:, 0:D])
            for name in ("g", "b", "bd"):
                dve.wait_ge(s.sem(name + "_in"), 16)
            link(dve.tensor_tensor(q[:, :], q[:, :], g[:, :], ALU.mult))
            link(dve.tensor_tensor(q[:, :], q[:, :], b[:, :], ALU.add))
            dve.tensor_scalar(q[:, :], q[:, :], 0.0, 1e-6, ALU.max, ALU.add).then_inc(s.sem("q"), 1)
            dve.wait_ge(s.sem("qT_ps"), 1)
            dve.tensor_copy(qT[:, :, :], cols(ps_a)).then_inc(s.sem("qT"), 1)
            dve.wait_ge(s.sem("att_ps"), 1)
            num = ps_c[:, 0:DC * 136].rearrange("p (c e) -> p c e", c=DC)
            link(dve.tensor_scalar(den[:, :, :], num[:, :, 128:136], 1e-6, None, ALU.add))
            link(dve.reciprocal(den[:, :, :], den[:, :, :]))
            for c in range(DC):
                dve.tensor_tensor(att[:, c * 128:(c + 1) * 128].rearrange("p (h e) -> p h e", h=8),
                                         num[:, c, 0:128].rearrange("p (h e) -> p h e", h=8),
                                         den[:, c, :].unsqueeze(2).to_broadcast([128, 8, 16]), ALU.mult).then_inc(s.sem("att"), 1)
            dve.wait_ge(s.sem("attT_ps"), 1)
            dve.tensor_copy(attT[:, :, :], cols(ps_a)).then_inc(s.sem("attT"), 1)
            dve.wait_ge(s.sem("y_ps"), 1)
            link(dve.tensor_tensor(y[:, :], ps_b[:, 0:D], bd[:, :], ALU.add))
            ny.dve(dve, link, y[:, :], y[:, :])
            link(dve.tensor_tensor(y[:, :], y[:, :], g[:, :], ALU.mult))
            link(dve.tensor_tensor(y[:, :], y[:, :], b[:, :], ALU.add))
            link(dve.tensor_tensor(x[:, :], x[:, :], y[:, :], ALU.add))


def stage_l3_xattn(nc, A, x, ident):
    H = 16
    with Stage(nc, "l3x") as s:
        qd = s.sb("qd", [128, H, T])
        ca = ContextAttention(s, H, 16, lambda h: [(qd[:, h, :], h // 8)], lambda h: (16 * h, 16 * h + 16),
                              A["ctxT"], A["ctx_rows"], ident, mask="full", mask_dram=A["mask_ik1"], bias_per_one=1e9)
        nx = NormX(s, x, ident, ca.ps_o[0])
        hm = A["head_mask"]
        block = s.block()

        @block.sync
        def _(sp):
            ca.sp(sp)

        @block.tensor
        def _(pe):
            nx.pe(pe)
            pe.wait_ge(s.sem("qd"), H)
            ca.pe(pe)

        @block.scalar
        def _(act):
            nx.act(act)
            ca.act(act)

        @block.vector
        def _(dve):
            link = linker(dve, s.sem("dve_steps"))
            nx.dve(dve, link)
            dve.wait_ge(s.sem("xnT"), 1)
            for h in range(H):
                dve.tensor_scalar(qd[:, h, :], nx.xnT[:, h // 8, :], hm[:, h % 8:h % 8 + 1], 0.25,
                                  ALU.mult, ALU.mult).then_inc(s.sem("qd"), 1)
            ca.dve(dve)
            dve.wait_ge(s.sem("attended"), H)
            link(dve.tensor_tensor(x[:, :], x[:, :], ca.acc[:, :, :].rearrange("p h e -> p (h e)"), ALU.add))


def add_cols(a, n):
    return a.unsqueeze(2).to_broadcast([a.shape[0], a.shape[1], n])


def stage_l0_attn(nc, A, x, ident):
    with Stage(nc, "l0a") as s:
        qk = s.sb("qk", [128, 2, DC])
        dl, osc = s.sb("dl", [128, 1]), s.sb("osc", [128, 1])
        e, ld = s.sb("e", [128, 2]), s.sb("ld", [128, 1])
        steps, w = s.sb("steps", [128, T]), s.sb("w", [128, T])
        qx, kx, sw = s.sb("qx", [128, DC, T]), s.sb("kx", [128, DC, T]), s.sb("sw", [128, T])
        ps_a, ps_s, ps_y = s.ps("ps_a"), s.ps("ps_s"), s.ps("ps_y")
        nx = NormX(s, x, ident, ps_a)
        block = s.block()

        @block.sync
        def _(sp):
            sp.dma_start(dl[:, :], A["L0_attn_decay_logit"].partition_broadcast(128)).then_inc(s.sem("dl_in"), 16)
            sp.dma_start(osc[:, :], A["L0_attn_out_scale"].partition_broadcast(128)).then_inc(s.sem("osc_in"), 16)
            sp.dma_start(qk[:, 0, :], A["L0_attn_q_scale"]).then_inc(s.sem("qk_in"), 16)
            sp.dma_start(qk[:, 1, :], A["L0_attn_k_scale"]).then_inc(s.sem("qk_in"), 16)

        @block.gpsimd
        def _(pool):
            pool.iota(steps[:, :], [[-1, T]], base=-1, channel_multiplier=1,
                      allow_small_or_imprecise_dtypes=True).then_inc(s.sem("iota"), 1)
            pool.wait_ge(s.sem("iota"), 1)
            pool.tensor_scalar(steps[:, :], steps[:, :], 0.0, None, ALU.max).then_inc(s.sem("steps"), 1)
            pool.wait_ge(s.sem("w_all"), 1)
            pool.affine_select(out=w[:, :], in_=w[:, :], compare_op=ALU.is_gt, fill=0.0, base=0,
                               pattern=[[-1, T]], channel_multiplier=1).then_inc(s.sem("w"), 1)

        @block.tensor
        def _(pe):
            nx.pe(pe)
            pe.wait_ge(s.sem("kx"), 2 * DC)
            pe_dense(pe, ps_s[:, 0:T], lambda c: kx[:, c, :], lambda c: qx[:, c, :]).then_inc(s.sem("s_ps"), 1)
            pe.wait_ge(s.sem("sw"), 1)
            pe.matmul(ps_y[:, 0:D], sw[:, :], nx.xn[:, :], start=True, stop=True).then_inc(s.sem("y_ps"), 1)

        @block.scalar
        def _(act):
            nx.act(act)
            act.wait_ge(s.sem("neg"), 1)
            act.activation(e[:, 1:2], e[:, 0:1], ACT.Exp).then_inc(s.sem("exp"), 1)
            act.wait_ge(s.sem("decay"), 1)
            act.activation(ld[:, :], e[:, 1:2], ACT.Ln).then_inc(s.sem("ln"), 1)
            act.wait_ge(s.sem("ln"), 1)
            act.wait_ge(s.sem("steps"), 1)
            act.activation(w[:, :], steps[:, :], ACT.Exp, scale=ld[:, 0:1]).then_inc(s.sem("w_all"), 1)

        @block.vector
        def _(dve):
            link = linker(dve, s.sem("dve_steps"))
            dve.wait_ge(s.sem("dl_in"), 16)
            dve.tensor_scalar(e[:, 0:1], dl[:, :], -1.0, 87.0, ALU.mult, ALU.min).then_inc(s.sem("neg"), 1)
            nx.dve(dve, link)
            dve.wait_ge(s.sem("exp"), 1)
            link(dve.tensor_scalar(e[:, 1:2], e[:, 1:2], 1.0, None, ALU.add))
            dve.reciprocal(e[:, 1:2], e[:, 1:2]).then_inc(s.sem("decay"), 1)
            dve.wait_ge(s.sem("qk_in"), 32)
            dve.wait_ge(s.sem("xnT"), 1)
            for c in range(DC):
                dve.tensor_scalar(qx[:, c, :], nx.xnT[:, c, :], qk[:, 0, c:c + 1], None, ALU.mult).then_inc(s.sem("kx"), 1)
                dve.tensor_scalar(kx[:, c, :], nx.xnT[:, c, :], qk[:, 1, c:c + 1], None, ALU.mult).then_inc(s.sem("kx"), 1)
            dve.wait_ge(s.sem("s_ps"), 1)
            dve.wait_ge(s.sem("w"), 1)
            dve.tensor_tensor(sw[:, :], ps_s[:, 0:T], w[:, :], ALU.mult).then_inc(s.sem("sw"), 1)
            dve.wait_ge(s.sem("y_ps"), 1)
            dve.wait_ge(s.sem("osc_in"), 16)
            link(dve.scalar_tensor_tensor(out=x[:, :], in0=ps_y[:, 0:D], scalar=osc[:, 0:1], in1=x[:, :],
                                          op0=ALU.mult, op1=ALU.add))


class SmallHeads:

    H, HD = 16, 16

    def __init__(self, s, A, x, ident, w, bias=None, q_scale=1.0):
        self.s, self.A, self.ident, self.w_dram, self.bias_dram, self.q_scale = s, A, ident, w, bias, q_scale
        self.w = s.sb("w_qkv", [128, DC, 3 * D])
        self.bias = s.sb("b_qkv", [128, 3 * D]) if bias else None
        self.qkv = s.sb("qkv", [128, 3 * D])
        self.qkT = s.sb("qkT", [128, 4, T])
        self.qd = s.sb("qd", [128, self.H, T])
        self.ps_a, self.ps_b = s.ps("ps_a"), s.ps("ps_b")
        self.ps_h = [s.ps(f"ps_h{g}") for g in range(4)]
        self.nx = NormX(s, x, ident, self.ps_a)

    def sp(self, sp):
        sp.dma_start(self.w[:, :, :], self.A[self.w_dram]).then_inc(self.s.sem("w_qkv_in"), 16)
        if self.bias:
            sp.dma_start(self.bias[:, :], self.A[self.bias_dram].partition_broadcast(128)).then_inc(self.s.sem("b_qkv_in"), 16)

    def pe_project(self, pe):
        s = self.s
        self.nx.pe(pe)
        pe.wait_ge(s.sem("w_qkv_in"), 16)
        pe.wait_ge(s.sem("xnT"), 1)
        pe_dense(pe, self.ps_a[:, :], lambda c: self.nx.xnT[:, c, :], lambda c: self.w[:, c, 0:512])
        pe_dense(pe, self.ps_b[:, 0:D], lambda c: self.nx.xnT[:, c, :],
                 lambda c: self.w[:, c, 512:768]).then_inc(s.sem("qkv_ps"), 1)

    def dve_project(self, dve, link):
        s = self.s
        self.nx.dve(dve, link)
        dve.wait_ge(s.sem("qkv_ps"), 1)
        if self.bias:
            dve.wait_ge(s.sem("b_qkv_in"), 16)
        for lo, hi, ps in ((0, 512, self.ps_a[:, :]), (512, 768, self.ps_b[:, 0:D])):
            if self.bias:
                link(dve.tensor_tensor(self.qkv[:, lo:hi], ps, self.bias[:, lo:hi], ALU.add))
            else:
                link(dve.tensor_copy(self.qkv[:, lo:hi], ps))

    def pe_scores(self, pe):
        s = self.s
        pe.wait_ge(s.sem("qkv_ready"), 1)
        pe_transposes(pe, self.ps_a, self.qkv, self.ident, 4).then_inc(s.sem("qkT_ps"), 1)
        pe.wait_ge(s.sem("qd"), self.H)
        for g in range(4):
            pe.matmul(self.ps_h[g][:, :], self.qkT[:, 2 + g // 2, :], self.qd[:, 4 * g:4 * g + 4, :],
                      start=True, stop=True).then_inc(s.sem("scores"), 1)

    def dve_heads(self, dve):
        s, hm = self.s, self.A["head_mask"]
        dve.wait_ge(s.sem("qkT_ps"), 1)
        finish(dve, dve.tensor_copy(self.qkT[:, :, :], cols(self.ps_a, 4)), s.sem("qkT"))
        for h in range(self.H):
            dve.tensor_scalar(self.qd[:, h, :], self.qkT[:, h // 8, :], hm[:, h % 8:h % 8 + 1], self.q_scale,
                              ALU.mult, ALU.mult).then_inc(s.sem("qd"), 1)

    def v(self, h):
        return self.qkv[:, 512 + 16 * h:512 + 16 * h + 16]


class OutProjection:

    def __init__(self, s, A, x, ident, w, ps_t, ps_o, bias=None):
        self.s, self.A, self.x, self.ident, self.w_dram, self.bias_dram = s, A, x, ident, w, bias
        self.ps_t, self.ps_o = ps_t, ps_o
        self.w, self.yT = s.sb("w_out", [128, DC, D]), s.sb("yT", [128, DC, T])
        self.y = s.sb("y", [128, D])
        self.bias = s.sb("b_out", [128, D]) if bias else None

    def sp(self, sp):
        sp.dma_start(self.w[:, :, :], self.A[self.w_dram]).then_inc(self.s.sem("w_out_in"), 16)
        if self.bias:
            sp.dma_start(self.bias[:, :], self.A[self.bias_dram].partition_broadcast(128)).then_inc(self.s.sem("b_out_in"), 16)

    def pe(self, pe):
        s = self.s
        pe.wait_ge(s.sem("y_ready"), 1)
        pe_transposes(pe, self.ps_t, self.y, self.ident).then_inc(s.sem("yT_ps"), 1)
        pe.wait_ge(s.sem("w_out_in"), 16)
        pe.wait_ge(s.sem("yT"), 1)
        pe_dense(pe, self.ps_o[:, 0:D], lambda c: self.yT[:, c, :], lambda c: self.w[:, c, :]).then_inc(s.sem("out_ps"), 1)

    def dve(self, dve, link):
        s, x = self.s, self.x
        dve.wait_ge(s.sem("yT_ps"), 1)
        dve.tensor_copy(self.yT[:, :, :], cols(self.ps_t)).then_inc(s.sem("yT"), 1)
        if self.bias:
            dve.wait_ge(s.sem("b_out_in"), 16)
            link(dve.tensor_tensor(x[:, :], x[:, :], self.bias[:, :], ALU.add))
        dve.wait_ge(s.sem("out_ps"), 1)
        link(dve.tensor_tensor(x[:, :], x[:, :], self.ps_o[:, 0:D], ALU.add))


def stage_l2_attn(nc, A, x, ident):
    with Stage(nc, "l2a") as s:
        hd = SmallHeads(s, A, x, ident, "L2_attn_W_qkv")
        op = OutProjection(s, A, x, ident, "L2_attn_W_o", hd.ps_a, hd.ps_b)
        mu, var, std = s.sb("mu", [128, 16]), s.sb("var", [128, 16]), s.sb("std", [128, 16])
        sq = s.sb("sq", [128, D])
        st = s.sb("st", [128, 4, 4, T])
        ps_y = s.ps("ps_y")
        block = s.block()

        @block.sync
        def _(sp):
            hd.sp(sp)
            op.sp(sp)

        @block.tensor
        def _(pe):
            hd.pe_project(pe)
            hd.pe_scores(pe)
            for h in range(16):
                pe.wait_ge(s.sem("st"), h // 4 + 1)
                mm = pe.matmul(ps_y[:, 16 * h:16 * h + 16], st[:, h // 4, h % 4, :], hd.v(h), start=True, stop=True)
            mm.then_inc(s.sem("y_ps"), 1)
            op.pe(pe)

        @block.scalar
        def _(act):
            hd.nx.act(act)
            act.wait_ge(s.sem("k_var"), 1)
            act.activation(std[:, :], var[:, :], ACT.Sqrt).then_inc(s.sem("k_std"), 1)

        @block.vector
        def _(dve):
            link = linker(dve, s.sem("dve_steps"))
            hd.dve_project(dve, link)
            k = hd.qkv[:, 256:512].rearrange("p (h e) -> p h e", h=16)
            sq3 = sq[:, :].rearrange("p (h e) -> p h e", h=16)
            link(dve.tensor_reduce(mu[:, :], k, AX.X, ALU.add))
            link(dve.tensor_scalar(mu[:, :], mu[:, :], 1 / 16, None, ALU.mult))
            link(dve.tensor_tensor(k, k, add_cols(mu[:, :], 16), ALU.subtract))
            link(dve.tensor_tensor(sq3, k, k, ALU.mult))
            link(dve.tensor_reduce(var[:, :], sq3, AX.X, ALU.add))
            dve.tensor_scalar(var[:, :], var[:, :], 1 / 16, 1e-5, ALU.mult, ALU.add).then_inc(s.sem("k_var"), 1)
            dve.wait_ge(s.sem("k_std"), 1)
            dve_rsqrt(dve, link, mu[:, :], std[:, :], var[:, :])
            dve.tensor_tensor(k, k, add_cols(mu[:, :], 16), ALU.mult).then_inc(s.sem("qkv_ready"), 1)
            hd.dve_heads(dve)
            for g in range(4):
                dve.wait_ge(s.sem("scores"), g + 1)
                dve.tensor_tensor(st[:, g, :, :], cols(hd.ps_h[g], 4),
                                  A["causal"][:, :].unsqueeze(1).to_broadcast([128, 4, T]), ALU.mult).then_inc(s.sem("st"), 1)
            dve.wait_ge(s.sem("y_ps"), 1)
            dve.tensor_copy(op.y[:, :], ps_y[:, 0:D]).then_inc(s.sem("y_ready"), 1)
            op.dve(dve, link)


class SmallSoftmax:

    def __init__(self, s, name):
        self.s, self.name = s, name
        self.p, self.m, self.l = s.sb(name + "_p", [128, 16, T]), s.sb(name + "_m", [128, 16]), s.sb(name + "_l", [128, 16])

    def dve(self, dve, link, src, bias=None):
        s = self.s
        for g in range(4):
            dst, gs = self.p[:, 4 * g:4 * g + 4, :], slice(4 * g, 4 * g + 4)
            a = src(g)
            if bias is not None:
                link(dve.tensor_tensor(dst, a, bias.unsqueeze(1).to_broadcast([128, 4, T]), ALU.add))
                a = dst
            link(dve.tensor_reduce(self.m[:, gs], a, AX.X, ALU.max))
            dve.tensor_tensor(dst, a, add_cols(self.m[:, gs], T), ALU.subtract).then_inc(s.sem(self.name + "_shifted"), 1)

    def act(self, act):
        s = self.s
        for g in range(4):
            act.wait_ge(s.sem(self.name + "_shifted"), g + 1)
            dst = self.p[:, 4 * g:4 * g + 4, :]
            act.activation(dst, dst, ACT.Exp).then_inc(s.sem(self.name + "_exp"), 1)

    def dve_sums(self, dve, link):
        for g in range(4):
            dve.wait_ge(self.s.sem(self.name + "_exp"), g + 1)
            link(dve.tensor_reduce(self.l[:, 4 * g:4 * g + 4], self.p[:, 4 * g:4 * g + 4, :], AX.X, ALU.add))
        link(dve.reciprocal(self.l[:, :], self.l[:, :]))


class SmallValues:

    def __init__(self, s, hd, p, ps_y):
        self.s, self.hd, self.p, self.ps_y = s, hd, p, ps_y
        self.pT = s.sb("pT", [128, 16, T])

    def pe(self, pe, ready, count):
        s, hd = self.s, self.hd
        for g in range(4):
            pe.wait_ge(ready, count(g))
            for h in range(4 * g, 4 * g + 4):
                mm = pe.transpose(hd.ps_h[g][:, (h % 4) * T:(h % 4 + 1) * T], self.p[:, h, :], hd.ident[:, :])
            mm.then_inc(s.sem("pT_ps"), 1)
        for g in range(4):
            pe.wait_ge(s.sem("pT"), g + 1)
            for h in range(4 * g, 4 * g + 4):
                mm = pe.matmul(self.ps_y[:, 16 * h:16 * h + 16], self.pT[:, h, :], hd.v(h), start=True, stop=True)
        mm.then_inc(s.sem("y_ps"), 1)

    def act(self, act):
        for g in range(4):
            act.wait_ge(self.s.sem("pT_ps"), g + 1)
            act.activation(self.pT[:, 4 * g:4 * g + 4, :], cols(self.hd.ps_h[g], 4), ACT.Copy).then_inc(self.s.sem("pT"), 1)


def stage_l3_attn(nc, A, x, ident):
    with Stage(nc, "l3a") as s:
        hd = SmallHeads(s, A, x, ident, "L3_attn_W_qkv", bias="L3_attn_b_qkv", q_scale=D ** -0.5)
        op = OutProjection(s, A, x, ident, "L3_attn_Wo", hd.ps_a, hd.ps_b, bias="L3_attn_bo")
        sm = SmallSoftmax(s, "sm")
        ps_y = s.ps("ps_y")
        vals = SmallValues(s, hd, sm.p, ps_y)
        block = s.block()

        @block.sync
        def _(sp):
            hd.sp(sp)
            op.sp(sp)

        @block.tensor
        def _(pe):
            hd.pe_project(pe)
            hd.pe_scores(pe)
            vals.pe(pe, s.sem("sm_exp"), lambda g: g + 1)
            op.pe(pe)

        @block.scalar
        def _(act):
            hd.nx.act(act)
            sm.act(act)
            vals.act(act)

        @block.vector
        def _(dve):
            link = linker(dve, s.sem("dve_steps"))
            hd.dve_project(dve, link)
            dve.sem_inc(s.sem("qkv_ready"), 1)
            hd.dve_heads(dve)

            def scores(g):
                dve.wait_ge(s.sem("scores"), g + 1)
                return cols(hd.ps_h[g], 4)

            sm.dve(dve, link, scores)
            sm.dve_sums(dve, link)
            dve.wait_ge(s.sem("y_ps"), 1)
            dve.tensor_tensor(op.y[:, :].rearrange("p (h e) -> p h e", h=16), ps_y[:, 0:D].rearrange("p (h e) -> p h e", h=16),
                              add_cols(sm.l[:, :], 16), ALU.mult).then_inc(s.sem("y_ready"), 1)
            op.dve(dve, link)


def stage_l3_ffn(nc, A, x, ident):
    REG = 5
    with Stage(nc, "l3f") as s:
        hd = SmallHeads(s, A, x, ident, "L3_ffn_W_kqv", q_scale=0.25)
        op = OutProjection(s, A, x, ident, "L3_ffn_W_proj", hd.ps_a, hd.ps_b, bias="L3_ffn_b_proj")
        smp, smn = SmallSoftmax(s, "smp"), SmallSoftmax(s, "smn")
        guide = s.sb("guide", [128, D])
        prod = s.sb("prod", [128, D])
        n2 = s.sb("n2", [128, 2, 16])
        nrm, dot, sim = s.sb("nrm", [128, 2, 16]), s.sb("dot", [128, 16]), s.sb("sim", [128, 1])
        srow, mm1 = s.sb("srow", [1, T]), s.sb("mm1", [1, 4])
        pos = s.sb("pos", [1, T])
        bp, bn = s.sb("bp", [128, T]), s.sb("bn", [128, T])
        wt = s.sb("wt", [128, 4])
        cf = s.sb("cf", [128, 2, 16])
        ps_y, ps_m = s.ps("ps_y"), s.ps("ps_m")
        vals = SmallValues(s, hd, smp.p, ps_y)
        block = s.block()

        @block.sync
        def _(sp):
            hd.sp(sp)
            sp.dma_start(guide[:, :], A["L3_ffn_guide"].partition_broadcast(128)).then_inc(s.sem("guide_in"), 16)
            op.sp(sp)

        @block.gpsimd
        def _(pool):
            pool.affine_select(out=wt[:, 3:4], in_=A["ones"][:, 0:1], compare_op=ALU.is_ge, fill=0.0, base=REG - 1,
                               pattern=[[0, 1]], channel_multiplier=-1).then_inc(s.sem("reg"), 1)

        @block.tensor
        def _(pe):
            hd.pe_project(pe)
            hd.pe_scores(pe)
            pe.wait_ge(s.sem("sim"), 1)
            pe.matmul(ps_m[0:1, 0:T], sim[:, 0:1], ident[:, :], start=True, stop=True).then_inc(s.sem("srow_ps"), 1)
            pe.wait_ge(s.sem("pos"), 1)
            pe.matmul(ps_m[:, 128:256], A["ones"][0:1, :], pos[:, :], start=True, stop=True)
            pe.matmul(ps_m[:, 256:257], pos[:, :], A["ones"][0:1, 0:1], start=True, stop=True).then_inc(s.sem("pos_ps"), 1)
            vals.pe(pe, s.sem("mixed"), lambda g: g + 1)
            op.pe(pe)

        @block.scalar
        def _(act):
            hd.nx.act(act)
            act.wait_ge(s.sem("n2"), 1)
            act.activation(nrm[:, :, :], n2[:, :, :], ACT.Sqrt).then_inc(s.sem("nrm"), 1)
            smp.act(act)
            smn.act(act)
            vals.act(act)

        @block.vector
        def _(dve):
            link = linker(dve, s.sem("dve_steps"))
            hd.dve_project(dve, link)
            dve.sem_inc(s.sem("qkv_ready"), 1)
            hd.dve_heads(dve)

            dve.wait_ge(s.sem("guide_in"), 16)
            q = hd.qkv[:, D:2 * D]
            p3 = prod[:, :].rearrange("p (h e) -> p h e", h=16)
            for i, (a, b) in enumerate(((q, q), (guide[:, :], guide[:, :]), (q, guide[:, :]))):
                link(dve.tensor_tensor(prod[:, :], a, b, ALU.mult))
                link(dve.tensor_reduce(n2[:, i, :] if i < 2 else dot[:, :], p3, AX.X, ALU.add))
            dve.sem_inc(s.sem("n2"), 1)
            dve.wait_ge(s.sem("nrm"), 1)
            link(dve.tensor_tensor(nrm[:, 0, :], nrm[:, 0, :], nrm[:, 1, :], ALU.mult))
            link(dve.reciprocal(nrm[:, 0, :], nrm[:, 0, :]))
            link(dve.tensor_tensor(dot[:, :], dot[:, :], nrm[:, 0, :], ALU.mult))
            link(dve.tensor_reduce(sim[:, :], dot[:, :], AX.X, ALU.add))
            dve.tensor_scalar(sim[:, :], sim[:, :], 1 / 16, None, ALU.mult).then_inc(s.sem("sim"), 1)
            dve.wait_ge(s.sem("srow_ps"), 1)
            link(dve.tensor_copy(srow[:, :], ps_m[0:1, 0:T]))
            link(dve.tensor_reduce(mm1[:, 0:1], srow[:, REG:T], AX.X, ALU.min))
            link(dve.tensor_reduce(mm1[:, 1:2], srow[:, REG:T], AX.X, ALU.max))
            link(dve.tensor_tensor(mm1[:, 2:3], mm1[:, 1:2], mm1[:, 0:1], ALU.subtract))
            link(dve.reciprocal(mm1[:, 3:4], mm1[:, 2:3]))
            link(dve.tensor_scalar(srow[:, :], srow[:, :], mm1[:, 0:1], mm1[:, 3:4], ALU.subtract, ALU.mult))
            dve.tensor_scalar(pos[:, :], srow[:, :], 0.9, None, ALU.is_gt).then_inc(s.sem("pos"), 1)
            dve.wait_ge(s.sem("pos_ps"), 1)
            link(dve.tensor_scalar(bp[:, :], ps_m[:, 128:256], 1.0, -FAR, ALU.subtract, ALU.mult))
            link(dve.tensor_scalar(bn[:, :], ps_m[:, 128:256], FAR, None, ALU.mult))
            link(dve.memset(bp[:, 0:REG], 0.0))
            link(dve.memset(bn[:, 0:REG], 0.0))
            dve.wait_ge(s.sem("reg"), 1)
            link(dve.tensor_scalar(wt[:, 2:3], wt[:, 3:4], -1.0, 1.0, ALU.mult, ALU.add))
            link(dve.tensor_tensor(wt[:, 0:1], wt[:, 2:3], ps_m[:, 256:257], ALU.mult))
            link(dve.tensor_tensor(wt[:, 1:2], wt[:, 2:3], wt[:, 0:1], ALU.subtract))
            for i in range(2):
                link(dve.scalar_tensor_tensor(out=wt[:, i:i + 1], in0=wt[:, 3:4], scalar=0.5, in1=wt[:, i:i + 1],
                                              op0=ALU.mult, op1=ALU.add))

            def scores(g):
                dve.wait_ge(s.sem("scores"), g + 1)
                return cols(hd.ps_h[g], 4)

            smp.dve(dve, link, scores, bp[:, :])
            smn.dve(dve, link, scores, bn[:, :])
            for i, sm in enumerate((smp, smn)):
                sm.dve_sums(dve, link)
                link(dve.tensor_scalar(cf[:, i, :], sm.l[:, :], wt[:, i:i + 1], None, ALU.mult))
            for g in range(4):
                gs = slice(4 * g, 4 * g + 4)
                link(dve.tensor_tensor(smp.p[:, gs, :], smp.p[:, gs, :], add_cols(cf[:, 0, gs], T), ALU.mult))
                link(dve.tensor_tensor(smn.p[:, gs, :], smn.p[:, gs, :], add_cols(cf[:, 1, gs], T), ALU.mult))
                dve.tensor_tensor(smp.p[:, gs, :], smp.p[:, gs, :], smn.p[:, gs, :], ALU.add).then_inc(s.sem("mixed"), 1)
            dve.wait_ge(s.sem("y_ps"), 1)
            dve.tensor_copy(op.y[:, :], ps_y[:, 0:D]).then_inc(s.sem("y_ready"), 1)
            op.dve(dve, link)


def dve_first_max(dve, link, A, scores, n, m, key, onehot):
    iota = A["iota16"][:, 0:n]
    link(dve.tensor_reduce(m, scores, AX.X, ALU.max))
    link(dve.tensor_scalar(onehot, scores, m, None, ALU.is_equal))
    link(dve.scalar_tensor_tensor(out=onehot, in0=onehot, scalar=-1000.0, in1=iota, op0=ALU.mult, op1=ALU.add))
    link(dve.tensor_reduce(key, onehot, AX.X, ALU.min))
    link(dve.tensor_scalar(onehot, iota, -1000.0, key, ALU.add, ALU.is_equal))


class DenseExperts:

    E, F = 8, 1024
    FC = F // 128

    def __init__(self, s, A, x, ident, prefix):
        self.s, self.A, self.x, self.ident, self.prefix = s, A, x, ident, prefix
        self.w1, self.w2 = s.sb("w1", [128, 2, DC, self.F]), s.sb("w2", [128, 2, self.FC, D])
        self.b1, self.b2 = s.sb("b1", [128, self.E * self.FC]), s.sb("b2", [self.E, D])
        self.gate, self.gateT = s.sb("gate", [128, self.E]), s.sb("gateT", [self.E, T])
        self.hT = s.sb("hT", [128, 2, self.FC, T])
        self.acc = s.sb("acc", [128, D])
        self.ps_h = [[s.ps(f"ps_h{j}{i}") for i in range(2)] for j in range(2)]
        self.ps_y = [s.ps(f"ps_y{j}") for j in range(2)]

    def load(self, sp, j, e):
        s, A, p = self.s, self.A, self.prefix
        sp.dma_start(self.w1[:, j, :, :], A[p + "W1"][bass.ds(e, 1), :, :, :]).then_inc(s.sem(f"w1_in{j}"), 16)
        sp.dma_start(self.w2[:, j, :, :], A[p + "W2"][bass.ds(e, 1), :, :, :]).then_inc(s.sem(f"w2_in{j}"), 16)

    def sp(self, sp):
        s, A, p = self.s, self.A, self.prefix
        for j in range(2):
            self.load(sp, j, j)
            if j == 0:
                sp.dma_start(self.b1[:, :], A[p + "b1"]).then_inc(s.sem("b1_in"), 16)
                sp.dma_start(self.b2[:, :], A[p + "b2"]).then_inc(s.sem("b2_in"), 16)
        with sp.Fori(0, self.E // 2 - 1) as it:
            for j in range(2):
                sp.wait_ge(s.sem("expert_ps"), it * 2 + (j + 1))
                self.load(sp, j, it * 2 + (2 + j))

    def pe(self, pe, xnT):
        s = self.s
        with pe.Fori(0, self.E // 2) as it:
            for j in range(2):
                pe.wait_ge(s.sem(f"w1_in{j}"), it * 16 + 16)
                pe.wait_ge(s.sem("hT"), it * 2 * self.FC)
                for f in range(self.FC):
                    out = self.ps_h[j][f // 4][:, (f % 4) * T:(f % 4 + 1) * T]
                    mm = pe_dense(pe, out, lambda c: self.w1[:, j, c, f * 128:(f + 1) * 128], lambda c: xnT[:, c, :])
                    if f % 4 == 3:
                        mm.then_inc(s.sem("h_ps"), 1)
            for j in range(2):
                pe.wait_ge(s.sem(f"w2_in{j}"), it * 16 + 16)
                pe.wait_ge(s.sem("acc"), it * 2)
                for f in range(self.FC):
                    pe.wait_ge(s.sem("hT"), (it * 2 + j) * self.FC + (f + 1))
                    mm = pe.matmul(self.ps_y[j][:, 0:D], self.hT[:, j, f, :], self.w2[:, j, f, :],
                                   start=(f == 0), stop=(f == self.FC - 1))
                mm.then_inc(s.sem("expert_ps"), 1)
        pe.wait_ge(s.sem("gate"), 1)
        pe.wait_ge(s.sem("hT"), self.E * self.FC)
        pe.matmul(self.ps_h[0][0][0:self.E, 0:T], self.gate[:, :], self.ident[:, :], start=True,
                  stop=True).then_inc(s.sem("gateT_ps"), 1)
        pe.wait_ge(s.sem("b2_in"), 16)
        pe.wait_ge(s.sem("gateT"), 1)
        pe.matmul(self.ps_h[1][0][:, 0:D], self.gateT[:, :], self.b2[:, :], start=True, stop=True).then_inc(s.sem("b2_ps"), 1)

    def dve(self, dve, link):
        s, x = self.s, self.x
        finish(dve, dve.memset(self.acc[:, :], 0.0), s.sem("acc0"))
        dve.wait_ge(s.sem("b1_in"), 16)
        with dve.Fori(0, self.E // 2) as it:
            for j in range(2):
                dve.wait_ge(s.sem("expert_ps"), it * 2)
                for f in range(self.FC):
                    if f % 4 == 0:
                        dve.wait_ge(s.sem("h_ps"), (it * 2 + j) * (self.FC // 4) + (f // 4 + 1))
                    dve.tensor_scalar(self.hT[:, j, f, :], self.ps_h[j][f // 4][:, (f % 4) * T:(f % 4 + 1) * T],
                                      self.b1[:, bass.ds((it * 2 + j) * self.FC + f, 1)], 0.0, ALU.add, ALU.max).then_inc(s.sem("hT"), 1)
            for j in range(2):
                dve.wait_ge(s.sem("expert_ps"), it * 2 + (j + 1))
                dve.wait_ge(s.sem("acc"), it * 2 + j)
                dve.scalar_tensor_tensor(out=self.acc[:, :], in0=self.ps_y[j][:, 0:D],
                                         scalar=self.gate[:, bass.ds(it * 2 + j, 1)], in1=self.acc[:, :],
                                         op0=ALU.mult, op1=ALU.add).then_inc(s.sem("acc"), 1)
        dve.wait_ge(s.sem("acc"), self.E)
        link(dve.tensor_tensor(x[:, :], x[:, :], self.acc[:, :], ALU.add))
        dve.wait_ge(s.sem("gateT_ps"), 1)
        dve.tensor_copy(self.gateT[:, :], self.ps_h[0][0][0:self.E, 0:T]).then_inc(s.sem("gateT"), 1)
        dve.wait_ge(s.sem("b2_ps"), 1)
        link(dve.tensor_tensor(x[:, :], x[:, :], self.ps_h[1][0][:, 0:D], ALU.add))


def dve_floor(dve, link, dst, src, whole, above):
    link(dve.tensor_copy(whole, src))
    link(dve.tensor_copy(dst, whole))
    link(dve.tensor_tensor(above, dst, src, ALU.is_gt))
    link(dve.tensor_tensor(dst, dst, above, ALU.subtract))


def stage_l1_ffn(nc, A, x, ident):
    with Stage(nc, "l1f") as s:
        ex = DenseExperts(s, A, x, ident, "L1_ffn_")
        ps_a, ps_k = s.ps("ps_a"), s.ps("ps_k")
        nx = NormX(s, x, ident, ps_a)
        wr, br = s.sb("wr", [128, DC]), s.sb("br", [128, 1])
        key, fl, g8, q8, ab = (s.sb(n, [128, 1]) for n in ("key", "fl", "g8", "q8", "ab"))
        whole = s.sb("whole", [128, 1], I32)
        block = s.block()

        @block.sync
        def _(sp):
            sp.dma_start(wr[:, :], A["L1_ffn_wr"]).then_inc(s.sem("wr_in"), 16)
            sp.dma_start(br[:, :], A["L1_ffn_br"].partition_broadcast(128)).then_inc(s.sem("wr_in"), 16)
            ex.sp(sp)

        @block.tensor
        def _(pe):
            nx.pe(pe)
            pe.wait_ge(s.sem("wr_in"), 32)
            pe.wait_ge(s.sem("xnT"), 1)
            pe_dense(pe, ps_k[:, 0:1], lambda c: nx.xnT[:, c, :], lambda c: wr[:, c:c + 1]).then_inc(s.sem("key_ps"), 1)
            ex.pe(pe, nx.xnT)

        @block.scalar
        def _(act):
            nx.act(act)

        @block.vector
        def _(dve):
            link = linker(dve, s.sem("dve_steps"))
            nx.dve(dve, link)
            dve.wait_ge(s.sem("wr_in"), 32)
            dve.wait_ge(s.sem("key_ps"), 1)
            link(dve.tensor_tensor(key[:, :], ps_k[:, 0:1], br[:, :], ALU.add))
            dve_floor(dve, link, fl[:, :], key[:, :], whole[:, :], ab[:, :])
            link(dve.tensor_scalar(q8[:, :], fl[:, :], 1 / 8, None, ALU.mult))
            dve_floor(dve, link, g8[:, :], q8[:, :], whole[:, :], ab[:, :])
            link(dve.scalar_tensor_tensor(out=fl[:, :], in0=g8[:, :], scalar=-8.0, in1=fl[:, :], op0=ALU.mult, op1=ALU.add))
            finish(dve, dve.tensor_scalar(ex.gate[:, :], A["iota16"][:, 0:8], fl[:, 0:1], None, ALU.is_equal), s.sem("gate"))
            ex.dve(dve, link)


def stage_l2_ffn(nc, A, x, ident):
    E = 8
    CAP = 2 * -(-T // E)
    with Stage(nc, "l2f") as s:
        ex = DenseExperts(s, A, x, ident, "L2_ffn_")
        ps_a, ps_k = s.ps("ps_a"), s.ps("ps_k")
        nx = NormX(s, x, ident, ps_a)
        wg = s.sb("wg", [128, DC, E])
        sc, s2, oh = s.sb("sc", [128, E]), s.sb("s2", [128, E]), s.sb("oh", [128, 2, E])
        m, r = s.sb("m", [128, 2]), s.sb("r", [128, 4])
        ok = s.sb("ok", [128, 2, E])
        block = s.block()

        @block.sync
        def _(sp):
            sp.dma_start(wg[:, :, :], A["L2_ffn_gate_w"]).then_inc(s.sem("wg_in"), 16)
            ex.sp(sp)

        @block.tensor
        def _(pe):
            nx.pe(pe)
            pe.wait_ge(s.sem("wg_in"), 16)
            pe.wait_ge(s.sem("xnT"), 1)
            pe_dense(pe, ps_k[:, 0:E], lambda c: nx.xnT[:, c, :], lambda c: wg[:, c, :]).then_inc(s.sem("logit_ps"), 1)
            pe.wait_ge(s.sem("chosen"), 1)
            pe.matmul(ps_a[:, 0:2 * E], A["causal"][:, :], oh[:, :, :], start=True, stop=False, skip_group_check=True)
            pe.matmul(ps_a[:, E:2 * E], A["ones"][:, :], oh[:, 0, :], start=False, stop=True,
                      skip_group_check=True).then_inc(s.sem("place_ps"), 1)
            ex.pe(pe, nx.xnT)

        @block.scalar
        def _(act):
            nx.act(act)
            act.wait_ge(s.sem("shifted"), 1)
            act.activation(sc[:, :], sc[:, :], ACT.Exp, accum_out=r[:, 0:1]).then_inc(s.sem("exp"), 1)

        @block.vector
        def _(dve):
            link = linker(dve, s.sem("dve_steps"))
            nx.dve(dve, link)
            dve.wait_ge(s.sem("logit_ps"), 1)
            link(dve.tensor_reduce(r[:, 1:2], ps_k[:, 0:E], AX.X, ALU.max))
            dve.tensor_scalar(sc[:, :], ps_k[:, 0:E], r[:, 1:2], None, ALU.subtract).then_inc(s.sem("shifted"), 1)
            dve.wait_ge(s.sem("exp"), 1)
            link(dve.reciprocal(r[:, 2:3], r[:, 0:1]))
            link(dve.tensor_scalar(sc[:, :], sc[:, :], r[:, 2:3], None, ALU.mult))
            dve_first_max(dve, link, A, sc[:, :], E, m[:, 0:1], r[:, 3:4], oh[:, 0, :])
            link(dve.scalar_tensor_tensor(out=s2[:, :], in0=oh[:, 0, :], scalar=-2.0, in1=sc[:, :], op0=ALU.mult, op1=ALU.add))
            dve_first_max(dve, link, A, s2[:, :], E, m[:, 1:2], r[:, 3:4], oh[:, 1, :])
            dve.sem_inc(s.sem("chosen"), 1)
            link(dve.tensor_tensor(r[:, 0:1], m[:, 0:1], m[:, 1:2], ALU.add))
            link(dve.reciprocal(r[:, 0:1], r[:, 0:1]))
            link(dve.tensor_scalar(m[:, :], m[:, :], r[:, 0:1], None, ALU.mult))
            dve.wait_ge(s.sem("place_ps"), 1)
            link(dve.tensor_scalar(ok[:, :, :], ps_a[:, 0:2 * E].rearrange("p (k e) -> p k e", k=2), float(CAP), None, ALU.is_le))
            link(dve.tensor_tensor(ok[:, :, :], ok[:, :, :], oh[:, :, :], ALU.mult))
            link(dve.tensor_scalar(ex.gate[:, :], ok[:, 0, :], m[:, 0:1], None, ALU.mult))
            finish(dve, dve.scalar_tensor_tensor(out=ex.gate[:, :], in0=ok[:, 1, :], scalar=m[:, 1:2], in1=ex.gate[:, :],
                                                 op0=ALU.mult, op1=ALU.add), s.sem("gate"))
            ex.dve(dve, link)


def stage_l0_ffn(nc, A, x, ident):
    E, F = 16, 512
    FC = F // 128
    TWO_PI = 6.283185307179586
    C1 = 6.28125
    C2 = TWO_PI - C1
    PI = 3.1415925
    with Stage(nc, "l0f") as s:
        wm, wf = s.sb("wm", [128, 2, DC, F]), s.sb("wf", [128, 2, DC, F])
        wd = s.sb("wd", [128, 2, FC, D])
        ph = s.sb("ph", [128, 2, F])
        wr, br = s.sb("wr", [128, DC, E]), s.sb("br", [128, E])
        nw = s.sb("nw", [128, D])
        sc, oh = s.sb("sc", [128, E]), s.sb("oh", [128, 2, E])
        m, r, gate = s.sb("m", [128, 2]), s.sb("r", [128, 4]), s.sb("gate", [128, E])
        sp_, pos, mag = s.sb("sp", [128, 2, F]), s.sb("pos", [128, 2, F]), s.sb("mag", [128, 2, F])
        turns, arg = s.sb("turns", [128, 2, F]), s.sb("arg", [128, 2, F])
        whole = s.sb("whole", [128, 2, F], I32)
        hid, hT = s.sb("hid", [128, 2, F]), s.sb("hT", [128, 2, FC, T])
        acc, sq = s.sb("acc", [128, D]), s.sb("sq", [128, D])
        ps_m, ps_f = [s.ps(f"ps_m{j}") for j in range(2)], [s.ps(f"ps_f{j}") for j in range(2)]
        ps_t, ps_y = [s.ps(f"ps_t{j}") for j in range(2)], [s.ps(f"ps_y{j}") for j in range(2)]
        nx = NormX(s, x, ident, ps_t[0])
        block = s.block()

        @block.sync
        def _(sp):
            def load(j, e):
                for name, dst in (("mag", wm), ("freq", wf), ("down", wd)):
                    sp.dma_start(dst[:, j, :, :], A["L0_ffn_bank_" + name][bass.ds(e, 1), :, :, :]).then_inc(s.sem(f"{name}_in{j}"), 16)
                sp.dma_start(ph[:, j, :], A["L0_ffn_bank_phase"][bass.ds(e, 1), :].partition_broadcast(128)).then_inc(s.sem(f"phase_in{j}"), 16)

            sp.dma_start(wr[:, :, :], A["L0_ffn_router_w"]).then_inc(s.sem("wr_in"), 16)
            load_rows(sp, s, A, [("br", br, "L0_ffn_router_bias"), ("nw", nw, "L0_ffn_norm_w")])
            for j in range(2):
                load(j, j)
            with sp.Fori(0, E // 2 - 1) as it:
                for j in range(2):
                    sp.wait_ge(s.sem("expert_ps"), it * 2 + (j + 1))
                    load(j, it * 2 + (2 + j))

        @block.tensor
        def _(pe):
            nx.pe(pe)
            pe.wait_ge(s.sem("wr_in"), 16)
            pe.wait_ge(s.sem("xnT"), 1)
            pe_dense(pe, ps_y[0][:, 0:E], lambda c: nx.xnT[:, c, :], lambda c: wr[:, c, :]).then_inc(s.sem("router_ps"), 1)
            pe.wait_ge(s.sem("router"), 1)
            with pe.Fori(0, E // 2) as it:
                for j in range(2):
                    pe.wait_ge(s.sem(f"freq_in{j}"), it * 16 + 16)
                    pe.wait_ge(s.sem("freq_read"), it * 2)
                    pe_dense(pe, ps_f[j][:, :], lambda c: nx.xnT[:, c, :], lambda c: wf[:, j, c, :]).then_inc(s.sem("freq_ps"), 1)
                    pe.wait_ge(s.sem(f"mag_in{j}"), it * 16 + 16)
                    pe.wait_ge(s.sem("tanh"), it * 2)
                    pe_dense(pe, ps_m[j][:, :], lambda c: nx.xnT[:, c, :], lambda c: wm[:, j, c, :]).then_inc(s.sem("mag_ps"), 1)
                for j in range(2):
                    pe.wait_ge(s.sem("hid"), it * 2 + (j + 1))
                    pe.wait_ge(s.sem("hT"), it * 2)
                    pe_transposes(pe, ps_t[j], hid[:, j, :], ident, FC).then_inc(s.sem("hT_ps"), 1)
                for j in range(2):
                    pe.wait_ge(s.sem(f"down_in{j}"), it * 16 + 16)
                    pe.wait_ge(s.sem("acc"), it * 2)
                    pe.wait_ge(s.sem("hT"), it * 2 + (j + 1))
                    pe_dense(pe, ps_y[j][:, 0:D], lambda c: hT[:, j, c, :], lambda c: wd[:, j, c, :], FC).then_inc(s.sem("expert_ps"), 1)

        @block.scalar
        def _(act):
            nx.act(act)
            act.wait_ge(s.sem("second"), 1)
            act.activation(r[:, 1:2], r[:, 0:1], ACT.Exp).then_inc(s.sem("ratio"), 1)
            with act.Fori(0, E // 2) as it:
                for j in range(2):
                    act.wait_ge(s.sem("negabs"), it * 2 + (j + 1))
                    act.activation(sp_[:, j, :], sp_[:, j, :], ACT.Exp).then_inc(s.sem("exp"), 1)
                    act.wait_ge(s.sem("mag_ps"), it * 2 + (j + 1))
                    act.wait_ge(s.sem("hid"), it * 2)
                    act.activation(mag[:, j, :], ps_m[j][:, :], ACT.Tanh).then_inc(s.sem("tanh"), 1)
                act.wait_ge(s.sem("exp"), it * 2 + 2)
                act.activation(sp_[:, :, :], sp_[:, :, :], ACT.Ln, bias=A["ones"][:, 0:1]).then_inc(s.sem("log"), 1)
                for j in range(2):
                    act.wait_ge(s.sem("angle"), it * 2 + (j + 1))
                    act.activation(arg[:, j, :], arg[:, j, :], ACT.Sin).then_inc(s.sem("cos"), 1)
                for j in range(2):
                    act.wait_ge(s.sem("hT_ps"), it * 2 + (j + 1))
                    act.wait_ge(s.sem("expert_ps"), it * 2)
                    act.activation(hT[:, j, :, :], cols(ps_t[j], FC), ACT.Copy).then_inc(s.sem("hT"), 1)
            act.wait_ge(s.sem("ms"), 1)
            act.activation(r[:, 1:2], r[:, 2:3], ACT.Sqrt).then_inc(s.sem("rms"), 1)

        @block.vector
        def _(dve):
            link = linker(dve, s.sem("dve_steps"))
            nx.dve(dve, link)
            dve.wait_ge(s.sem("br_in"), 16)
            dve.wait_ge(s.sem("router_ps"), 1)
            finish(dve, dve.tensor_tensor(sc[:, :], ps_y[0][:, 0:E], br[:, :], ALU.add), s.sem("router"))
            dve_first_max(dve, link, A, sc[:, :], E, m[:, 0:1], r[:, 3:4], oh[:, 0, :])
            link(dve.scalar_tensor_tensor(out=sc[:, :], in0=oh[:, 0, :], scalar=FAR, in1=sc[:, :], op0=ALU.mult, op1=ALU.add))
            dve_first_max(dve, link, A, sc[:, :], E, m[:, 1:2], r[:, 3:4], oh[:, 1, :])
            dve.tensor_tensor(r[:, 0:1], m[:, 1:2], m[:, 0:1], ALU.subtract).then_inc(s.sem("second"), 1)
            dve.wait_ge(s.sem("ratio"), 1)
            link(dve.tensor_scalar(r[:, 2:3], r[:, 1:2], 1.0, None, ALU.add))
            link(dve.reciprocal(r[:, 2:3], r[:, 2:3]))
            link(dve.tensor_tensor(r[:, 3:4], r[:, 1:2], r[:, 2:3], ALU.mult))
            link(dve.tensor_scalar(gate[:, :], oh[:, 0, :], r[:, 2:3], None, ALU.mult))
            link(dve.scalar_tensor_tensor(out=gate[:, :], in0=oh[:, 1, :], scalar=r[:, 3:4], in1=gate[:, :],
                                          op0=ALU.mult, op1=ALU.add))
            link(dve.memset(acc[:, :], 0.0))
            STEPS = 2 * 9
            with dve.Fori(0, E // 2) as it:
                link = linker(dve, s.sem("dve_loop"), it * STEPS)
                for j in range(2):
                    n = it * 2 + j
                    dve.wait_ge(s.sem("freq_ps"), n + 1)
                    dve.wait_ge(s.sem("hid"), it * 2)
                    link(dve.tensor_scalar(pos[:, j, :], ps_f[j][:, :], 0.0, None, ALU.max))
                    dve.scalar_tensor_tensor(out=sp_[:, j, :], in0=pos[:, j, :], scalar=-2.0, in1=ps_f[j][:, :],
                                             op0=ALU.mult, op1=ALU.add).then_inc(s.sem("negabs"), 1)
                    dve.wait_ge(s.sem("negabs"), n + 1)
                    dve.sem_inc(s.sem("freq_read"), 1)
                for j in range(2):
                    n = it * 2 + j
                    dve.wait_ge(s.sem(f"phase_in{j}"), it * 16 + 16)
                    dve.wait_ge(s.sem("log"), it + 1)
                    link(dve.tensor_tensor(arg[:, j, :], sp_[:, j, :], pos[:, j, :], ALU.add))
                    link(dve.scalar_tensor_tensor(out=arg[:, j, :], in0=arg[:, j, :], scalar=0.1, in1=ph[:, j, :],
                                                  op0=ALU.add, op1=ALU.add))
                    link(dve.tensor_scalar(turns[:, j, :], arg[:, j, :], 1 / TWO_PI, 0.25, ALU.mult, ALU.add))
                    link(dve.tensor_copy(whole[:, j, :], turns[:, j, :]))
                    link(dve.tensor_copy(turns[:, j, :], whole[:, j, :]))
                    link(dve.scalar_tensor_tensor(out=arg[:, j, :], in0=turns[:, j, :], scalar=-C1, in1=arg[:, j, :],
                                                  op0=ALU.mult, op1=ALU.add))
                    link(dve.scalar_tensor_tensor(out=arg[:, j, :], in0=turns[:, j, :], scalar=-C2, in1=arg[:, j, :],
                                                  op0=ALU.mult, op1=ALU.add))
                    link(dve.tensor_scalar(arg[:, j, :], arg[:, j, :], TWO_PI / 4, PI, ALU.add, ALU.min))
                    dve.tensor_scalar(arg[:, j, :], arg[:, j, :], -PI, None, ALU.max).then_inc(s.sem("angle"), 1)
                for j in range(2):
                    n = it * 2 + j
                    dve.wait_ge(s.sem("cos"), n + 1)
                    dve.wait_ge(s.sem("tanh"), n + 1)
                    dve.wait_ge(s.sem("hT_ps"), it * 2)
                    dve.tensor_tensor(hid[:, j, :], mag[:, j, :], arg[:, j, :], ALU.mult).then_inc(s.sem("hid"), 1)
                assert link.count[0] == STEPS, link.count
                for j in range(2):
                    n = it * 2 + j
                    dve.wait_ge(s.sem("expert_ps"), n + 1)
                    dve.wait_ge(s.sem("acc"), n)
                    dve.scalar_tensor_tensor(out=acc[:, :], in0=ps_y[j][:, 0:D], scalar=gate[:, bass.ds(n, 1)],
                                             in1=acc[:, :], op0=ALU.mult, op1=ALU.add).then_inc(s.sem("acc"), 1)
            dve.wait_ge(s.sem("acc"), E)
            link = linker(dve, s.sem("dve_end"))
            link(dve.tensor_tensor(sq[:, :], acc[:, :], acc[:, :], ALU.mult))
            link(dve.tensor_reduce(r[:, 2:3], sq[:, :], AX.X, ALU.add))
            dve.tensor_scalar(r[:, 2:3], r[:, 2:3], 1 / D, 1e-6, ALU.mult, ALU.add).then_inc(s.sem("ms"), 1)
            dve.wait_ge(s.sem("rms"), 1)
            dve_rsqrt(dve, link, r[:, 0:1], r[:, 1:2], r[:, 2:3])
            dve.wait_ge(s.sem("nw_in"), 16)
            link(dve.scalar_tensor_tensor(out=acc[:, :], in0=acc[:, :], scalar=r[:, 0:1], in1=nw[:, :],
                                          op0=ALU.mult, op1=ALU.mult))
            link(dve.tensor_tensor(x[:, :], x[:, :], acc[:, :], ALU.add))


def stage_l1_attn(nc, A, x, ident):
    H, HD, I = 8, 64, 512
    IC = I // 128
    K = 4
    CAP = 15.0
    PFX = "L1_attn_"
    with Stage(nc, "mls") as s:
        wup = s.sb("wup", [128, DC, 2 * I])
        wts = {n: s.sb("w_" + n, [128, IC, I]) for n in ("skip", "q", "k", "v", "o")}
        wif, wdn = s.sb("wif", [128, IC, 16]), s.sb("wdn", [128, IC, D])
        rows = {n: s.sb("r_" + n, [128, w]) for n, w in (
            ("ln_g", D), ("ln_b", D), ("b_up_l", I), ("b_up_r", I), ("b_skip", I), ("b_v", I), ("b_o", I),
            ("mh_g", I), ("mh_b", I), ("b_down", D), ("conv_w", K), ("conv_b", 1))}
        bqk, bif = s.sb("bqk", [128, 2, IC]), s.sb("bif", [H, 2])
        xa, xaT = s.sb("xa", [128, D]), s.sb("xaT", [128, DC, T])
        xt, rt = s.sb("xt", [128, K - 1 + I]), s.sb("rt", [128, I])
        xc, sg, sr = s.sb("xc", [128, I]), s.sb("sg", [128, I]), s.sb("sr", [128, I])
        xtT, xcT = s.sb("xtT", [128, IC, T]), s.sb("xcT", [128, IC, T])
        skip, v, o = s.sb("skip", [128, I]), s.sb("v", [128, H, HD + 1]), s.sb("o", [128, I])
        qT, kT = s.sb("qT", [128, IC, T]), s.sb("kT", [128, IC, T])
        gi, gf, fs = s.sb("gi", [H, T]), s.sb("gf", [H, T]), s.sb("fs", [H, T])
        one8 = s.sb("one8", [H, T])
        b, mx, em = s.sb("b", [H, T]), s.sb("mx", [H, T]), s.sb("em", [H, T])
        hsel = s.sb("hsel", [H, H, T])
        halves = s.sb("halves", [128, 2])
        cb = s.sb("cb", [128, 16])
        dm, sd = s.sb("dm", [128, H, T]), s.sb("sd", [128, H, T])
        den, hh, hn = s.sb("den", [128, H]), s.sb("hh", [128, I]), s.sb("hn", [128, I])
        hst, hmv = s.sb("hst", [128, H, 6]), s.sb("hmv", [128, H, 2])
        hsd, hvar = s.sb("hsd", [128, H]), s.sb("hvar", [128, H])
        oT = s.sb("oT", [128, IC, T])
        P = [s.ps(f"P{n}") for n in range(8)]
        nx, n1 = NormX(s, x, ident, P[0]), RowNorm(s, "n1", 1e-6)
        block = s.block()

        @block.sync
        def _(sp):
            sp.dma_start(wup[:, :, :], A[PFX + "W_up"]).then_inc(s.sem("wup_in"), 16)
            for n in ("ln_g", "ln_b", "b_up_l", "b_up_r", "conv_w", "conv_b"):
                sp.dma_start(rows[n][:, :], A[PFX + n].partition_broadcast(128)).then_inc(s.sem("rows1_in"), 16)
            for n in ("skip", "v", "o", "q", "k"):
                sp.dma_start(wts[n][:, :, :], A[PFX + "W_" + n]).then_inc(s.sem(f"w_{n}_in"), 16)
            sp.dma_start(wif[:, :, :], A[PFX + "W_if"]).then_inc(s.sem("wif_in"), 16)
            for n in ("b_skip", "b_v", "b_o", "mh_g", "mh_b", "b_down"):
                sp.dma_start(rows[n][:, :], A[PFX + n].partition_broadcast(128)).then_inc(s.sem("rows2_in"), 16)
            sp.dma_start(bqk[:, :, :], A[PFX + "b_qk"]).then_inc(s.sem("rows2_in"), 16)
            sp.dma_start(bif[:, :], A[PFX + "b_if"]).then_inc(s.sem("rows2_in"), 16)
            sp.dma_start(wdn[:, :, :], A[PFX + "W_down"]).then_inc(s.sem("wdn_in"), 16)

        @block.gpsimd
        def _(pool):
            pool.memset(hsel[:, :, :], 0.0).then_inc(s.sem("hsel0"), 1)
            pool.wait_ge(s.sem("hsel0"), 1)
            pool.affine_select(out=hsel[:, :, :], in_=hsel[:, :, :], compare_op=ALU.not_equal, fill=1.0, base=0,
                               pattern=[[-1, H], [0, T]], channel_multiplier=1).then_inc(s.sem("hsel"), 1)
            pool.affine_select(out=halves[:, 0:1], in_=A["ones"][:, 0:1], compare_op=ALU.is_ge, fill=0.0, base=HD - 1,
                               pattern=[[0, 1]], channel_multiplier=-1).then_inc(s.sem("half0"), 1)
            pool.affine_select(out=halves[:, 1:2], in_=A["ones"][:, 0:1], compare_op=ALU.is_ge, fill=0.0, base=-HD,
                               pattern=[[0, 1]], channel_multiplier=1).then_inc(s.sem("half1"), 1)
            pool.wait_ge(s.sem("half0"), 1)
            pool.wait_ge(s.sem("half1"), 1)
            pool.sem_inc(s.sem("halves"), 1)
            for g in range(2):
                pool.wait_ge(s.sem("decay_all"), g + 1)
                pool.tensor_tensor(dm[:, 4 * g:4 * g + 4, :], dm[:, 4 * g:4 * g + 4, :],
                                   A["causal"][:, :].unsqueeze(1).to_broadcast([128, 4, T]), ALU.mult).then_inc(s.sem("decay"), 1)

        @block.tensor
        def _(pe):
            def dense(out, aT, w, n=IC):
                return pe_dense(pe, out, lambda c: aT[:, c, :], lambda c: w[:, c, :], n)

            nx.pe(pe)
            pe.wait_ge(s.sem("xa"), 1)
            pe.wait_ge(s.sem("xnT"), 1)
            pe_transposes(pe, P[0], xa, ident).then_inc(s.sem("xaT_ps"), 1)
            pe.wait_ge(s.sem("wup_in"), 16)
            pe.wait_ge(s.sem("xaT"), 1)
            pe_dense(pe, P[1][:, :], lambda c: xaT[:, c, :], lambda c: wup[:, c, 0:I]).then_inc(s.sem("up_ps"), 1)
            pe_dense(pe, P[2][:, :], lambda c: xaT[:, c, :], lambda c: wup[:, c, I:2 * I]).then_inc(s.sem("up_ps"), 1)
            pe.wait_ge(s.sem("xt"), 1)
            for c in range(IC):
                mm = pe.transpose(P[3][:, c * T:(c + 1) * T], xt[:, K - 1 + c * 128:K - 1 + (c + 1) * 128], ident[:, :])
            mm.then_inc(s.sem("xtT_ps"), 1)
            pe.wait_ge(s.sem("w_v_in"), 16)
            pe.wait_ge(s.sem("xtT"), 1)
            dense(P[6][:, :], xtT, wts["v"]).then_inc(s.sem("v_ps"), 1)
            pe.wait_ge(s.sem("w_o_in"), 16)
            dense(P[7][:, :], xtT, wts["o"]).then_inc(s.sem("o_ps"), 1)
            pe.wait_ge(s.sem("xc"), 1)
            pe_transposes(pe, P[4], xc, ident, IC).then_inc(s.sem("xcT_ps"), 1)
            pe.wait_ge(s.sem("wif_in"), 16)
            pe.wait_ge(s.sem("xcT"), 1)
            pe.wait_ge(s.sem("rt"), 1)
            for g in range(2):
                mm = pe_dense(pe, P[2][0:H, g * T:(g + 1) * T], lambda c: wif[:, c, g * H:(g + 1) * H],
                              lambda c: xcT[:, c, :], IC)
            mm.then_inc(s.sem("if_ps"), 1)
            for n, ps in (("q", P[0]), ("k", P[1])):
                pe.wait_ge(s.sem(f"w_{n}_in"), 16)
                for e in range(IC):
                    mm = pe_dense(pe, ps[:, e * T:(e + 1) * T], lambda c: wts[n][:, c, e * 128:(e + 1) * 128],
                                  lambda c: xcT[:, c, :], IC)
                mm.then_inc(s.sem(f"{n}_ps"), 1)
            pe.wait_ge(s.sem("w_skip_in"), 16)
            dense(P[5][:, :], xcT, wts["skip"]).then_inc(s.sem("skip_ps"), 1)
            pe.wait_ge(s.sem("em"), 1)
            pe.matmul(P[3][:, 0:H], b[:, :], ident[0:H, 0:H], start=True, stop=True)
            pe.matmul(P[3][:, H:2 * H], em[:, :], ident[0:H, 0:H], start=True, stop=True).then_inc(s.sem("cb_ps"), 1)
            pe.wait_ge(s.sem("hsel"), 1)
            pe.wait_ge(s.sem("skip"), 1)
            for h in range(H):
                mm = pe.matmul(P[4 + h // 4][:, (h % 4) * T:(h % 4 + 1) * T], hsel[:, h, :], mx[:, :], start=True, stop=True)
                if h % 4 == 3:
                    mm.then_inc(s.sem("mx_ps"), 1)
            pe.wait_ge(s.sem("qT"), 1)
            pe.wait_ge(s.sem("kT"), 1)
            pe.wait_ge(s.sem("v"), 1)
            pe.wait_ge(s.sem("o"), 1)
            for c in range(IC):
                for odd in range(2):
                    lo = HD * odd
                    mm = pe.matmul(P[6 + odd][:, c * T:(c + 1) * T], kT[lo:lo + HD, c, :], qT[lo:lo + HD, c, :],
                                   start=True, stop=True)
                    if c == IC - 1:
                        mm.then_inc(s.sem(f"scores{odd}"), 1)
            pe.wait_ge(s.sem("halves"), 1)
            for c in range(IC):
                mm = pe.matmul(P[2][:, 2 * c:2 * c + 2], qT[:, c, :], halves[:, :], start=True, stop=True)
            mm.then_inc(s.sem("qsum_ps"), 1)
            pe.wait_ge(s.sem("sd"), 2)
            for h in range(H):
                mm = pe.matmul(P[h // 4][:, (h % 4) * 65:(h % 4 + 1) * 65], sd[:, h, :], v[:, h, :], start=True, stop=True)
                if h % 4 == 3:
                    mm.then_inc(s.sem("num_ps"), 1)
            pe.wait_ge(s.sem("hn"), 1)
            pe_transposes(pe, P[3], hn, ident, IC).then_inc(s.sem("oT_ps"), 1)
            pe.wait_ge(s.sem("wdn_in"), 16)
            pe.wait_ge(s.sem("oT"), 1)
            dense(P[4][:, 0:D], oT, wdn).then_inc(s.sem("down_ps"), 1)

        @block.scalar
        def _(act):
            nx.act(act)
            n1.act(act)
            for name, tile in (("c", sg), ("r", sr), ("o", o)):
                act.wait_ge(s.sem(name + "_neg"), 1)
                act.activation(tile[:, :], tile[:, :], ACT.Exp).then_inc(s.sem(name + "_exp"), 1)
            act.wait_ge(s.sem("if_pre"), 1)
            act.activation(gi[:, :], gi[:, :], ACT.Tanh).then_inc(s.sem("tanh"), 1)
            act.activation(gf[:, :], gf[:, :], ACT.Tanh).then_inc(s.sem("tanh"), 1)
            act.wait_ge(s.sem("mx"), 1)
            act.activation(em[:, :], mx[:, :], ACT.Exp, scale=-1.0).then_inc(s.sem("em"), 1)
            for g in range(2):
                act.wait_ge(s.sem("dm"), 4 * g + 4)
                act.activation(dm[:, 4 * g:4 * g + 4, :], dm[:, 4 * g:4 * g + 4, :], ACT.Exp,
                               scale=-1.0).then_inc(s.sem("decay_all"), 1)
            act.wait_ge(s.sem("h_var"), 1)
            act.activation(hsd[:, :], hvar[:, :], ACT.Sqrt).then_inc(s.sem("h_std"), 1)

        @block.vector
        def _(dve):
            def sigmoid_in(name, tile, z):
                dve.tensor_scalar(tile[:, :], z[:, :], -1.0, 87.0, ALU.mult, ALU.min).then_inc(s.sem(name + "_neg"), 1)

            def sigmoid_out(link, name, tile):
                dve.wait_ge(s.sem(name + "_exp"), 1)
                link(dve.tensor_scalar(tile[:, :], tile[:, :], 1.0, None, ALU.add))
                link(dve.reciprocal(tile[:, :], tile[:, :]))

            link = linker(dve, s.sem("dve_steps"))
            link(dve.memset(xt[:, 0:K - 1], 0.0))
            link(dve.memset(v[:, :, HD:HD + 1], 1.0))
            link(dve.memset(one8[:, :], 1.0))
            nx.dve(dve, link)
            n1.dve(dve, link, xa[:, :], nx.xn[:, :])
            dve.wait_ge(s.sem("rows1_in"), 6 * 16)
            link(dve.tensor_tensor(xa[:, :], xa[:, :], rows["ln_g"][:, :], ALU.mult))
            dve.tensor_tensor(xa[:, :], xa[:, :], rows["ln_b"][:, :], ALU.add).then_inc(s.sem("xa"), 1)
            dve.wait_ge(s.sem("xaT_ps"), 1)
            dve.tensor_copy(xaT[:, :, :], cols(P[0])).then_inc(s.sem("xaT"), 1)
            dve.wait_ge(s.sem("up_ps"), 1)
            finish(dve, dve.tensor_tensor(xt[:, K - 1:], P[1][:, :], rows["b_up_l"][:, :], ALU.add), s.sem("xt"))
            link(dve.tensor_scalar(xc[:, :], xt[:, 0:I], rows["conv_w"][:, 0:1], rows["conv_b"][:, 0:1], ALU.mult, ALU.add))
            for m in range(1, K):
                ins = dve.scalar_tensor_tensor(out=xc[:, :], in0=xt[:, m:m + I], scalar=rows["conv_w"][:, m:m + 1],
                                               in1=xc[:, :], op0=ALU.mult, op1=ALU.add)
                if m < K - 1:
                    link(ins)
                else:
                    finish(dve, ins, s.sem("conv"))
            sigmoid_in("c", sg, xc)
            dve.wait_ge(s.sem("up_ps"), 2)
            finish(dve, dve.tensor_tensor(rt[:, :], P[2][:, :], rows["b_up_r"][:, :], ALU.add), s.sem("rt"))
            sigmoid_in("r", sr, rt)
            dve.wait_ge(s.sem("xtT_ps"), 1)
            dve.tensor_copy(xtT[:, :, :], cols(P[3], IC)).then_inc(s.sem("xtT"), 1)
            sigmoid_out(link, "c", sg)
            dve.tensor_tensor(xc[:, :], xc[:, :], sg[:, :], ALU.mult).then_inc(s.sem("xc"), 1)
            sigmoid_out(link, "r", sr)
            link(dve.tensor_tensor(sr[:, :], sr[:, :], rt[:, :], ALU.mult))
            dve.wait_ge(s.sem("xcT_ps"), 1)
            dve.tensor_copy(xcT[:, :, :], cols(P[4], IC)).then_inc(s.sem("xcT"), 1)
            dve.wait_ge(s.sem("rows2_in"), 8 * 16)
            dve.wait_ge(s.sem("v_ps"), 1)
            heads = "p (h e) -> p h e"
            dve.tensor_tensor(v[:, :, 0:HD], P[6][:, :].rearrange(heads, h=H),
                              rows["b_v"][:, :].rearrange(heads, h=H), ALU.add).then_inc(s.sem("v"), 1)
            dve.wait_ge(s.sem("o_ps"), 1)
            finish(dve, dve.tensor_tensor(o[:, :], P[7][:, :], rows["b_o"][:, :], ALU.add), s.sem("o"))
            sigmoid_in("o", o, o)
            dve.wait_ge(s.sem("if_ps"), 1)
            link(dve.tensor_scalar(gi[:, :], P[2][0:H, 0:T], bif[:, 0:1], 1 / CAP, ALU.add, ALU.mult))
            dve.tensor_scalar(gf[:, :], P[2][0:H, T:2 * T], bif[:, 1:2], 1 / CAP, ALU.add, ALU.mult).then_inc(s.sem("if_pre"), 1)
            dve.wait_ge(s.sem("tanh"), 2)
            link(dve.tensor_scalar(gi[:, :], gi[:, :], CAP, None, ALU.mult))
            link(dve.tensor_scalar(gf[:, :], gf[:, :], CAP, None, ALU.mult))
            link(dve.tensor_tensor_scan(fs[:, :], one8[:, :], gf[:, :], 0.0, ALU.mult, ALU.add))
            link(dve.tensor_tensor(b[:, :], gi[:, :], fs[:, :], ALU.subtract))
            dve.tensor_tensor_scan(mx[:, :], b[:, :], b[:, :], 0.0, ALU.max, ALU.max).then_inc(s.sem("mx"), 1)
            dve.wait_ge(s.sem("q_ps"), 1)
            for c in range(IC):
                ins = dve.tensor_scalar(qT[:, c, :], P[0][:, c * T:(c + 1) * T], bqk[:, 0, c:c + 1], None, ALU.add)
            ins.then_inc(s.sem("qT"), 1)
            dve.wait_ge(s.sem("k_ps"), 1)
            for c in range(IC):
                ins = dve.tensor_scalar(kT[:, c, :], P[1][:, c * T:(c + 1) * T], bqk[:, 1, c:c + 1], HD ** -0.5,
                                        ALU.add, ALU.mult)
            ins.then_inc(s.sem("kT"), 1)
            dve.wait_ge(s.sem("skip_ps"), 1)
            dve.tensor_tensor(skip[:, :], P[5][:, :], rows["b_skip"][:, :], ALU.add).then_inc(s.sem("skip"), 1)
            dve.wait_ge(s.sem("cb_ps"), 1)
            link(dve.tensor_copy(cb[:, :], P[3][:, 0:2 * H]))
            for h in range(H):
                dve.wait_ge(s.sem("mx_ps"), h // 4 + 1)
                dve.tensor_scalar(dm[:, h, :], P[4 + h // 4][:, (h % 4) * T:(h % 4 + 1) * T], cb[:, h:h + 1], 0.0,
                                  ALU.subtract, ALU.max).then_inc(s.sem("dm"), 1)
            dve.wait_ge(s.sem("decay"), 2)
            for odd in range(2):
                dve.wait_ge(s.sem(f"scores{odd}"), 1)
                by_row = "p (c odd) t -> p odd c t"
                dve.tensor_tensor(sd[:, :, :].rearrange(by_row, odd=2)[:, odd], cols(P[6 + odd], 4),
                                  dm[:, :, :].rearrange(by_row, odd=2)[:, odd], ALU.mult).then_inc(s.sem("sd"), 1)
            dve.wait_ge(s.sem("qsum_ps"), 1)
            link(dve.tensor_tensor(den[:, :], P[2][:, 0:H], cb[:, H:2 * H], ALU.mult))
            for g in range(2):
                dve.wait_ge(s.sem("num_ps"), g + 1)
                num = P[g][:, 0:260].rearrange("p (h e) -> p h e", h=4)
                gs = slice(4 * g, 4 * g + 4)
                link(dve.tensor_tensor(den[:, gs], den[:, gs], num[:, :, 64], ALU.add))
                link(dve.tensor_scalar(den[:, gs], den[:, gs], 1.0, None, ALU.max))
                link(dve.reciprocal(den[:, gs], den[:, gs]))
                link(dve.tensor_tensor(hh[:, g * 256:(g + 1) * 256].rearrange("p (h e) -> p h e", h=4), num[:, :, 0:64],
                                       add_cols(den[:, gs], HD), ALU.mult))
            sigmoid_out(link, "o", o)
            link(dve.tensor_tensor(hh[:, :], hh[:, :], o[:, :], ALU.mult))
            for h in range(H):
                link(dve.bn_stats(hst[:, h, :], hh[:, h * HD:(h + 1) * HD]))
                link(dve.bn_aggr(hmv[:, h, :], hst[:, h, :]))
            dve.tensor_scalar(hvar[:, :], hmv[:, :, 1], 1e-6, None, ALU.add).then_inc(s.sem("h_var"), 1)
            h3 = hh[:, :].rearrange("p (h e) -> p h e", h=H)
            link(dve.tensor_tensor(h3, h3, hmv[:, :, 0:1].to_broadcast([128, H, HD]), ALU.subtract))
            dve.wait_ge(s.sem("h_std"), 1)
            dve_rsqrt(dve, link, den[:, :], hsd[:, :], hvar[:, :])
            link(dve.tensor_tensor(h3, h3, add_cols(den[:, :], HD), ALU.mult))
            link(dve.tensor_tensor(hh[:, :], hh[:, :], rows["mh_g"][:, :], ALU.mult))
            link(dve.tensor_tensor(hh[:, :], hh[:, :], rows["mh_b"][:, :], ALU.add))
            link(dve.tensor_tensor(hh[:, :], hh[:, :], skip[:, :], ALU.add))
            dve.tensor_tensor(hn[:, :], hh[:, :], sr[:, :], ALU.mult).then_inc(s.sem("hn"), 1)
            dve.wait_ge(s.sem("oT_ps"), 1)
            dve.tensor_copy(oT[:, :, :], cols(P[3], IC)).then_inc(s.sem("oT"), 1)
            dve.wait_ge(s.sem("down_ps"), 1)
            link(dve.tensor_tensor(xa[:, :], P[4][:, 0:D], rows["b_down"][:, :], ALU.add))
            link(dve.tensor_tensor(xa[:, :], xa[:, :], nx.xn[:, :], ALU.add))
            link(dve.tensor_tensor(x[:, :], x[:, :], xa[:, :], ALU.add))


def more_layouts(i, out):
    import numpy as np
    w = i["L1_xattn_Wkv"]
    out["L1_xattn_wq"] = chunked(i["L1_xattn_Wq"])
    out["L1_xattn_wkT"] = chunked(w[:, :512].T, 64)
    out["L1_xattn_wv"] = chunked(w[:, 512:])
    out["L1_xattn_wo"] = chunked(i["L1_xattn_Wo"], 64)
    for n in ("ln_x_g", "ln_x_b", "ln_l_g", "ln_l_b", "ln_o_g", "ln_o_b"):
        out["L1_xattn_" + n] = i["L1_xattn_" + n]
    out["mask_bk1"] = i["mask_BxS2_bk1"][0].astype(np.int32)
    out["mask_ff1"] = i["mask_BxS2_ff1"][0].reshape(-1, 128).T
    out["mask_ik1"] = i["mask_BxSxS2_ik1"][0]
    out["L2_xattn_wq"] = chunked(i["L2_xattn_wq"])
    out["L2_xattn_wkv"] = chunked(np.concatenate([i["L2_xattn_wk"], i["L2_xattn_wv"]], 1))
    out["L2_xattn_dense_w"] = chunked(i["L2_xattn_dense_w"])
    for n in ("ln_gamma", "ln_beta", "dense_b"):
        out["L2_xattn_" + n] = i["L2_xattn_" + n]
    out["L0_attn_decay_logit"] = i["L0_attn_decay_logit"].reshape(1)
    out["L0_attn_out_scale"] = i["L0_attn_out_scale"].reshape(1)
    out["L0_attn_q_scale"] = i["L0_attn_q_scale"].reshape(DC, 128).T
    out["L0_attn_k_scale"] = i["L0_attn_k_scale"].reshape(DC, 128).T
    out["L2_attn_W_qkv"] = chunked(i["L2_attn_W_qkv"])
    out["L2_attn_W_o"] = chunked(i["L2_attn_W_o"])
    out["L3_attn_W_qkv"] = chunked(np.concatenate([i["L3_attn_W" + n].T for n in "qkv"], 1))
    out["L3_attn_b_qkv"] = np.concatenate([i["L3_attn_b" + n] for n in "qkv"])
    out["L3_attn_Wo"] = chunked(i["L3_attn_Wo"].T)
    out["L3_attn_bo"] = i["L3_attn_bo"]
    w = i["L3_ffn_W_qkv"]
    out["L3_ffn_W_kqv"] = chunked(np.concatenate([w[:, D:2 * D], w[:, :D], w[:, 2 * D:]], 1))
    out["L3_ffn_guide"] = i["L3_ffn_g_info"][0, 0]
    out["L3_ffn_W_proj"] = chunked(i["L3_ffn_W_proj"])
    out["L3_ffn_b_proj"] = i["L3_ffn_b_proj"]
    for p, w1, b1, w2, b2 in (("L1_ffn_", i["L1_ffn_W1"], i["L1_ffn_b1"], i["L1_ffn_W2"], i["L1_ffn_b2"]),
                              ("L2_ffn_", i["L2_ffn_fc1_w"].transpose(0, 2, 1), i["L2_ffn_fc1_b"][:, 0],
                               i["L2_ffn_fc2_w"], i["L2_ffn_fc2_b"][:, 0])):
        out[p + "W1"] = np.stack([chunked(w) for w in w1])
        out[p + "W2"] = np.stack([chunked(w) for w in w2])
        out[p + "b1"] = b1.reshape(-1, 128).T
        out[p + "b2"] = b2
    out["L1_ffn_wr"] = i["L1_ffn_wr"].reshape(DC, 128).T
    out["L1_ffn_br"] = i["L1_ffn_br"].reshape(1)
    out["L2_ffn_gate_w"] = chunked(i["L2_ffn_gate_w"].T)
    out["L0_ffn_router_w"] = chunked(i["L0_ffn_router_w"].T)
    for n in ("router_bias", "norm_w", "bank_phase"):
        out["L0_ffn_" + n] = i["L0_ffn_" + n]
    for n in ("mag", "freq", "down"):
        out["L0_ffn_bank_" + n] = np.stack([chunked(w) for w in i["L0_ffn_bank_" + n]])
    p = "L1_attn_"
    out[p + "W_up"] = chunked(np.concatenate([i[p + "W_up_l"].T, i[p + "W_up_r"].T], 1))
    for n in ("skip", "q", "k", "v", "o", "down"):
        out[p + "W_" + n] = chunked(i[p + "W_" + n].T)
    out[p + "W_if"] = chunked(np.concatenate([i[p + "W_i"].T, i[p + "W_f"].T], 1))
    for n in ("ln_g", "ln_b", "b_up_l", "b_up_r", "b_skip", "b_v", "b_o", "mh_g", "mh_b", "b_down", "conv_w", "conv_b"):
        out[p + n] = i[p + n].reshape(-1)
    out[p + "b_qk"] = np.stack([i[p + "b_q"].reshape(-1, 128).T, i[p + "b_k"].reshape(-1, 128).T], 1)
    out[p + "b_if"] = np.stack([i[p + "b_i"], i[p + "b_f"]], 1)


def stage_load(nc, A, x, ident):
    with Stage(nc, "load") as s:
        block = s.block()

        @block.sync
        def _(sp):
            sp.dma_start(x[:, :], A["x"]).then_inc(s.sem("x_in"), 16)
            sp.wait_ge(s.sem("x_in"), 16)

        @block.gpsimd
        def _(pool):
            pool.memset(ident[:, :], 0.0).then_inc(s.sem("zero"), 1)
            pool.wait_ge(s.sem("zero"), 1)
            pool.affine_select(out=ident[:, :], in_=ident[:, :], compare_op=ALU.not_equal, fill=1.0, base=0,
                               pattern=[[-1, 128]], channel_multiplier=1).then_inc(s.sem("ident"), 1)
            pool.wait_ge(s.sem("ident"), 1)
            hm = A["head_mask"]
            pool.memset(hm[:, :], 1.0).then_inc(s.sem("ones"), 1)
            pool.wait_ge(s.sem("ones"), 1)
            pool.affine_select(out=hm[:, :], in_=hm[:, :], compare_op=ALU.is_ge, fill=0.0, base=0,
                               pattern=[[-16, 8]], channel_multiplier=1).then_inc(s.sem("from"), 1)
            pool.wait_ge(s.sem("from"), 1)
            pool.affine_select(out=hm[:, :], in_=hm[:, :], compare_op=ALU.is_ge, fill=0.0, base=15,
                               pattern=[[16, 8]], channel_multiplier=-1).then_inc(s.sem("head_mask"), 1)
            pool.wait_ge(s.sem("head_mask"), 1)
            cm = A["causal"]
            pool.memset(cm[:, :], 1.0).then_inc(s.sem("ones2"), 1)
            pool.wait_ge(s.sem("ones2"), 1)
            pool.affine_select(out=cm[:, :], in_=cm[:, :], compare_op=ALU.is_ge, fill=0.0, base=0,
                               pattern=[[1, 128]], channel_multiplier=-1).then_inc(s.sem("causal"), 1)
            pool.iota(A["iota16"][:, :], [[1, 16]], base=0, channel_multiplier=0,
                      allow_small_or_imprecise_dtypes=True).then_inc(s.sem("iota16"), 1)
            pool.memset(A["ones"][:, :], 1.0).then_inc(s.sem("ones3"), 1)
            pool.wait_ge(s.sem("causal"), 1)
            pool.wait_ge(s.sem("iota16"), 1)
            pool.wait_ge(s.sem("ones3"), 1)


def stage_store(nc, A, x, ident):
    with Stage(nc, "store") as s:
        block = s.block()

        @block.sync
        def _(sp):
            sp.dma_start(A["out"], x[:, :]).then_inc(s.sem("x_out"), 16)
            sp.wait_ge(s.sem("x_out"), 16)


STAGES = [stage_prepare, stage_l0_xattn, stage_l0_attn, stage_l0_ffn, stage_l1_xattn, stage_l1_attn, stage_l1_ffn,
          stage_l2_xattn, stage_l2_attn, stage_l2_ffn, stage_l3_xattn, stage_l3_attn, stage_l3_ffn]


def program(nc, A, stages):
    with ExitStack() as ctx:
        x = ctx.enter_context(nc.sbuf_tensor("x", [T, D], F32))
        ident = ctx.enter_context(nc.sbuf_tensor("ident", [128, 128], F32))
        A["head_mask"] = ctx.enter_context(nc.sbuf_tensor("head_mask", [128, 8], F32))
        A["causal"] = ctx.enter_context(nc.sbuf_tensor("causal", [128, 128], F32))
        A["iota16"] = ctx.enter_context(nc.sbuf_tensor("iota16", [128, 16], F32))
        A["ones"] = ctx.enter_context(nc.sbuf_tensor("ones", [128, 128], F32))
        A["kv_sum"] = ctx.enter_context(nc.sbuf_tensor("kv_sum", [128, DC, 129], F32))
        A["xn_rows"] = nc.dram_tensor("xn_rows", (128, S2 // 128, D), F32, kind="Internal").ap()
        A["att_order"] = nc.dram_tensor("att_order", (16, T, 16), F32, kind="Internal").ap()
        A["xnT"] = nc.dram_tensor("xnT", (128, DC, S2), F32, kind="Internal").ap()
        for stage in [stage_load, *stages, stage_store]:
            stage(nc, A, x, ident)


def chunked(a, p=128):
    import numpy as np
    a = np.asarray(a)
    return np.ascontiguousarray(a.reshape(-1, p, a.shape[-1]).transpose(1, 0, 2))


def layouts(i):
    import numpy as np
    i = {k: np.asarray(v) for k, v in i.items()}
    ctx = i["ctx_1024"][0]
    out = {"x": i["x"][0], "ctx_rows": chunked(ctx), "ctxT": chunked(ctx.T)}
    w = i["L0_xattn_w_kv"]
    out["L0_xattn_wq"] = chunked(i["L0_xattn_w_q"])
    out["L0_xattn_wkT"] = chunked(w[:, :1024].T, 64)
    out["L0_xattn_wv"] = chunked(w[:, 1024:])
    out["L0_xattn_wo"] = chunked(i["L0_xattn_w_out1"], 64)
    out["L0_xattn_w_out2"] = chunked(i["L0_xattn_w_out2"])
    out["L0_xattn_gamma"] = i["L0_xattn_gamma"]
    more_layouts(i, out)
    return {k: np.ascontiguousarray(v) for k, v in out.items()}


def kernel(**inputs):
    import numpy as np
    import concourse.bacc as bacc
    from concourse.bass_utils import run_bass_kernel_spmd

    nc = bacc.Bacc("TRN2", target_bir_lowering=False, num_devices=1)
    arrays, A = {}, {}
    for name, a in layouts(inputs).items():
        arrays[f"in_{name}"] = a
        A[name] = nc.dram_tensor(f"in_{name}", a.shape, mybir.dt.from_np(a.dtype), kind="ExternalInput").ap()
    A["out"] = nc.dram_tensor("out_0", (T, D), F32, kind="ExternalOutput").ap()
    program(nc, A, STAGES)
    r = run_bass_kernel_spmd(nc, [arrays], core_ids=[0])
    return r.results[0]["out_0"].reshape(1, T, D)
```

```python
from contextlib import ExitStack

import concourse.bass as bass
from concourse import mybir

ALU = mybir.AluOpType
ACT = mybir.ActivationFunctionType
AX = mybir.AxisListType
F32 = mybir.dt.float32
I32 = mybir.dt.int32
F32R = mybir.dt.float32r

T = 128
D = 256
DC = D // 128
S2 = 12544
CH = 896
CT = CH // 128
HALF = CH // 2
NCH = S2 // CH
ARENA = 51200
FAR = -2.0 ** 100


class Stage:

    def __init__(self, nc, name, fast=0):
        self.fast, self.arena_size = fast, ARENA - fast
        self.nc, self.name, self.ctx, self.sems = nc, name, ExitStack(), {}

    def __enter__(self):
        self.ctx.__enter__()
        self.arena = self.ctx.enter_context(self.nc.sbuf_tensor(f"{self.name}_sbuf", [128, self.arena_size], F32))
        if self.fast:
            self.fast_arena = self.ctx.enter_context(self.nc.sbuf_tensor(f"{self.name}_fast", [128, self.fast], F32R))
        self.psum = self.ctx.enter_context(self.nc.psum_tensor(f"{self.name}_psum", [128, 8, 512], F32))
        self.used = self.banks = self.used_fast = 0
        return self

    def __exit__(self, *e):
        self.region.__exit__(*e)
        self.nc.clear_and_free_semaphores(list(self.sems.values()))
        self.nc.all_engine_barrier()
        return self.ctx.__exit__(*e)

    def sb(self, name, shape, dt=F32):
        n = 1
        for d in shape[1:]:
            n *= d
        if dt == F32R:
            assert self.used_fast + n <= self.fast, f"{self.name}: no room for {name}"
            v = self.fast_arena[0:shape[0], self.used_fast:self.used_fast + n]
            self.used_fast += n
        else:
            assert self.used + n <= self.arena_size, f"{self.name}: no room for {name}"
            v = self.arena[0:shape[0], self.used:self.used + n]
            self.used += n
            if dt != F32:
                v = v.bitcast(dt)
        names = "abcd"[:len(shape) - 1]
        if len(names) > 1:
            v = v.rearrange(f"p ({' '.join(names)}) -> p {' '.join(names)}", **dict(zip(names, shape[1:])))
        return v

    def ps(self, name, banks=1):
        at = self.banks
        self.banks += banks
        assert self.banks <= 8, f"{self.name}: no bank for {name}"
        return self.psum[:, at, :] if banks == 1 else self.psum[:, at:at + banks, :]

    def sem(self, name):
        if name not in self.sems:
            self.sems[name] = self.nc.alloc_semaphore(f"{self.name}_{name}")
        return self.sems[name]

    def block(self):
        self.region = self.nc.Block()
        return self.region.__enter__()


def linker(eng, sem, base=0):
    count = [0]

    def link(ins):
        count[0] += 1
        ins.then_inc(sem, 1)
        eng.wait_ge(sem, base + count[0])

    link.count = count
    return link


def dve_moments(dve, link, src, st, mv, eps, done):
    link(dve.bn_stats(st, src))
    link(dve.bn_aggr(mv[:, 0:2], st))
    dve.tensor_scalar(mv[:, 1:2], mv[:, 1:2], eps, None, ALU.add).then_inc(done, 1)


def dve_rsqrt(dve, link, r, root, var):
    link(dve.reciprocal(r, root))
    link(dve.tensor_tensor(root, r, r, ALU.mult))
    link(dve.tensor_tensor(root, root, var, ALU.mult))
    link(dve.tensor_scalar(root, root, -0.5, 1.5, ALU.mult, ALU.add))
    link(dve.tensor_tensor(r, r, root, ALU.mult))


def dve_rescale(dve, link, dst, src, mv, done):
    dve_rsqrt(dve, link, mv[:, 3:4], mv[:, 2:3], mv[:, 1:2])
    dve.tensor_scalar(dst, src, mv[:, 0:1], mv[:, 3:4], ALU.subtract, ALU.mult).then_inc(done, 1)
    dve.wait_ge(done, 1)


class NormX:

    def __init__(self, s, x, ident, ps):
        self.s, self.x, self.ident, self.ps = s, x, ident, ps
        self.st, self.mv = s.sb("x_st", [128, 6]), s.sb("x_mv", [128, 4])
        self.xn, self.xnT = s.sb("xn", [128, D]), s.sb("xnT", [128, DC, T])

    def dve(self, dve, link):
        s = self.s
        dve_moments(dve, link, self.x[:, :], self.st[:, :], self.mv, 1e-5, s.sem("x_var"))
        dve.wait_ge(s.sem("x_std"), 1)
        dve_rescale(dve, link, self.xn[:, :], self.x[:, :], self.mv, s.sem("xn"))
        dve.wait_ge(s.sem("xnT_ps"), 1)
        dve.tensor_copy(self.xnT[:, :, :], self.ps[:, 0:D].rearrange("p (c t) -> p c t", c=DC)).then_inc(s.sem("xnT"), 1)

    def act(self, act):
        s = self.s
        act.wait_ge(s.sem("x_var"), 1)
        act.activation(self.mv[:, 2:3], self.mv[:, 1:2], ACT.Sqrt).then_inc(s.sem("x_std"), 1)

    def pe(self, pe):
        s = self.s
        pe.wait_ge(s.sem("xn"), 1)
        for c in range(DC):
            mm = pe.transpose(self.ps[:, c * 128:(c + 1) * 128], self.xn[:, c * 128:(c + 1) * 128], self.ident[:, :])
        mm.then_inc(s.sem("xnT_ps"), 1)


class ContextAttention:

    def __init__(self, s, heads, width, qt, values, kT_dram, v_dram, ident, mask=None, mask_dram=None,
                 bias_per_one=1.0e9, tail=None, split=False):
        self.s, self.H, self.W, self.qt, self.values = s, heads, width, qt, values
        self.kT_dram, self.v_dram, self.ident = kT_dram, v_dram, ident
        self.mask, self.mask_dram, self.bias_per_one, self.tail = mask, mask_dram, bias_per_one, tail
        self.U = 2 * heads
        self.split = split
        halves = 1 if split else 2
        self.kT = s.sb("ca_kT", [128, halves, DC, CH])
        self.v = s.sb("ca_v", [128, halves, CT, D])
        self.bufs = 4 if mask == "full" else 2
        self.p = s.sb("ca_p", [128, self.bufs, CH])
        if split:
            self.kT_parts = [s.sb(f"ca_kT_{i}", [128, 2, DC, CH], F32R) for i in ("high", "low")]
            self.v_parts = [s.sb(f"ca_v_{i}", [128, 2, CT, D], F32R) for i in ("high", "low")]
            self.pT_parts = [s.sb(f"ca_pT_{i}", [128, 2, CT, T], F32R) for i in ("high", "low")]
        else:
            self.pT = s.sb("ca_pT", [128, 2, CT, T])
        self.acc = s.sb("ca_acc", [128, heads, width])
        self.l = s.sb("ca_l", [128, heads])
        self.mb = s.sb("ca_mb", [128, 2])
        self.negm = s.sb("ca_negm", [128, 2, heads])
        self.alpha = s.sb("ca_alpha", [128, 8])
        self.rs = s.sb("ca_rs", [128, 8])
        if mask == "rows":
            self.raw = s.sb("ca_raw", [1, CH], I32)
            self.bias = s.sb("ca_bias", [1, 2, CH], F32R)
            self.one = s.sb("ca_one", [1, T], F32R)
        if mask == "full":
            self.raw = s.sb("ca_raw", [128, 2, CH], I32)
            self.bias = s.sb("ca_bias", [128, 2, CH])
            self.sm = s.sb("ca_sm", [128, self.bufs, CH])
        self.ps_s = [s.ps(f"ca_s{i}", 2) for i in range(2)]
        self.ps_t = s.ps("ca_t", 2).rearrange("p b (t k) -> p (b t) k", k=T)
        self.ps_o = [s.ps(f"ca_o{i}") for i in range(2)]
        self.max_lag = 1 if mask == "full" else 0
        self.t_lag, self.v_lag, self.acc_lag = (self.max_lag + i for i in (2, 3, 4))
        self.pre = heads if tail else 0

    def load_split(self, sp, chunk):
        loads = [("kT", self.kT[:, 0, :, :], self.kT_dram[:, :, bass.ds(chunk * CH, CH)]),
                 ("v", self.v[:, 0, :, :], self.v_dram[:, bass.ds(chunk * CT, CT), :])]
        if self.mask:
            loads.append(("bias", self.raw[:, :], self.mask_dram[:, bass.ds(chunk * CH, CH)]))
        for name, dst, src in loads:
            self.wait(sp, name if name == "bias" else name + "_low", chunk, 0)
            sp.dma_start(dst, src).then_inc(self.s.sem(name + "_in"), 16)

    def load(self, sp, j, chunk):
        s = self.s
        sp.dma_start(self.kT[:, j, :, :], self.kT_dram[:, :, bass.ds(chunk * CH, CH)]).then_inc(s.sem(f"kv_in{j}"), 16)
        sp.dma_start(self.v[:, j, :, :], self.v_dram[:, bass.ds(chunk * CT, CT), :]).then_inc(s.sem(f"kv_in{j}"), 16)
        if self.mask:
            sp.dma_start(self.raw[:, j, :], self.mask_dram[:, bass.ds(chunk * CH, CH)]).then_inc(s.sem(f"kv_in{j}"), 16)

    def sp(self, sp):
        s, H, U = self.s, self.H, self.U
        if self.split:
            self.load_split(sp, 0)
            with sp.Fori(1, NCH) as it:
                self.load_split(sp, it)
            return
        self.load(sp, 0, 0)
        self.load(sp, 1, 1)
        with sp.Fori(0, NCH // 2 - 1) as it:
            for j in range(2):
                sp.wait_ge(s.sem("pv"), it * U + (self.pre + H * (j + 1)))
                if self.mask:
                    sp.wait_ge(s.sem("bias"), it * 2 + (j + 1))
                self.load(sp, j, it * 2 + (2 + j))

    def chunk(self, j, loads, number):
        return [(h, j, loads, number) for h in range(self.H)]

    def run(self, eng, step):
        def steps(base, before, units, more=0):
            def unit(u):
                return units[u] if 0 <= u < len(units) else before[u] if u < 0 and before else None

            for k in range(len(units) + more):
                step(eng, base, k, unit)

        H, pre = self.H, self.pre
        even = self.chunk(0, 1, 0)
        steps(0, [], [(h, None, 0, -1) for h in range(pre)] + even)
        with eng.Fori(0, NCH // 2 - 1) as it:
            steps(it * self.U + (pre + H), even, self.chunk(1, it + 1, it * 2 + 1) + self.chunk(0, it + 2, it * 2 + 2))
        steps(pre + (NCH - 1) * H, even, self.chunk(1, NCH // 2, NCH - 1), self.acc_lag)

    def wait(self, eng, name, base, off):
        if not isinstance(base, int) or base + off > 0:
            eng.wait_ge(self.s.sem(name), base + off)

    def wait_chunk(self, eng, j, loads):
        eng.wait_ge(self.s.sem(f"kv_in{j}"), loads * (48 if self.mask else 32))

    def products(self, pe, out, pairs):
        terms = [(x, y) for a, b in pairs for i, x in enumerate(a) for k, y in enumerate(b) if i + k < 2]
        for n, (x, y) in enumerate(terms):
            mm = pe.matmul(out, x, y, start=(n == 0), stop=(n == len(terms) - 1))
        return mm

    def pe_scores(self, pe, base, u, h, j):
        b = u % 2
        self.wait(pe, "masked" if self.mask == "full" else "p", base, u - 1)
        for i in range(2 if j is not None else 1):
            cut = slice(i * HALF, (i + 1) * HALF)
            pairs = []
            for q, c in self.qt(h):
                if j is None:
                    pairs.append((q, [k[:, c, :] for k in self.tail[0]]))
                else:
                    pairs.append((q, [k[:, j, c, cut] for k in (self.kT_parts if self.split else [self.kT])]))
            if self.mask == "rows" and j is not None:
                pairs.append(([self.one[:, :]], [self.bias[:, j, cut]]))
            mm = self.products(pe, self.ps_s[b][:, i, 0:HALF if j is not None else T], pairs)
        mm.then_inc(self.s.sem("scores"), 1)

    def pe_transposes(self, pe, base, u, j):
        self.wait(pe, "p", base, u + 1)
        self.wait(pe, "pT_low" if self.split else "pT", base, u)
        for t in range(CT if j is not None else 1):
            mm = pe.transpose(self.ps_t[:, t, :], self.p[:, u % self.bufs, t * 128:(t + 1) * 128], self.ident[:, :])
        mm.then_inc(self.s.sem("pT_ps"), 1)

    def pe_values(self, pe, base, u, h, j):
        b = u % 2
        self.wait(pe, "pT_low" if self.split else "pT", base, u + 1)
        self.wait(pe, "acc", base, u - 1)
        lo, hi = self.values(h)
        pairs = []
        for t in range(CT if j is not None else 1):
            w = [p[:, b, t, :] for p in (self.pT_parts if self.split else [self.pT])]
            if j is None:
                pairs.append((w, [v[:, lo:hi] for v in self.tail[1]]))
            else:
                pairs.append((w, [v[:, j, t, lo:hi] for v in (self.v_parts if self.split else [self.v])]))
        self.products(pe, self.ps_o[b][:, 0:self.W], pairs).then_inc(self.s.sem("pv"), 1)

    def pe_step(self, pe, base, k, unit):
        s = self.s
        if unit(k):
            h, j, loads, number = unit(k)
            if h == 0 and j is not None:
                if self.split:
                    pe.wait_ge(s.sem("kT_low"), number + 1)
                    if self.mask:
                        pe.wait_ge(s.sem("bias"), number + 1)
                else:
                    self.wait_chunk(pe, j, loads)
            self.pe_scores(pe, base, k, h, j)
        u = k - self.t_lag
        if unit(u):
            self.pe_transposes(pe, base, u, unit(u)[1])
        u = k - self.v_lag
        if unit(u):
            h, j, loads, number = unit(u)
            if self.split and h == 0 and j is not None:
                pe.wait_ge(s.sem("v_low"), number + 1)
            self.pe_values(pe, base, u, h, j)

    def pe(self, pe):
        if self.mask == "rows":
            pe.wait_ge(self.s.sem("one"), 1)
        self.run(pe, self.pe_step)

    def act_step(self, act, base, k, unit):
        s = self.s
        u = k - self.t_lag
        if unit(u):
            n = CT if unit(u)[1] is not None else 1
            self.wait(act, "pT_ps", base, u + 1)
            self.wait(act, "pv", base, u - 1)
            dst = self.pT_parts[0] if self.split else self.pT
            act.activation(dst[:, u % 2, 0:n, :], self.ps_t[:, 0:n, :], ACT.Copy).then_inc(s.sem("pT"), 1)
        u = k - self.max_lag
        if unit(u):
            h, j, _, _ = unit(u)
            q = u % 8
            self.wait(act, "new_max", base, u + 1)
            self.wait(act, "sums", base, u - 7)
            self.wait(act, "acc", base, u - 7)
            old, new = (1, 0) if j is None else (j, 1 - j)
            negm = self.negm[:, new, h:h + 1]
            act.activation(self.alpha[:, q:q + 1], self.negm[:, old, h:h + 1], ACT.Exp, bias=negm, scale=-1.0)
            self.wait(act, "pT_ps", base, u - self.bufs + 1)
            p = self.p[:, u % self.bufs, :]
            if j is None:
                src, dst = self.ps_s[u % 2][:, 0, 0:T], p[:, 0:T]
            elif self.mask == "full":
                src, dst = self.sm[:, u % self.bufs, :], p
            else:
                src, dst = self.ps_s[u % 2][:, :, 0:HALF], p.rearrange("p (i c) -> p i c", i=2)
            act.activation(dst, src, ACT.Exp, bias=negm, accum_out=self.rs[:, q:q + 1]).then_inc(s.sem("p"), 1)
        following = self.following(unit(k))
        if following:
            self.wait(act, "pv", base, k - unit(k)[0])
            self.act_high(act, *following)

    def act_high(self, act, name, j, number):
        act.wait_ge(self.s.sem(name + "_in"), number * 16 + 16)
        raw, (high, low) = self.parts(name, j)
        act.activation(high, raw, ACT.Copy).then_inc(self.s.sem(name + "_high"), 1)

    def act(self, act):
        if self.split:
            for name in ("kT", "v"):
                self.act_high(act, name, 0, 0)
        self.run(act, self.act_step)

    def dve_step(self, dve, base, k, unit):
        s = self.s
        if unit(k) and self.mask == "full" and unit(k)[1] is not None:
            h, j, loads, number = unit(k)
            if h == 0:
                self.wait_chunk(dve, j, loads)
                dve.tensor_scalar(self.bias[:, j, :], self.raw[:, j, :], 1.0, self.bias_per_one,
                                  ALU.subtract, ALU.mult).then_inc(s.sem("bias"), 1)
                dve.wait_ge(s.sem("bias"), number + 1)
            self.wait(dve, "scores", base, k + 1)
            self.wait(dve, "p", base, k - self.bufs + 1)
            dve.tensor_tensor(self.sm[:, k % self.bufs, :].rearrange("p (i c) -> p i c", i=2),
                              self.ps_s[k % 2][:, :, 0:HALF],
                              self.bias[:, j, :].rearrange("p (i c) -> p i c", i=2),
                              ALU.add).then_inc(s.sem("masked"), 1)
        m = k - self.max_lag
        if unit(m):
            j = unit(m)[1]
            if j is None:
                self.wait(dve, "scores", base, m + 1)
                src = self.ps_s[m % 2][:, 0, 0:T]
            elif self.mask == "full":
                self.wait(dve, "masked", base, m + 1)
                src = self.sm[:, m % self.bufs, :]
            else:
                self.wait(dve, "scores", base, m + 1)
                src = self.ps_s[m % 2][:, :, 0:HALF]
            dve.tensor_reduce(self.mb[:, m % 2:m % 2 + 1], src, AX.XY if len(src.shape) == 3 else AX.X,
                              ALU.max).then_inc(s.sem("unit_max"), 1)
        w = k - self.acc_lag
        if unit(w):
            self.dve_update(dve, base, w, unit(w)[0])
        if unit(m):
            h, j, _, _ = unit(m)
            old, new = (1, 0) if j is None else (j, 1 - j)
            self.wait(dve, "unit_max", base, m + 1)
            self.wait(dve, "p", base, m - 3)
            dve.scalar_tensor_tensor(out=self.negm[:, new, h:h + 1], in0=self.mb[:, m % 2:m % 2 + 1], scalar=-1.0,
                                     in1=self.negm[:, old, h:h + 1], op0=ALU.mult,
                                     op1=ALU.min).then_inc(s.sem("new_max"), 1)
        u = k - self.t_lag
        if self.split and unit(u):
            n = CT if unit(u)[1] is not None else 1
            self.wait(dve, "pT", base, u + 1)
            high, low = (p[:, u % 2, 0:n, :] for p in self.pT_parts)
            dve.tensor_tensor(low, self.ps_t[:, 0:n, :], high.bitcast(F32), ALU.subtract).then_inc(s.sem("pT_low"), 1)
        following = self.following(unit(k))
        if following and following[0] == "v" and self.mask:
            self.wait(dve, "scores", base, k - unit(k)[0])
            self.dve_bias(dve, following[1], following[2])

    def dve_bias(self, dve, j, number):
        dve.wait_ge(self.s.sem("bias_in"), number * 16 + 16)
        dve.tensor_scalar(self.bias[:, j, :], self.raw[:, :], 1.0, self.bias_per_one,
                          ALU.subtract, ALU.mult).then_inc(self.s.sem("bias"), 1)

    def following(self, unit):
        if not self.split or not unit or unit[1] is None or unit[0] - self.H // 2 not in (0, 1):
            return None
        h, j, loads, number = unit
        if isinstance(number, int) and number == NCH - 1:
            return None
        return "kT" if h == self.H // 2 else "v", 1 - j, number + 1

    def parts(self, name, j):
        raw, parts = (self.kT, self.kT_parts) if name == "kT" else (self.v, self.v_parts)
        return raw[:, 0, :, :], [p[:, j, :, :] for p in parts]

    def pool_low(self, pool, name, j, number):
        raw, (high, low) = self.parts(name, j)
        pool.wait_ge(self.s.sem(name + "_high"), number + 1)
        pool.tensor_tensor(low, raw, high.bitcast(F32), ALU.subtract).then_inc(self.s.sem(name + "_low"), 1)

    def pool(self, pool):
        for name in ("kT", "v"):
            self.pool_low(pool, name, 0, 0)
        with pool.Fori(0, NCH // 2 - 1) as it:
            for j in (1, 0):
                for name in ("kT", "v"):
                    self.pool_low(pool, name, j, it * 2 + (2 - j))
        for name in ("kT", "v"):
            self.pool_low(pool, name, 1, NCH - 1)

    def dve_update(self, dve, base, u, h):
        s, q = self.s, u % 8
        self.wait(dve, "pv", base, u + 1)
        self.wait(dve, "p", base, u + 1)
        self.wait(dve, "sums", base, u)
        dve.scalar_tensor_tensor(out=self.l[:, h:h + 1], in0=self.l[:, h:h + 1],
                                 scalar=self.alpha[:, q:q + 1], in1=self.rs[:, q:q + 1],
                                 op0=ALU.mult, op1=ALU.add).then_inc(s.sem("sums"), 1)
        self.wait(dve, "acc", base, u)
        dve.scalar_tensor_tensor(out=self.acc[:, h, :], in0=self.acc[:, h, :],
                                 scalar=self.alpha[:, q:q + 1], in1=self.ps_o[u % 2][:, 0:self.W],
                                 op0=ALU.mult, op1=ALU.add).then_inc(s.sem("acc"), 1)

    def dve(self, dve):
        s = self.s
        link = linker(dve, s.sem("dve_init"))
        link(dve.memset(self.acc[:, :, :], 0.0))
        link(dve.memset(self.l[:, :], 0.0))
        link(dve.memset(self.negm[:, :, :], -FAR))
        if self.mask == "rows":
            dve.tensor_scalar(self.one[:, :], self.ident[0:1, 0:T], 0.0, 1.0, ALU.mult, ALU.add).then_inc(s.sem("one"), 1)
            self.dve_bias(dve, 0, 0)
        self.run(dve, self.dve_step)
        dve.wait_ge(s.sem("sums"), NCH * self.H + self.pre)
        dve.wait_ge(s.sem("acc"), NCH * self.H + self.pre)
        link = linker(dve, s.sem("dve_end"))
        link(dve.reciprocal(self.l[:, :], self.l[:, :]))
        for h in range(self.H):
            dve.tensor_scalar(self.acc[:, h, :], self.acc[:, h, :], self.l[:, h:h + 1], None,
                              ALU.mult).then_inc(s.sem("attended"), 1)


def cols(ps, c=DC):
    return ps[:, 0:c * 128].rearrange("p (c t) -> p c t", c=c)


def finish(eng, ins, sem, n=1):
    ins.then_inc(sem, 1)
    eng.wait_ge(sem, n)


def pe_transposes(pe, ps, src, ident, n=DC):
    for c in range(n):
        mm = pe.transpose(ps[:, c * 128:(c + 1) * 128], src[:, c * 128:(c + 1) * 128], ident[:, :])
    return mm


def pe_dense(pe, out, lhsT, rhs, n=DC):
    for c in range(n):
        mm = pe.matmul(out, lhsT(c), rhs(c), start=(c == 0), stop=(c == n - 1))
    return mm


class WideHeads:

    HD = 64

    def __init__(self, s, H, A, prefix, ident, scale):
        self.s, self.H, self.A, self.prefix, self.ident, self.scale = s, H, A, prefix, ident, scale
        HD = self.HD
        self.wq, self.wkT = s.sb("wq", [128, DC, H * HD]), s.sb("wkT", [HD, H, D])
        self.wv, self.wo = self.wq, self.wkT
        self.qT = s.sb("qT", [HD, H, T])
        self.qk = [s.sb(f"qk_{i}", [128, H, DC, T], F32R) for i in ("high", "low")]
        self.aT, self.oT = s.sb("aT", [128, 2, DC, T]), s.sb("oT", [HD, 2, T])

    def qt(self, h):
        return [([q[:, h, c, :] for q in self.qk], c) for c in range(DC)]

    def use(self, ca, nxT, nxT_sem):
        self.ca, self.nxT, self.nxT_sem = ca, nxT, nxT_sem
        self.banks = [ca.ps_o[1], ca.ps_o[0]]

    def sp(self, sp):
        for name, dst in (("wq", self.wq), ("wkT", self.wkT)):
            sp.dma_start(dst[:, :, :], self.A[self.prefix + name]).then_inc(self.s.sem(name + "_in"), 16)

    def sp_outputs(self, sp):
        sp.wait_ge(self.s.sem("qk_ps"), self.H // 2)
        for name, dst in (("wv", self.wv), ("wo", self.wo)):
            sp.dma_start(dst[:, :, :], self.A[self.prefix + name]).then_inc(self.s.sem(name + "_in"), 16)

    def pe_queries(self, pe):
        s, H, HD = self.s, self.H, self.HD
        pe.wait_ge(s.sem("wq_in"), 16)
        pe.wait_ge(self.nxT_sem, 1)
        for g in range(H // 4):
            if g >= 2:
                pe.wait_ge(s.sem("qT"), g - 1)
            for h in range(4 * g, 4 * g + 4):
                mm = pe_dense(pe, self.banks[g % 2][0:HD, (h % 4) * T:(h % 4 + 1) * T],
                              lambda c: self.wq[:, c, h * HD:(h + 1) * HD], lambda c: self.nxT[:, c, :])
            mm.then_inc(s.sem("qT_ps"), 1)
        pe.wait_ge(s.sem("wkT_in"), 16)
        pe.wait_ge(s.sem("qT"), H // 4)
        for g in range(H // 2):
            if g >= 2:
                pe.wait_ge(s.sem("qk_low"), g - 1)
            for h in range(2 * g, 2 * g + 2):
                for c in range(DC):
                    k = (h % 2) * DC + c
                    mm = pe.matmul(self.banks[g % 2][:, k * T:(k + 1) * T], self.wkT[:, h, c * 128:(c + 1) * 128],
                                   self.qT[:, h, :], start=True, stop=True)
            mm.then_inc(s.sem("qk_ps"), 1)
        pe.wait_ge(s.sem("qk_low"), H // 2)

    def dve_queries(self, dve):
        s, HD = self.s, self.HD
        for g in range(self.H // 4):
            dve.wait_ge(s.sem("qT_ps"), g + 1)
            dve.tensor_scalar(self.qT[:, 4 * g:4 * g + 4, :],
                              self.banks[g % 2][0:HD, :].rearrange("p (h t) -> p h t", h=4),
                              self.scale, None, ALU.mult).then_inc(s.sem("qT"), 1)
        for g in range(self.H // 2):
            high, low = (q[:, 2 * g:2 * g + 2, :, :] for q in self.qk)
            dve.wait_ge(s.sem("qk"), g + 1)
            dve.tensor_tensor(low, self.banks[g % 2][:, :].rearrange("p (h c t) -> p h c t", h=2, c=DC),
                              high.bitcast(F32), ALU.subtract).then_inc(s.sem("qk_low"), 1)

    def act_queries(self, act):
        s = self.s
        for g in range(self.H // 2):
            act.wait_ge(s.sem("qk_ps"), g + 1)
            act.activation(self.qk[0][:, 2 * g:2 * g + 2, :, :],
                           self.banks[g % 2][:, :].rearrange("p (h c t) -> p h c t", h=2, c=DC),
                           ACT.Copy).then_inc(s.sem("qk"), 1)

    def pe_outputs(self, pe, ps):
        s, H, HD, ca = self.s, self.H, self.HD, self.ca
        pe.wait_ge(s.sem("wv_in"), 16)
        pe.wait_ge(s.sem("wo_in"), 16)
        for h in range(H + 2):
            if h < H:
                pe.wait_ge(s.sem("attended"), h + 1)
                if h >= 2:
                    pe.wait_ge(s.sem("aT"), h - 1)
                pe_transposes(pe, ca.ps_s[h % 2][:, 0, :], ca.acc[:, h, :], self.ident).then_inc(s.sem("aT_ps"), 1)
            if 1 <= h <= H:
                g = h - 1
                pe.wait_ge(s.sem("aT"), g + 1)
                if g >= 2:
                    pe.wait_ge(s.sem("oT"), g - 1)
                pe_dense(pe, ca.ps_s[g % 2][0:HD, 1, 0:T], lambda c: self.wv[:, c, g * HD:(g + 1) * HD],
                         lambda c: self.aT[:, g % 2, c, :]).then_inc(s.sem("oT_ps"), 1)
            if h >= 2:
                g = h - 2
                pe.wait_ge(s.sem("oT"), g + 1)
                pe.matmul(ps[:, 0:D], self.oT[:, g % 2, :], self.wo[:, g, :], start=(g == 0),
                          stop=(g == H - 1)).then_inc(s.sem("out_ps"), 1)

    def dve_outputs(self, dve):
        s = self.s
        for h in range(self.H):
            dve.wait_ge(s.sem("aT_ps"), h + 1)
            if h >= 2:
                dve.wait_ge(s.sem("oT_ps"), h - 1)
            dve.tensor_copy(self.aT[:, h % 2, :, :], cols(self.ca.ps_s[h % 2][:, 0, :])).then_inc(s.sem("aT"), 1)

    def act_outputs(self, act):
        s = self.s
        for h in range(self.H):
            act.wait_ge(s.sem("oT_ps"), h + 1)
            if h >= 2:
                act.wait_ge(s.sem("out_ps"), h - 1)
            act.activation(self.oT[:, h % 2, :], self.ca.ps_s[h % 2][0:self.HD, 1, 0:T],
                           ACT.Copy).then_inc(s.sem("oT"), 1)


class RowNorm:

    def __init__(self, s, name, eps):
        self.s, self.name, self.eps = s, name, eps
        self.st, self.mv = s.sb(name + "_st", [128, 6]), s.sb(name + "_mv", [128, 4])

    def dve(self, dve, link, dst, src):
        s = self.s
        dve_moments(dve, link, src, self.st[:, :], self.mv, self.eps, s.sem(self.name + "_var"))
        dve.wait_ge(s.sem(self.name + "_std"), 1)
        dve_rescale(dve, link, dst, src, self.mv, s.sem(self.name))

    def act(self, act):
        act.wait_ge(self.s.sem(self.name + "_var"), 1)
        act.activation(self.mv[:, 2:3], self.mv[:, 1:2], ACT.Sqrt).then_inc(self.s.sem(self.name + "_std"), 1)


def load_rows(sp, s, A, rows):
    for name, dst, src in rows:
        sp.dma_start(dst[:, :], A[src].partition_broadcast(128)).then_inc(s.sem(name + "_in"), 16)


def stage_l0_xattn(nc, A, x, ident):
    H = 16
    with Stage(nc, "l0x", fast=2 * (2 * DC * CH + 2 * CT * D + 2 * CT * T + H * DC * T)) as s:
        heads = WideHeads(s, H, A, "L0_xattn_", ident, WideHeads.HD ** -0.5)
        ca = ContextAttention(s, H, D, heads.qt, lambda h: (0, D), A["ctxT"], A["ctx_rows"], ident, split=True)
        wo2, gam = s.sb("wo2", [128, DC, D]), s.sb("gamma", [128, D])
        h1, h1T, y = s.sb("h1", [128, D]), s.sb("h1T", [128, DC, T]), s.sb("y", [128, D])
        ps_a, ps_b = ca.ps_o[0], ca.ps_o[1]
        nx, ny = NormX(s, x, ident, ps_a), RowNorm(s, "y", 1e-5)
        heads.use(ca, nx.xnT, s.sem("xnT"))
        block = s.block()

        @block.sync
        def _(sp):
            heads.sp(sp)
            sp.dma_start(wo2[:, :, :], A["L0_xattn_w_out2"]).then_inc(s.sem("wo2_in"), 16)
            load_rows(sp, s, A, [("gamma", gam, "L0_xattn_gamma")])
            ca.sp(sp)
            heads.sp_outputs(sp)

        @block.tensor
        def _(pe):
            nx.pe(pe)
            heads.pe_queries(pe)
            ca.pe(pe)
            heads.pe_outputs(pe, ps_a)
            pe.wait_ge(s.sem("h1"), 1)
            pe_transposes(pe, ps_b, h1, ident).then_inc(s.sem("h1T_ps"), 1)
            pe.wait_ge(s.sem("wo2_in"), 16)
            pe.wait_ge(s.sem("h1T"), 1)
            pe_dense(pe, ps_a[:, 0:D], lambda c: h1T[:, c, :], lambda c: wo2[:, c, :]).then_inc(s.sem("y_ps"), 1)

        @block.scalar
        def _(act):
            nx.act(act)
            heads.act_queries(act)
            ca.act(act)
            heads.act_outputs(act)
            ny.act(act)

        @block.gpsimd
        def _(pool):
            ca.pool(pool)

        @block.vector
        def _(dve):
            link = linker(dve, s.sem("dve_steps"))
            nx.dve(dve, link)
            heads.dve_queries(dve)
            ca.dve(dve)
            heads.dve_outputs(dve)
            dve.wait_ge(s.sem("out_ps"), H)
            dve.tensor_scalar(h1[:, :], ps_a[:, 0:D], 0.0, None, ALU.max).then_inc(s.sem("h1"), 1)
            dve.wait_ge(s.sem("h1T_ps"), 1)
            dve.tensor_copy(h1T[:, :, :], cols(ps_b)).then_inc(s.sem("h1T"), 1)
            dve.wait_ge(s.sem("y_ps"), 1)
            ny.dve(dve, link, y[:, :], ps_a[:, 0:D])
            dve.wait_ge(s.sem("gamma_in"), 16)
            link(dve.tensor_tensor(y[:, :], y[:, :], gam[:, :], ALU.mult))
            link(dve.tensor_tensor(x[:, :], x[:, :], y[:, :], ALU.add))


def stage_prepare(nc, A, x, ident):
    NT = S2 // 128
    with Stage(nc, "prep") as s:
        rows, cT = s.sb("rows", [128, 2, D]), s.sb("cT", [128, 2, DC, 128])
        wkv = s.sb("wkv", [128, DC, 2 * D])
        g1, b1 = s.sb("g1", [128, D]), s.sb("b1", [128, D])
        g2, b2 = s.sb("g2", [128, D]), s.sb("b2", [128, D])
        mask = s.sb("mask", [128, NT])
        st, mv = s.sb("st", [128, 2, 3, 6]), s.sb("mv", [128, 2, 3, 2])
        std, rstd = s.sb("std", [128, 2, 3]), s.sb("rstd", [128, 2, 3])
        xh, xn, xnT = s.sb("xh", [128, 2, D]), s.sb("xn", [128, 2, D]), s.sb("xnT", [128, 2, DC, 128])
        kva = s.sb("kva", [128, 2, 2, D])
        kp, vp = s.sb("kp", [128, 2, D]), s.sb("vp", [128, 2, DC, 129])
        zero = s.sb("zero", [128, DC * 129])
        ps_kv = [s.ps(f"kv{j}") for j in range(2)]
        ps_t = [s.ps(f"t{j}") for j in range(2)]
        ps_sum = s.ps("sum")
        block = s.block()

        @block.sync
        def _(sp):
            def load(j, tile):
                sp.dma_start(rows[:, j, :], A["ctx_rows"][:, bass.ds(tile, 1), :]).then_inc(s.sem(f"ctx_in{j}"), 16)
                sp.dma_start(cT[:, j, :, :], A["ctxT"][:, :, bass.ds(tile * 128, 128)]).then_inc(s.sem(f"ctx_in{j}"), 16)

            load(0, 0)
            sp.dma_start(wkv[:, :, :], A["L2_xattn_wkv"]).then_inc(s.sem("wkv_in"), 16)
            load(1, 1)
            for name, dst, src in (("g1", g1, "L1_xattn_ln_x_g"), ("b1", b1, "L1_xattn_ln_x_b"),
                                   ("g2", g2, "L2_xattn_ln_gamma"), ("b2", b2, "L2_xattn_ln_beta")):
                sp.dma_start(dst[:, :], A[src].partition_broadcast(128)).then_inc(s.sem("gb_in"), 16)
            sp.dma_start(mask[:, :], A["mask_ff1"]).then_inc(s.sem("gb_in"), 16)
            with sp.Fori(0, NT // 2 - 1) as it:
                for j in range(2):
                    sp.wait_ge(s.sem("kv_ps"), it * 2 + (j + 1))
                    sp.wait_ge(s.sem("xhat"), it * 2 + (j + 1))
                    load(j, it * 2 + (2 + j))

        @block.tensor
        def _(pe):
            def project(j, n, seen):
                pe.wait_ge(s.sem(f"ctx_in{j}"), n)
                pe.wait_ge(s.sem("kv_read"), seen)
                pe_dense(pe, ps_kv[j][:, :], lambda c: cT[:, j, c, :], lambda c: wkv[:, c, :]).then_inc(s.sem("kv_ps"), 1)

            def collect(j, it):
                pe.wait_ge(s.sem("xn"), it * 2 + (j + 1))
                pe.wait_ge(s.sem("xnT"), it * 2)
                pe_transposes(pe, ps_t[j], xn[:, j, :], ident).then_inc(s.sem("xnT_ps"), 1)
                pe.wait_ge(s.sem("vp"), it * 2 + (j + 1))
                for c in range(DC):
                    mm = pe.matmul(ps_sum[:, c * 129:(c + 1) * 129], kp[:, j, c * 128:(c + 1) * 128],
                                   vp[:, j, c, :], start=False, stop=False, skip_group_check=True)
                mm.then_inc(s.sem("sum_ps"), 1)

            pe.wait_ge(s.sem("zero"), 1)
            pe.matmul(ps_sum[:, 0:DC * 129], zero[:, 0:128], zero[:, :], start=True, stop=False, skip_group_check=True)
            pe.wait_ge(s.sem("wkv_in"), 16)
            project(0, 32, 0)
            with pe.Fori(0, NT // 2 - 1) as it:
                project(1, it * 32 + 32, it * 2)
                collect(0, it)
                project(0, it * 32 + 64, it * 2 + 1)
                collect(1, it)
            project(1, NT // 2 * 32, NT - 2)
            collect(0, NT // 2 - 1)
            collect(1, NT // 2 - 1)
            pe.matmul(ps_sum[:, 0:DC * 129], zero[:, 0:128], zero[:, :], start=False, stop=True,
                      skip_group_check=True).then_inc(s.sem("all_ps"), 1)

        @block.scalar
        def _(act):
            with act.Fori(0, NT // 2) as it:
                for j in range(2):
                    n = it * 2 + j
                    m = mask[:, bass.ds(n, 1)]
                    act.wait_ge(s.sem("var"), n + 1)
                    act.activation(std[:, j, :], mv[:, j, :, 1], ACT.Sqrt).then_inc(s.sem("std"), 1)
                    act.wait_ge(s.sem("gb_in"), 5 * 16)
                    act.wait_ge(s.sem("v_affine"), n + 1)
                    act.wait_ge(s.sem("sum_ps"), it * 2)
                    act.activation(vp[:, j, :, 0:128], kva[:, j, 1, :].rearrange("p (c e) -> p c e", c=DC),
                                   ACT.Copy, scale=m).then_inc(s.sem("vp0"), 1)
                    act.wait_ge(s.sem("ones"), 1)
                    act.wait_ge(s.sem("k_pos"), n + 1)
                    act.activation(kp[:, j, :], kva[:, j, 0, :], ACT.Copy, scale=m).then_inc(s.sem("vp"), 1)
                    act.wait_ge(s.sem("xnT_ps"), n + 1)
                    act.wait_ge(s.sem(f"stored{j}"), it * 32)
                    act.activation(xnT[:, j, :, :], cols(ps_t[j]), ACT.Copy).then_inc(s.sem("xnT"), 1)
                    act.wait_ge(s.sem("xnT"), n + 1)
                    act.dma_start(A["xnT"][:, :, bass.ds(n * 128, 128)], xnT[:, j, :, :]).then_inc(s.sem(f"stored{j}"), 16)
                    act.dma_start(A["xn_rows"][:, bass.ds(n, 1), :], xn[:, j, :]).then_inc(s.sem(f"stored{j}"), 16)
            for j in range(2):
                act.wait_ge(s.sem(f"stored{j}"), NT // 2 * 32)

        @block.vector
        def _(dve):
            dve.memset(zero[:, :], 0.0).then_inc(s.sem("zero"), 1)
            dve.memset(vp[:, :, :, 128:129], 1.0).then_inc(s.sem("ones"), 1)
            dve.wait_ge(s.sem("gb_in"), 5 * 16)
            STEPS = 12
            with dve.Fori(0, NT // 2) as it:
                link = linker(dve, s.sem("dve_steps"), it * STEPS)
                for j in range(2):
                    n = it * 2 + j
                    dve.wait_ge(s.sem(f"ctx_in{j}"), it * 32 + 32)
                    dve.bn_stats(st[:, j, 0, :], rows[:, j, :]).then_inc(s.sem("stats"), 1)
                    dve.wait_ge(s.sem("kv_ps"), n + 1)
                    for i in range(2):
                        dve.bn_stats(st[:, j, 1 + i, :], ps_kv[j][:, i * D:(i + 1) * D]).then_inc(s.sem("stats"), 1)
                    dve.wait_ge(s.sem("stats"), n * 3 + 3)
                    dve.sem_inc(s.sem("stats_seen"), 1)
                    for i in range(3):
                        dve.bn_aggr(mv[:, j, i, :], st[:, j, i, :]).then_inc(s.sem("aggr"), 1)
                    dve.wait_ge(s.sem("aggr"), n * 3 + 3)
                    dve.tensor_scalar(mv[:, j, 0, 1:2], mv[:, j, 0, 1:2], 1e-5, None, ALU.add).then_inc(s.sem("eps"), 1)
                    dve.wait_ge(s.sem("eps"), n + 1)
                    dve.tensor_scalar(mv[:, j, 1:3, 1], mv[:, j, 1:3, 1], 1e-6, None, ALU.add).then_inc(s.sem("var"), 1)
                    dve.wait_ge(s.sem("vp"), it * 2)
                    for i in range(2):
                        last = dve.scalar_tensor_tensor(out=kva[:, j, i, :], in0=ps_kv[j][:, i * D:(i + 1) * D],
                                                        scalar=mv[:, j, 1 + i, 0:1], in1=g2[:, :],
                                                        op0=ALU.subtract, op1=ALU.mult)
                    last.then_inc(s.sem("kv_read"), 1)
                    dve.wait_ge(s.sem("std"), n + 1)
                    dve_rsqrt(dve, link, rstd[:, j, :], std[:, j, :], mv[:, j, :, 1])
                    dve.wait_ge(s.sem("xn"), it * 2)
                    dve.tensor_scalar(xh[:, j, :], rows[:, j, :], mv[:, j, 0, 0:1], rstd[:, j, 0:1],
                                      ALU.subtract, ALU.mult).then_inc(s.sem("xhat"), 1)
                    dve.wait_ge(s.sem("kv_read"), n + 1)
                    for i in (1, 0):
                        last = dve.scalar_tensor_tensor(out=kva[:, j, i, :], in0=kva[:, j, i, :],
                                                        scalar=rstd[:, j, 1 + i:2 + i], in1=b2[:, :],
                                                        op0=ALU.mult, op1=ALU.add)
                        if i == 1:
                            last.then_inc(s.sem("v_affine"), 1)
                        else:
                            link(last)
                    dve.tensor_scalar(kva[:, j, 0, :], kva[:, j, 0, :], 0.0, 1e-6, ALU.max, ALU.add).then_inc(s.sem("k_pos"), 1)
                assert link.count[0] == STEPS
            dve.wait_ge(s.sem("all_ps"), 1)
            finish(dve, dve.tensor_copy(A["kv_sum"][:, :, :], ps_sum[:, 0:DC * 129].rearrange("p (c e) -> p c e", c=DC)),
                   s.sem("kv_sum"))

        @block.gpsimd
        def _(pool):
            pool.wait_ge(s.sem("gb_in"), 5 * 16)
            with pool.Fori(0, NT // 2) as it:
                for j in range(2):
                    n = it * 2 + j
                    pool.wait_ge(s.sem("xhat"), n + 1)
                    pool.wait_ge(s.sem(f"stored{j}"), it * 32)
                    pool.tensor_tensor(xn[:, j, :], xh[:, j, :], g1[:, :], ALU.mult).then_inc(s.sem("xn_g"), 1)
                    pool.wait_ge(s.sem("xn_g"), n + 1)
                    pool.tensor_tensor(xn[:, j, :], xn[:, j, :], b1[:, :], ALU.add).then_inc(s.sem("xn"), 1)


def stage_l1_xattn(nc, A, x, ident):
    H = 8
    with Stage(nc, "l1x", fast=2 * (2 * DC * CH + 2 * CT * D + 2 * CT * T + H * DC * T + D + DC * T) + 2 * CH + T) as s:
        heads = WideHeads(s, H, A, "L1_xattn_", ident, WideHeads.HD ** -1.0)
        lat, latT = s.sb("lat", [128, D]), s.sb("latT", [128, DC, T])
        lat_high, lat_low = (s.sb(f"lat_{i}", [128, D], F32R) for i in ("high", "low"))
        latT_high, latT_low = (s.sb(f"latT_{i}", [128, DC, T], F32R) for i in ("high", "low"))
        ca = ContextAttention(s, H, D, heads.qt, lambda h: (0, D), A["xnT"], A["xn_rows"], ident, mask="rows",
                              mask_dram=A["mask_bk1"].partition_broadcast(1), bias_per_one=-FAR, 
                              tail=((latT_high, latT_low), (lat_high, lat_low)), split=True)
        lg, lb, og, ob = (s.sb(n, [128, D]) for n in ("lg", "lb", "og", "ob"))
        y = s.sb("y", [128, D])
        ps_a, ps_b = ca.ps_o[0], ca.ps_o[1]
        n0, n1, ny = RowNorm(s, "n0", 1e-5), RowNorm(s, "n1", 1e-5), RowNorm(s, "y", 1e-5)
        heads.use(ca, latT, s.sem("latT"))
        block = s.block()

        @block.sync
        def _(sp):
            heads.sp(sp)
            load_rows(sp, s, A, [("lg", lg, "L1_xattn_ln_l_g"), ("lb", lb, "L1_xattn_ln_l_b"),
                                 ("og", og, "L1_xattn_ln_o_g"), ("ob", ob, "L1_xattn_ln_o_b")])
            ca.sp(sp)
            heads.sp_outputs(sp)

        @block.tensor
        def _(pe):
            pe.wait_ge(s.sem("lat"), 1)
            pe_transposes(pe, ps_a, lat, ident).then_inc(s.sem("latT_ps"), 1)
            heads.pe_queries(pe)
            pe.wait_ge(s.sem("tail"), 1)
            ca.pe(pe)
            heads.pe_outputs(pe, ps_a)

        @block.scalar
        def _(act):
            n0.act(act)
            n1.act(act)
            heads.act_queries(act)
            ca.act(act)
            heads.act_outputs(act)
            ny.act(act)

        @block.gpsimd
        def _(pool):
            ca.pool(pool)

        @block.vector
        def _(dve):
            link = linker(dve, s.sem("dve_steps"))
            n0.dve(dve, link, lat[:, :], x[:, :])
            n1.dve(dve, link, lat[:, :], lat[:, :])
            dve.wait_ge(s.sem("lg_in"), 16)
            link(dve.tensor_tensor(lat[:, :], lat[:, :], lg[:, :], ALU.mult))
            dve.wait_ge(s.sem("lb_in"), 16)
            finish(dve, dve.tensor_tensor(lat[:, :], lat[:, :], lb[:, :], ALU.add), s.sem("lat"))
            dve.wait_ge(s.sem("latT_ps"), 1)
            dve.tensor_copy(latT[:, :, :], cols(ps_a)).then_inc(s.sem("latT"), 1)
            heads.dve_queries(dve)
            dve.wait_ge(s.sem("latT"), 1)
            link(dve.tensor_copy(lat_high[:, :], lat[:, :]))
            link(dve.tensor_copy(latT_high[:, :, :], latT[:, :, :]))
            link(dve.tensor_tensor(lat_low[:, :], lat[:, :], lat_high[:, :].bitcast(F32), ALU.subtract))
            dve.tensor_tensor(latT_low[:, :, :], latT[:, :, :], latT_high[:, :, :].bitcast(F32), ALU.subtract).then_inc(s.sem("tail"), 1)
            ca.dve(dve)
            heads.dve_outputs(dve)
            dve.wait_ge(s.sem("out_ps"), H)
            ny.dve(dve, link, y[:, :], ps_a[:, 0:D])
            dve.wait_ge(s.sem("og_in"), 16)
            link(dve.tensor_tensor(y[:, :], y[:, :], og[:, :], ALU.mult))
            dve.wait_ge(s.sem("ob_in"), 16)
            link(dve.tensor_tensor(y[:, :], y[:, :], ob[:, :], ALU.add))
            link(dve.tensor_tensor(x[:, :], x[:, :], y[:, :], ALU.add))


def stage_l2_xattn(nc, A, x, ident):
    with Stage(nc, "l2x") as s:
        wq, wd = s.sb("wq", [128, DC, D]), s.sb("wd", [128, DC, D])
        g, b, bd = s.sb("g", [128, D]), s.sb("b", [128, D]), s.sb("bd", [128, D])
        kvd = s.sb("kvd", [128, DC, 136])
        q, qT, den = s.sb("q", [128, D]), s.sb("qT", [128, DC, T]), s.sb("den", [128, DC, 8])
        att2 = s.sb("att2", [128, D])
        att, attT, y = s.sb("att", [128, D]), s.sb("attT", [128, DC, T]), s.sb("y", [128, D])
        ps_a, ps_b, ps_c = s.ps("ps_a"), s.ps("ps_b"), s.ps("ps_c")
        nx, nq, ny = NormX(s, x, ident, ps_a), RowNorm(s, "nq", 1e-6), RowNorm(s, "ny", 1e-6)
        hm, kv = A["head_mask"], A["kv_sum"]
        block = s.block()

        @block.sync
        def _(sp):
            sp.dma_start(wq[:, :, :], A["L2_xattn_wq"]).then_inc(s.sem("wq_in"), 16)
            sp.dma_start(wd[:, :, :], A["L2_xattn_dense_w"]).then_inc(s.sem("wd_in"), 16)
            load_rows(sp, s, A, [("g", g, "L2_xattn_ln_gamma"), ("b", b, "L2_xattn_ln_beta"), ("bd", bd, "L2_xattn_dense_b")])
            sp.wait_ge(s.sem("att"), DC)
            sp.dma_start(A["att_order"].rearrange("h n e -> n h e"),
                         att[:, :].rearrange("p (h e) -> p h e", h=16)).then_inc(s.sem("att_out"), 16)
            sp.wait_ge(s.sem("att_out"), 16)
            sp.dma_start(att2[:, :], A["att_order"].rearrange("h (a b) e -> (h a) (b e)", b=16)).then_inc(s.sem("att_in"), 16)

        @block.tensor
        def _(pe):
            nx.pe(pe)
            pe.wait_ge(s.sem("xnT"), 1)
            pe.wait_ge(s.sem("wq_in"), 16)
            pe_dense(pe, ps_b[:, 0:D], lambda c: nx.xnT[:, c, :], lambda c: wq[:, c, :]).then_inc(s.sem("q_ps"), 1)
            pe.wait_ge(s.sem("q"), 1)
            pe_transposes(pe, ps_a, q, ident).then_inc(s.sem("qT_ps"), 1)
            pe.wait_ge(s.sem("kvd"), 1)
            pe.wait_ge(s.sem("qT"), 1)
            for c in range(DC):
                mm = pe.matmul(ps_c[:, c * 136:(c + 1) * 136], qT[:, c, :], kvd[:, c, :], start=True, stop=True)
            mm.then_inc(s.sem("att_ps"), 1)
            pe.wait_ge(s.sem("att_in"), 16)
            pe_transposes(pe, ps_a, att2, ident).then_inc(s.sem("attT_ps"), 1)
            pe.wait_ge(s.sem("wd_in"), 16)
            pe.wait_ge(s.sem("attT"), 1)
            pe_dense(pe, ps_b[:, 0:D], lambda c: attT[:, c, :], lambda c: wd[:, c, :]).then_inc(s.sem("y_ps"), 1)

        @block.scalar
        def _(act):
            nx.act(act)
            nq.act(act)
            ny.act(act)

        @block.vector
        def _(dve):
            link = linker(dve, s.sem("dve_steps"))
            nx.dve(dve, link)
            link(dve.tensor_tensor(kvd[:, :, 0:128].rearrange("p c (h e) -> p c h e", h=8),
                                   kv[:, :, 0:128].rearrange("p c (h e) -> p c h e", h=8),
                                   hm[:, :].unsqueeze(1).unsqueeze(3).to_broadcast([128, DC, 8, 16]), ALU.mult))
            dve.tensor_tensor(kvd[:, :, 128:136], hm[:, :].unsqueeze(1).to_broadcast([128, DC, 8]),
                              kv[:, :, 128:129].to_broadcast([128, DC, 8]), ALU.mult).then_inc(s.sem("kvd"), 1)
            dve.wait_ge(s.sem("q_ps"), 1)
            nq.dve(dve, link, q[:, :], ps_b[:, 0:D])
            for name in ("g", "b", "bd"):
                dve.wait_ge(s.sem(name + "_in"), 16)
            link(dve.tensor_tensor(q[:, :], q[:, :], g[:, :], ALU.mult))
            link(dve.tensor_tensor(q[:, :], q[:, :], b[:, :], ALU.add))
            dve.tensor_scalar(q[:, :], q[:, :], 0.0, 1e-6, ALU.max, ALU.add).then_inc(s.sem("q"), 1)
            dve.wait_ge(s.sem("qT_ps"), 1)
            dve.tensor_copy(qT[:, :, :], cols(ps_a)).then_inc(s.sem("qT"), 1)
            dve.wait_ge(s.sem("att_ps"), 1)
            num = ps_c[:, 0:DC * 136].rearrange("p (c e) -> p c e", c=DC)
            link(dve.tensor_scalar(den[:, :, :], num[:, :, 128:136], 1e-6, None, ALU.add))
            link(dve.reciprocal(den[:, :, :], den[:, :, :]))
            for c in range(DC):
                dve.tensor_tensor(att[:, c * 128:(c + 1) * 128].rearrange("p (h e) -> p h e", h=8),
                                         num[:, c, 0:128].rearrange("p (h e) -> p h e", h=8),
                                         den[:, c, :].unsqueeze(2).to_broadcast([128, 8, 16]), ALU.mult).then_inc(s.sem("att"), 1)
            dve.wait_ge(s.sem("attT_ps"), 1)
            dve.tensor_copy(attT[:, :, :], cols(ps_a)).then_inc(s.sem("attT"), 1)
            dve.wait_ge(s.sem("y_ps"), 1)
            link(dve.tensor_tensor(y[:, :], ps_b[:, 0:D], bd[:, :], ALU.add))
            ny.dve(dve, link, y[:, :], y[:, :])
            link(dve.tensor_tensor(y[:, :], y[:, :], g[:, :], ALU.mult))
            link(dve.tensor_tensor(y[:, :], y[:, :], b[:, :], ALU.add))
            link(dve.tensor_tensor(x[:, :], x[:, :], y[:, :], ALU.add))


def stage_l3_xattn(nc, A, x, ident):
    H = 16
    with Stage(nc, "l3x") as s:
        qd = s.sb("qd", [128, H, T])
        ca = ContextAttention(s, H, 16, lambda h: [([qd[:, h, :]], h // 8)], lambda h: (16 * h, 16 * h + 16),
                              A["ctxT"], A["ctx_rows"], ident, mask="full", mask_dram=A["mask_ik1"], bias_per_one=1e9)
        nx = NormX(s, x, ident, ca.ps_o[0])
        hm = A["head_mask"]
        block = s.block()

        @block.sync
        def _(sp):
            ca.sp(sp)

        @block.tensor
        def _(pe):
            nx.pe(pe)
            pe.wait_ge(s.sem("qd"), H)
            ca.pe(pe)

        @block.scalar
        def _(act):
            nx.act(act)
            ca.act(act)

        @block.vector
        def _(dve):
            link = linker(dve, s.sem("dve_steps"))
            nx.dve(dve, link)
            dve.wait_ge(s.sem("xnT"), 1)
            for h in range(H):
                dve.tensor_scalar(qd[:, h, :], nx.xnT[:, h // 8, :], hm[:, h % 8:h % 8 + 1], 0.25,
                                  ALU.mult, ALU.mult).then_inc(s.sem("qd"), 1)
            ca.dve(dve)
            dve.wait_ge(s.sem("attended"), H)
            link(dve.tensor_tensor(x[:, :], x[:, :], ca.acc[:, :, :].rearrange("p h e -> p (h e)"), ALU.add))


def add_cols(a, n):
    return a.unsqueeze(2).to_broadcast([a.shape[0], a.shape[1], n])


def stage_l0_attn(nc, A, x, ident):
    with Stage(nc, "l0a") as s:
        qk = s.sb("qk", [128, 2, DC])
        dl, osc = s.sb("dl", [128, 1]), s.sb("osc", [128, 1])
        BITS = 7
        dk, dm1 = s.sb("dk", [128, BITS]), s.sb("dm1", [128, BITS])
        steps, bit = s.sb("steps", [128, T], I32), s.sb("bit", [128, T], I32)
        w, fac = s.sb("w", [128, T]), s.sb("fac", [128, T])
        qx, kx, sw = s.sb("qx", [128, DC, T]), s.sb("kx", [128, DC, T]), s.sb("sw", [128, T])
        ps_a, ps_s, ps_y = s.ps("ps_a"), s.ps("ps_s"), s.ps("ps_y")
        nx = NormX(s, x, ident, ps_a)
        block = s.block()

        @block.sync
        def _(sp):
            sp.dma_start(dl[:, :], A["L0_attn_decay_logit"].partition_broadcast(128)).then_inc(s.sem("dl_in"), 16)
            sp.dma_start(osc[:, :], A["L0_attn_out_scale"].partition_broadcast(128)).then_inc(s.sem("osc_in"), 16)
            sp.dma_start(qk[:, 0, :], A["L0_attn_q_scale"]).then_inc(s.sem("qk_in"), 16)
            sp.dma_start(qk[:, 1, :], A["L0_attn_k_scale"]).then_inc(s.sem("qk_in"), 16)

        @block.gpsimd
        def _(pool):
            pool.iota(steps[:, :], [[-1, T]], base=-1, channel_multiplier=1).then_inc(s.sem("steps"), 1)
            pool.wait_ge(s.sem("w_all"), 1)
            pool.affine_select(out=w[:, :], in_=w[:, :], compare_op=ALU.is_gt, fill=0.0, base=0,
                               pattern=[[-1, T]], channel_multiplier=1).then_inc(s.sem("w"), 1)

        @block.tensor
        def _(pe):
            nx.pe(pe)
            pe.wait_ge(s.sem("kx"), 2 * DC)
            pe_dense(pe, ps_s[:, 0:T], lambda c: kx[:, c, :], lambda c: qx[:, c, :]).then_inc(s.sem("s_ps"), 1)
            pe.wait_ge(s.sem("sw"), 1)
            pe.matmul(ps_y[:, 0:D], sw[:, :], nx.xn[:, :], start=True, stop=True).then_inc(s.sem("y_ps"), 1)

        @block.scalar
        def _(act):
            nx.act(act)
            act.wait_ge(s.sem("dl_in"), 16)
            act.activation(dk[:, 0:1], dl[:, :], ACT.Tanh, scale=0.5).then_inc(s.sem("tanh"), 1)

        @block.vector
        def _(dve):
            link = linker(dve, s.sem("dve_steps"))
            nx.dve(dve, link)
            dve.wait_ge(s.sem("tanh"), 1)
            link(dve.tensor_scalar(dk[:, 0:1], dk[:, 0:1], 1.0, 0.5, ALU.add, ALU.mult))
            for k in range(1, BITS):
                link(dve.tensor_tensor(dk[:, k:k + 1], dk[:, k - 1:k], dk[:, k - 1:k], ALU.mult))
            link(dve.tensor_scalar(dm1[:, :], dk[:, :], -1.0, None, ALU.add))
            dve.wait_ge(s.sem("steps"), 1)
            for k in range(BITS):
                link(dve.tensor_scalar(bit[:, :], steps[:, :], k, 1, ALU.logical_shift_right, ALU.bitwise_and))
                dst = w if k == 0 else fac
                ins = dve.tensor_scalar(dst[:, :], bit[:, :], dm1[:, k:k + 1], 1.0, ALU.mult, ALU.add)
                link(ins)
                if k > 0:
                    ins = dve.tensor_tensor(w[:, :], w[:, :], fac[:, :], ALU.mult)
                    if k == BITS - 1:
                        ins.then_inc(s.sem("w_all"), 1)
                    else:
                        link(ins)
            dve.wait_ge(s.sem("qk_in"), 32)
            dve.wait_ge(s.sem("xnT"), 1)
            for c in range(DC):
                dve.tensor_scalar(qx[:, c, :], nx.xnT[:, c, :], qk[:, 0, c:c + 1], None, ALU.mult).then_inc(s.sem("kx"), 1)
                dve.tensor_scalar(kx[:, c, :], nx.xnT[:, c, :], qk[:, 1, c:c + 1], None, ALU.mult).then_inc(s.sem("kx"), 1)
            dve.wait_ge(s.sem("s_ps"), 1)
            dve.wait_ge(s.sem("w"), 1)
            dve.tensor_tensor(sw[:, :], ps_s[:, 0:T], w[:, :], ALU.mult).then_inc(s.sem("sw"), 1)
            dve.wait_ge(s.sem("y_ps"), 1)
            dve.wait_ge(s.sem("osc_in"), 16)
            link(dve.scalar_tensor_tensor(out=x[:, :], in0=ps_y[:, 0:D], scalar=osc[:, 0:1], in1=x[:, :],
                                          op0=ALU.mult, op1=ALU.add))


class SmallHeads:

    H, HD = 16, 16

    def __init__(self, s, A, x, ident, w, bias=None, q_scale=1.0):
        self.s, self.A, self.ident, self.w_dram, self.bias_dram, self.q_scale = s, A, ident, w, bias, q_scale
        self.w = s.sb("w_qkv", [128, DC, 3 * D])
        self.bias = s.sb("b_qkv", [128, 3 * D]) if bias else None
        self.qkv = s.sb("qkv", [128, 3 * D])
        self.qkT = s.sb("qkT", [128, 4, T])
        self.qd = s.sb("qd", [128, self.H, T])
        self.ps_a, self.ps_b = s.ps("ps_a"), s.ps("ps_b")
        self.ps_h = [s.ps(f"ps_h{g}") for g in range(4)]
        self.nx = NormX(s, x, ident, self.ps_a)

    def sp(self, sp):
        sp.dma_start(self.w[:, :, :], self.A[self.w_dram]).then_inc(self.s.sem("w_qkv_in"), 16)
        if self.bias:
            sp.dma_start(self.bias[:, :], self.A[self.bias_dram].partition_broadcast(128)).then_inc(self.s.sem("b_qkv_in"), 16)

    def pe_project(self, pe):
        s = self.s
        self.nx.pe(pe)
        pe.wait_ge(s.sem("w_qkv_in"), 16)
        pe.wait_ge(s.sem("xnT"), 1)
        pe_dense(pe, self.ps_a[:, :], lambda c: self.nx.xnT[:, c, :], lambda c: self.w[:, c, 0:512])
        pe_dense(pe, self.ps_b[:, 0:D], lambda c: self.nx.xnT[:, c, :],
                 lambda c: self.w[:, c, 512:768]).then_inc(s.sem("qkv_ps"), 1)

    def dve_project(self, dve, link):
        s = self.s
        self.nx.dve(dve, link)
        dve.wait_ge(s.sem("qkv_ps"), 1)
        if self.bias:
            dve.wait_ge(s.sem("b_qkv_in"), 16)
        for lo, hi, ps in ((0, 512, self.ps_a[:, :]), (512, 768, self.ps_b[:, 0:D])):
            if self.bias:
                link(dve.tensor_tensor(self.qkv[:, lo:hi], ps, self.bias[:, lo:hi], ALU.add))
            else:
                link(dve.tensor_copy(self.qkv[:, lo:hi], ps))

    def pe_scores(self, pe):
        s = self.s
        pe.wait_ge(s.sem("qkv_ready"), 1)
        pe_transposes(pe, self.ps_a, self.qkv, self.ident, 4).then_inc(s.sem("qkT_ps"), 1)
        pe.wait_ge(s.sem("qd"), self.H)
        for g in range(4):
            pe.matmul(self.ps_h[g][:, :], self.qkT[:, 2 + g // 2, :], self.qd[:, 4 * g:4 * g + 4, :],
                      start=True, stop=True).then_inc(s.sem("scores"), 1)

    def dve_heads(self, dve):
        s, hm = self.s, self.A["head_mask"]
        dve.wait_ge(s.sem("qkT_ps"), 1)
        finish(dve, dve.tensor_copy(self.qkT[:, :, :], cols(self.ps_a, 4)), s.sem("qkT"))
        for h in range(self.H):
            dve.tensor_scalar(self.qd[:, h, :], self.qkT[:, h // 8, :], hm[:, h % 8:h % 8 + 1], self.q_scale,
                              ALU.mult, ALU.mult).then_inc(s.sem("qd"), 1)

    def v(self, h):
        return self.qkv[:, 512 + 16 * h:512 + 16 * h + 16]


class OutProjection:

    def __init__(self, s, A, x, ident, w, ps_t, ps_o, bias=None):
        self.s, self.A, self.x, self.ident, self.w_dram, self.bias_dram = s, A, x, ident, w, bias
        self.ps_t, self.ps_o = ps_t, ps_o
        self.w, self.yT = s.sb("w_out", [128, DC, D]), s.sb("yT", [128, DC, T])
        self.y = s.sb("y", [128, D])
        self.bias = s.sb("b_out", [128, D]) if bias else None

    def sp(self, sp):
        sp.dma_start(self.w[:, :, :], self.A[self.w_dram]).then_inc(self.s.sem("w_out_in"), 16)
        if self.bias:
            sp.dma_start(self.bias[:, :], self.A[self.bias_dram].partition_broadcast(128)).then_inc(self.s.sem("b_out_in"), 16)

    def pe(self, pe):
        s = self.s
        pe.wait_ge(s.sem("y_ready"), 1)
        pe_transposes(pe, self.ps_t, self.y, self.ident).then_inc(s.sem("yT_ps"), 1)
        pe.wait_ge(s.sem("w_out_in"), 16)
        pe.wait_ge(s.sem("yT"), 1)
        pe_dense(pe, self.ps_o[:, 0:D], lambda c: self.yT[:, c, :], lambda c: self.w[:, c, :]).then_inc(s.sem("out_ps"), 1)

    def dve(self, dve, link):
        s, x = self.s, self.x
        dve.wait_ge(s.sem("yT_ps"), 1)
        dve.tensor_copy(self.yT[:, :, :], cols(self.ps_t)).then_inc(s.sem("yT"), 1)
        if self.bias:
            dve.wait_ge(s.sem("b_out_in"), 16)
            link(dve.tensor_tensor(x[:, :], x[:, :], self.bias[:, :], ALU.add))
        dve.wait_ge(s.sem("out_ps"), 1)
        link(dve.tensor_tensor(x[:, :], x[:, :], self.ps_o[:, 0:D], ALU.add))


def stage_l2_attn(nc, A, x, ident):
    with Stage(nc, "l2a") as s:
        hd = SmallHeads(s, A, x, ident, "L2_attn_W_qkv")
        op = OutProjection(s, A, x, ident, "L2_attn_W_o", hd.ps_a, hd.ps_b)
        mu, var, std = s.sb("mu", [128, 16]), s.sb("var", [128, 16]), s.sb("std", [128, 16])
        sq = s.sb("sq", [128, D])
        st = s.sb("st", [128, 4, 4, T])
        ps_y = s.ps("ps_y")
        block = s.block()

        @block.sync
        def _(sp):
            hd.sp(sp)
            op.sp(sp)

        @block.tensor
        def _(pe):
            hd.pe_project(pe)
            hd.pe_scores(pe)
            for h in range(16):
                pe.wait_ge(s.sem("st"), h // 4 + 1)
                mm = pe.matmul(ps_y[:, 16 * h:16 * h + 16], st[:, h // 4, h % 4, :], hd.v(h), start=True, stop=True)
            mm.then_inc(s.sem("y_ps"), 1)
            op.pe(pe)

        @block.scalar
        def _(act):
            hd.nx.act(act)
            act.wait_ge(s.sem("k_var"), 1)
            act.activation(std[:, :], var[:, :], ACT.Sqrt).then_inc(s.sem("k_std"), 1)

        @block.vector
        def _(dve):
            link = linker(dve, s.sem("dve_steps"))
            hd.dve_project(dve, link)
            k = hd.qkv[:, 256:512].rearrange("p (h e) -> p h e", h=16)
            sq3 = sq[:, :].rearrange("p (h e) -> p h e", h=16)
            link(dve.tensor_reduce(mu[:, :], k, AX.X, ALU.add))
            link(dve.tensor_scalar(mu[:, :], mu[:, :], 1 / 16, None, ALU.mult))
            link(dve.tensor_tensor(k, k, add_cols(mu[:, :], 16), ALU.subtract))
            link(dve.tensor_tensor(sq3, k, k, ALU.mult))
            link(dve.tensor_reduce(var[:, :], sq3, AX.X, ALU.add))
            dve.tensor_scalar(var[:, :], var[:, :], 1 / 16, 1e-5, ALU.mult, ALU.add).then_inc(s.sem("k_var"), 1)
            dve.wait_ge(s.sem("k_std"), 1)
            dve_rsqrt(dve, link, mu[:, :], std[:, :], var[:, :])
            dve.tensor_tensor(k, k, add_cols(mu[:, :], 16), ALU.mult).then_inc(s.sem("qkv_ready"), 1)
            hd.dve_heads(dve)
            for g in range(4):
                dve.wait_ge(s.sem("scores"), g + 1)
                dve.tensor_tensor(st[:, g, :, :], cols(hd.ps_h[g], 4),
                                  A["causal"][:, :].unsqueeze(1).to_broadcast([128, 4, T]), ALU.mult).then_inc(s.sem("st"), 1)
            dve.wait_ge(s.sem("y_ps"), 1)
            dve.tensor_copy(op.y[:, :], ps_y[:, 0:D]).then_inc(s.sem("y_ready"), 1)
            op.dve(dve, link)


class SmallSoftmax:

    def __init__(self, s, name):
        self.s, self.name = s, name
        self.p, self.m, self.l = s.sb(name + "_p", [128, 16, T]), s.sb(name + "_m", [128, 16]), s.sb(name + "_l", [128, 16])

    def dve(self, dve, link, src, bias=None):
        s = self.s
        for g in range(4):
            dst, gs = self.p[:, 4 * g:4 * g + 4, :], slice(4 * g, 4 * g + 4)
            a = src(g)
            if bias is not None:
                link(dve.tensor_tensor(dst, a, bias.unsqueeze(1).to_broadcast([128, 4, T]), ALU.add))
                a = dst
            link(dve.tensor_reduce(self.m[:, gs], a, AX.X, ALU.max))
            dve.tensor_tensor(dst, a, add_cols(self.m[:, gs], T), ALU.subtract).then_inc(s.sem(self.name + "_shifted"), 1)

    def act(self, act):
        s = self.s
        for g in range(4):
            act.wait_ge(s.sem(self.name + "_shifted"), g + 1)
            dst = self.p[:, 4 * g:4 * g + 4, :]
            act.activation(dst, dst, ACT.Exp).then_inc(s.sem(self.name + "_exp"), 1)

    def dve_sums(self, dve, link):
        for g in range(4):
            dve.wait_ge(self.s.sem(self.name + "_exp"), g + 1)
            link(dve.tensor_reduce(self.l[:, 4 * g:4 * g + 4], self.p[:, 4 * g:4 * g + 4, :], AX.X, ALU.add))
        link(dve.reciprocal(self.l[:, :], self.l[:, :]))


class SmallValues:

    def __init__(self, s, hd, p, ps_y):
        self.s, self.hd, self.p, self.ps_y = s, hd, p, ps_y
        self.pT = s.sb("pT", [128, 16, T])

    def pe(self, pe, ready, count):
        s, hd = self.s, self.hd
        for g in range(4):
            pe.wait_ge(ready, count(g))
            for h in range(4 * g, 4 * g + 4):
                mm = pe.transpose(hd.ps_h[g][:, (h % 4) * T:(h % 4 + 1) * T], self.p[:, h, :], hd.ident[:, :])
            mm.then_inc(s.sem("pT_ps"), 1)
        for g in range(4):
            pe.wait_ge(s.sem("pT"), g + 1)
            for h in range(4 * g, 4 * g + 4):
                mm = pe.matmul(self.ps_y[:, 16 * h:16 * h + 16], self.pT[:, h, :], hd.v(h), start=True, stop=True)
        mm.then_inc(s.sem("y_ps"), 1)

    def act(self, act):
        for g in range(4):
            act.wait_ge(self.s.sem("pT_ps"), g + 1)
            act.activation(self.pT[:, 4 * g:4 * g + 4, :], cols(self.hd.ps_h[g], 4), ACT.Copy).then_inc(self.s.sem("pT"), 1)


def stage_l3_attn(nc, A, x, ident):
    with Stage(nc, "l3a") as s:
        hd = SmallHeads(s, A, x, ident, "L3_attn_W_qkv", bias="L3_attn_b_qkv", q_scale=D ** -0.5)
        op = OutProjection(s, A, x, ident, "L3_attn_Wo", hd.ps_a, hd.ps_b, bias="L3_attn_bo")
        sm = SmallSoftmax(s, "sm")
        ps_y = s.ps("ps_y")
        vals = SmallValues(s, hd, sm.p, ps_y)
        block = s.block()

        @block.sync
        def _(sp):
            hd.sp(sp)
            op.sp(sp)

        @block.tensor
        def _(pe):
            hd.pe_project(pe)
            hd.pe_scores(pe)
            vals.pe(pe, s.sem("sm_exp"), lambda g: g + 1)
            op.pe(pe)

        @block.scalar
        def _(act):
            hd.nx.act(act)
            sm.act(act)
            vals.act(act)

        @block.vector
        def _(dve):
            link = linker(dve, s.sem("dve_steps"))
            hd.dve_project(dve, link)
            dve.sem_inc(s.sem("qkv_ready"), 1)
            hd.dve_heads(dve)

            def scores(g):
                dve.wait_ge(s.sem("scores"), g + 1)
                return cols(hd.ps_h[g], 4)

            sm.dve(dve, link, scores)
            sm.dve_sums(dve, link)
            dve.wait_ge(s.sem("y_ps"), 1)
            dve.tensor_tensor(op.y[:, :].rearrange("p (h e) -> p h e", h=16), ps_y[:, 0:D].rearrange("p (h e) -> p h e", h=16),
                              add_cols(sm.l[:, :], 16), ALU.mult).then_inc(s.sem("y_ready"), 1)
            op.dve(dve, link)


def stage_l3_ffn(nc, A, x, ident):
    REG = 5
    with Stage(nc, "l3f") as s:
        hd = SmallHeads(s, A, x, ident, "L3_ffn_W_kqv", q_scale=0.25)
        op = OutProjection(s, A, x, ident, "L3_ffn_W_proj", hd.ps_a, hd.ps_b, bias="L3_ffn_b_proj")
        smp, smn = SmallSoftmax(s, "smp"), SmallSoftmax(s, "smn")
        guide = s.sb("guide", [128, D])
        prod = s.sb("prod", [128, D])
        n2 = s.sb("n2", [128, 2, 16])
        nrm, dot, sim = s.sb("nrm", [128, 2, 16]), s.sb("dot", [128, 16]), s.sb("sim", [128, 1])
        srow, mm1 = s.sb("srow", [1, T]), s.sb("mm1", [1, 4])
        pos = s.sb("pos", [1, T])
        bp, bn = s.sb("bp", [128, T]), s.sb("bn", [128, T])
        wt = s.sb("wt", [128, 4])
        cf = s.sb("cf", [128, 2, 16])
        ps_y, ps_m = s.ps("ps_y"), s.ps("ps_m")
        vals = SmallValues(s, hd, smp.p, ps_y)
        block = s.block()

        @block.sync
        def _(sp):
            hd.sp(sp)
            sp.dma_start(guide[:, :], A["L3_ffn_guide"].partition_broadcast(128)).then_inc(s.sem("guide_in"), 16)
            op.sp(sp)

        @block.gpsimd
        def _(pool):
            pool.affine_select(out=wt[:, 3:4], in_=A["ones"][:, 0:1], compare_op=ALU.is_ge, fill=0.0, base=REG - 1,
                               pattern=[[0, 1]], channel_multiplier=-1).then_inc(s.sem("reg"), 1)

        @block.tensor
        def _(pe):
            hd.pe_project(pe)
            hd.pe_scores(pe)
            pe.wait_ge(s.sem("sim"), 1)
            pe.matmul(ps_m[0:1, 0:T], sim[:, 0:1], ident[:, :], start=True, stop=True).then_inc(s.sem("srow_ps"), 1)
            pe.wait_ge(s.sem("pos"), 1)
            pe.matmul(ps_m[:, 128:256], A["ones"][0:1, :], pos[:, :], start=True, stop=True)
            pe.matmul(ps_m[:, 256:257], pos[:, :], A["ones"][0:1, 0:1], start=True, stop=True).then_inc(s.sem("pos_ps"), 1)
            vals.pe(pe, s.sem("mixed"), lambda g: g + 1)
            op.pe(pe)

        @block.scalar
        def _(act):
            hd.nx.act(act)
            act.wait_ge(s.sem("n2"), 1)
            act.activation(nrm[:, :, :], n2[:, :, :], ACT.Sqrt).then_inc(s.sem("nrm"), 1)
            smp.act(act)
            smn.act(act)
            vals.act(act)

        @block.vector
        def _(dve):
            link = linker(dve, s.sem("dve_steps"))
            hd.dve_project(dve, link)
            dve.sem_inc(s.sem("qkv_ready"), 1)
            hd.dve_heads(dve)

            dve.wait_ge(s.sem("guide_in"), 16)
            q = hd.qkv[:, D:2 * D]
            p3 = prod[:, :].rearrange("p (h e) -> p h e", h=16)
            for i, (a, b) in enumerate(((q, q), (guide[:, :], guide[:, :]), (q, guide[:, :]))):
                link(dve.tensor_tensor(prod[:, :], a, b, ALU.mult))
                link(dve.tensor_reduce(n2[:, i, :] if i < 2 else dot[:, :], p3, AX.X, ALU.add))
            dve.sem_inc(s.sem("n2"), 1)
            dve.wait_ge(s.sem("nrm"), 1)
            link(dve.tensor_tensor(nrm[:, 0, :], nrm[:, 0, :], nrm[:, 1, :], ALU.mult))
            link(dve.reciprocal(nrm[:, 0, :], nrm[:, 0, :]))
            link(dve.tensor_tensor(dot[:, :], dot[:, :], nrm[:, 0, :], ALU.mult))
            link(dve.tensor_reduce(sim[:, :], dot[:, :], AX.X, ALU.add))
            dve.tensor_scalar(sim[:, :], sim[:, :], 1 / 16, None, ALU.mult).then_inc(s.sem("sim"), 1)
            dve.wait_ge(s.sem("srow_ps"), 1)
            link(dve.tensor_copy(srow[:, :], ps_m[0:1, 0:T]))
            link(dve.tensor_reduce(mm1[:, 0:1], srow[:, REG:T], AX.X, ALU.min))
            link(dve.tensor_reduce(mm1[:, 1:2], srow[:, REG:T], AX.X, ALU.max))
            link(dve.tensor_tensor(mm1[:, 2:3], mm1[:, 1:2], mm1[:, 0:1], ALU.subtract))
            link(dve.reciprocal(mm1[:, 3:4], mm1[:, 2:3]))
            link(dve.tensor_scalar(srow[:, :], srow[:, :], mm1[:, 0:1], mm1[:, 3:4], ALU.subtract, ALU.mult))
            dve.tensor_scalar(pos[:, :], srow[:, :], 0.9, None, ALU.is_gt).then_inc(s.sem("pos"), 1)
            dve.wait_ge(s.sem("pos_ps"), 1)
            link(dve.tensor_scalar(bp[:, :], ps_m[:, 128:256], 1.0, -FAR, ALU.subtract, ALU.mult))
            link(dve.tensor_scalar(bn[:, :], ps_m[:, 128:256], FAR, None, ALU.mult))
            link(dve.memset(bp[:, 0:REG], 0.0))
            link(dve.memset(bn[:, 0:REG], 0.0))
            dve.wait_ge(s.sem("reg"), 1)
            link(dve.tensor_scalar(wt[:, 2:3], wt[:, 3:4], -1.0, 1.0, ALU.mult, ALU.add))
            link(dve.tensor_tensor(wt[:, 0:1], wt[:, 2:3], ps_m[:, 256:257], ALU.mult))
            link(dve.tensor_tensor(wt[:, 1:2], wt[:, 2:3], wt[:, 0:1], ALU.subtract))
            for i in range(2):
                link(dve.scalar_tensor_tensor(out=wt[:, i:i + 1], in0=wt[:, 3:4], scalar=0.5, in1=wt[:, i:i + 1],
                                              op0=ALU.mult, op1=ALU.add))

            def scores(g):
                dve.wait_ge(s.sem("scores"), g + 1)
                return cols(hd.ps_h[g], 4)

            smp.dve(dve, link, scores, bp[:, :])
            smn.dve(dve, link, scores, bn[:, :])
            for i, sm in enumerate((smp, smn)):
                sm.dve_sums(dve, link)
                link(dve.tensor_scalar(cf[:, i, :], sm.l[:, :], wt[:, i:i + 1], None, ALU.mult))
            for g in range(4):
                gs = slice(4 * g, 4 * g + 4)
                link(dve.tensor_tensor(smp.p[:, gs, :], smp.p[:, gs, :], add_cols(cf[:, 0, gs], T), ALU.mult))
                link(dve.tensor_tensor(smn.p[:, gs, :], smn.p[:, gs, :], add_cols(cf[:, 1, gs], T), ALU.mult))
                dve.tensor_tensor(smp.p[:, gs, :], smp.p[:, gs, :], smn.p[:, gs, :], ALU.add).then_inc(s.sem("mixed"), 1)
            dve.wait_ge(s.sem("y_ps"), 1)
            dve.tensor_copy(op.y[:, :], ps_y[:, 0:D]).then_inc(s.sem("y_ready"), 1)
            op.dve(dve, link)


def dve_first_max(dve, link, A, scores, n, m, key, onehot):
    iota = A["iota16"][:, 0:n]
    link(dve.tensor_reduce(m, scores, AX.X, ALU.max))
    link(dve.tensor_scalar(onehot, scores, m, None, ALU.is_equal))
    link(dve.scalar_tensor_tensor(out=onehot, in0=onehot, scalar=-1000.0, in1=iota, op0=ALU.mult, op1=ALU.add))
    link(dve.tensor_reduce(key, onehot, AX.X, ALU.min))
    link(dve.tensor_scalar(onehot, iota, -1000.0, key, ALU.add, ALU.is_equal))


class DenseExperts:

    E, F = 8, 1024
    FC = F // 128

    def __init__(self, s, A, x, ident, prefix):
        self.s, self.A, self.x, self.ident, self.prefix = s, A, x, ident, prefix
        self.w1, self.w2 = s.sb("w1", [128, 2, DC, self.F]), s.sb("w2", [128, 2, self.FC, D])
        self.b1, self.b2 = s.sb("b1", [128, self.E * self.FC]), s.sb("b2", [self.E, D])
        self.gate, self.gateT = s.sb("gate", [128, self.E]), s.sb("gateT", [self.E, T])
        self.hT = s.sb("hT", [128, 2, self.FC, T])
        self.acc = s.sb("acc", [128, D])
        self.ps_h = [[s.ps(f"ps_h{j}{i}") for i in range(2)] for j in range(2)]
        self.ps_y = [s.ps(f"ps_y{j}") for j in range(2)]

    def load(self, sp, j, e):
        s, A, p = self.s, self.A, self.prefix
        sp.dma_start(self.w1[:, j, :, :], A[p + "W1"][bass.ds(e, 1), :, :, :]).then_inc(s.sem(f"w1_in{j}"), 16)
        sp.dma_start(self.w2[:, j, :, :], A[p + "W2"][bass.ds(e, 1), :, :, :]).then_inc(s.sem(f"w2_in{j}"), 16)

    def sp(self, sp):
        s, A, p = self.s, self.A, self.prefix
        for j in range(2):
            self.load(sp, j, j)
            if j == 0:
                sp.dma_start(self.b1[:, :], A[p + "b1"]).then_inc(s.sem("b1_in"), 16)
                sp.dma_start(self.b2[:, :], A[p + "b2"]).then_inc(s.sem("b2_in"), 16)
        with sp.Fori(0, self.E // 2 - 1) as it:
            for j in range(2):
                sp.wait_ge(s.sem("expert_ps"), it * 2 + (j + 1))
                self.load(sp, j, it * 2 + (2 + j))

    def pe(self, pe, xnT):
        s = self.s
        with pe.Fori(0, self.E // 2) as it:
            for j in range(2):
                pe.wait_ge(s.sem(f"w1_in{j}"), it * 16 + 16)
                pe.wait_ge(s.sem("hT"), it * 2 * self.FC)
                for f in range(self.FC):
                    out = self.ps_h[j][f // 4][:, (f % 4) * T:(f % 4 + 1) * T]
                    mm = pe_dense(pe, out, lambda c: self.w1[:, j, c, f * 128:(f + 1) * 128], lambda c: xnT[:, c, :])
                    if f % 4 == 3:
                        mm.then_inc(s.sem("h_ps"), 1)
            for j in range(2):
                pe.wait_ge(s.sem(f"w2_in{j}"), it * 16 + 16)
                pe.wait_ge(s.sem("acc"), it * 2)
                for f in range(self.FC):
                    pe.wait_ge(s.sem("hT"), (it * 2 + j) * self.FC + (f + 1))
                    mm = pe.matmul(self.ps_y[j][:, 0:D], self.hT[:, j, f, :], self.w2[:, j, f, :],
                                   start=(f == 0), stop=(f == self.FC - 1))
                mm.then_inc(s.sem("expert_ps"), 1)
        pe.wait_ge(s.sem("gate"), 1)
        pe.wait_ge(s.sem("hT"), self.E * self.FC)
        pe.matmul(self.ps_h[0][0][0:self.E, 0:T], self.gate[:, :], self.ident[:, :], start=True,
                  stop=True).then_inc(s.sem("gateT_ps"), 1)
        pe.wait_ge(s.sem("b2_in"), 16)
        pe.wait_ge(s.sem("gateT"), 1)
        pe.matmul(self.ps_h[1][0][:, 0:D], self.gateT[:, :], self.b2[:, :], start=True, stop=True).then_inc(s.sem("b2_ps"), 1)

    def dve(self, dve, link):
        s, x = self.s, self.x
        finish(dve, dve.memset(self.acc[:, :], 0.0), s.sem("acc0"))
        dve.wait_ge(s.sem("b1_in"), 16)
        with dve.Fori(0, self.E // 2) as it:
            for j in range(2):
                dve.wait_ge(s.sem("expert_ps"), it * 2)
                for f in range(self.FC):
                    if f % 4 == 0:
                        dve.wait_ge(s.sem("h_ps"), (it * 2 + j) * (self.FC // 4) + (f // 4 + 1))
                    dve.tensor_scalar(self.hT[:, j, f, :], self.ps_h[j][f // 4][:, (f % 4) * T:(f % 4 + 1) * T],
                                      self.b1[:, bass.ds((it * 2 + j) * self.FC + f, 1)], 0.0, ALU.add, ALU.max).then_inc(s.sem("hT"), 1)
            for j in range(2):
                dve.wait_ge(s.sem("expert_ps"), it * 2 + (j + 1))
                dve.wait_ge(s.sem("acc"), it * 2 + j)
                dve.scalar_tensor_tensor(out=self.acc[:, :], in0=self.ps_y[j][:, 0:D],
                                         scalar=self.gate[:, bass.ds(it * 2 + j, 1)], in1=self.acc[:, :],
                                         op0=ALU.mult, op1=ALU.add).then_inc(s.sem("acc"), 1)
        dve.wait_ge(s.sem("acc"), self.E)
        link(dve.tensor_tensor(x[:, :], x[:, :], self.acc[:, :], ALU.add))
        dve.wait_ge(s.sem("gateT_ps"), 1)
        dve.tensor_copy(self.gateT[:, :], self.ps_h[0][0][0:self.E, 0:T]).then_inc(s.sem("gateT"), 1)
        dve.wait_ge(s.sem("b2_ps"), 1)
        link(dve.tensor_tensor(x[:, :], x[:, :], self.ps_h[1][0][:, 0:D], ALU.add))


def dve_floor(dve, link, dst, src, whole, above):
    link(dve.tensor_copy(whole, src))
    link(dve.tensor_copy(dst, whole))
    link(dve.tensor_tensor(above, dst, src, ALU.is_gt))
    link(dve.tensor_tensor(dst, dst, above, ALU.subtract))


def stage_l1_ffn(nc, A, x, ident):
    with Stage(nc, "l1f") as s:
        ex = DenseExperts(s, A, x, ident, "L1_ffn_")
        ps_a, ps_k = s.ps("ps_a"), s.ps("ps_k")
        nx = NormX(s, x, ident, ps_a)
        wr, br = s.sb("wr", [128, DC]), s.sb("br", [128, 1])
        key, fl, g8, q8, ab = (s.sb(n, [128, 1]) for n in ("key", "fl", "g8", "q8", "ab"))
        whole = s.sb("whole", [128, 1], I32)
        block = s.block()

        @block.sync
        def _(sp):
            sp.dma_start(wr[:, :], A["L1_ffn_wr"]).then_inc(s.sem("wr_in"), 16)
            sp.dma_start(br[:, :], A["L1_ffn_br"].partition_broadcast(128)).then_inc(s.sem("wr_in"), 16)
            ex.sp(sp)

        @block.tensor
        def _(pe):
            nx.pe(pe)
            pe.wait_ge(s.sem("wr_in"), 32)
            pe.wait_ge(s.sem("xnT"), 1)
            pe_dense(pe, ps_k[:, 0:1], lambda c: nx.xnT[:, c, :], lambda c: wr[:, c:c + 1]).then_inc(s.sem("key_ps"), 1)
            ex.pe(pe, nx.xnT)

        @block.scalar
        def _(act):
            nx.act(act)

        @block.vector
        def _(dve):
            link = linker(dve, s.sem("dve_steps"))
            nx.dve(dve, link)
            dve.wait_ge(s.sem("wr_in"), 32)
            dve.wait_ge(s.sem("key_ps"), 1)
            link(dve.tensor_tensor(key[:, :], ps_k[:, 0:1], br[:, :], ALU.add))
            dve_floor(dve, link, fl[:, :], key[:, :], whole[:, :], ab[:, :])
            link(dve.tensor_scalar(q8[:, :], fl[:, :], 1 / 8, None, ALU.mult))
            dve_floor(dve, link, g8[:, :], q8[:, :], whole[:, :], ab[:, :])
            link(dve.scalar_tensor_tensor(out=fl[:, :], in0=g8[:, :], scalar=-8.0, in1=fl[:, :], op0=ALU.mult, op1=ALU.add))
            finish(dve, dve.tensor_scalar(ex.gate[:, :], A["iota16"][:, 0:8], fl[:, 0:1], None, ALU.is_equal), s.sem("gate"))
            ex.dve(dve, link)


def stage_l2_ffn(nc, A, x, ident):
    E = 8
    CAP = 2 * -(-T // E)
    with Stage(nc, "l2f") as s:
        ex = DenseExperts(s, A, x, ident, "L2_ffn_")
        ps_a, ps_k = s.ps("ps_a"), s.ps("ps_k")
        nx = NormX(s, x, ident, ps_a)
        wg = s.sb("wg", [128, DC, E])
        sc, s2, oh = s.sb("sc", [128, E]), s.sb("s2", [128, E]), s.sb("oh", [128, 2, E])
        m, r = s.sb("m", [128, 2]), s.sb("r", [128, 4])
        ok = s.sb("ok", [128, 2, E])
        block = s.block()

        @block.sync
        def _(sp):
            sp.dma_start(wg[:, :, :], A["L2_ffn_gate_w"]).then_inc(s.sem("wg_in"), 16)
            ex.sp(sp)

        @block.tensor
        def _(pe):
            nx.pe(pe)
            pe.wait_ge(s.sem("wg_in"), 16)
            pe.wait_ge(s.sem("xnT"), 1)
            pe_dense(pe, ps_k[:, 0:E], lambda c: nx.xnT[:, c, :], lambda c: wg[:, c, :]).then_inc(s.sem("logit_ps"), 1)
            pe.wait_ge(s.sem("chosen"), 1)
            pe.matmul(ps_a[:, 0:2 * E], A["causal"][:, :], oh[:, :, :], start=True, stop=False, skip_group_check=True)
            pe.matmul(ps_a[:, E:2 * E], A["ones"][:, :], oh[:, 0, :], start=False, stop=True,
                      skip_group_check=True).then_inc(s.sem("place_ps"), 1)
            ex.pe(pe, nx.xnT)

        @block.scalar
        def _(act):
            nx.act(act)
            act.wait_ge(s.sem("shifted"), 1)
            act.activation(sc[:, :], sc[:, :], ACT.Exp, accum_out=r[:, 0:1]).then_inc(s.sem("exp"), 1)

        @block.vector
        def _(dve):
            link = linker(dve, s.sem("dve_steps"))
            nx.dve(dve, link)
            dve.wait_ge(s.sem("logit_ps"), 1)
            link(dve.tensor_reduce(r[:, 1:2], ps_k[:, 0:E], AX.X, ALU.max))
            dve.tensor_scalar(sc[:, :], ps_k[:, 0:E], r[:, 1:2], None, ALU.subtract).then_inc(s.sem("shifted"), 1)
            dve.wait_ge(s.sem("exp"), 1)
            link(dve.reciprocal(r[:, 2:3], r[:, 0:1]))
            link(dve.tensor_scalar(sc[:, :], sc[:, :], r[:, 2:3], None, ALU.mult))
            dve_first_max(dve, link, A, sc[:, :], E, m[:, 0:1], r[:, 3:4], oh[:, 0, :])
            link(dve.scalar_tensor_tensor(out=s2[:, :], in0=oh[:, 0, :], scalar=-2.0, in1=sc[:, :], op0=ALU.mult, op1=ALU.add))
            dve_first_max(dve, link, A, s2[:, :], E, m[:, 1:2], r[:, 3:4], oh[:, 1, :])
            dve.sem_inc(s.sem("chosen"), 1)
            link(dve.tensor_tensor(r[:, 0:1], m[:, 0:1], m[:, 1:2], ALU.add))
            link(dve.reciprocal(r[:, 0:1], r[:, 0:1]))
            link(dve.tensor_scalar(m[:, :], m[:, :], r[:, 0:1], None, ALU.mult))
            dve.wait_ge(s.sem("place_ps"), 1)
            link(dve.tensor_scalar(ok[:, :, :], ps_a[:, 0:2 * E].rearrange("p (k e) -> p k e", k=2), float(CAP), None, ALU.is_le))
            link(dve.tensor_tensor(ok[:, :, :], ok[:, :, :], oh[:, :, :], ALU.mult))
            link(dve.tensor_scalar(ex.gate[:, :], ok[:, 0, :], m[:, 0:1], None, ALU.mult))
            finish(dve, dve.scalar_tensor_tensor(out=ex.gate[:, :], in0=ok[:, 1, :], scalar=m[:, 1:2], in1=ex.gate[:, :],
                                                 op0=ALU.mult, op1=ALU.add), s.sem("gate"))
            ex.dve(dve, link)


def stage_l0_ffn(nc, A, x, ident):
    E, F = 16, 512
    FC = F // 128
    TWO_PI = 6.283185307179586
    C1 = 6.28125
    C2 = TWO_PI - C1
    PI = 3.1415925
    with Stage(nc, "l0f") as s:
        wm, wf = s.sb("wm", [128, 2, DC, F]), s.sb("wf", [128, 2, DC, F])
        wd = s.sb("wd", [128, 2, FC, D])
        ph = s.sb("ph", [128, 2, F])
        wr, br = s.sb("wr", [128, DC, E]), s.sb("br", [128, E])
        nw = s.sb("nw", [128, D])
        sc, oh = s.sb("sc", [128, E]), s.sb("oh", [128, 2, E])
        m, r, gate = s.sb("m", [128, 2]), s.sb("r", [128, 4]), s.sb("gate", [128, E])
        sp_, pos, mag = s.sb("sp", [128, 2, F]), s.sb("pos", [128, 2, F]), s.sb("mag", [128, 2, F])
        turns, arg = s.sb("turns", [128, 2, F]), s.sb("arg", [128, 2, F])
        whole = s.sb("whole", [128, 2, F], I32)
        hid, hT = s.sb("hid", [128, 2, F]), s.sb("hT", [128, 2, FC, T])
        acc, sq = s.sb("acc", [128, D]), s.sb("sq", [128, D])
        ps_m, ps_f = [s.ps(f"ps_m{j}") for j in range(2)], [s.ps(f"ps_f{j}") for j in range(2)]
        ps_t, ps_y = [s.ps(f"ps_t{j}") for j in range(2)], [s.ps(f"ps_y{j}") for j in range(2)]
        nx = NormX(s, x, ident, ps_t[0])
        block = s.block()

        @block.sync
        def _(sp):
            def load(j, e):
                for name, dst in (("mag", wm), ("freq", wf), ("down", wd)):
                    sp.dma_start(dst[:, j, :, :], A["L0_ffn_bank_" + name][bass.ds(e, 1), :, :, :]).then_inc(s.sem(f"{name}_in{j}"), 16)
                sp.dma_start(ph[:, j, :], A["L0_ffn_bank_phase"][bass.ds(e, 1), :].partition_broadcast(128)).then_inc(s.sem(f"phase_in{j}"), 16)

            sp.dma_start(wr[:, :, :], A["L0_ffn_router_w"]).then_inc(s.sem("wr_in"), 16)
            load_rows(sp, s, A, [("br", br, "L0_ffn_router_bias"), ("nw", nw, "L0_ffn_norm_w")])
            for j in range(2):
                load(j, j)
            with sp.Fori(0, E // 2 - 1) as it:
                for j in range(2):
                    sp.wait_ge(s.sem("expert_ps"), it * 2 + (j + 1))
                    load(j, it * 2 + (2 + j))

        @block.tensor
        def _(pe):
            nx.pe(pe)
            pe.wait_ge(s.sem("wr_in"), 16)
            pe.wait_ge(s.sem("xnT"), 1)
            pe_dense(pe, ps_y[0][:, 0:E], lambda c: nx.xnT[:, c, :], lambda c: wr[:, c, :]).then_inc(s.sem("router_ps"), 1)
            pe.wait_ge(s.sem("router"), 1)
            with pe.Fori(0, E // 2) as it:
                for j in range(2):
                    pe.wait_ge(s.sem(f"freq_in{j}"), it * 16 + 16)
                    pe.wait_ge(s.sem("freq_read"), it * 2)
                    pe_dense(pe, ps_f[j][:, :], lambda c: nx.xnT[:, c, :], lambda c: wf[:, j, c, :]).then_inc(s.sem("freq_ps"), 1)
                    pe.wait_ge(s.sem(f"mag_in{j}"), it * 16 + 16)
                    pe.wait_ge(s.sem("tanh"), it * 2)
                    pe_dense(pe, ps_m[j][:, :], lambda c: nx.xnT[:, c, :], lambda c: wm[:, j, c, :]).then_inc(s.sem("mag_ps"), 1)
                for j in range(2):
                    pe.wait_ge(s.sem("hid"), it * 2 + (j + 1))
                    pe.wait_ge(s.sem("hT"), it * 2)
                    pe_transposes(pe, ps_t[j], hid[:, j, :], ident, FC).then_inc(s.sem("hT_ps"), 1)
                for j in range(2):
                    pe.wait_ge(s.sem(f"down_in{j}"), it * 16 + 16)
                    pe.wait_ge(s.sem("acc"), it * 2)
                    pe.wait_ge(s.sem("hT"), it * 2 + (j + 1))
                    pe_dense(pe, ps_y[j][:, 0:D], lambda c: hT[:, j, c, :], lambda c: wd[:, j, c, :], FC).then_inc(s.sem("expert_ps"), 1)

        @block.scalar
        def _(act):
            nx.act(act)
            act.wait_ge(s.sem("second"), 1)
            act.activation(r[:, 1:2], r[:, 0:1], ACT.Exp).then_inc(s.sem("ratio"), 1)
            with act.Fori(0, E // 2) as it:
                for j in range(2):
                    act.wait_ge(s.sem("negabs"), it * 2 + (j + 1))
                    act.activation(sp_[:, j, :], sp_[:, j, :], ACT.Exp).then_inc(s.sem("exp"), 1)
                    act.wait_ge(s.sem("mag_ps"), it * 2 + (j + 1))
                    act.wait_ge(s.sem("hid"), it * 2)
                    act.activation(mag[:, j, :], ps_m[j][:, :], ACT.Tanh).then_inc(s.sem("tanh"), 1)
                act.wait_ge(s.sem("exp"), it * 2 + 2)
                act.activation(sp_[:, :, :], sp_[:, :, :], ACT.Ln, bias=A["ones"][:, 0:1]).then_inc(s.sem("log"), 1)
                for j in range(2):
                    act.wait_ge(s.sem("angle"), it * 2 + (j + 1))
                    act.activation(arg[:, j, :], arg[:, j, :], ACT.Sin).then_inc(s.sem("cos"), 1)
                for j in range(2):
                    act.wait_ge(s.sem("hT_ps"), it * 2 + (j + 1))
                    act.wait_ge(s.sem("expert_ps"), it * 2)
                    act.activation(hT[:, j, :, :], cols(ps_t[j], FC), ACT.Copy).then_inc(s.sem("hT"), 1)
            act.wait_ge(s.sem("ms"), 1)
            act.activation(r[:, 1:2], r[:, 2:3], ACT.Sqrt).then_inc(s.sem("rms"), 1)

        @block.vector
        def _(dve):
            link = linker(dve, s.sem("dve_steps"))
            nx.dve(dve, link)
            dve.wait_ge(s.sem("br_in"), 16)
            dve.wait_ge(s.sem("router_ps"), 1)
            finish(dve, dve.tensor_tensor(sc[:, :], ps_y[0][:, 0:E], br[:, :], ALU.add), s.sem("router"))
            dve_first_max(dve, link, A, sc[:, :], E, m[:, 0:1], r[:, 3:4], oh[:, 0, :])
            link(dve.scalar_tensor_tensor(out=sc[:, :], in0=oh[:, 0, :], scalar=FAR, in1=sc[:, :], op0=ALU.mult, op1=ALU.add))
            dve_first_max(dve, link, A, sc[:, :], E, m[:, 1:2], r[:, 3:4], oh[:, 1, :])
            dve.tensor_tensor(r[:, 0:1], m[:, 1:2], m[:, 0:1], ALU.subtract).then_inc(s.sem("second"), 1)
            dve.wait_ge(s.sem("ratio"), 1)
            link(dve.tensor_scalar(r[:, 2:3], r[:, 1:2], 1.0, None, ALU.add))
            link(dve.reciprocal(r[:, 2:3], r[:, 2:3]))
            link(dve.tensor_tensor(r[:, 3:4], r[:, 1:2], r[:, 2:3], ALU.mult))
            link(dve.tensor_scalar(gate[:, :], oh[:, 0, :], r[:, 2:3], None, ALU.mult))
            link(dve.scalar_tensor_tensor(out=gate[:, :], in0=oh[:, 1, :], scalar=r[:, 3:4], in1=gate[:, :],
                                          op0=ALU.mult, op1=ALU.add))
            link(dve.memset(acc[:, :], 0.0))
            STEPS = 2 * 9
            with dve.Fori(0, E // 2) as it:
                link = linker(dve, s.sem("dve_loop"), it * STEPS)
                for j in range(2):
                    n = it * 2 + j
                    dve.wait_ge(s.sem("freq_ps"), n + 1)
                    dve.wait_ge(s.sem("hid"), it * 2)
                    link(dve.tensor_scalar(pos[:, j, :], ps_f[j][:, :], 0.0, None, ALU.max))
                    dve.scalar_tensor_tensor(out=sp_[:, j, :], in0=pos[:, j, :], scalar=-2.0, in1=ps_f[j][:, :],
                                             op0=ALU.mult, op1=ALU.add).then_inc(s.sem("negabs"), 1)
                    dve.wait_ge(s.sem("negabs"), n + 1)
                    dve.sem_inc(s.sem("freq_read"), 1)
                for j in range(2):
                    n = it * 2 + j
                    dve.wait_ge(s.sem(f"phase_in{j}"), it * 16 + 16)
                    dve.wait_ge(s.sem("log"), it + 1)
                    link(dve.tensor_tensor(arg[:, j, :], sp_[:, j, :], pos[:, j, :], ALU.add))
                    link(dve.scalar_tensor_tensor(out=arg[:, j, :], in0=arg[:, j, :], scalar=0.1, in1=ph[:, j, :],
                                                  op0=ALU.add, op1=ALU.add))
                    link(dve.tensor_scalar(turns[:, j, :], arg[:, j, :], 1 / TWO_PI, 0.25, ALU.mult, ALU.add))
                    link(dve.tensor_copy(whole[:, j, :], turns[:, j, :]))
                    link(dve.tensor_copy(turns[:, j, :], whole[:, j, :]))
                    link(dve.scalar_tensor_tensor(out=arg[:, j, :], in0=turns[:, j, :], scalar=-C1, in1=arg[:, j, :],
                                                  op0=ALU.mult, op1=ALU.add))
                    link(dve.scalar_tensor_tensor(out=arg[:, j, :], in0=turns[:, j, :], scalar=-C2, in1=arg[:, j, :],
                                                  op0=ALU.mult, op1=ALU.add))
                    link(dve.tensor_scalar(arg[:, j, :], arg[:, j, :], TWO_PI / 4, PI, ALU.add, ALU.min))
                    dve.tensor_scalar(arg[:, j, :], arg[:, j, :], -PI, None, ALU.max).then_inc(s.sem("angle"), 1)
                for j in range(2):
                    n = it * 2 + j
                    dve.wait_ge(s.sem("cos"), n + 1)
                    dve.wait_ge(s.sem("tanh"), n + 1)
                    dve.wait_ge(s.sem("hT_ps"), it * 2)
                    dve.tensor_tensor(hid[:, j, :], mag[:, j, :], arg[:, j, :], ALU.mult).then_inc(s.sem("hid"), 1)
                assert link.count[0] == STEPS, link.count
                for j in range(2):
                    n = it * 2 + j
                    dve.wait_ge(s.sem("expert_ps"), n + 1)
                    dve.wait_ge(s.sem("acc"), n)
                    dve.scalar_tensor_tensor(out=acc[:, :], in0=ps_y[j][:, 0:D], scalar=gate[:, bass.ds(n, 1)],
                                             in1=acc[:, :], op0=ALU.mult, op1=ALU.add).then_inc(s.sem("acc"), 1)
            dve.wait_ge(s.sem("acc"), E)
            link = linker(dve, s.sem("dve_end"))
            link(dve.tensor_tensor(sq[:, :], acc[:, :], acc[:, :], ALU.mult))
            link(dve.tensor_reduce(r[:, 2:3], sq[:, :], AX.X, ALU.add))
            dve.tensor_scalar(r[:, 2:3], r[:, 2:3], 1 / D, 1e-6, ALU.mult, ALU.add).then_inc(s.sem("ms"), 1)
            dve.wait_ge(s.sem("rms"), 1)
            dve_rsqrt(dve, link, r[:, 0:1], r[:, 1:2], r[:, 2:3])
            dve.wait_ge(s.sem("nw_in"), 16)
            link(dve.scalar_tensor_tensor(out=acc[:, :], in0=acc[:, :], scalar=r[:, 0:1], in1=nw[:, :],
                                          op0=ALU.mult, op1=ALU.mult))
            link(dve.tensor_tensor(x[:, :], x[:, :], acc[:, :], ALU.add))


def stage_l1_attn(nc, A, x, ident):
    H, HD, I = 8, 64, 512
    IC = I // 128
    K = 4
    CAP = 15.0
    PFX = "L1_attn_"
    with Stage(nc, "mls") as s:
        wup = s.sb("wup", [128, DC, 2 * I])
        wts = {n: s.sb("w_" + n, [128, IC, I]) for n in ("skip", "q", "k", "v", "o")}
        wif, wdn = s.sb("wif", [128, IC, 16]), s.sb("wdn", [128, IC, D])
        rows = {n: s.sb("r_" + n, [128, w]) for n, w in (
            ("ln_g", D), ("ln_b", D), ("b_up_l", I), ("b_up_r", I), ("b_skip", I), ("b_v", I), ("b_o", I),
            ("mh_g", I), ("mh_b", I), ("b_down", D), ("conv_w", K), ("conv_b", 1))}
        bqk, bif = s.sb("bqk", [128, 2, IC]), s.sb("bif", [H, 2])
        xa, xaT = s.sb("xa", [128, D]), s.sb("xaT", [128, DC, T])
        xt, rt = s.sb("xt", [128, K - 1 + I]), s.sb("rt", [128, I])
        xc, sg, sr = s.sb("xc", [128, I]), s.sb("sg", [128, I]), s.sb("sr", [128, I])
        xtT, xcT = s.sb("xtT", [128, IC, T]), s.sb("xcT", [128, IC, T])
        skip, v, o = s.sb("skip", [128, I]), s.sb("v", [128, H, HD + 1]), s.sb("o", [128, I])
        qT, kT = s.sb("qT", [128, IC, T]), s.sb("kT", [128, IC, T])
        gi, gf, fs = s.sb("gi", [H, T]), s.sb("gf", [H, T]), s.sb("fs", [H, T])
        one8 = s.sb("one8", [H, T])
        b, mx, em = s.sb("b", [H, T]), s.sb("mx", [H, T]), s.sb("em", [H, T])
        hsel = s.sb("hsel", [H, H, T])
        halves = s.sb("halves", [128, 2])
        cb = s.sb("cb", [128, 16])
        dm, sd = s.sb("dm", [128, H, T]), s.sb("sd", [128, H, T])
        den, hh, hn = s.sb("den", [128, H]), s.sb("hh", [128, I]), s.sb("hn", [128, I])
        hst, hmv = s.sb("hst", [128, H, 6]), s.sb("hmv", [128, H, 2])
        hsd, hvar = s.sb("hsd", [128, H]), s.sb("hvar", [128, H])
        oT = s.sb("oT", [128, IC, T])
        P = [s.ps(f"P{n}") for n in range(8)]
        nx, n1 = NormX(s, x, ident, P[0]), RowNorm(s, "n1", 1e-6)
        block = s.block()

        @block.sync
        def _(sp):
            sp.dma_start(wup[:, :, :], A[PFX + "W_up"]).then_inc(s.sem("wup_in"), 16)
            for n in ("ln_g", "ln_b", "b_up_l", "b_up_r", "conv_w", "conv_b"):
                sp.dma_start(rows[n][:, :], A[PFX + n].partition_broadcast(128)).then_inc(s.sem("rows1_in"), 16)
            for n in ("skip", "v", "o", "q", "k"):
                sp.dma_start(wts[n][:, :, :], A[PFX + "W_" + n]).then_inc(s.sem(f"w_{n}_in"), 16)
            sp.dma_start(wif[:, :, :], A[PFX + "W_if"]).then_inc(s.sem("wif_in"), 16)
            for n in ("b_skip", "b_v", "b_o", "mh_g", "mh_b", "b_down"):
                sp.dma_start(rows[n][:, :], A[PFX + n].partition_broadcast(128)).then_inc(s.sem("rows2_in"), 16)
            sp.dma_start(bqk[:, :, :], A[PFX + "b_qk"]).then_inc(s.sem("rows2_in"), 16)
            sp.dma_start(bif[:, :], A[PFX + "b_if"]).then_inc(s.sem("rows2_in"), 16)
            sp.dma_start(wdn[:, :, :], A[PFX + "W_down"]).then_inc(s.sem("wdn_in"), 16)

        @block.gpsimd
        def _(pool):
            pool.memset(hsel[:, :, :], 0.0).then_inc(s.sem("hsel0"), 1)
            pool.wait_ge(s.sem("hsel0"), 1)
            pool.affine_select(out=hsel[:, :, :], in_=hsel[:, :, :], compare_op=ALU.not_equal, fill=1.0, base=0,
                               pattern=[[-1, H], [0, T]], channel_multiplier=1).then_inc(s.sem("hsel"), 1)
            pool.affine_select(out=halves[:, 0:1], in_=A["ones"][:, 0:1], compare_op=ALU.is_ge, fill=0.0, base=HD - 1,
                               pattern=[[0, 1]], channel_multiplier=-1).then_inc(s.sem("half0"), 1)
            pool.affine_select(out=halves[:, 1:2], in_=A["ones"][:, 0:1], compare_op=ALU.is_ge, fill=0.0, base=-HD,
                               pattern=[[0, 1]], channel_multiplier=1).then_inc(s.sem("half1"), 1)
            pool.wait_ge(s.sem("half0"), 1)
            pool.wait_ge(s.sem("half1"), 1)
            pool.sem_inc(s.sem("halves"), 1)
            for g in range(2):
                pool.wait_ge(s.sem("decay_all"), g + 1)
                pool.tensor_tensor(dm[:, 4 * g:4 * g + 4, :], dm[:, 4 * g:4 * g + 4, :],
                                   A["causal"][:, :].unsqueeze(1).to_broadcast([128, 4, T]), ALU.mult).then_inc(s.sem("decay"), 1)

        @block.tensor
        def _(pe):
            def dense(out, aT, w, n=IC):
                return pe_dense(pe, out, lambda c: aT[:, c, :], lambda c: w[:, c, :], n)

            nx.pe(pe)
            pe.wait_ge(s.sem("xa"), 1)
            pe.wait_ge(s.sem("xnT"), 1)
            pe_transposes(pe, P[0], xa, ident).then_inc(s.sem("xaT_ps"), 1)
            pe.wait_ge(s.sem("wup_in"), 16)
            pe.wait_ge(s.sem("xaT"), 1)
            pe_dense(pe, P[1][:, :], lambda c: xaT[:, c, :], lambda c: wup[:, c, 0:I]).then_inc(s.sem("up_ps"), 1)
            pe_dense(pe, P[2][:, :], lambda c: xaT[:, c, :], lambda c: wup[:, c, I:2 * I]).then_inc(s.sem("up_ps"), 1)
            pe.wait_ge(s.sem("xt"), 1)
            for c in range(IC):
                mm = pe.transpose(P[3][:, c * T:(c + 1) * T], xt[:, K - 1 + c * 128:K - 1 + (c + 1) * 128], ident[:, :])
            mm.then_inc(s.sem("xtT_ps"), 1)
            pe.wait_ge(s.sem("w_v_in"), 16)
            pe.wait_ge(s.sem("xtT"), 1)
            dense(P[6][:, :], xtT, wts["v"]).then_inc(s.sem("v_ps"), 1)
            pe.wait_ge(s.sem("w_o_in"), 16)
            dense(P[7][:, :], xtT, wts["o"]).then_inc(s.sem("o_ps"), 1)
            pe.wait_ge(s.sem("xc"), 1)
            pe_transposes(pe, P[4], xc, ident, IC).then_inc(s.sem("xcT_ps"), 1)
            pe.wait_ge(s.sem("wif_in"), 16)
            pe.wait_ge(s.sem("xcT"), 1)
            pe.wait_ge(s.sem("rt"), 1)
            for g in range(2):
                mm = pe_dense(pe, P[2][0:H, g * T:(g + 1) * T], lambda c: wif[:, c, g * H:(g + 1) * H],
                              lambda c: xcT[:, c, :], IC)
            mm.then_inc(s.sem("if_ps"), 1)
            for n, ps in (("q", P[0]), ("k", P[1])):
                pe.wait_ge(s.sem(f"w_{n}_in"), 16)
                for e in range(IC):
                    mm = pe_dense(pe, ps[:, e * T:(e + 1) * T], lambda c: wts[n][:, c, e * 128:(e + 1) * 128],
                                  lambda c: xcT[:, c, :], IC)
                mm.then_inc(s.sem(f"{n}_ps"), 1)
            pe.wait_ge(s.sem("w_skip_in"), 16)
            dense(P[5][:, :], xcT, wts["skip"]).then_inc(s.sem("skip_ps"), 1)
            pe.wait_ge(s.sem("em"), 1)
            pe.matmul(P[3][:, 0:H], b[:, :], ident[0:H, 0:H], start=True, stop=True)
            pe.matmul(P[3][:, H:2 * H], em[:, :], ident[0:H, 0:H], start=True, stop=True).then_inc(s.sem("cb_ps"), 1)
            pe.wait_ge(s.sem("hsel"), 1)
            pe.wait_ge(s.sem("skip"), 1)
            for h in range(H):
                mm = pe.matmul(P[4 + h // 4][:, (h % 4) * T:(h % 4 + 1) * T], hsel[:, h, :], mx[:, :], start=True, stop=True)
                if h % 4 == 3:
                    mm.then_inc(s.sem("mx_ps"), 1)
            pe.wait_ge(s.sem("qT"), 1)
            pe.wait_ge(s.sem("kT"), 1)
            pe.wait_ge(s.sem("v"), 1)
            pe.wait_ge(s.sem("o"), 1)
            for c in range(IC):
                for odd in range(2):
                    lo = HD * odd
                    mm = pe.matmul(P[6 + odd][:, c * T:(c + 1) * T], kT[lo:lo + HD, c, :], qT[lo:lo + HD, c, :],
                                   start=True, stop=True)
                    if c == IC - 1:
                        mm.then_inc(s.sem(f"scores{odd}"), 1)
            pe.wait_ge(s.sem("halves"), 1)
            for c in range(IC):
                mm = pe.matmul(P[2][:, 2 * c:2 * c + 2], qT[:, c, :], halves[:, :], start=True, stop=True)
            mm.then_inc(s.sem("qsum_ps"), 1)
            pe.wait_ge(s.sem("sd"), 2)
            for h in range(H):
                mm = pe.matmul(P[h // 4][:, (h % 4) * 65:(h % 4 + 1) * 65], sd[:, h, :], v[:, h, :], start=True, stop=True)
                if h % 4 == 3:
                    mm.then_inc(s.sem("num_ps"), 1)
            pe.wait_ge(s.sem("hn"), 1)
            pe_transposes(pe, P[3], hn, ident, IC).then_inc(s.sem("oT_ps"), 1)
            pe.wait_ge(s.sem("wdn_in"), 16)
            pe.wait_ge(s.sem("oT"), 1)
            dense(P[4][:, 0:D], oT, wdn).then_inc(s.sem("down_ps"), 1)

        @block.scalar
        def _(act):
            nx.act(act)
            n1.act(act)
            for name, tile in (("c", sg), ("r", sr), ("o", o)):
                act.wait_ge(s.sem(name + "_neg"), 1)
                act.activation(tile[:, :], tile[:, :], ACT.Exp).then_inc(s.sem(name + "_exp"), 1)
            act.wait_ge(s.sem("if_pre"), 1)
            act.activation(gi[:, :], gi[:, :], ACT.Tanh).then_inc(s.sem("tanh"), 1)
            act.activation(gf[:, :], gf[:, :], ACT.Tanh).then_inc(s.sem("tanh"), 1)
            act.wait_ge(s.sem("mx"), 1)
            act.activation(em[:, :], mx[:, :], ACT.Exp, scale=-1.0).then_inc(s.sem("em"), 1)
            for g in range(2):
                act.wait_ge(s.sem("dm"), 4 * g + 4)
                act.activation(dm[:, 4 * g:4 * g + 4, :], dm[:, 4 * g:4 * g + 4, :], ACT.Exp,
                               scale=-1.0).then_inc(s.sem("decay_all"), 1)
            act.wait_ge(s.sem("h_var"), 1)
            act.activation(hsd[:, :], hvar[:, :], ACT.Sqrt).then_inc(s.sem("h_std"), 1)

        @block.vector
        def _(dve):
            def sigmoid_in(name, tile, z):
                dve.tensor_scalar(tile[:, :], z[:, :], -1.0, 87.0, ALU.mult, ALU.min).then_inc(s.sem(name + "_neg"), 1)

            def sigmoid_out(link, name, tile):
                dve.wait_ge(s.sem(name + "_exp"), 1)
                link(dve.tensor_scalar(tile[:, :], tile[:, :], 1.0, None, ALU.add))
                link(dve.reciprocal(tile[:, :], tile[:, :]))

            link = linker(dve, s.sem("dve_steps"))
            link(dve.memset(xt[:, 0:K - 1], 0.0))
            link(dve.memset(v[:, :, HD:HD + 1], 1.0))
            link(dve.memset(one8[:, :], 1.0))
            nx.dve(dve, link)
            n1.dve(dve, link, xa[:, :], nx.xn[:, :])
            dve.wait_ge(s.sem("rows1_in"), 6 * 16)
            link(dve.tensor_tensor(xa[:, :], xa[:, :], rows["ln_g"][:, :], ALU.mult))
            dve.tensor_tensor(xa[:, :], xa[:, :], rows["ln_b"][:, :], ALU.add).then_inc(s.sem("xa"), 1)
            dve.wait_ge(s.sem("xaT_ps"), 1)
            dve.tensor_copy(xaT[:, :, :], cols(P[0])).then_inc(s.sem("xaT"), 1)
            dve.wait_ge(s.sem("up_ps"), 1)
            finish(dve, dve.tensor_tensor(xt[:, K - 1:], P[1][:, :], rows["b_up_l"][:, :], ALU.add), s.sem("xt"))
            link(dve.tensor_scalar(xc[:, :], xt[:, 0:I], rows["conv_w"][:, 0:1], rows["conv_b"][:, 0:1], ALU.mult, ALU.add))
            for m in range(1, K):
                ins = dve.scalar_tensor_tensor(out=xc[:, :], in0=xt[:, m:m + I], scalar=rows["conv_w"][:, m:m + 1],
                                               in1=xc[:, :], op0=ALU.mult, op1=ALU.add)
                if m < K - 1:
                    link(ins)
                else:
                    finish(dve, ins, s.sem("conv"))
            sigmoid_in("c", sg, xc)
            dve.wait_ge(s.sem("up_ps"), 2)
            finish(dve, dve.tensor_tensor(rt[:, :], P[2][:, :], rows["b_up_r"][:, :], ALU.add), s.sem("rt"))
            sigmoid_in("r", sr, rt)
            dve.wait_ge(s.sem("xtT_ps"), 1)
            dve.tensor_copy(xtT[:, :, :], cols(P[3], IC)).then_inc(s.sem("xtT"), 1)
            sigmoid_out(link, "c", sg)
            dve.tensor_tensor(xc[:, :], xc[:, :], sg[:, :], ALU.mult).then_inc(s.sem("xc"), 1)
            sigmoid_out(link, "r", sr)
            link(dve.tensor_tensor(sr[:, :], sr[:, :], rt[:, :], ALU.mult))
            dve.wait_ge(s.sem("xcT_ps"), 1)
            dve.tensor_copy(xcT[:, :, :], cols(P[4], IC)).then_inc(s.sem("xcT"), 1)
            dve.wait_ge(s.sem("rows2_in"), 8 * 16)
            dve.wait_ge(s.sem("v_ps"), 1)
            heads = "p (h e) -> p h e"
            dve.tensor_tensor(v[:, :, 0:HD], P[6][:, :].rearrange(heads, h=H),
                              rows["b_v"][:, :].rearrange(heads, h=H), ALU.add).then_inc(s.sem("v"), 1)
            dve.wait_ge(s.sem("o_ps"), 1)
            finish(dve, dve.tensor_tensor(o[:, :], P[7][:, :], rows["b_o"][:, :], ALU.add), s.sem("o"))
            sigmoid_in("o", o, o)
            dve.wait_ge(s.sem("if_ps"), 1)
            link(dve.tensor_scalar(gi[:, :], P[2][0:H, 0:T], bif[:, 0:1], 1 / CAP, ALU.add, ALU.mult))
            dve.tensor_scalar(gf[:, :], P[2][0:H, T:2 * T], bif[:, 1:2], 1 / CAP, ALU.add, ALU.mult).then_inc(s.sem("if_pre"), 1)
            dve.wait_ge(s.sem("tanh"), 2)
            link(dve.tensor_scalar(gi[:, :], gi[:, :], CAP, None, ALU.mult))
            link(dve.tensor_scalar(gf[:, :], gf[:, :], CAP, None, ALU.mult))
            link(dve.tensor_tensor_scan(fs[:, :], one8[:, :], gf[:, :], 0.0, ALU.mult, ALU.add))
            link(dve.tensor_tensor(b[:, :], gi[:, :], fs[:, :], ALU.subtract))
            dve.tensor_tensor_scan(mx[:, :], b[:, :], b[:, :], 0.0, ALU.max, ALU.max).then_inc(s.sem("mx"), 1)
            dve.wait_ge(s.sem("q_ps"), 1)
            for c in range(IC):
                ins = dve.tensor_scalar(qT[:, c, :], P[0][:, c * T:(c + 1) * T], bqk[:, 0, c:c + 1], None, ALU.add)
            ins.then_inc(s.sem("qT"), 1)
            dve.wait_ge(s.sem("k_ps"), 1)
            for c in range(IC):
                ins = dve.tensor_scalar(kT[:, c, :], P[1][:, c * T:(c + 1) * T], bqk[:, 1, c:c + 1], HD ** -0.5,
                                        ALU.add, ALU.mult)
            ins.then_inc(s.sem("kT"), 1)
            dve.wait_ge(s.sem("skip_ps"), 1)
            dve.tensor_tensor(skip[:, :], P[5][:, :], rows["b_skip"][:, :], ALU.add).then_inc(s.sem("skip"), 1)
            dve.wait_ge(s.sem("cb_ps"), 1)
            link(dve.tensor_copy(cb[:, :], P[3][:, 0:2 * H]))
            for h in range(H):
                dve.wait_ge(s.sem("mx_ps"), h // 4 + 1)
                dve.tensor_scalar(dm[:, h, :], P[4 + h // 4][:, (h % 4) * T:(h % 4 + 1) * T], cb[:, h:h + 1], 0.0,
                                  ALU.subtract, ALU.max).then_inc(s.sem("dm"), 1)
            dve.wait_ge(s.sem("decay"), 2)
            for odd in range(2):
                dve.wait_ge(s.sem(f"scores{odd}"), 1)
                by_row = "p (c odd) t -> p odd c t"
                dve.tensor_tensor(sd[:, :, :].rearrange(by_row, odd=2)[:, odd], cols(P[6 + odd], 4),
                                  dm[:, :, :].rearrange(by_row, odd=2)[:, odd], ALU.mult).then_inc(s.sem("sd"), 1)
            dve.wait_ge(s.sem("qsum_ps"), 1)
            link(dve.tensor_tensor(den[:, :], P[2][:, 0:H], cb[:, H:2 * H], ALU.mult))
            for g in range(2):
                dve.wait_ge(s.sem("num_ps"), g + 1)
                num = P[g][:, 0:260].rearrange("p (h e) -> p h e", h=4)
                gs = slice(4 * g, 4 * g + 4)
                link(dve.tensor_tensor(den[:, gs], den[:, gs], num[:, :, 64], ALU.add))
                link(dve.tensor_scalar(den[:, gs], den[:, gs], 1.0, None, ALU.max))
                link(dve.reciprocal(den[:, gs], den[:, gs]))
                link(dve.tensor_tensor(hh[:, g * 256:(g + 1) * 256].rearrange("p (h e) -> p h e", h=4), num[:, :, 0:64],
                                       add_cols(den[:, gs], HD), ALU.mult))
            sigmoid_out(link, "o", o)
            link(dve.tensor_tensor(hh[:, :], hh[:, :], o[:, :], ALU.mult))
            for h in range(H):
                link(dve.bn_stats(hst[:, h, :], hh[:, h * HD:(h + 1) * HD]))
                link(dve.bn_aggr(hmv[:, h, :], hst[:, h, :]))
            dve.tensor_scalar(hvar[:, :], hmv[:, :, 1], 1e-6, None, ALU.add).then_inc(s.sem("h_var"), 1)
            h3 = hh[:, :].rearrange("p (h e) -> p h e", h=H)
            link(dve.tensor_tensor(h3, h3, hmv[:, :, 0:1].to_broadcast([128, H, HD]), ALU.subtract))
            dve.wait_ge(s.sem("h_std"), 1)
            dve_rsqrt(dve, link, den[:, :], hsd[:, :], hvar[:, :])
            link(dve.tensor_tensor(h3, h3, add_cols(den[:, :], HD), ALU.mult))
            link(dve.tensor_tensor(hh[:, :], hh[:, :], rows["mh_g"][:, :], ALU.mult))
            link(dve.tensor_tensor(hh[:, :], hh[:, :], rows["mh_b"][:, :], ALU.add))
            link(dve.tensor_tensor(hh[:, :], hh[:, :], skip[:, :], ALU.add))
            dve.tensor_tensor(hn[:, :], hh[:, :], sr[:, :], ALU.mult).then_inc(s.sem("hn"), 1)
            dve.wait_ge(s.sem("oT_ps"), 1)
            dve.tensor_copy(oT[:, :, :], cols(P[3], IC)).then_inc(s.sem("oT"), 1)
            dve.wait_ge(s.sem("down_ps"), 1)
            link(dve.tensor_tensor(xa[:, :], P[4][:, 0:D], rows["b_down"][:, :], ALU.add))
            link(dve.tensor_tensor(xa[:, :], xa[:, :], nx.xn[:, :], ALU.add))
            link(dve.tensor_tensor(x[:, :], x[:, :], xa[:, :], ALU.add))


def more_layouts(i, out):
    import numpy as np
    w = i["L1_xattn_Wkv"]
    out["L1_xattn_wq"] = chunked(i["L1_xattn_Wq"])
    out["L1_xattn_wkT"] = chunked(w[:, :512].T, 64)
    out["L1_xattn_wv"] = chunked(w[:, 512:])
    out["L1_xattn_wo"] = chunked(i["L1_xattn_Wo"], 64)
    for n in ("ln_x_g", "ln_x_b", "ln_l_g", "ln_l_b", "ln_o_g", "ln_o_b"):
        out["L1_xattn_" + n] = i["L1_xattn_" + n]
    out["mask_bk1"] = i["mask_BxS2_bk1"][0].astype(np.int32)
    out["mask_ff1"] = i["mask_BxS2_ff1"][0].reshape(-1, 128).T
    out["mask_ik1"] = i["mask_BxSxS2_ik1"][0]
    out["L2_xattn_wq"] = chunked(i["L2_xattn_wq"])
    out["L2_xattn_wkv"] = chunked(np.concatenate([i["L2_xattn_wk"], i["L2_xattn_wv"]], 1))
    out["L2_xattn_dense_w"] = chunked(i["L2_xattn_dense_w"])
    for n in ("ln_gamma", "ln_beta", "dense_b"):
        out["L2_xattn_" + n] = i["L2_xattn_" + n]
    out["L0_attn_decay_logit"] = i["L0_attn_decay_logit"].reshape(1)
    out["L0_attn_out_scale"] = i["L0_attn_out_scale"].reshape(1)
    out["L0_attn_q_scale"] = i["L0_attn_q_scale"].reshape(DC, 128).T
    out["L0_attn_k_scale"] = i["L0_attn_k_scale"].reshape(DC, 128).T
    out["L2_attn_W_qkv"] = chunked(i["L2_attn_W_qkv"])
    out["L2_attn_W_o"] = chunked(i["L2_attn_W_o"])
    out["L3_attn_W_qkv"] = chunked(np.concatenate([i["L3_attn_W" + n].T for n in "qkv"], 1))
    out["L3_attn_b_qkv"] = np.concatenate([i["L3_attn_b" + n] for n in "qkv"])
    out["L3_attn_Wo"] = chunked(i["L3_attn_Wo"].T)
    out["L3_attn_bo"] = i["L3_attn_bo"]
    w = i["L3_ffn_W_qkv"]
    out["L3_ffn_W_kqv"] = chunked(np.concatenate([w[:, D:2 * D], w[:, :D], w[:, 2 * D:]], 1))
    out["L3_ffn_guide"] = i["L3_ffn_g_info"][0, 0]
    out["L3_ffn_W_proj"] = chunked(i["L3_ffn_W_proj"])
    out["L3_ffn_b_proj"] = i["L3_ffn_b_proj"]
    for p, w1, b1, w2, b2 in (("L1_ffn_", i["L1_ffn_W1"], i["L1_ffn_b1"], i["L1_ffn_W2"], i["L1_ffn_b2"]),
                              ("L2_ffn_", i["L2_ffn_fc1_w"].transpose(0, 2, 1), i["L2_ffn_fc1_b"][:, 0],
                               i["L2_ffn_fc2_w"], i["L2_ffn_fc2_b"][:, 0])):
        out[p + "W1"] = np.stack([chunked(w) for w in w1])
        out[p + "W2"] = np.stack([chunked(w) for w in w2])
        out[p + "b1"] = b1.reshape(-1, 128).T
        out[p + "b2"] = b2
    out["L1_ffn_wr"] = i["L1_ffn_wr"].reshape(DC, 128).T
    out["L1_ffn_br"] = i["L1_ffn_br"].reshape(1)
    out["L2_ffn_gate_w"] = chunked(i["L2_ffn_gate_w"].T)
    out["L0_ffn_router_w"] = chunked(i["L0_ffn_router_w"].T)
    for n in ("router_bias", "norm_w", "bank_phase"):
        out["L0_ffn_" + n] = i["L0_ffn_" + n]
    for n in ("mag", "freq", "down"):
        out["L0_ffn_bank_" + n] = np.stack([chunked(w) for w in i["L0_ffn_bank_" + n]])
    p = "L1_attn_"
    out[p + "W_up"] = chunked(np.concatenate([i[p + "W_up_l"].T, i[p + "W_up_r"].T], 1))
    for n in ("skip", "q", "k", "v", "o", "down"):
        out[p + "W_" + n] = chunked(i[p + "W_" + n].T)
    out[p + "W_if"] = chunked(np.concatenate([i[p + "W_i"].T, i[p + "W_f"].T], 1))
    for n in ("ln_g", "ln_b", "b_up_l", "b_up_r", "b_skip", "b_v", "b_o", "mh_g", "mh_b", "b_down", "conv_w", "conv_b"):
        out[p + n] = i[p + n].reshape(-1)
    out[p + "b_qk"] = np.stack([i[p + "b_q"].reshape(-1, 128).T, i[p + "b_k"].reshape(-1, 128).T], 1)
    out[p + "b_if"] = np.stack([i[p + "b_i"], i[p + "b_f"]], 1)


def stage_load(nc, A, x, ident):
    with Stage(nc, "load") as s:
        block = s.block()

        @block.sync
        def _(sp):
            sp.dma_start(x[:, :], A["x"]).then_inc(s.sem("x_in"), 16)
            sp.wait_ge(s.sem("x_in"), 16)

        @block.gpsimd
        def _(pool):
            pool.memset(ident[:, :], 0.0).then_inc(s.sem("zero"), 1)
            pool.wait_ge(s.sem("zero"), 1)
            pool.affine_select(out=ident[:, :], in_=ident[:, :], compare_op=ALU.not_equal, fill=1.0, base=0,
                               pattern=[[-1, 128]], channel_multiplier=1).then_inc(s.sem("ident"), 1)
            pool.wait_ge(s.sem("ident"), 1)
            hm = A["head_mask"]
            pool.memset(hm[:, :], 1.0).then_inc(s.sem("ones"), 1)
            pool.wait_ge(s.sem("ones"), 1)
            pool.affine_select(out=hm[:, :], in_=hm[:, :], compare_op=ALU.is_ge, fill=0.0, base=0,
                               pattern=[[-16, 8]], channel_multiplier=1).then_inc(s.sem("from"), 1)
            pool.wait_ge(s.sem("from"), 1)
            pool.affine_select(out=hm[:, :], in_=hm[:, :], compare_op=ALU.is_ge, fill=0.0, base=15,
                               pattern=[[16, 8]], channel_multiplier=-1).then_inc(s.sem("head_mask"), 1)
            pool.wait_ge(s.sem("head_mask"), 1)
            cm = A["causal"]
            pool.memset(cm[:, :], 1.0).then_inc(s.sem("ones2"), 1)
            pool.wait_ge(s.sem("ones2"), 1)
            pool.affine_select(out=cm[:, :], in_=cm[:, :], compare_op=ALU.is_ge, fill=0.0, base=0,
                               pattern=[[1, 128]], channel_multiplier=-1).then_inc(s.sem("causal"), 1)
            pool.iota(A["iota16"][:, :], [[1, 16]], base=0, channel_multiplier=0,
                      allow_small_or_imprecise_dtypes=True).then_inc(s.sem("iota16"), 1)
            pool.memset(A["ones"][:, :], 1.0).then_inc(s.sem("ones3"), 1)
            pool.wait_ge(s.sem("causal"), 1)
            pool.wait_ge(s.sem("iota16"), 1)
            pool.wait_ge(s.sem("ones3"), 1)


def stage_store(nc, A, x, ident):
    with Stage(nc, "store") as s:
        block = s.block()

        @block.sync
        def _(sp):
            sp.dma_start(A["out"], x[:, :]).then_inc(s.sem("x_out"), 16)
            sp.wait_ge(s.sem("x_out"), 16)


STAGES = [stage_prepare, stage_l0_xattn, stage_l0_attn, stage_l0_ffn, stage_l1_xattn, stage_l1_attn, stage_l1_ffn,
          stage_l2_xattn, stage_l2_attn, stage_l2_ffn, stage_l3_xattn, stage_l3_attn, stage_l3_ffn]


def program(nc, A, stages):
    with ExitStack() as ctx:
        x = ctx.enter_context(nc.sbuf_tensor("x", [T, D], F32))
        ident = ctx.enter_context(nc.sbuf_tensor("ident", [128, 128], F32))
        A["head_mask"] = ctx.enter_context(nc.sbuf_tensor("head_mask", [128, 8], F32))
        A["causal"] = ctx.enter_context(nc.sbuf_tensor("causal", [128, 128], F32))
        A["iota16"] = ctx.enter_context(nc.sbuf_tensor("iota16", [128, 16], F32))
        A["ones"] = ctx.enter_context(nc.sbuf_tensor("ones", [128, 128], F32))
        A["kv_sum"] = ctx.enter_context(nc.sbuf_tensor("kv_sum", [128, DC, 129], F32))
        A["xn_rows"] = nc.dram_tensor("xn_rows", (128, S2 // 128, D), F32, kind="Internal").ap()
        A["att_order"] = nc.dram_tensor("att_order", (16, T, 16), F32, kind="Internal").ap()
        A["xnT"] = nc.dram_tensor("xnT", (128, DC, S2), F32, kind="Internal").ap()
        for stage in [stage_load, *stages, stage_store]:
            stage(nc, A, x, ident)


def chunked(a, p=128):
    import numpy as np
    a = np.asarray(a)
    return np.ascontiguousarray(a.reshape(-1, p, a.shape[-1]).transpose(1, 0, 2))


def layouts(i):
    import numpy as np
    i = {k: np.asarray(v) for k, v in i.items()}
    ctx = i["ctx_1024"][0]
    out = {"x": i["x"][0], "ctx_rows": chunked(ctx), "ctxT": chunked(ctx.T)}
    w = i["L0_xattn_w_kv"]
    out["L0_xattn_wq"] = chunked(i["L0_xattn_w_q"])
    out["L0_xattn_wkT"] = chunked(w[:, :1024].T, 64)
    out["L0_xattn_wv"] = chunked(w[:, 1024:])
    out["L0_xattn_wo"] = chunked(i["L0_xattn_w_out1"], 64)
    out["L0_xattn_w_out2"] = chunked(i["L0_xattn_w_out2"])
    out["L0_xattn_gamma"] = i["L0_xattn_gamma"]
    more_layouts(i, out)
    return {k: np.ascontiguousarray(v) for k, v in out.items()}


def kernel(**inputs):
    import numpy as np
    import concourse.bacc as bacc
    from concourse.bass_utils import run_bass_kernel_spmd

    nc = bacc.Bacc("TRN2", target_bir_lowering=False, num_devices=1)
    arrays, A = {}, {}
    for name, a in layouts(inputs).items():
        arrays[f"in_{name}"] = a
        A[name] = nc.dram_tensor(f"in_{name}", a.shape, mybir.dt.from_np(a.dtype), kind="ExternalInput").ap()
    A["out"] = nc.dram_tensor("out_0", (T, D), F32, kind="ExternalOutput").ap()
    program(nc, A, STAGES)
    r = run_bass_kernel_spmd(nc, [arrays], core_ids=[0])
    return r.results[0]["out_0"].reshape(1, T, D)
```

```python
from contextlib import ExitStack

import concourse.bass as bass
from concourse import mybir

ALU = mybir.AluOpType
ACT = mybir.ActivationFunctionType
AX = mybir.AxisListType
F32 = mybir.dt.float32
I32 = mybir.dt.int32
F32R = mybir.dt.float32r

T = 128
D = 256
DC = D // 128
S2 = 12544
CH = 896
CT = CH // 128
HALF = CH // 2
NCH = S2 // CH
ARENA = 51200
FAR = -2.0 ** 100


class Stage:

    def __init__(self, nc, name, fast=0):
        self.fast, self.arena_size = fast, ARENA - fast
        self.nc, self.name, self.ctx, self.sems = nc, name, ExitStack(), {}

    def __enter__(self):
        self.ctx.__enter__()
        self.arena = self.ctx.enter_context(self.nc.sbuf_tensor(f"{self.name}_sbuf", [128, self.arena_size], F32))
        if self.fast:
            self.fast_arena = self.ctx.enter_context(self.nc.sbuf_tensor(f"{self.name}_fast", [128, self.fast], F32R))
        self.psum = self.ctx.enter_context(self.nc.psum_tensor(f"{self.name}_psum", [128, 8, 512], F32))
        self.used = self.banks = self.used_fast = 0
        return self

    def __exit__(self, *e):
        self.region.__exit__(*e)
        self.nc.clear_and_free_semaphores(list(self.sems.values()))
        self.nc.all_engine_barrier()
        return self.ctx.__exit__(*e)

    def sb(self, name, shape, dt=F32):
        n = 1
        for d in shape[1:]:
            n *= d
        if dt == F32R:
            assert self.used_fast + n <= self.fast, f"{self.name}: no room for {name}"
            v = self.fast_arena[0:shape[0], self.used_fast:self.used_fast + n]
            self.used_fast += n
        else:
            assert self.used + n <= self.arena_size, f"{self.name}: no room for {name}"
            v = self.arena[0:shape[0], self.used:self.used + n]
            self.used += n
            if dt != F32:
                v = v.bitcast(dt)
        names = "abcd"[:len(shape) - 1]
        if len(names) > 1:
            v = v.rearrange(f"p ({' '.join(names)}) -> p {' '.join(names)}", **dict(zip(names, shape[1:])))
        return v

    def ps(self, name, banks=1):
        at = self.banks
        self.banks += banks
        assert self.banks <= 8, f"{self.name}: no bank for {name}"
        return self.psum[:, at, :] if banks == 1 else self.psum[:, at:at + banks, :]

    def sem(self, name):
        if name not in self.sems:
            self.sems[name] = self.nc.alloc_semaphore(f"{self.name}_{name}")
        return self.sems[name]

    def block(self):
        self.region = self.nc.Block()
        return self.region.__enter__()


def head_start(eng, s, *names):
    for name in names:
        eng.sem_inc(s.sem(name), 1)


def linker(eng, sem, base=0):
    count = [0]

    def link(ins):
        count[0] += 1
        ins.then_inc(sem, 1)
        eng.wait_ge(sem, base + count[0])

    link.count = count
    return link


def dve_moments(dve, link, src, st, mv, eps, done):
    link(dve.bn_stats(st, src))
    link(dve.bn_aggr(mv[:, 0:2], st))
    dve.tensor_scalar(mv[:, 1:2], mv[:, 1:2], eps, None, ALU.add).then_inc(done, 1)


def dve_rsqrt(dve, link, r, root, var):
    link(dve.reciprocal(r, root))
    link(dve.tensor_tensor(root, r, r, ALU.mult))
    link(dve.tensor_tensor(root, root, var, ALU.mult))
    link(dve.tensor_scalar(root, root, -0.5, 1.5, ALU.mult, ALU.add))
    link(dve.tensor_tensor(r, r, root, ALU.mult))


def dve_rescale(dve, link, dst, src, mv, done):
    dve_rsqrt(dve, link, mv[:, 3:4], mv[:, 2:3], mv[:, 1:2])
    dve.tensor_scalar(dst, src, mv[:, 0:1], mv[:, 3:4], ALU.subtract, ALU.mult).then_inc(done, 1)
    dve.wait_ge(done, 1)


class NormX:

    def __init__(self, s, x, ident, ps):
        self.s, self.x, self.ident, self.ps = s, x, ident, ps
        self.st, self.mv = s.sb("x_st", [128, 6]), s.sb("x_mv", [128, 4])
        self.xn, self.xnT = s.sb("xn", [128, D]), s.sb("xnT", [128, DC, T])

    def dve(self, dve, link):
        s = self.s
        dve_moments(dve, link, self.x[:, :], self.st[:, :], self.mv, 1e-5, s.sem("x_var"))
        dve.wait_ge(s.sem("x_std"), 1)
        dve_rescale(dve, link, self.xn[:, :], self.x[:, :], self.mv, s.sem("xn"))
        dve.wait_ge(s.sem("xnT_ps"), 1)
        dve.tensor_copy(self.xnT[:, :, :], self.ps[:, 0:D].rearrange("p (c t) -> p c t", c=DC)).then_inc(s.sem("xnT"), 1)

    def act(self, act):
        s = self.s
        act.wait_ge(s.sem("x_var"), 1)
        act.activation(self.mv[:, 2:3], self.mv[:, 1:2], ACT.Sqrt).then_inc(s.sem("x_std"), 1)

    def pe(self, pe):
        s = self.s
        pe.wait_ge(s.sem("xn"), 1)
        for c in range(DC):
            mm = pe.transpose(self.ps[:, c * 128:(c + 1) * 128], self.xn[:, c * 128:(c + 1) * 128], self.ident[:, :])
        mm.then_inc(s.sem("xnT_ps"), 1)


class ContextAttention:

    def __init__(self, s, heads, width, qt, values, kT_dram, v_dram, ident, mask=None, mask_dram=None,
                 bias_per_one=1.0e9, tail=None, split=None):
        self.s, self.H, self.W, self.qt, self.values = s, heads, width, qt, values
        self.kT_dram, self.v_dram, self.ident = kT_dram, v_dram, ident
        self.mask, self.mask_dram, self.bias_per_one, self.tail = mask, mask_dram, bias_per_one, tail
        self.U = 2 * heads
        self.split = split
        self.kT = s.sb("ca_kT", [128, 2, 2, CH] if split == "keys" else [128, 1 if split else 2, DC, CH])
        self.v = s.sb("ca_v", [128, 1 if split == "both" else 2, CT, D])
        self.bufs = 4 if mask == "full" else 2
        self.p = s.sb("ca_p", [128, self.bufs, CH])
        if split == "keys":
            self.kT_stack = s.sb("ca_kT_stack", [128, 2, 4, CH], F32R)
        if split == "both":
            self.kT_parts = [s.sb(f"ca_kT_{i}", [128, 2, DC, CH], F32R) for i in ("high", "low")]
            self.v_parts = [s.sb(f"ca_v_{i}", [128, 2, CT, D], F32R) for i in ("high", "low")]
            self.pT_parts = [s.sb(f"ca_pT_{i}", [128, 2, CT, T], F32R) for i in ("high", "low")]
        else:
            self.pT = s.sb("ca_pT", [128, 2, CT, T])
        self.acc = s.sb("ca_acc", [128, heads, width])
        self.l = s.sb("ca_l", [128, heads])
        self.mb = s.sb("ca_mb", [128, 2])
        self.negm = s.sb("ca_negm", [128, 2, heads])
        self.alpha = s.sb("ca_alpha", [128, 8])
        self.rs = s.sb("ca_rs", [128, 8])
        if mask == "rows":
            self.raw = s.sb("ca_raw", [1, CH], I32)
            self.bias = s.sb("ca_bias", [1, 2, CH], F32R)
            self.one = s.sb("ca_one", [1, T], F32R)
        if mask == "full":
            self.raw = s.sb("ca_raw", [128, 2, CH], I32)
            self.bias = s.sb("ca_bias", [128, 2, CH])
            self.sm = s.sb("ca_sm", [128, self.bufs, CH])
        self.ps_s = [s.ps(f"ca_s{i}", 2) for i in range(2)]
        self.ps_t = s.ps("ca_t", 2).rearrange("p b (t k) -> p (b t) k", k=T)
        self.ps_o = [s.ps(f"ca_o{i}") for i in range(2)]
        self.max_lag = 1 if mask == "full" else 0
        self.t_lag, self.v_lag, self.acc_lag = (self.max_lag + i for i in (2, 3, 4))
        self.pre = heads if tail else 0

    def load_split(self, sp, chunk):
        loads = [("kT", self.kT[:, 0, :, :], self.kT_dram[:, :, bass.ds(chunk * CH, CH)]),
                 ("v", self.v[:, 0, :, :], self.v_dram[:, bass.ds(chunk * CT, CT), :])]
        if self.mask:
            loads.append(("bias", self.raw[:, :], self.mask_dram[:, bass.ds(chunk * CH, CH)]))
        for name, dst, src in loads:
            self.wait(sp, name if name == "bias" else name + "_low", chunk, 0)
            sp.dma_start(dst, src).then_inc(self.s.sem(name + "_in"), 16)

    def load_keys(self, sp, chunk):
        self.wait(sp, "kT_low", chunk, 0)
        for half in range(2):
            for i in range(2):
                sp.dma_start(self.kT[64 * half:64 * half + 64, i, :, :],
                             self.kT_dram[64 * i:64 * i + 64, :, bass.ds(chunk * CH, CH)]).then_inc(self.s.sem("kT_in"), 16)

    def load_half(self, sp, j, chunk):
        s = self.s
        sp.dma_start(self.v[:, j, :, :], self.v_dram[:, bass.ds(chunk * CT, CT), :]).then_inc(s.sem(f"kv_in{j}"), 16)
        sp.dma_start(self.raw[:, j, :], self.mask_dram[:, bass.ds(chunk * CH, CH)]).then_inc(s.sem(f"kv_in{j}"), 16)

    def load(self, sp, j, chunk):
        s = self.s
        sp.dma_start(self.kT[:, j, :, :], self.kT_dram[:, :, bass.ds(chunk * CH, CH)]).then_inc(s.sem(f"kv_in{j}"), 16)
        sp.dma_start(self.v[:, j, :, :], self.v_dram[:, bass.ds(chunk * CT, CT), :]).then_inc(s.sem(f"kv_in{j}"), 16)
        if self.mask:
            sp.dma_start(self.raw[:, j, :], self.mask_dram[:, bass.ds(chunk * CH, CH)]).then_inc(s.sem(f"kv_in{j}"), 16)

    def sp(self, sp):
        s, H, U = self.s, self.H, self.U
        if self.split == "keys":
            self.load_keys(sp, 0)
            self.load_half(sp, 0, 0)
            self.load_half(sp, 1, 1)
            with sp.Fori(0, NCH // 2 - 1) as it:
                for j in range(2):
                    self.load_keys(sp, it * 2 + (j + 1))
                    sp.wait_ge(s.sem("pv"), it * U + (self.pre + H * (j + 1)))
                    sp.wait_ge(s.sem("bias"), it * 2 + (j + 1))
                    self.load_half(sp, j, it * 2 + (2 + j))
            self.load_keys(sp, NCH - 1)
            return
        if self.split:
            self.load_split(sp, 0)
            with sp.Fori(1, NCH) as it:
                self.load_split(sp, it)
            return
        self.load(sp, 0, 0)
        self.load(sp, 1, 1)
        with sp.Fori(0, NCH // 2 - 1) as it:
            for j in range(2):
                sp.wait_ge(s.sem("pv"), it * U + (self.pre + H * (j + 1)))
                if self.mask:
                    sp.wait_ge(s.sem("bias"), it * 2 + (j + 1))
                self.load(sp, j, it * 2 + (2 + j))

    def chunk(self, j, loads, number):
        return [(h, j, loads, number) for h in range(self.H)]

    def run(self, eng, step):
        def steps(base, before, units, more=0):
            def unit(u):
                return units[u] if 0 <= u < len(units) else before[u] if u < 0 and before else None

            for k in range(len(units) + more):
                step(eng, base, k, unit)

        H, pre = self.H, self.pre
        even = self.chunk(0, 1, 0)
        steps(0, [], [(h, None, 0, -1) for h in range(pre)] + even)
        with eng.Fori(0, NCH // 2 - 1) as it:
            steps(it * self.U + (pre + H), even, self.chunk(1, it + 1, it * 2 + 1) + self.chunk(0, it + 2, it * 2 + 2))
        steps(pre + (NCH - 1) * H, even, self.chunk(1, NCH // 2, NCH - 1), self.acc_lag)

    def wait(self, eng, name, base, off):
        if not isinstance(base, int) or base + off > 0:
            eng.wait_ge(self.s.sem(name), base + off)

    def wait_chunk(self, eng, j, loads):
        eng.wait_ge(self.s.sem(f"kv_in{j}"), loads * (48 if self.mask and not self.split else 32))

    def products(self, pe, out, pairs):
        terms = [(x, y) for a, b in pairs for i, x in enumerate(a) for k, y in enumerate(b) if i + k < 2]
        for n, (x, y) in enumerate(terms):
            mm = pe.matmul(out, x, y, start=(n == 0), stop=(n == len(terms) - 1))
        return mm

    def pe_scores(self, pe, base, u, h, j):
        b = u % 2
        self.wait(pe, "masked" if self.mask == "full" else "p", base, u - 1)
        for i in range(2 if j is not None else 1):
            cut = slice(i * HALF, (i + 1) * HALF)
            pairs = []
            for q, c in self.qt(h):
                if j is None:
                    pairs.append((q, [k[:, c, :] for k in self.tail[0]]))
                elif self.split == "keys":
                    pairs.append((q, [self.kT_stack[:, j, c, cut]]))
                else:
                    pairs.append((q, [k[:, j, c, cut] for k in (self.kT_parts if self.split else [self.kT])]))
            if self.mask == "rows" and j is not None:
                pairs.append(([self.one[:, :]], [self.bias[:, j, cut]]))
            mm = self.products(pe, self.ps_s[b][:, i, 0:HALF if j is not None else T], pairs)
        mm.then_inc(self.s.sem("scores"), 1)

    def pe_transposes(self, pe, base, u, j):
        self.wait(pe, "p", base, u + 1)
        self.wait(pe, "pT_low" if self.split == "both" else "pT", base, u)
        for t in range(CT if j is not None else 1):
            mm = pe.transpose(self.ps_t[:, t, :], self.p[:, u % self.bufs, t * 128:(t + 1) * 128], self.ident[:, :])
        mm.then_inc(self.s.sem("pT_ps"), 1)

    def pe_values(self, pe, base, u, h, j):
        b = u % 2
        self.wait(pe, "pT_low" if self.split == "both" else "pT", base, u + 1)
        self.wait(pe, "acc", base, u - 1)
        lo, hi = self.values(h)
        pairs = []
        for t in range(CT if j is not None else 1):
            w = [p[:, b, t, :] for p in (self.pT_parts if self.split == "both" else [self.pT])]
            if j is None:
                pairs.append((w, [v[:, lo:hi] for v in self.tail[1]]))
            else:
                pairs.append((w, [v[:, j, t, lo:hi] for v in (self.v_parts if self.split == "both" else [self.v])]))
        self.products(pe, self.ps_o[b][:, 0:self.W], pairs).then_inc(self.s.sem("pv"), 1)

    def pe_step(self, pe, base, k, unit):
        s = self.s
        if unit(k):
            h, j, loads, number = unit(k)
            if h == 0 and j is not None:
                if self.split:
                    pe.wait_ge(s.sem("kT_low"), number + 1)
                    if self.mask == "rows":
                        pe.wait_ge(s.sem("bias"), number + 1)
                if self.split != "both":
                    self.wait_chunk(pe, j, loads)
            self.pe_scores(pe, base, k, h, j)
        u = k - self.t_lag
        if unit(u):
            self.pe_transposes(pe, base, u, unit(u)[1])
        u = k - self.v_lag
        if unit(u):
            h, j, loads, number = unit(u)
            if self.split == "both" and h == 0 and j is not None:
                pe.wait_ge(s.sem("v_low"), number + 1)
            self.pe_values(pe, base, u, h, j)

    def pe(self, pe):
        if self.mask == "rows":
            pe.wait_ge(self.s.sem("one"), 1)
        self.run(pe, self.pe_step)

    def act_step(self, act, base, k, unit):
        s = self.s
        u = k - self.t_lag
        if unit(u):
            n = CT if unit(u)[1] is not None else 1
            self.wait(act, "pT_ps", base, u + 1)
            self.wait(act, "pv", base, u - 1)
            dst = self.pT_parts[0] if self.split == "both" else self.pT
            act.activation(dst[:, u % 2, 0:n, :], self.ps_t[:, 0:n, :], ACT.Copy).then_inc(s.sem("pT"), 1)
        u = k - self.max_lag
        if unit(u):
            h, j, _, _ = unit(u)
            q = u % 8
            self.wait(act, "new_max", base, u + 1)
            self.wait(act, "sums", base, u - 7)
            self.wait(act, "acc", base, u - 7)
            old, new = (1, 0) if j is None else (j, 1 - j)
            negm = self.negm[:, new, h:h + 1]
            act.activation(self.alpha[:, q:q + 1], self.negm[:, old, h:h + 1], ACT.Exp, bias=negm, scale=-1.0)
            self.wait(act, "pT_ps", base, u - self.bufs + 1)
            p = self.p[:, u % self.bufs, :]
            if j is None:
                src, dst = self.ps_s[u % 2][:, 0, 0:T], p[:, 0:T]
            elif self.mask == "full":
                src, dst = self.sm[:, u % self.bufs, :], p
            else:
                src, dst = self.ps_s[u % 2][:, :, 0:HALF], p.rearrange("p (i c) -> p i c", i=2)
            act.activation(dst, src, ACT.Exp, bias=negm, accum_out=self.rs[:, q:q + 1]).then_inc(s.sem("p"), 1)
        following = self.following(unit(k))
        if following:
            self.wait(act, "pv", base, k - unit(k)[0])
            self.act_high(act, *following, unit(k)[0] - self.H // 2)

    def act_high(self, act, name, j, number, part):
        n = 64 if self.split == "keys" else 16
        act.wait_ge(self.s.sem(name + "_in"), number * n + n)
        raw, (high, low) = self.parts(name, j)
        if self.split == "keys":
            raw, high = raw[:, part, :], high[:, part, :]
        act.activation(high, raw, ACT.Copy).then_inc(self.s.sem(name + "_high"), 1)

    def act(self, act):
        if self.split:
            for part in range(4 if self.split == "keys" else 2):
                self.act_high(act, self.cut_names[part % len(self.cut_names)], 0, 0, part)
        self.run(act, self.act_step)

    def dve_step(self, dve, base, k, unit):
        s = self.s
        if unit(k) and self.mask == "full" and unit(k)[1] is not None:
            h, j, loads, number = unit(k)
            if h == 0:
                self.wait_chunk(dve, j, loads)
                dve.tensor_scalar(self.bias[:, j, :], self.raw[:, j, :], 1.0, self.bias_per_one,
                                  ALU.subtract, ALU.mult).then_inc(s.sem("bias"), 1)
                dve.wait_ge(s.sem("bias"), number + 1)
            self.wait(dve, "scores", base, k + 1)
            self.wait(dve, "p", base, k - self.bufs + 1)
            dve.tensor_tensor(self.sm[:, k % self.bufs, :].rearrange("p (i c) -> p i c", i=2),
                              self.ps_s[k % 2][:, :, 0:HALF],
                              self.bias[:, j, :].rearrange("p (i c) -> p i c", i=2),
                              ALU.add).then_inc(s.sem("masked"), 1)
        m = k - self.max_lag
        if unit(m):
            j = unit(m)[1]
            if j is None:
                self.wait(dve, "scores", base, m + 1)
                src = self.ps_s[m % 2][:, 0, 0:T]
            elif self.mask == "full":
                self.wait(dve, "masked", base, m + 1)
                src = self.sm[:, m % self.bufs, :]
            else:
                self.wait(dve, "scores", base, m + 1)
                src = self.ps_s[m % 2][:, :, 0:HALF]
            dve.tensor_reduce(self.mb[:, m % 2:m % 2 + 1], src, AX.XY if len(src.shape) == 3 else AX.X,
                              ALU.max).then_inc(s.sem("unit_max"), 1)
        w = k - self.acc_lag
        if unit(w):
            self.dve_update(dve, base, w, unit(w)[0])
        if unit(m):
            h, j, _, _ = unit(m)
            old, new = (1, 0) if j is None else (j, 1 - j)
            self.wait(dve, "unit_max", base, m + 1)
            self.wait(dve, "p", base, m - 3)
            dve.scalar_tensor_tensor(out=self.negm[:, new, h:h + 1], in0=self.mb[:, m % 2:m % 2 + 1], scalar=-1.0,
                                     in1=self.negm[:, old, h:h + 1], op0=ALU.mult,
                                     op1=ALU.min).then_inc(s.sem("new_max"), 1)
        u = k - self.t_lag
        if self.split == "both" and unit(u):
            n = CT if unit(u)[1] is not None else 1
            self.wait(dve, "pT", base, u + 1)
            high, low = (p[:, u % 2, 0:n, :] for p in self.pT_parts)
            dve.tensor_tensor(low, self.ps_t[:, 0:n, :], high.bitcast(F32), ALU.subtract).then_inc(s.sem("pT_low"), 1)
        following = self.following(unit(k))
        if following and following[0] == "v" and self.mask == "rows":
            self.wait(dve, "scores", base, k - unit(k)[0])
            self.dve_bias(dve, following[1], following[2])

    def dve_bias(self, dve, j, number):
        dve.wait_ge(self.s.sem("bias_in"), number * 16 + 16)
        dve.tensor_scalar(self.bias[:, j, :], self.raw[:, :], 1.0, self.bias_per_one,
                          ALU.subtract, ALU.mult).then_inc(self.s.sem("bias"), 1)

    def following(self, unit):
        if not self.split or not unit or unit[1] is None:
            return None
        if unit[0] - self.H // 2 not in range(4 if self.split == "keys" else 2):
            return None
        h, j, loads, number = unit
        if isinstance(number, int) and number == NCH - 1:
            return None
        return "v" if self.split == "both" and h > self.H // 2 else "kT", 1 - j, number + 1

    @property
    def cut_names(self):
        return ("kT",) if self.split == "keys" else ("kT", "v")

    def parts(self, name, j):
        if self.split == "keys":
            stack = self.kT_stack[:, j, :, :]
            return self.kT[:, :, :, :].rearrange("p i c k -> p (i c) k"), (stack, stack)
        raw, parts = (self.kT, self.kT_parts) if name == "kT" else (self.v, self.v_parts)
        return raw[:, 0, :, :], [p[:, j, :, :] for p in parts]

    def pool_low(self, pool, name, j, number):
        raw, (high, low) = self.parts(name, j)
        n = 4 if self.split == "keys" else 1
        pool.wait_ge(self.s.sem(name + "_high"), number * n + n)
        if self.split == "keys":
            raw, high, low = raw[64:128], high[64:128], low[64:128]
        pool.tensor_tensor(low, raw, high.bitcast(F32), ALU.subtract).then_inc(self.s.sem(name + "_low"), 1)

    def pool(self, pool):
        for name in self.cut_names:
            self.pool_low(pool, name, 0, 0)
        with pool.Fori(0, NCH // 2 - 1) as it:
            for j in (1, 0):
                for name in self.cut_names:
                    self.pool_low(pool, name, j, it * 2 + (2 - j))
        for name in self.cut_names:
            self.pool_low(pool, name, 1, NCH - 1)

    def dve_update(self, dve, base, u, h):
        s, q = self.s, u % 8
        self.wait(dve, "pv", base, u + 1)
        self.wait(dve, "p", base, u + 1)
        self.wait(dve, "sums", base, u)
        dve.scalar_tensor_tensor(out=self.l[:, h:h + 1], in0=self.l[:, h:h + 1],
                                 scalar=self.alpha[:, q:q + 1], in1=self.rs[:, q:q + 1],
                                 op0=ALU.mult, op1=ALU.add).then_inc(s.sem("sums"), 1)
        self.wait(dve, "acc", base, u)
        dve.scalar_tensor_tensor(out=self.acc[:, h, :], in0=self.acc[:, h, :],
                                 scalar=self.alpha[:, q:q + 1], in1=self.ps_o[u % 2][:, 0:self.W],
                                 op0=ALU.mult, op1=ALU.add).then_inc(s.sem("acc"), 1)

    def dve(self, dve):
        s = self.s
        link = linker(dve, s.sem("dve_init"))
        link(dve.memset(self.acc[:, :, :], 0.0))
        link(dve.memset(self.l[:, :], 0.0))
        link(dve.memset(self.negm[:, :, :], -FAR))
        if self.mask == "rows":
            dve.tensor_scalar(self.one[:, :], self.ident[0:1, 0:T], 0.0, 1.0, ALU.mult, ALU.add).then_inc(s.sem("one"), 1)
            self.dve_bias(dve, 0, 0)
        self.run(dve, self.dve_step)
        dve.wait_ge(s.sem("sums"), NCH * self.H + self.pre)
        dve.wait_ge(s.sem("acc"), NCH * self.H + self.pre)
        link = linker(dve, s.sem("dve_end"))
        link(dve.reciprocal(self.l[:, :], self.l[:, :]))
        for h in range(self.H):
            dve.tensor_scalar(self.acc[:, h, :], self.acc[:, h, :], self.l[:, h:h + 1], None,
                              ALU.mult).then_inc(s.sem("attended"), 1)


def cols(ps, c=DC):
    return ps[:, 0:c * 128].rearrange("p (c t) -> p c t", c=c)


def finish(eng, ins, sem, n=1):
    ins.then_inc(sem, 1)
    eng.wait_ge(sem, n)


def pe_transposes(pe, ps, src, ident, n=DC):
    for c in range(n):
        mm = pe.transpose(ps[:, c * 128:(c + 1) * 128], src[:, c * 128:(c + 1) * 128], ident[:, :])
    return mm


def pe_dense(pe, out, lhsT, rhs, n=DC):
    for c in range(n):
        mm = pe.matmul(out, lhsT(c), rhs(c), start=(c == 0), stop=(c == n - 1))
    return mm


class WideHeads:

    HD = 64

    def __init__(self, s, H, A, prefix, ident, scale):
        self.s, self.H, self.A, self.prefix, self.ident, self.scale = s, H, A, prefix, ident, scale
        HD = self.HD
        self.wq, self.wkT = s.sb("wq", [128, DC, H * HD]), s.sb("wkT", [HD, H, D])
        self.wv, self.wo = self.wq, self.wkT
        self.qT = s.sb("qT", [HD, H, T])
        self.qk = [s.sb(f"qk_{i}", [128, H, DC, T], F32R) for i in ("high", "low")]
        self.aT, self.oT = s.sb("aT", [128, 2, DC, T]), s.sb("oT", [HD, 2, T])

    def qt(self, h):
        return [([q[:, h, c, :] for q in self.qk], c) for c in range(DC)]

    def use(self, ca, nxT, nxT_sem):
        self.ca, self.nxT, self.nxT_sem = ca, nxT, nxT_sem
        self.banks = [ca.ps_o[1], ca.ps_o[0]]

    def sp(self, sp):
        for name, dst in (("wq", self.wq), ("wkT", self.wkT)):
            sp.dma_start(dst[:, :, :], self.A[self.prefix + name]).then_inc(self.s.sem(name + "_in"), 16)

    def sp_outputs(self, sp):
        sp.wait_ge(self.s.sem("qk_ps"), self.H // 2)
        for name, dst in (("wv", self.wv), ("wo", self.wo)):
            sp.dma_start(dst[:, :, :], self.A[self.prefix + name]).then_inc(self.s.sem(name + "_in"), 16)

    def pe_queries(self, pe):
        s, H, HD = self.s, self.H, self.HD
        pe.wait_ge(s.sem("wq_in"), 16)
        pe.wait_ge(self.nxT_sem, 1)
        for g in range(H // 4):
            if g >= 2:
                pe.wait_ge(s.sem("qT"), g - 1)
            for h in range(4 * g, 4 * g + 4):
                mm = pe_dense(pe, self.banks[g % 2][0:HD, (h % 4) * T:(h % 4 + 1) * T],
                              lambda c: self.wq[:, c, h * HD:(h + 1) * HD], lambda c: self.nxT[:, c, :])
            mm.then_inc(s.sem("qT_ps"), 1)
        pe.wait_ge(s.sem("wkT_in"), 16)
        pe.wait_ge(s.sem("qT"), H // 4)
        for g in range(H // 2):
            if g >= 2:
                pe.wait_ge(s.sem("qk_low"), g - 1)
            for h in range(2 * g, 2 * g + 2):
                for c in range(DC):
                    k = (h % 2) * DC + c
                    mm = pe.matmul(self.banks[g % 2][:, k * T:(k + 1) * T], self.wkT[:, h, c * 128:(c + 1) * 128],
                                   self.qT[:, h, :], start=True, stop=True)
            mm.then_inc(s.sem("qk_ps"), 1)
        pe.wait_ge(s.sem("qk_low"), H // 2)

    def dve_queries(self, dve):
        s, HD = self.s, self.HD
        for g in range(self.H // 4):
            dve.wait_ge(s.sem("qT_ps"), g + 1)
            dve.tensor_scalar(self.qT[:, 4 * g:4 * g + 4, :],
                              self.banks[g % 2][0:HD, :].rearrange("p (h t) -> p h t", h=4),
                              self.scale, None, ALU.mult).then_inc(s.sem("qT"), 1)
        for g in range(self.H // 2):
            high, low = (q[:, 2 * g:2 * g + 2, :, :] for q in self.qk)
            dve.wait_ge(s.sem("qk"), g + 1)
            dve.tensor_tensor(low, self.banks[g % 2][:, :].rearrange("p (h c t) -> p h c t", h=2, c=DC),
                              high.bitcast(F32), ALU.subtract).then_inc(s.sem("qk_low"), 1)

    def act_queries(self, act):
        s = self.s
        for g in range(self.H // 2):
            act.wait_ge(s.sem("qk_ps"), g + 1)
            act.activation(self.qk[0][:, 2 * g:2 * g + 2, :, :],
                           self.banks[g % 2][:, :].rearrange("p (h c t) -> p h c t", h=2, c=DC),
                           ACT.Copy).then_inc(s.sem("qk"), 1)

    def pe_outputs(self, pe, ps):
        s, H, HD, ca = self.s, self.H, self.HD, self.ca
        pe.wait_ge(s.sem("wv_in"), 16)
        pe.wait_ge(s.sem("wo_in"), 16)
        for h in range(H + 2):
            if h < H:
                pe.wait_ge(s.sem("attended"), h + 1)
                if h >= 2:
                    pe.wait_ge(s.sem("aT"), h - 1)
                pe_transposes(pe, ca.ps_s[h % 2][:, 0, :], ca.acc[:, h, :], self.ident).then_inc(s.sem("aT_ps"), 1)
            if 1 <= h <= H:
                g = h - 1
                pe.wait_ge(s.sem("aT"), g + 1)
                if g >= 2:
                    pe.wait_ge(s.sem("oT"), g - 1)
                pe_dense(pe, ca.ps_s[g % 2][0:HD, 1, 0:T], lambda c: self.wv[:, c, g * HD:(g + 1) * HD],
                         lambda c: self.aT[:, g % 2, c, :]).then_inc(s.sem("oT_ps"), 1)
            if h >= 2:
                g = h - 2
                pe.wait_ge(s.sem("oT"), g + 1)
                pe.matmul(ps[:, 0:D], self.oT[:, g % 2, :], self.wo[:, g, :], start=(g == 0),
                          stop=(g == H - 1)).then_inc(s.sem("out_ps"), 1)

    def dve_outputs(self, dve):
        s = self.s
        for h in range(self.H):
            dve.wait_ge(s.sem("aT_ps"), h + 1)
            if h >= 2:
                dve.wait_ge(s.sem("oT_ps"), h - 1)
            dve.tensor_copy(self.aT[:, h % 2, :, :], cols(self.ca.ps_s[h % 2][:, 0, :])).then_inc(s.sem("aT"), 1)

    def act_outputs(self, act):
        s = self.s
        for h in range(self.H):
            act.wait_ge(s.sem("oT_ps"), h + 1)
            if h >= 2:
                act.wait_ge(s.sem("out_ps"), h - 1)
            act.activation(self.oT[:, h % 2, :], self.ca.ps_s[h % 2][0:self.HD, 1, 0:T],
                           ACT.Copy).then_inc(s.sem("oT"), 1)


class RowNorm:

    def __init__(self, s, name, eps):
        self.s, self.name, self.eps = s, name, eps
        self.st, self.mv = s.sb(name + "_st", [128, 6]), s.sb(name + "_mv", [128, 4])

    def dve(self, dve, link, dst, src):
        s = self.s
        dve_moments(dve, link, src, self.st[:, :], self.mv, self.eps, s.sem(self.name + "_var"))
        dve.wait_ge(s.sem(self.name + "_std"), 1)
        dve_rescale(dve, link, dst, src, self.mv, s.sem(self.name))

    def act(self, act):
        act.wait_ge(self.s.sem(self.name + "_var"), 1)
        act.activation(self.mv[:, 2:3], self.mv[:, 1:2], ACT.Sqrt).then_inc(self.s.sem(self.name + "_std"), 1)


def load_rows(sp, s, A, rows):
    for name, dst, src in rows:
        sp.dma_start(dst[:, :], A[src].partition_broadcast(128)).then_inc(s.sem(name + "_in"), 16)


def stage_l0_xattn(nc, A, x, ident):
    H = 16
    with Stage(nc, "l0x", fast=2 * (2 * DC * CH + 2 * CT * D + 2 * CT * T + H * DC * T)) as s:
        heads = WideHeads(s, H, A, "L0_xattn_", ident, WideHeads.HD ** -0.5)
        ca = ContextAttention(s, H, D, heads.qt, lambda h: (0, D), A["ctxT"], A["ctx_rows"], ident, split="both")
        wo2, gam = s.sb("wo2", [128, DC, D]), s.sb("gamma", [128, D])
        h1, h1T, y = s.sb("h1", [128, D]), s.sb("h1T", [128, DC, T]), s.sb("y", [128, D])
        ps_a, ps_b = ca.ps_o[0], ca.ps_o[1]
        nx, ny = NormX(s, x, ident, ps_a), RowNorm(s, "y", 1e-5)
        heads.use(ca, nx.xnT, s.sem("xnT"))
        block = s.block()

        @block.sync
        def _(sp):
            heads.sp(sp)
            sp.dma_start(wo2[:, :, :], A["L0_xattn_w_out2"]).then_inc(s.sem("wo2_in"), 16)
            load_rows(sp, s, A, [("gamma", gam, "L0_xattn_gamma")])
            ca.sp(sp)
            heads.sp_outputs(sp)

        @block.tensor
        def _(pe):
            nx.pe(pe)
            heads.pe_queries(pe)
            ca.pe(pe)
            heads.pe_outputs(pe, ps_a)
            pe.wait_ge(s.sem("h1"), 1)
            pe_transposes(pe, ps_b, h1, ident).then_inc(s.sem("h1T_ps"), 1)
            pe.wait_ge(s.sem("wo2_in"), 16)
            pe.wait_ge(s.sem("h1T"), 1)
            pe_dense(pe, ps_a[:, 0:D], lambda c: h1T[:, c, :], lambda c: wo2[:, c, :]).then_inc(s.sem("y_ps"), 1)

        @block.scalar
        def _(act):
            nx.act(act)
            heads.act_queries(act)
            ca.act(act)
            heads.act_outputs(act)
            ny.act(act)

        @block.gpsimd
        def _(pool):
            ca.pool(pool)

        @block.vector
        def _(dve):
            link = linker(dve, s.sem("dve_steps"))
            nx.dve(dve, link)
            heads.dve_queries(dve)
            ca.dve(dve)
            heads.dve_outputs(dve)
            dve.wait_ge(s.sem("out_ps"), H)
            dve.tensor_scalar(h1[:, :], ps_a[:, 0:D], 0.0, None, ALU.max).then_inc(s.sem("h1"), 1)
            dve.wait_ge(s.sem("h1T_ps"), 1)
            dve.tensor_copy(h1T[:, :, :], cols(ps_b)).then_inc(s.sem("h1T"), 1)
            dve.wait_ge(s.sem("y_ps"), 1)
            ny.dve(dve, link, y[:, :], ps_a[:, 0:D])
            dve.wait_ge(s.sem("gamma_in"), 16)
            link(dve.tensor_tensor(y[:, :], y[:, :], gam[:, :], ALU.mult))
            link(dve.tensor_tensor(x[:, :], x[:, :], y[:, :], ALU.add))


def stage_prepare(nc, A, x, ident):
    NT = S2 // 128
    AHEAD = 4
    W = 130
    with Stage(nc, "prep") as s:
        rows, cT = s.sb("rows", [128, AHEAD, D]), s.sb("cT", [128, AHEAD, DC, 128])
        wkv = s.sb("wkv", [128, DC, 2 * D])
        g1, b1 = s.sb("g1", [128, D]), s.sb("b1", [128, D])
        g2, b2 = s.sb("g2", [128, D]), s.sb("b2", [128, D])
        mask, eps, one = s.sb("mask", [128, NT]), s.sb("eps", [128, 3]), s.sb("one", [128, DC])
        st, mv = s.sb("st", [128, 2, 3, 6]), s.sb("mv", [128, 2, 3, 2])
        std, tmp = s.sb("std", [128, 2, 3]), s.sb("tmp", [128, 2, 3])
        norm = s.sb("norm", [128, 2, 9])
        vm = s.sb("vm", [128, 2, 3])
        xh, xn, xnT = s.sb("xh", [128, 2, D]), s.sb("xn", [128, AHEAD, D]), s.sb("xnT", [128, 2, DC, 128])
        kc, vraw = s.sb("kc", [128, 2, D]), s.sb("vraw", [128, AHEAD, D])
        kp, vp = s.sb("kp", [128, AHEAD, D]), s.sb("vp", [128, AHEAD, DC, W])
        zero, beta = s.sb("zero", [128, DC * W]), s.sb("beta", [128, D])
        ps_k, ps_v, ps_t = ([s.ps(f"{n}{j}") for j in range(2)] for n in "kvt")
        ps_sum = s.ps("sum")
        block = s.block()

        def wait(eng, name, count):
            if not isinstance(count, int) or count > 0:
                eng.wait_ge(s.sem(name), count)

        def exists(n):
            return not isinstance(n, int) or 0 <= n < NT

        def steps(eng, step):
            first = 5
            loops = (NT - 2 - first) // AHEAD
            for n in range(-1, first):
                step(n, n % AHEAD)
            with eng.Fori(0, loops) as it:
                for d in range(first, first + AHEAD):
                    step(it * AHEAD + d, d % AHEAD)
            for n in range(first + loops * AHEAD, NT + 2):
                step(n, n % AHEAD)

        def loaded(n, i):
            return (n - i) * (32 // AHEAD) + 32

        @block.sync
        def _(sp):
            def load(j, tile):
                sp.dma_start(rows[:, j, :], A["ctx_rows"][:, bass.ds(tile, 1), :]).then_inc(s.sem(f"ctx_in{j}"), 16)
                sp.dma_start(cT[:, j, :, :], A["ctxT"][:, :, bass.ds(tile * 128, 128)]).then_inc(s.sem(f"ctx_in{j}"), 16)

            load(0, 0)
            sp.dma_start(wkv[:, :, :], A["L2_xattn_wkv"]).then_inc(s.sem("wkv_in"), 16)
            for j in range(1, AHEAD):
                load(j, j)
            for name, dst, src in (("g1", g1, "L1_xattn_ln_x_g"), ("b1", b1, "L1_xattn_ln_x_b"),
                                   ("g2", g2, "L2_xattn_ln_gamma"), ("b2", b2, "L2_xattn_ln_beta")):
                sp.dma_start(dst[:, :], A[src].partition_broadcast(128)).then_inc(s.sem("gb_in"), 16)
            sp.dma_start(mask[:, :], A["mask_ff1"]).then_inc(s.sem("gb_in"), 16)

            def reload(j, tile):
                sp.wait_ge(s.sem("v_ps"), tile - AHEAD + 1)
                sp.wait_ge(s.sem("xhat"), tile - AHEAD + 1)
                load(j, tile)

            with sp.Fori(0, NT // AHEAD - 1) as it:
                for j in range(AHEAD):
                    reload(j, it * AHEAD + (AHEAD + j))
            for tile in range(NT // AHEAD * AHEAD, NT):
                reload(tile % AHEAD, tile)

        @block.tensor
        def _(pe):
            def project(n, i):
                j = i % 2
                pe.wait_ge(s.sem(f"ctx_in{i}"), loaded(n, i))
                wait(pe, "k_centered", n - 1)
                pe_dense(pe, ps_k[j][:, 0:D], lambda c: cT[:, i, c, :], lambda c: wkv[:, c, 0:D]).then_inc(s.sem("k_ps"), 1)
                wait(pe, "v_copied", n - 1)
                pe_dense(pe, ps_v[j][:, 0:D], lambda c: cT[:, i, c, :], lambda c: wkv[:, c, D:2 * D]).then_inc(s.sem("v_ps"), 1)

            def collect(n, i):
                wait(pe, "xn", n + 1)
                wait(pe, "xnT", n - 1)
                pe_transposes(pe, ps_t[i % 2], xn[:, i, :], ident).then_inc(s.sem("xnT_ps"), 1)
                wait(pe, "kp", n + 1)
                for c in range(DC):
                    mm = pe.matmul(ps_sum[:, c * W:(c + 1) * W], kp[:, i, c * 128:(c + 1) * 128],
                                   vp[:, i, c, :], start=False, stop=False, skip_group_check=True)
                mm.then_inc(s.sem("sum_ps"), 1)

            def step(n, i):
                if exists(n + 2):
                    project(n + 2, (i + 2) % AHEAD)
                if exists(n - 2):
                    collect(n - 2, (i + 2) % AHEAD)

            pe.wait_ge(s.sem("zero"), 1)
            pe.matmul(ps_sum[:, 0:DC * W], zero[:, 0:128], zero[:, :], start=True, stop=False, skip_group_check=True)
            pe.wait_ge(s.sem("wkv_in"), 16)
            project(0, 0)
            steps(pe, step)
            pe.matmul(ps_sum[:, 0:DC * W], zero[:, 0:128], zero[:, :], start=False, stop=True,
                      skip_group_check=True).then_inc(s.sem("all_ps"), 1)

        @block.scalar
        def _(act):
            def copy_v(n, i):
                wait(act, "v_ps", n + 1)
                wait(act, "vp", n - 3)
                act.activation(vraw[:, i, :], ps_v[i % 2][:, 0:D], ACT.Copy).then_inc(s.sem("v_copied"), 1)

            def step(n, i):
                j = i % 2
                k = 1 - j
                if exists(n + 1):
                    wait(act, "var", n + 2)
                    act.activation(std[:, k, :], mv[:, k, :, 1], ACT.Sqrt).then_inc(s.sem("std"), 1)
                if exists(n + 2):
                    copy_v(n + 2, (i + 2) % AHEAD)
                if exists(n):
                    wait(act, "norm", n + 1)
                    wait(act, "xn", n - 1)
                    act.activation(xh[:, j, :], rows[:, i, :], ACT.Identity, scale=norm[:, j, 0:1],
                                   bias=norm[:, j, 3:4]).then_inc(s.sem("xhat"), 1)
                    wait(act, "vm", n + 1)
                    wait(act, "sum_ps", n - 3)
                    act.activation(vp[:, i, :, 0:128], vraw[:, i, :].rearrange("p (c e) -> p c e", c=DC), ACT.Identity,
                                   scale=vm[:, j, 0:1], bias=vm[:, j, 1:2]).then_inc(s.sem("vp"), 1)
                    act.activation(vp[:, i, :, 129], one[:, :], ACT.Copy, scale=vm[:, j, 2:3]).then_inc(s.sem("vp_mask"), 1)
                    wait(act, "k_pos", n + 1)
                    act.activation(kp[:, i, :], kc[:, j, :], ACT.Copy, scale=vm[:, j, 2:3]).then_inc(s.sem("kp"), 1)
                if exists(n - 2):
                    wait(act, "xnT_ps", n - 1)
                    wait(act, f"stored{j}", 16 * (n - 2 - j))
                    act.activation(xnT[:, j, :, :], cols(ps_t[j]), ACT.Copy).then_inc(s.sem("xnT"), 1)
                    wait(act, "xnT", n - 1)
                    act.dma_start(A["xnT"][:, :, bass.ds((n - 2) * 128, 128)], xnT[:, j, :, :]).then_inc(s.sem(f"stored{j}"), 16)
                    act.dma_start(A["xn_rows"][:, bass.ds(n - 2, 1), :], xn[:, (i + 2) % AHEAD, :]).then_inc(s.sem(f"stored{j}"), 16)

            act.wait_ge(s.sem("ones"), 3)
            copy_v(0, 0)
            steps(act, step)
            for j in range(2):
                act.wait_ge(s.sem(f"stored{j}"), NT // 2 * 32)

        @block.vector
        def _(dve):
            dve.memset(zero[:, :], 0.0).then_inc(s.sem("zero"), 1)
            dve.memset(vp[:, :, :, 128:129], 1.0).then_inc(s.sem("ones"), 1)
            dve.memset(one[:, :], 1.0).then_inc(s.sem("ones"), 1)
            dve.memset(norm[:, :, 8:9], 1.0).then_inc(s.sem("ones"), 1)
            dve.memset(eps[:, 0:1], 1e-5).then_inc(s.sem("eps"), 1)
            dve.memset(eps[:, 1:3], 1e-6).then_inc(s.sem("eps"), 1)
            dve.wait_ge(s.sem("gb_in"), 5 * 16)
            dve.wait_ge(s.sem("ones"), 3)
            dve.wait_ge(s.sem("eps"), 2)

            def step(n, i):
                j, at = i % 2, (i + 1) % AHEAD
                k = 1 - j
                new, old = exists(n + 1), exists(n)
                r, root = norm[:, j, 0:3], tmp[:, j, :]

                if new:
                    dve.wait_ge(s.sem(f"ctx_in{at}"), loaded(n + 1, at))
                    wait(dve, "std", n)
                    dve.bn_stats(st[:, k, 0, :], rows[:, at, :]).then_inc(s.sem("stats"), 1)
                if old:
                    wait(dve, "std", n + 1)
                    dve.reciprocal(r, std[:, j, :]).then_inc(s.sem("r0"), 1)
                if new:
                    wait(dve, "k_ps", n + 2)
                    dve.bn_stats(st[:, k, 1, :], ps_k[k][:, 0:D]).then_inc(s.sem("stats"), 1)
                if old:
                    wait(dve, "r0", n + 1)
                    dve.tensor_tensor(root, r, r, ALU.mult).then_inc(s.sem("r1"), 1)
                if new:
                    wait(dve, "v_copied", n + 2)
                    dve.bn_stats(st[:, k, 2, :], vraw[:, at, :]).then_inc(s.sem("stats"), 1)
                if old:
                    wait(dve, "r1", n + 1)
                    dve.tensor_tensor(root, root, mv[:, j, :, 1], ALU.mult).then_inc(s.sem("r2"), 1)
                if new:
                    wait(dve, "stats", n * 3 + 6)
                    dve.sem_inc(s.sem("stats_seen"), 1)
                    for i in range(3):
                        dve.bn_aggr(mv[:, k, i, :], st[:, k, i, :]).then_inc(s.sem("aggr"), 1)
                if old:
                    wait(dve, "r2", n + 1)
                    dve.tensor_scalar(root, root, -0.5, 1.5, ALU.mult, ALU.add).then_inc(s.sem("r3"), 1)
                if new:
                    wait(dve, "aggr", n * 3 + 6)
                    dve.tensor_tensor(mv[:, k, :, 1], mv[:, k, :, 1], eps[:, :], ALU.add).then_inc(s.sem("var"), 1)
                if old:
                    wait(dve, "r3", n + 1)
                    dve.tensor_tensor(r, r, root, ALU.mult).then_inc(s.sem("r4"), 1)
                if new:
                    wait(dve, "kp", n)
                    dve.scalar_tensor_tensor(out=kc[:, k, :], in0=ps_k[k][:, 0:D], scalar=mv[:, k, 1, 0:1], in1=g2[:, :],
                                             op0=ALU.subtract, op1=ALU.mult).then_inc(s.sem("k_centered"), 1)
                if old:
                    wait(dve, "r4", n + 1)
                    wait(dve, "vp_mask", n - 1)
                    dve.scalar_tensor_tensor(out=norm[:, j, 3:6], in0=mv[:, j, :, 0], scalar=-1.0, in1=r,
                                             op0=ALU.mult, op1=ALU.mult).then_inc(s.sem("norm"), 1)
                    dve.scalar_tensor_tensor(out=kc[:, j, :], in0=kc[:, j, :], scalar=r[:, 1:2], in1=b2[:, :],
                                             op0=ALU.mult, op1=ALU.add).then_inc(s.sem("k_affine"), 1)
                    wait(dve, "norm", n + 1)
                    wait(dve, "kp", n - 1)
                    dve.tensor_scalar(vm[:, j, :], norm[:, j, 2:9:3], mask[:, bass.ds(n, 1)], None,
                                      ALU.mult).then_inc(s.sem("vm"), 1)
                    wait(dve, "k_affine", n + 1)
                    dve.tensor_scalar(kc[:, j, :], kc[:, j, :], 0.0, 1e-6, ALU.max, ALU.add).then_inc(s.sem("k_pos"), 1)

            steps(dve, step)
            dve.wait_ge(s.sem("all_ps"), 1)
            total = ps_sum[:, 0:DC * W].rearrange("p (c e) -> p c e", c=DC)
            kv = A["kv_sum"]
            link = linker(dve, s.sem("dve_end"))
            for c in range(DC):
                cut = slice(c * 128, (c + 1) * 128)
                link(dve.tensor_scalar(beta[:, cut], b2[:, cut], total[:, c, 129:130], None, ALU.mult))
                link(dve.tensor_tensor(kv[:, c, 0:128], total[:, c, 0:128], g2[:, cut], ALU.mult))
                link(dve.tensor_tensor(kv[:, c, 0:128], kv[:, c, 0:128], beta[:, cut], ALU.add))
            link(dve.tensor_copy(kv[:, :, 128:129], total[:, :, 128:129]))

        @block.gpsimd
        def _(pool):
            def step(n, i):
                j = i % 2
                if exists(n):
                    wait(pool, "xhat", n + 1)
                    wait(pool, f"stored{j}", 16 * (n - j) - 32)
                    pool.tensor_tensor(xn[:, i, :], xh[:, j, :], g1[:, :], ALU.mult).then_inc(s.sem("xn_g"), 1)
                    wait(pool, "xn_g", n + 1)
                    pool.tensor_tensor(xn[:, i, :], xn[:, i, :], b1[:, :], ALU.add).then_inc(s.sem("xn"), 1)

            pool.wait_ge(s.sem("gb_in"), 5 * 16)
            steps(pool, step)


def stage_l1_xattn(nc, A, x, ident):
    H = 8
    with Stage(nc, "l1x", fast=2 * (2 * DC * CH + 2 * CT * D + 2 * CT * T + H * DC * T + D + DC * T) + 2 * CH + T) as s:
        heads = WideHeads(s, H, A, "L1_xattn_", ident, WideHeads.HD ** -1.0)
        lat, latT = s.sb("lat", [128, D]), s.sb("latT", [128, DC, T])
        lat_high, lat_low = (s.sb(f"lat_{i}", [128, D], F32R) for i in ("high", "low"))
        latT_high, latT_low = (s.sb(f"latT_{i}", [128, DC, T], F32R) for i in ("high", "low"))
        ca = ContextAttention(s, H, D, heads.qt, lambda h: (0, D), A["xnT"], A["xn_rows"], ident, mask="rows",
                              mask_dram=A["mask_bk1"].partition_broadcast(1), bias_per_one=-FAR, 
                              tail=((latT_high, latT_low), (lat_high, lat_low)), split="both")
        lg, lb, og, ob = (s.sb(n, [128, D]) for n in ("lg", "lb", "og", "ob"))
        y = s.sb("y", [128, D])
        ps_a, ps_b = ca.ps_o[0], ca.ps_o[1]
        n0, n1, ny = RowNorm(s, "n0", 1e-5), RowNorm(s, "n1", 1e-5), RowNorm(s, "y", 1e-5)
        heads.use(ca, latT, s.sem("latT"))
        block = s.block()

        @block.sync
        def _(sp):
            heads.sp(sp)
            load_rows(sp, s, A, [("lg", lg, "L1_xattn_ln_l_g"), ("lb", lb, "L1_xattn_ln_l_b"),
                                 ("og", og, "L1_xattn_ln_o_g"), ("ob", ob, "L1_xattn_ln_o_b")])
            ca.sp(sp)
            heads.sp_outputs(sp)

        @block.tensor
        def _(pe):
            pe.wait_ge(s.sem("lat"), 1)
            pe_transposes(pe, ps_a, lat, ident).then_inc(s.sem("latT_ps"), 1)
            heads.pe_queries(pe)
            pe.wait_ge(s.sem("tail"), 1)
            ca.pe(pe)
            heads.pe_outputs(pe, ps_a)

        @block.scalar
        def _(act):
            n0.act(act)
            n1.act(act)
            heads.act_queries(act)
            ca.act(act)
            heads.act_outputs(act)
            ny.act(act)

        @block.gpsimd
        def _(pool):
            ca.pool(pool)

        @block.vector
        def _(dve):
            link = linker(dve, s.sem("dve_steps"))
            n0.dve(dve, link, lat[:, :], x[:, :])
            n1.dve(dve, link, lat[:, :], lat[:, :])
            dve.wait_ge(s.sem("lg_in"), 16)
            link(dve.tensor_tensor(lat[:, :], lat[:, :], lg[:, :], ALU.mult))
            dve.wait_ge(s.sem("lb_in"), 16)
            finish(dve, dve.tensor_tensor(lat[:, :], lat[:, :], lb[:, :], ALU.add), s.sem("lat"))
            dve.wait_ge(s.sem("latT_ps"), 1)
            dve.tensor_copy(latT[:, :, :], cols(ps_a)).then_inc(s.sem("latT"), 1)
            heads.dve_queries(dve)
            dve.wait_ge(s.sem("latT"), 1)
            link(dve.tensor_copy(lat_high[:, :], lat[:, :]))
            link(dve.tensor_copy(latT_high[:, :, :], latT[:, :, :]))
            link(dve.tensor_tensor(lat_low[:, :], lat[:, :], lat_high[:, :].bitcast(F32), ALU.subtract))
            dve.tensor_tensor(latT_low[:, :, :], latT[:, :, :], latT_high[:, :, :].bitcast(F32), ALU.subtract).then_inc(s.sem("tail"), 1)
            ca.dve(dve)
            heads.dve_outputs(dve)
            dve.wait_ge(s.sem("out_ps"), H)
            ny.dve(dve, link, y[:, :], ps_a[:, 0:D])
            dve.wait_ge(s.sem("og_in"), 16)
            link(dve.tensor_tensor(y[:, :], y[:, :], og[:, :], ALU.mult))
            dve.wait_ge(s.sem("ob_in"), 16)
            link(dve.tensor_tensor(y[:, :], y[:, :], ob[:, :], ALU.add))
            link(dve.tensor_tensor(x[:, :], x[:, :], y[:, :], ALU.add))


def stage_l2_xattn(nc, A, x, ident):
    with Stage(nc, "l2x") as s:
        wq, wd = s.sb("wq", [128, DC, D]), s.sb("wd", [128, DC, D])
        g, b, bd = s.sb("g", [128, D]), s.sb("b", [128, D]), s.sb("bd", [128, D])
        kvd = s.sb("kvd", [128, DC, 136])
        q, qT, den = s.sb("q", [128, D]), s.sb("qT", [128, DC, T]), s.sb("den", [128, DC, 8])
        att2 = s.sb("att2", [128, D])
        att, attT, y = s.sb("att", [128, D]), s.sb("attT", [128, DC, T]), s.sb("y", [128, D])
        ps_a, ps_b, ps_c = s.ps("ps_a"), s.ps("ps_b"), s.ps("ps_c")
        nx, nq, ny = NormX(s, x, ident, ps_a), RowNorm(s, "nq", 1e-6), RowNorm(s, "ny", 1e-6)
        hm, kv = A["head_mask"], A["kv_sum"]
        block = s.block()

        @block.sync
        def _(sp):
            sp.dma_start(wq[:, :, :], A["L2_xattn_wq"]).then_inc(s.sem("wq_in"), 16)
            sp.dma_start(wd[:, :, :], A["L2_xattn_dense_w"]).then_inc(s.sem("wd_in"), 16)
            load_rows(sp, s, A, [("g", g, "L2_xattn_ln_gamma"), ("b", b, "L2_xattn_ln_beta"), ("bd", bd, "L2_xattn_dense_b")])
            sp.wait_ge(s.sem("att"), DC)
            sp.dma_start(A["att_order"].rearrange("h n e -> n h e"),
                         att[:, :].rearrange("p (h e) -> p h e", h=16)).then_inc(s.sem("att_out"), 16)
            sp.wait_ge(s.sem("att_out"), 16)
            sp.dma_start(att2[:, :], A["att_order"].rearrange("h (a b) e -> (h a) (b e)", b=16)).then_inc(s.sem("att_in"), 16)

        @block.tensor
        def _(pe):
            nx.pe(pe)
            pe.wait_ge(s.sem("xnT"), 1)
            pe.wait_ge(s.sem("wq_in"), 16)
            pe_dense(pe, ps_b[:, 0:D], lambda c: nx.xnT[:, c, :], lambda c: wq[:, c, :]).then_inc(s.sem("q_ps"), 1)
            pe.wait_ge(s.sem("q"), 1)
            pe_transposes(pe, ps_a, q, ident).then_inc(s.sem("qT_ps"), 1)
            pe.wait_ge(s.sem("kvd"), 1)
            pe.wait_ge(s.sem("qT"), 1)
            for c in range(DC):
                mm = pe.matmul(ps_c[:, c * 136:(c + 1) * 136], qT[:, c, :], kvd[:, c, :], start=True, stop=True)
            mm.then_inc(s.sem("att_ps"), 1)
            pe.wait_ge(s.sem("att_in"), 16)
            pe_transposes(pe, ps_a, att2, ident).then_inc(s.sem("attT_ps"), 1)
            pe.wait_ge(s.sem("wd_in"), 16)
            pe.wait_ge(s.sem("attT"), 1)
            pe_dense(pe, ps_b[:, 0:D], lambda c: attT[:, c, :], lambda c: wd[:, c, :]).then_inc(s.sem("y_ps"), 1)

        @block.scalar
        def _(act):
            nx.act(act)
            nq.act(act)
            ny.act(act)

        @block.vector
        def _(dve):
            link = linker(dve, s.sem("dve_steps"))
            nx.dve(dve, link)
            link(dve.tensor_tensor(kvd[:, :, 0:128].rearrange("p c (h e) -> p c h e", h=8),
                                   kv[:, :, 0:128].rearrange("p c (h e) -> p c h e", h=8),
                                   hm[:, :].unsqueeze(1).unsqueeze(3).to_broadcast([128, DC, 8, 16]), ALU.mult))
            dve.tensor_tensor(kvd[:, :, 128:136], hm[:, :].unsqueeze(1).to_broadcast([128, DC, 8]),
                              kv[:, :, 128:129].to_broadcast([128, DC, 8]), ALU.mult).then_inc(s.sem("kvd"), 1)
            dve.wait_ge(s.sem("q_ps"), 1)
            nq.dve(dve, link, q[:, :], ps_b[:, 0:D])
            for name in ("g", "b", "bd"):
                dve.wait_ge(s.sem(name + "_in"), 16)
            link(dve.tensor_tensor(q[:, :], q[:, :], g[:, :], ALU.mult))
            link(dve.tensor_tensor(q[:, :], q[:, :], b[:, :], ALU.add))
            dve.tensor_scalar(q[:, :], q[:, :], 0.0, 1e-6, ALU.max, ALU.add).then_inc(s.sem("q"), 1)
            dve.wait_ge(s.sem("qT_ps"), 1)
            dve.tensor_copy(qT[:, :, :], cols(ps_a)).then_inc(s.sem("qT"), 1)
            dve.wait_ge(s.sem("att_ps"), 1)
            num = ps_c[:, 0:DC * 136].rearrange("p (c e) -> p c e", c=DC)
            link(dve.tensor_scalar(den[:, :, :], num[:, :, 128:136], 1e-6, None, ALU.add))
            link(dve.reciprocal(den[:, :, :], den[:, :, :]))
            for c in range(DC):
                dve.tensor_tensor(att[:, c * 128:(c + 1) * 128].rearrange("p (h e) -> p h e", h=8),
                                         num[:, c, 0:128].rearrange("p (h e) -> p h e", h=8),
                                         den[:, c, :].unsqueeze(2).to_broadcast([128, 8, 16]), ALU.mult).then_inc(s.sem("att"), 1)
            dve.wait_ge(s.sem("attT_ps"), 1)
            dve.tensor_copy(attT[:, :, :], cols(ps_a)).then_inc(s.sem("attT"), 1)
            dve.wait_ge(s.sem("y_ps"), 1)
            link(dve.tensor_tensor(y[:, :], ps_b[:, 0:D], bd[:, :], ALU.add))
            ny.dve(dve, link, y[:, :], y[:, :])
            link(dve.tensor_tensor(y[:, :], y[:, :], g[:, :], ALU.mult))
            link(dve.tensor_tensor(y[:, :], y[:, :], b[:, :], ALU.add))
            link(dve.tensor_tensor(x[:, :], x[:, :], y[:, :], ALU.add))


def stage_l3_xattn(nc, A, x, ident):
    H = 16
    with Stage(nc, "l3x", fast=2 * 4 * CH + 2 * H * T) as s:
        qd = s.sb("qd", [128, H, T])
        q_high, q_low = (s.sb(f"q_{i}", [128, H, T], F32R) for i in ("high", "low"))
        group = lambda h: h % 8 // 4 * 2 + h // 8
        ca = ContextAttention(s, H, 16, lambda h: [([q[:, h, :]], group(h)) for q in (q_high, q_low)],
                              lambda h: (16 * h, 16 * h + 16), A["ctxT"], A["ctx_rows"], ident, mask="full",
                              mask_dram=A["mask_ik1"], bias_per_one=1e9, split="keys")
        nx = NormX(s, x, ident, ca.ps_o[0])
        twice, rows = s.sb("twice", [128, 4, 2, 64]), s.sb("rows", [128, 4])
        ps_q = ca.ps_o[1]
        hm = A["head_mask"]
        block = s.block()

        @block.sync
        def _(sp):
            ca.sp(sp)

        @block.tensor
        def _(pe):
            nx.pe(pe)
            pe.wait_ge(s.sem("twice"), 4)
            for g in range(4):
                mm = pe.transpose(ps_q[:, g * T:(g + 1) * T], twice[:, g, :, :].rearrange("p n e -> p (n e)"), ident[:, :])
            mm.then_inc(s.sem("q_ps"), 1)
            pe.wait_ge(s.sem("q_low"), 1)
            ca.pe(pe)

        @block.scalar
        def _(act):
            nx.act(act)
            act.wait_ge(s.sem("qd"), H)
            act.activation(q_high[:, :, :], qd[:, :, :], ACT.Copy).then_inc(s.sem("q_high"), 1)
            ca.act(act)

        @block.gpsimd
        def _(pool):
            ca.pool(pool)

        @block.vector
        def _(dve):
            link = linker(dve, s.sem("dve_steps"))
            nx.dve(dve, link)
            for i in range(2):
                for n in range(2):
                    dve.tensor_copy(twice[:, 2 * i:2 * i + 2, n, :],
                                    nx.xn[:, :].rearrange("p (c i e) -> p c i e", c=2, i=2)[:, :, i, :]).then_inc(s.sem("twice"), 1)
            link(dve.tensor_tensor(rows[:, :], hm[:, 0:4], hm[:, 4:8], ALU.add))
            dve.wait_ge(s.sem("q_ps"), 1)
            for h in range(H):
                dve.tensor_scalar(qd[:, h, :], ps_q[:, group(h) * T:(group(h) + 1) * T], rows[:, h % 4:h % 4 + 1], 0.25,
                                  ALU.mult, ALU.mult).then_inc(s.sem("qd"), 1)
            dve.wait_ge(s.sem("q_high"), 1)
            dve.tensor_tensor(q_low[:, :, :], qd[:, :, :], q_high[:, :, :].bitcast(F32), ALU.subtract).then_inc(s.sem("q_low"), 1)
            ca.dve(dve)
            dve.wait_ge(s.sem("attended"), H)
            link(dve.tensor_tensor(x[:, :], x[:, :], ca.acc[:, :, :].rearrange("p h e -> p (h e)"), ALU.add))


def add_cols(a, n):
    return a.unsqueeze(2).to_broadcast([a.shape[0], a.shape[1], n])


def stage_l0_attn(nc, A, x, ident):
    with Stage(nc, "l0a") as s:
        qk = s.sb("qk", [128, 2, DC])
        dl, osc = s.sb("dl", [128, 1]), s.sb("osc", [128, 1])
        BITS = 7
        dk, dm1 = s.sb("dk", [128, BITS]), s.sb("dm1", [128, BITS])
        steps, bit = s.sb("steps", [128, T], I32), s.sb("bit", [128, T], I32)
        w, fac = s.sb("w", [128, T]), s.sb("fac", [128, T])
        qx, kx, sw = s.sb("qx", [128, DC, T]), s.sb("kx", [128, DC, T]), s.sb("sw", [128, T])
        ps_a, ps_s, ps_y = s.ps("ps_a"), s.ps("ps_s"), s.ps("ps_y")
        nx = NormX(s, x, ident, ps_a)
        block = s.block()

        @block.sync
        def _(sp):
            sp.dma_start(dl[:, :], A["L0_attn_decay_logit"].partition_broadcast(128)).then_inc(s.sem("dl_in"), 16)
            sp.dma_start(osc[:, :], A["L0_attn_out_scale"].partition_broadcast(128)).then_inc(s.sem("osc_in"), 16)
            sp.dma_start(qk[:, 0, :], A["L0_attn_q_scale"]).then_inc(s.sem("qk_in"), 16)
            sp.dma_start(qk[:, 1, :], A["L0_attn_k_scale"]).then_inc(s.sem("qk_in"), 16)

        @block.gpsimd
        def _(pool):
            pool.iota(steps[:, :], [[-1, T]], base=-1, channel_multiplier=1).then_inc(s.sem("steps"), 1)
            pool.wait_ge(s.sem("w_all"), 1)
            pool.affine_select(out=w[:, :], in_=w[:, :], compare_op=ALU.is_gt, fill=0.0, base=0,
                               pattern=[[-1, T]], channel_multiplier=1).then_inc(s.sem("w"), 1)

        @block.tensor
        def _(pe):
            nx.pe(pe)
            pe.wait_ge(s.sem("kx"), 2 * DC)
            pe_dense(pe, ps_s[:, 0:T], lambda c: kx[:, c, :], lambda c: qx[:, c, :]).then_inc(s.sem("s_ps"), 1)
            pe.wait_ge(s.sem("sw"), 1)
            pe.matmul(ps_y[:, 0:D], sw[:, :], nx.xn[:, :], start=True, stop=True).then_inc(s.sem("y_ps"), 1)

        @block.scalar
        def _(act):
            nx.act(act)
            act.wait_ge(s.sem("dl_in"), 16)
            act.activation(dk[:, 0:1], dl[:, :], ACT.Tanh, scale=0.5).then_inc(s.sem("tanh"), 1)

        @block.vector
        def _(dve):
            link = linker(dve, s.sem("dve_steps"))
            nx.dve(dve, link)
            dve.wait_ge(s.sem("tanh"), 1)
            link(dve.tensor_scalar(dk[:, 0:1], dk[:, 0:1], 1.0, 0.5, ALU.add, ALU.mult))
            for k in range(1, BITS):
                link(dve.tensor_tensor(dk[:, k:k + 1], dk[:, k - 1:k], dk[:, k - 1:k], ALU.mult))
            link(dve.tensor_scalar(dm1[:, :], dk[:, :], -1.0, None, ALU.add))
            dve.wait_ge(s.sem("steps"), 1)
            for k in range(BITS):
                link(dve.tensor_scalar(bit[:, :], steps[:, :], k, 1, ALU.logical_shift_right, ALU.bitwise_and))
                dst = w if k == 0 else fac
                ins = dve.tensor_scalar(dst[:, :], bit[:, :], dm1[:, k:k + 1], 1.0, ALU.mult, ALU.add)
                link(ins)
                if k > 0:
                    ins = dve.tensor_tensor(w[:, :], w[:, :], fac[:, :], ALU.mult)
                    if k == BITS - 1:
                        ins.then_inc(s.sem("w_all"), 1)
                    else:
                        link(ins)
            dve.wait_ge(s.sem("qk_in"), 32)
            dve.wait_ge(s.sem("xnT"), 1)
            for c in range(DC):
                dve.tensor_scalar(qx[:, c, :], nx.xnT[:, c, :], qk[:, 0, c:c + 1], None, ALU.mult).then_inc(s.sem("kx"), 1)
                dve.tensor_scalar(kx[:, c, :], nx.xnT[:, c, :], qk[:, 1, c:c + 1], None, ALU.mult).then_inc(s.sem("kx"), 1)
            dve.wait_ge(s.sem("s_ps"), 1)
            dve.wait_ge(s.sem("w"), 1)
            dve.tensor_tensor(sw[:, :], ps_s[:, 0:T], w[:, :], ALU.mult).then_inc(s.sem("sw"), 1)
            dve.wait_ge(s.sem("y_ps"), 1)
            dve.wait_ge(s.sem("osc_in"), 16)
            link(dve.scalar_tensor_tensor(out=x[:, :], in0=ps_y[:, 0:D], scalar=osc[:, 0:1], in1=x[:, :],
                                          op0=ALU.mult, op1=ALU.add))


class SmallHeads:

    H, HD = 16, 16

    def __init__(self, s, A, x, ident, w, bias=None, q_scale=1.0):
        self.s, self.A, self.ident, self.w_dram, self.bias_dram, self.q_scale = s, A, ident, w, bias, q_scale
        self.w = s.sb("w_qkv", [128, DC, 3 * D])
        self.bias = s.sb("b_qkv", [128, 3 * D]) if bias else None
        self.qkv = s.sb("qkv", [128, 3 * D])
        self.qkT = s.sb("qkT", [128, 4, T])
        self.qd = s.sb("qd", [128, self.H, T])
        self.ps_a, self.ps_b = s.ps("ps_a"), s.ps("ps_b")
        self.ps_h = [s.ps(f"ps_h{g}") for g in range(4)]
        self.nx = NormX(s, x, ident, self.ps_a)

    def sp(self, sp):
        sp.dma_start(self.w[:, :, :], self.A[self.w_dram]).then_inc(self.s.sem("w_qkv_in"), 16)
        if self.bias:
            sp.dma_start(self.bias[:, :], self.A[self.bias_dram].partition_broadcast(128)).then_inc(self.s.sem("b_qkv_in"), 16)

    def pe_project(self, pe):
        s = self.s
        self.nx.pe(pe)
        pe.wait_ge(s.sem("w_qkv_in"), 16)
        pe.wait_ge(s.sem("xnT"), 1)
        pe_dense(pe, self.ps_a[:, :], lambda c: self.nx.xnT[:, c, :], lambda c: self.w[:, c, 0:512])
        pe_dense(pe, self.ps_b[:, 0:D], lambda c: self.nx.xnT[:, c, :],
                 lambda c: self.w[:, c, 512:768]).then_inc(s.sem("qkv_ps"), 1)

    def dve_project(self, dve, link):
        s = self.s
        self.nx.dve(dve, link)
        dve.wait_ge(s.sem("qkv_ps"), 1)
        if self.bias:
            dve.wait_ge(s.sem("b_qkv_in"), 16)
        for lo, hi, ps in ((0, 512, self.ps_a[:, :]), (512, 768, self.ps_b[:, 0:D])):
            if self.bias:
                link(dve.tensor_tensor(self.qkv[:, lo:hi], ps, self.bias[:, lo:hi], ALU.add))
            else:
                link(dve.tensor_copy(self.qkv[:, lo:hi], ps))

    def pe_scores(self, pe):
        s = self.s
        pe.wait_ge(s.sem("qkv_ready"), 1)
        pe_transposes(pe, self.ps_a, self.qkv, self.ident, 4).then_inc(s.sem("qkT_ps"), 1)
        pe.wait_ge(s.sem("qd"), self.H)
        for g in range(4):
            pe.matmul(self.ps_h[g][:, :], self.qkT[:, 2 + g // 2, :], self.qd[:, 4 * g:4 * g + 4, :],
                      start=True, stop=True).then_inc(s.sem("scores"), 1)

    def dve_heads(self, dve):
        s, hm = self.s, self.A["head_mask"]
        dve.wait_ge(s.sem("qkT_ps"), 1)
        finish(dve, dve.tensor_copy(self.qkT[:, :, :], cols(self.ps_a, 4)), s.sem("qkT"))
        for h in range(self.H):
            dve.tensor_scalar(self.qd[:, h, :], self.qkT[:, h // 8, :], hm[:, h % 8:h % 8 + 1], self.q_scale,
                              ALU.mult, ALU.mult).then_inc(s.sem("qd"), 1)

    def v(self, h):
        return self.qkv[:, 512 + 16 * h:512 + 16 * h + 16]


class OutProjection:

    def __init__(self, s, A, x, ident, w, ps_t, ps_o, bias=None):
        self.s, self.A, self.x, self.ident, self.w_dram, self.bias_dram = s, A, x, ident, w, bias
        self.ps_t, self.ps_o = ps_t, ps_o
        self.w, self.yT = s.sb("w_out", [128, DC, D]), s.sb("yT", [128, DC, T])
        self.y = s.sb("y", [128, D])
        self.bias = s.sb("b_out", [128, D]) if bias else None

    def sp(self, sp):
        sp.dma_start(self.w[:, :, :], self.A[self.w_dram]).then_inc(self.s.sem("w_out_in"), 16)
        if self.bias:
            sp.dma_start(self.bias[:, :], self.A[self.bias_dram].partition_broadcast(128)).then_inc(self.s.sem("b_out_in"), 16)

    def pe(self, pe):
        s = self.s
        pe.wait_ge(s.sem("y_ready"), 1)
        pe_transposes(pe, self.ps_t, self.y, self.ident).then_inc(s.sem("yT_ps"), 1)
        pe.wait_ge(s.sem("w_out_in"), 16)
        pe.wait_ge(s.sem("yT"), 1)
        pe_dense(pe, self.ps_o[:, 0:D], lambda c: self.yT[:, c, :], lambda c: self.w[:, c, :]).then_inc(s.sem("out_ps"), 1)

    def dve(self, dve, link):
        s, x = self.s, self.x
        dve.wait_ge(s.sem("yT_ps"), 1)
        dve.tensor_copy(self.yT[:, :, :], cols(self.ps_t)).then_inc(s.sem("yT"), 1)
        if self.bias:
            dve.wait_ge(s.sem("b_out_in"), 16)
            link(dve.tensor_tensor(x[:, :], x[:, :], self.bias[:, :], ALU.add))
        dve.wait_ge(s.sem("out_ps"), 1)
        link(dve.tensor_tensor(x[:, :], x[:, :], self.ps_o[:, 0:D], ALU.add))


def stage_l2_attn(nc, A, x, ident):
    with Stage(nc, "l2a") as s:
        hd = SmallHeads(s, A, x, ident, "L2_attn_W_qkv")
        op = OutProjection(s, A, x, ident, "L2_attn_W_o", hd.ps_a, hd.ps_b)
        mu, var, std = s.sb("mu", [128, 16]), s.sb("var", [128, 16]), s.sb("std", [128, 16])
        sq = s.sb("sq", [128, D])
        st = s.sb("st", [128, 4, 4, T])
        ps_y = s.ps("ps_y")
        block = s.block()

        @block.sync
        def _(sp):
            hd.sp(sp)
            op.sp(sp)

        @block.tensor
        def _(pe):
            hd.pe_project(pe)
            hd.pe_scores(pe)
            for h in range(16):
                pe.wait_ge(s.sem("st"), h // 4 + 1)
                mm = pe.matmul(ps_y[:, 16 * h:16 * h + 16], st[:, h // 4, h % 4, :], hd.v(h), start=True, stop=True)
            mm.then_inc(s.sem("y_ps"), 1)
            op.pe(pe)

        @block.scalar
        def _(act):
            hd.nx.act(act)
            act.wait_ge(s.sem("k_var"), 1)
            act.activation(std[:, :], var[:, :], ACT.Sqrt).then_inc(s.sem("k_std"), 1)

        @block.vector
        def _(dve):
            link = linker(dve, s.sem("dve_steps"))
            hd.dve_project(dve, link)
            k = hd.qkv[:, 256:512].rearrange("p (h e) -> p h e", h=16)
            sq3 = sq[:, :].rearrange("p (h e) -> p h e", h=16)
            link(dve.tensor_reduce(mu[:, :], k, AX.X, ALU.add))
            link(dve.tensor_scalar(mu[:, :], mu[:, :], 1 / 16, None, ALU.mult))
            link(dve.tensor_tensor(k, k, add_cols(mu[:, :], 16), ALU.subtract))
            link(dve.tensor_tensor(sq3, k, k, ALU.mult))
            link(dve.tensor_reduce(var[:, :], sq3, AX.X, ALU.add))
            dve.tensor_scalar(var[:, :], var[:, :], 1 / 16, 1e-5, ALU.mult, ALU.add).then_inc(s.sem("k_var"), 1)
            dve.wait_ge(s.sem("k_std"), 1)
            dve_rsqrt(dve, link, mu[:, :], std[:, :], var[:, :])
            dve.tensor_tensor(k, k, add_cols(mu[:, :], 16), ALU.mult).then_inc(s.sem("qkv_ready"), 1)
            hd.dve_heads(dve)
            for g in range(4):
                dve.wait_ge(s.sem("scores"), g + 1)
                dve.tensor_tensor(st[:, g, :, :], cols(hd.ps_h[g], 4),
                                  A["causal"][:, :].unsqueeze(1).to_broadcast([128, 4, T]), ALU.mult).then_inc(s.sem("st"), 1)
            dve.wait_ge(s.sem("y_ps"), 1)
            dve.tensor_copy(op.y[:, :], ps_y[:, 0:D]).then_inc(s.sem("y_ready"), 1)
            op.dve(dve, link)


class SmallSoftmax:

    def __init__(self, s, name):
        self.s, self.name = s, name
        self.p, self.m, self.l = s.sb(name + "_p", [128, 16, T]), s.sb(name + "_m", [128, 16]), s.sb(name + "_l", [128, 16])

    def dve(self, dve, link, src, bias=None):
        s = self.s
        for g in range(4):
            dst, gs = self.p[:, 4 * g:4 * g + 4, :], slice(4 * g, 4 * g + 4)
            a = src(g)
            if bias is not None:
                link(dve.tensor_tensor(dst, a, bias.unsqueeze(1).to_broadcast([128, 4, T]), ALU.add))
                a = dst
            link(dve.tensor_reduce(self.m[:, gs], a, AX.X, ALU.max))
            dve.tensor_tensor(dst, a, add_cols(self.m[:, gs], T), ALU.subtract).then_inc(s.sem(self.name + "_shifted"), 1)

    def act(self, act):
        s = self.s
        for g in range(4):
            act.wait_ge(s.sem(self.name + "_shifted"), g + 1)
            dst = self.p[:, 4 * g:4 * g + 4, :]
            act.activation(dst, dst, ACT.Exp).then_inc(s.sem(self.name + "_exp"), 1)

    def dve_sums(self, dve, link):
        for g in range(4):
            dve.wait_ge(self.s.sem(self.name + "_exp"), g + 1)
            link(dve.tensor_reduce(self.l[:, 4 * g:4 * g + 4], self.p[:, 4 * g:4 * g + 4, :], AX.X, ALU.add))
        link(dve.reciprocal(self.l[:, :], self.l[:, :]))


class SmallValues:

    def __init__(self, s, hd, p, ps_y):
        self.s, self.hd, self.p, self.ps_y = s, hd, p, ps_y
        self.pT = s.sb("pT", [128, 16, T])

    def pe(self, pe, ready, count):
        s, hd = self.s, self.hd
        for g in range(4):
            pe.wait_ge(ready, count(g))
            for h in range(4 * g, 4 * g + 4):
                mm = pe.transpose(hd.ps_h[g][:, (h % 4) * T:(h % 4 + 1) * T], self.p[:, h, :], hd.ident[:, :])
            mm.then_inc(s.sem("pT_ps"), 1)
        for g in range(4):
            pe.wait_ge(s.sem("pT"), g + 1)
            for h in range(4 * g, 4 * g + 4):
                mm = pe.matmul(self.ps_y[:, 16 * h:16 * h + 16], self.pT[:, h, :], hd.v(h), start=True, stop=True)
        mm.then_inc(s.sem("y_ps"), 1)

    def act(self, act):
        for g in range(4):
            act.wait_ge(self.s.sem("pT_ps"), g + 1)
            act.activation(self.pT[:, 4 * g:4 * g + 4, :], cols(self.hd.ps_h[g], 4), ACT.Copy).then_inc(self.s.sem("pT"), 1)


def stage_l3_attn(nc, A, x, ident):
    with Stage(nc, "l3a") as s:
        hd = SmallHeads(s, A, x, ident, "L3_attn_W_qkv", bias="L3_attn_b_qkv", q_scale=D ** -0.5)
        op = OutProjection(s, A, x, ident, "L3_attn_Wo", hd.ps_a, hd.ps_b, bias="L3_attn_bo")
        sm = SmallSoftmax(s, "sm")
        ps_y = s.ps("ps_y")
        vals = SmallValues(s, hd, sm.p, ps_y)
        block = s.block()

        @block.sync
        def _(sp):
            hd.sp(sp)
            op.sp(sp)

        @block.tensor
        def _(pe):
            hd.pe_project(pe)
            hd.pe_scores(pe)
            vals.pe(pe, s.sem("sm_exp"), lambda g: g + 1)
            op.pe(pe)

        @block.scalar
        def _(act):
            hd.nx.act(act)
            sm.act(act)
            vals.act(act)

        @block.vector
        def _(dve):
            link = linker(dve, s.sem("dve_steps"))
            hd.dve_project(dve, link)
            dve.sem_inc(s.sem("qkv_ready"), 1)
            hd.dve_heads(dve)

            def scores(g):
                dve.wait_ge(s.sem("scores"), g + 1)
                return cols(hd.ps_h[g], 4)

            sm.dve(dve, link, scores)
            sm.dve_sums(dve, link)
            dve.wait_ge(s.sem("y_ps"), 1)
            dve.tensor_tensor(op.y[:, :].rearrange("p (h e) -> p h e", h=16), ps_y[:, 0:D].rearrange("p (h e) -> p h e", h=16),
                              add_cols(sm.l[:, :], 16), ALU.mult).then_inc(s.sem("y_ready"), 1)
            op.dve(dve, link)


def stage_l3_ffn(nc, A, x, ident):
    REG = 5
    with Stage(nc, "l3f") as s:
        hd = SmallHeads(s, A, x, ident, "L3_ffn_W_kqv", q_scale=0.25)
        op = OutProjection(s, A, x, ident, "L3_ffn_W_proj", hd.ps_a, hd.ps_b, bias="L3_ffn_b_proj")
        smp, smn = SmallSoftmax(s, "smp"), SmallSoftmax(s, "smn")
        guide = s.sb("guide", [128, D])
        prod = s.sb("prod", [128, D])
        n2 = s.sb("n2", [128, 2, 16])
        nrm, dot, sim = s.sb("nrm", [128, 2, 16]), s.sb("dot", [128, 16]), s.sb("sim", [128, 1])
        srow, mm1 = s.sb("srow", [1, T]), s.sb("mm1", [1, 4])
        pos = s.sb("pos", [1, T])
        bp, bn = s.sb("bp", [128, T]), s.sb("bn", [128, T])
        wt = s.sb("wt", [128, 4])
        cf = s.sb("cf", [128, 2, 16])
        ps_y, ps_m = s.ps("ps_y"), s.ps("ps_m")
        vals = SmallValues(s, hd, smp.p, ps_y)
        block = s.block()

        @block.sync
        def _(sp):
            hd.sp(sp)
            sp.dma_start(guide[:, :], A["L3_ffn_guide"].partition_broadcast(128)).then_inc(s.sem("guide_in"), 16)
            op.sp(sp)

        @block.gpsimd
        def _(pool):
            pool.affine_select(out=wt[:, 3:4], in_=A["ones"][:, 0:1], compare_op=ALU.is_ge, fill=0.0, base=REG - 1,
                               pattern=[[0, 1]], channel_multiplier=-1).then_inc(s.sem("reg"), 1)

        @block.tensor
        def _(pe):
            hd.pe_project(pe)
            hd.pe_scores(pe)
            pe.wait_ge(s.sem("sim"), 1)
            pe.matmul(ps_m[0:1, 0:T], sim[:, 0:1], ident[:, :], start=True, stop=True).then_inc(s.sem("srow_ps"), 1)
            pe.wait_ge(s.sem("pos"), 1)
            pe.matmul(ps_m[:, 128:256], A["ones"][0:1, :], pos[:, :], start=True, stop=True)
            pe.matmul(ps_m[:, 256:257], pos[:, :], A["ones"][0:1, 0:1], start=True, stop=True).then_inc(s.sem("pos_ps"), 1)
            vals.pe(pe, s.sem("mixed"), lambda g: g + 1)
            op.pe(pe)

        @block.scalar
        def _(act):
            hd.nx.act(act)
            act.wait_ge(s.sem("n2"), 1)
            act.activation(nrm[:, :, :], n2[:, :, :], ACT.Sqrt).then_inc(s.sem("nrm"), 1)
            smp.act(act)
            smn.act(act)
            vals.act(act)

        @block.vector
        def _(dve):
            link = linker(dve, s.sem("dve_steps"))
            hd.dve_project(dve, link)
            dve.sem_inc(s.sem("qkv_ready"), 1)
            hd.dve_heads(dve)

            dve.wait_ge(s.sem("guide_in"), 16)
            q = hd.qkv[:, D:2 * D]
            p3 = prod[:, :].rearrange("p (h e) -> p h e", h=16)
            for i, (a, b) in enumerate(((q, q), (guide[:, :], guide[:, :]), (q, guide[:, :]))):
                link(dve.tensor_tensor(prod[:, :], a, b, ALU.mult))
                link(dve.tensor_reduce(n2[:, i, :] if i < 2 else dot[:, :], p3, AX.X, ALU.add))
            dve.sem_inc(s.sem("n2"), 1)
            dve.wait_ge(s.sem("nrm"), 1)
            link(dve.tensor_tensor(nrm[:, 0, :], nrm[:, 0, :], nrm[:, 1, :], ALU.mult))
            link(dve.reciprocal(nrm[:, 0, :], nrm[:, 0, :]))
            link(dve.tensor_tensor(dot[:, :], dot[:, :], nrm[:, 0, :], ALU.mult))
            link(dve.tensor_reduce(sim[:, :], dot[:, :], AX.X, ALU.add))
            dve.tensor_scalar(sim[:, :], sim[:, :], 1 / 16, None, ALU.mult).then_inc(s.sem("sim"), 1)
            dve.wait_ge(s.sem("srow_ps"), 1)
            link(dve.tensor_copy(srow[:, :], ps_m[0:1, 0:T]))
            link(dve.tensor_reduce(mm1[:, 0:1], srow[:, REG:T], AX.X, ALU.min))
            link(dve.tensor_reduce(mm1[:, 1:2], srow[:, REG:T], AX.X, ALU.max))
            link(dve.tensor_tensor(mm1[:, 2:3], mm1[:, 1:2], mm1[:, 0:1], ALU.subtract))
            link(dve.reciprocal(mm1[:, 3:4], mm1[:, 2:3]))
            link(dve.tensor_scalar(srow[:, :], srow[:, :], mm1[:, 0:1], mm1[:, 3:4], ALU.subtract, ALU.mult))
            dve.tensor_scalar(pos[:, :], srow[:, :], 0.9, None, ALU.is_gt).then_inc(s.sem("pos"), 1)
            dve.wait_ge(s.sem("pos_ps"), 1)
            link(dve.tensor_scalar(bp[:, :], ps_m[:, 128:256], 1.0, -FAR, ALU.subtract, ALU.mult))
            link(dve.tensor_scalar(bn[:, :], ps_m[:, 128:256], FAR, None, ALU.mult))
            link(dve.memset(bp[:, 0:REG], 0.0))
            link(dve.memset(bn[:, 0:REG], 0.0))
            dve.wait_ge(s.sem("reg"), 1)
            link(dve.tensor_scalar(wt[:, 2:3], wt[:, 3:4], -1.0, 1.0, ALU.mult, ALU.add))
            link(dve.tensor_tensor(wt[:, 0:1], wt[:, 2:3], ps_m[:, 256:257], ALU.mult))
            link(dve.tensor_tensor(wt[:, 1:2], wt[:, 2:3], wt[:, 0:1], ALU.subtract))
            for i in range(2):
                link(dve.scalar_tensor_tensor(out=wt[:, i:i + 1], in0=wt[:, 3:4], scalar=0.5, in1=wt[:, i:i + 1],
                                              op0=ALU.mult, op1=ALU.add))

            def scores(g):
                dve.wait_ge(s.sem("scores"), g + 1)
                return cols(hd.ps_h[g], 4)

            smp.dve(dve, link, scores, bp[:, :])
            smn.dve(dve, link, scores, bn[:, :])
            for i, sm in enumerate((smp, smn)):
                sm.dve_sums(dve, link)
                link(dve.tensor_scalar(cf[:, i, :], sm.l[:, :], wt[:, i:i + 1], None, ALU.mult))
            for g in range(4):
                gs = slice(4 * g, 4 * g + 4)
                link(dve.tensor_tensor(smp.p[:, gs, :], smp.p[:, gs, :], add_cols(cf[:, 0, gs], T), ALU.mult))
                link(dve.tensor_tensor(smn.p[:, gs, :], smn.p[:, gs, :], add_cols(cf[:, 1, gs], T), ALU.mult))
                dve.tensor_tensor(smp.p[:, gs, :], smp.p[:, gs, :], smn.p[:, gs, :], ALU.add).then_inc(s.sem("mixed"), 1)
            dve.wait_ge(s.sem("y_ps"), 1)
            dve.tensor_copy(op.y[:, :], ps_y[:, 0:D]).then_inc(s.sem("y_ready"), 1)
            op.dve(dve, link)


def dve_first_max(dve, link, A, scores, n, m, key, onehot):
    iota = A["iota16"][:, 0:n]
    link(dve.tensor_reduce(m, scores, AX.X, ALU.max))
    link(dve.tensor_scalar(onehot, scores, m, None, ALU.is_equal))
    link(dve.scalar_tensor_tensor(out=onehot, in0=onehot, scalar=-1000.0, in1=iota, op0=ALU.mult, op1=ALU.add))
    link(dve.tensor_reduce(key, onehot, AX.X, ALU.min))
    link(dve.tensor_scalar(onehot, iota, -1000.0, key, ALU.add, ALU.is_equal))


class DenseExperts:

    E, F = 8, 1024
    FC = F // 128

    def __init__(self, s, A, x, ident, prefix):
        self.s, self.A, self.x, self.ident, self.prefix = s, A, x, ident, prefix
        self.w1, self.w2 = s.sb("w1", [128, 2, DC, self.F]), s.sb("w2", [128, 2, self.FC, D])
        self.b1, self.b2 = s.sb("b1", [128, self.E * self.FC]), s.sb("b2", [self.E, D])
        self.gate, self.gateT = s.sb("gate", [128, self.E]), s.sb("gateT", [self.E, T])
        self.hT = s.sb("hT", [128, 2, self.FC, T])
        self.acc = s.sb("acc", [128, D])
        self.ps_h = [[s.ps(f"ps_h{j}{i}") for i in range(2)] for j in range(2)]
        self.ps_y = [s.ps(f"ps_y{j}") for j in range(2)]

    def load(self, sp, j, e):
        s, A, p = self.s, self.A, self.prefix
        sp.dma_start(self.w1[:, j, :, :], A[p + "W1"][bass.ds(e, 1), :, :, :]).then_inc(s.sem(f"w1_in{j}"), 16)
        sp.dma_start(self.w2[:, j, :, :], A[p + "W2"][bass.ds(e, 1), :, :, :]).then_inc(s.sem(f"w2_in{j}"), 16)

    def sp(self, sp):
        s, A, p = self.s, self.A, self.prefix
        for j in range(2):
            self.load(sp, j, j)
            if j == 0:
                sp.dma_start(self.b1[:, :], A[p + "b1"]).then_inc(s.sem("b1_in"), 16)
                sp.dma_start(self.b2[:, :], A[p + "b2"]).then_inc(s.sem("b2_in"), 16)
        with sp.Fori(0, self.E // 2 - 1) as it:
            for j in range(2):
                sp.wait_ge(s.sem("expert_ps"), it * 2 + (j + 2))
                self.load(sp, j, it * 2 + (2 + j))

    def pe(self, pe, xnT):
        s = self.s
        head_start(pe, s, "expert_ps")
        with pe.Fori(0, self.E // 2) as it:
            for j in range(2):
                pe.wait_ge(s.sem(f"w1_in{j}"), it * 16 + 16)
                pe.wait_ge(s.sem("hT"), it * 2 * self.FC + 1)
                for f in range(self.FC):
                    out = self.ps_h[j][f // 4][:, (f % 4) * T:(f % 4 + 1) * T]
                    mm = pe_dense(pe, out, lambda c: self.w1[:, j, c, f * 128:(f + 1) * 128], lambda c: xnT[:, c, :])
                    if f % 4 == 3:
                        mm.then_inc(s.sem("h_ps"), 1)
            for j in range(2):
                pe.wait_ge(s.sem(f"w2_in{j}"), it * 16 + 16)
                pe.wait_ge(s.sem("acc"), it * 2 + 1)
                for f in range(self.FC):
                    pe.wait_ge(s.sem("hT"), (it * 2 + j) * self.FC + (f + 2))
                    mm = pe.matmul(self.ps_y[j][:, 0:D], self.hT[:, j, f, :], self.w2[:, j, f, :],
                                   start=(f == 0), stop=(f == self.FC - 1))
                mm.then_inc(s.sem("expert_ps"), 1)
        pe.wait_ge(s.sem("gate"), 1)
        pe.wait_ge(s.sem("hT"), self.E * self.FC + 1)
        pe.matmul(self.ps_h[0][0][0:self.E, 0:T], self.gate[:, :], self.ident[:, :], start=True,
                  stop=True).then_inc(s.sem("gateT_ps"), 1)
        pe.wait_ge(s.sem("b2_in"), 16)
        pe.wait_ge(s.sem("gateT"), 1)
        pe.matmul(self.ps_h[1][0][:, 0:D], self.gateT[:, :], self.b2[:, :], start=True, stop=True).then_inc(s.sem("b2_ps"), 1)

    def dve(self, dve, link):
        s, x = self.s, self.x
        finish(dve, dve.memset(self.acc[:, :], 0.0), s.sem("acc0"))
        dve.wait_ge(s.sem("b1_in"), 16)
        head_start(dve, s, "hT", "acc")
        with dve.Fori(0, self.E // 2) as it:
            for j in range(2):
                dve.wait_ge(s.sem("expert_ps"), it * 2 + 1)
                for f in range(self.FC):
                    if f % 4 == 0:
                        dve.wait_ge(s.sem("h_ps"), (it * 2 + j) * (self.FC // 4) + (f // 4 + 1))
                    dve.tensor_scalar(self.hT[:, j, f, :], self.ps_h[j][f // 4][:, (f % 4) * T:(f % 4 + 1) * T],
                                      self.b1[:, bass.ds((it * 2 + j) * self.FC + f, 1)], 0.0, ALU.add, ALU.max).then_inc(s.sem("hT"), 1)
            for j in range(2):
                dve.wait_ge(s.sem("expert_ps"), it * 2 + (j + 2))
                dve.wait_ge(s.sem("acc"), it * 2 + (j + 1))
                dve.scalar_tensor_tensor(out=self.acc[:, :], in0=self.ps_y[j][:, 0:D],
                                         scalar=self.gate[:, bass.ds(it * 2 + j, 1)], in1=self.acc[:, :],
                                         op0=ALU.mult, op1=ALU.add).then_inc(s.sem("acc"), 1)
        dve.wait_ge(s.sem("acc"), self.E + 1)
        link(dve.tensor_tensor(x[:, :], x[:, :], self.acc[:, :], ALU.add))
        dve.wait_ge(s.sem("gateT_ps"), 1)
        dve.tensor_copy(self.gateT[:, :], self.ps_h[0][0][0:self.E, 0:T]).then_inc(s.sem("gateT"), 1)
        dve.wait_ge(s.sem("b2_ps"), 1)
        link(dve.tensor_tensor(x[:, :], x[:, :], self.ps_h[1][0][:, 0:D], ALU.add))


def dve_floor(dve, link, dst, src, whole, above):
    link(dve.tensor_copy(whole, src))
    link(dve.tensor_copy(dst, whole))
    link(dve.tensor_tensor(above, dst, src, ALU.is_gt))
    link(dve.tensor_tensor(dst, dst, above, ALU.subtract))


def stage_l1_ffn(nc, A, x, ident):
    with Stage(nc, "l1f") as s:
        ex = DenseExperts(s, A, x, ident, "L1_ffn_")
        ps_a, ps_k = s.ps("ps_a"), s.ps("ps_k")
        nx = NormX(s, x, ident, ps_a)
        wr, br = s.sb("wr", [128, DC]), s.sb("br", [128, 1])
        key, fl, g8, q8, ab = (s.sb(n, [128, 1]) for n in ("key", "fl", "g8", "q8", "ab"))
        whole = s.sb("whole", [128, 1], I32)
        block = s.block()

        @block.sync
        def _(sp):
            sp.dma_start(wr[:, :], A["L1_ffn_wr"]).then_inc(s.sem("wr_in"), 16)
            sp.dma_start(br[:, :], A["L1_ffn_br"].partition_broadcast(128)).then_inc(s.sem("wr_in"), 16)
            ex.sp(sp)

        @block.tensor
        def _(pe):
            nx.pe(pe)
            pe.wait_ge(s.sem("wr_in"), 32)
            pe.wait_ge(s.sem("xnT"), 1)
            pe_dense(pe, ps_k[:, 0:1], lambda c: nx.xnT[:, c, :], lambda c: wr[:, c:c + 1]).then_inc(s.sem("key_ps"), 1)
            ex.pe(pe, nx.xnT)

        @block.scalar
        def _(act):
            nx.act(act)

        @block.vector
        def _(dve):
            link = linker(dve, s.sem("dve_steps"))
            nx.dve(dve, link)
            dve.wait_ge(s.sem("wr_in"), 32)
            dve.wait_ge(s.sem("key_ps"), 1)
            link(dve.tensor_tensor(key[:, :], ps_k[:, 0:1], br[:, :], ALU.add))
            dve_floor(dve, link, fl[:, :], key[:, :], whole[:, :], ab[:, :])
            link(dve.tensor_scalar(q8[:, :], fl[:, :], 1 / 8, None, ALU.mult))
            dve_floor(dve, link, g8[:, :], q8[:, :], whole[:, :], ab[:, :])
            link(dve.scalar_tensor_tensor(out=fl[:, :], in0=g8[:, :], scalar=-8.0, in1=fl[:, :], op0=ALU.mult, op1=ALU.add))
            finish(dve, dve.tensor_scalar(ex.gate[:, :], A["iota16"][:, 0:8], fl[:, 0:1], None, ALU.is_equal), s.sem("gate"))
            ex.dve(dve, link)


def stage_l2_ffn(nc, A, x, ident):
    E = 8
    CAP = 2 * -(-T // E)
    with Stage(nc, "l2f") as s:
        ex = DenseExperts(s, A, x, ident, "L2_ffn_")
        ps_a, ps_k = s.ps("ps_a"), s.ps("ps_k")
        nx = NormX(s, x, ident, ps_a)
        wg = s.sb("wg", [128, DC, E])
        sc, s2, oh = s.sb("sc", [128, E]), s.sb("s2", [128, E]), s.sb("oh", [128, 2, E])
        m, r = s.sb("m", [128, 2]), s.sb("r", [128, 4])
        ok = s.sb("ok", [128, 2, E])
        block = s.block()

        @block.sync
        def _(sp):
            sp.dma_start(wg[:, :, :], A["L2_ffn_gate_w"]).then_inc(s.sem("wg_in"), 16)
            ex.sp(sp)

        @block.tensor
        def _(pe):
            nx.pe(pe)
            pe.wait_ge(s.sem("wg_in"), 16)
            pe.wait_ge(s.sem("xnT"), 1)
            pe_dense(pe, ps_k[:, 0:E], lambda c: nx.xnT[:, c, :], lambda c: wg[:, c, :]).then_inc(s.sem("logit_ps"), 1)
            pe.wait_ge(s.sem("chosen"), 1)
            pe.matmul(ps_a[:, 0:2 * E], A["causal"][:, :], oh[:, :, :], start=True, stop=False, skip_group_check=True)
            pe.matmul(ps_a[:, E:2 * E], A["ones"][:, :], oh[:, 0, :], start=False, stop=True,
                      skip_group_check=True).then_inc(s.sem("place_ps"), 1)
            ex.pe(pe, nx.xnT)

        @block.scalar
        def _(act):
            nx.act(act)
            act.wait_ge(s.sem("shifted"), 1)
            act.activation(sc[:, :], sc[:, :], ACT.Exp, accum_out=r[:, 0:1]).then_inc(s.sem("exp"), 1)

        @block.vector
        def _(dve):
            link = linker(dve, s.sem("dve_steps"))
            nx.dve(dve, link)
            dve.wait_ge(s.sem("logit_ps"), 1)
            link(dve.tensor_reduce(r[:, 1:2], ps_k[:, 0:E], AX.X, ALU.max))
            dve.tensor_scalar(sc[:, :], ps_k[:, 0:E], r[:, 1:2], None, ALU.subtract).then_inc(s.sem("shifted"), 1)
            dve.wait_ge(s.sem("exp"), 1)
            link(dve.reciprocal(r[:, 2:3], r[:, 0:1]))
            link(dve.tensor_scalar(sc[:, :], sc[:, :], r[:, 2:3], None, ALU.mult))
            dve_first_max(dve, link, A, sc[:, :], E, m[:, 0:1], r[:, 3:4], oh[:, 0, :])
            link(dve.scalar_tensor_tensor(out=s2[:, :], in0=oh[:, 0, :], scalar=-2.0, in1=sc[:, :], op0=ALU.mult, op1=ALU.add))
            dve_first_max(dve, link, A, s2[:, :], E, m[:, 1:2], r[:, 3:4], oh[:, 1, :])
            dve.sem_inc(s.sem("chosen"), 1)
            link(dve.tensor_tensor(r[:, 0:1], m[:, 0:1], m[:, 1:2], ALU.add))
            link(dve.reciprocal(r[:, 0:1], r[:, 0:1]))
            link(dve.tensor_scalar(m[:, :], m[:, :], r[:, 0:1], None, ALU.mult))
            dve.wait_ge(s.sem("place_ps"), 1)
            link(dve.tensor_scalar(ok[:, :, :], ps_a[:, 0:2 * E].rearrange("p (k e) -> p k e", k=2), float(CAP), None, ALU.is_le))
            link(dve.tensor_tensor(ok[:, :, :], ok[:, :, :], oh[:, :, :], ALU.mult))
            link(dve.tensor_scalar(ex.gate[:, :], ok[:, 0, :], m[:, 0:1], None, ALU.mult))
            finish(dve, dve.scalar_tensor_tensor(out=ex.gate[:, :], in0=ok[:, 1, :], scalar=m[:, 1:2], in1=ex.gate[:, :],
                                                 op0=ALU.mult, op1=ALU.add), s.sem("gate"))
            ex.dve(dve, link)


def stage_l0_ffn(nc, A, x, ident):
    E, F = 16, 512
    FC = F // 128
    TWO_PI = 6.283185307179586
    C1 = 6.28125
    C2 = TWO_PI - C1
    PI = 3.1415925
    PAIRS = E // 2
    with Stage(nc, "l0f") as s:
        wm, wf = s.sb("wm", [128, 2, DC, F]), s.sb("wf", [128, 2, DC, F])
        wd = s.sb("wd", [128, 2, FC, D])
        ph = s.sb("ph", [128, 2, F])
        wr, br = s.sb("wr", [128, DC, E]), s.sb("br", [128, E])
        nw = s.sb("nw", [128, D])
        sc, oh = s.sb("sc", [128, E]), s.sb("oh", [128, 2, E])
        m, r, gate = s.sb("m", [128, 2]), s.sb("r", [128, 4]), s.sb("gate", [128, E])
        sp_, pos, mag = (s.sb(n, [128, 2, 2, F]) for n in ("sp", "pos", "mag"))
        turns, arg = s.sb("turns", [128, 2, F]), s.sb("arg", [128, 2, F])
        whole = s.sb("whole", [128, 2, F], I32)
        hid, hT = s.sb("hid", [128, 2, F]), s.sb("hT", [128, 2, FC, T])
        acc, sq = s.sb("acc", [128, D]), s.sb("sq", [128, D])
        ps_m, ps_f = [s.ps(f"ps_m{j}") for j in range(2)], [s.ps(f"ps_f{j}") for j in range(2)]
        ps_t, ps_y = [s.ps(f"ps_t{j}") for j in range(2)], [s.ps(f"ps_y{j}") for j in range(2)]
        nx = NormX(s, x, ident, ps_t[0])
        block = s.block()

        def wait(eng, name, count):
            if not isinstance(count, int) or count > 0:
                eng.wait_ge(s.sem(name), count)

        def exists(n):
            return not isinstance(n, int) or 0 <= n < PAIRS

        def steps(eng, step):
            step(-1, 1)
            step(0, 0)
            with eng.Fori(0, (PAIRS - 2) // 2) as it:
                for d in (1, 2):
                    step(it * 2 + d, d % 2)
            step(PAIRS - 1, (PAIRS - 1) % 2)
            step(PAIRS, PAIRS % 2)

        @block.sync
        def _(sp):
            def load(j, e):
                for name, dst in (("freq", wf), ("mag", wm)):
                    sp.dma_start(dst[:, j, :, :], A["L0_ffn_bank_" + name][bass.ds(e, 1), :, :, :]).then_inc(s.sem(f"{name}_in{j}"), 16)

            sp.dma_start(wr[:, :, :], A["L0_ffn_router_w"]).then_inc(s.sem("wr_in"), 16)
            for j in range(2):
                load(j, j)
            load_rows(sp, s, A, [("br", br, "L0_ffn_router_bias"), ("nw", nw, "L0_ffn_norm_w")])
            with sp.Fori(0, PAIRS - 1) as it:
                for j in range(2):
                    sp.wait_ge(s.sem("freq_ps"), it * 2 + (j + 1))
                    sp.wait_ge(s.sem("mag_ps"), it * 2 + (j + 1))
                    load(j, it * 2 + (2 + j))

        @block.gpsimd
        def _(pool):
            def load_phase(j, e):
                pool.dma_start(ph[:, j, :], A["L0_ffn_bank_phase"][bass.ds(e, 1), :].partition_broadcast(128)).then_inc(s.sem(f"phase_in{j}"), 16)

            def load_down(j, e):
                pool.dma_start(wd[:, j, :, :], A["L0_ffn_bank_down"][bass.ds(e, 1), :, :, :]).then_inc(s.sem(f"down_in{j}"), 16)

            for j in range(2):
                load_phase(j, j)
                load_down(j, j)
            with pool.Fori(0, PAIRS - 1) as it:
                for j in range(2):
                    pool.wait_ge(s.sem("angle"), it * 2 + (j + 1))
                    load_phase(j, it * 2 + (2 + j))
                for j in range(2):
                    pool.wait_ge(s.sem("expert_ps"), it * 2 + (j + 1))
                    load_down(j, it * 2 + (2 + j))

        @block.tensor
        def _(pe):
            nx.pe(pe)
            pe.wait_ge(s.sem("wr_in"), 16)
            pe.wait_ge(s.sem("xnT"), 1)
            pe_dense(pe, ps_y[0][:, 0:E], lambda c: nx.xnT[:, c, :], lambda c: wr[:, c, :]).then_inc(s.sem("router_ps"), 1)
            pe.wait_ge(s.sem("router"), 1)

            def step(n, k):
                if exists(n + 1):
                    for j in range(2):
                        pe.wait_ge(s.sem(f"freq_in{j}"), n * 16 + 32)
                        wait(pe, "negabs", n * 2 + 2)
                        pe_dense(pe, ps_f[j][:, :], lambda c: nx.xnT[:, c, :], lambda c: wf[:, j, c, :]).then_inc(s.sem("freq_ps"), 1)
                        pe.wait_ge(s.sem(f"mag_in{j}"), n * 16 + 32)
                        wait(pe, "tanh", n * 2 + 2)
                        pe_dense(pe, ps_m[j][:, :], lambda c: nx.xnT[:, c, :], lambda c: wm[:, j, c, :]).then_inc(s.sem("mag_ps"), 1)
                if exists(n - 1):
                    for j in range(2):
                        pe.wait_ge(s.sem(f"down_in{j}"), n * 16)
                        pe.wait_ge(s.sem("acc"), n * 2 - 1)
                        wait(pe, "hT", n * 2 - 1 + j)
                        pe_dense(pe, ps_y[j][:, 0:D], lambda c: hT[:, j, c, :], lambda c: wd[:, j, c, :], FC).then_inc(s.sem("expert_ps"), 1)
                if exists(n):
                    for j in range(2):
                        wait(pe, "hid", n * 2 + 1 + j)
                        wait(pe, "hT", n * 2)
                        pe_transposes(pe, ps_t[j], hid[:, j, :], ident, FC).then_inc(s.sem("hT_ps"), 1)

            steps(pe, step)

        @block.scalar
        def _(act):
            nx.act(act)
            act.wait_ge(s.sem("second"), 1)
            act.activation(r[:, 1:2], r[:, 0:1], ACT.Exp).then_inc(s.sem("ratio"), 1)

            def step(n, k):
                if exists(n + 1):
                    for j in range(2):
                        wait(act, "negabs", n * 2 + 3 + j)
                        act.activation(sp_[:, 1 - k, j, :], sp_[:, 1 - k, j, :], ACT.Exp).then_inc(s.sem("exp"), 1)
                    for j in range(2):
                        wait(act, "mag_ps", n * 2 + 3 + j)
                        wait(act, "hid", n * 2)
                        act.activation(mag[:, 1 - k, j, :], ps_m[j][:, :], ACT.Tanh).then_inc(s.sem("tanh"), 1)
                    wait(act, "exp", n * 2 + 4)
                    act.activation(sp_[:, 1 - k, :, :], sp_[:, 1 - k, :, :], ACT.Ln, bias=A["ones"][:, 0:1]).then_inc(s.sem("log"), 1)
                if exists(n):
                    for j in range(2):
                        wait(act, "angle", n * 2 + 1 + j)
                        act.activation(arg[:, j, :], arg[:, j, :], ACT.Sin).then_inc(s.sem("cos"), 1)
                    for j in range(2):
                        wait(act, "hT_ps", n * 2 + 1 + j)
                        wait(act, "expert_ps", n * 2)
                        act.activation(hT[:, j, :, :], cols(ps_t[j], FC), ACT.Copy).then_inc(s.sem("hT"), 1)

            steps(act, step)
            act.wait_ge(s.sem("ms"), 1)
            act.activation(r[:, 1:2], r[:, 2:3], ACT.Sqrt).then_inc(s.sem("rms"), 1)

        @block.vector
        def _(dve):
            link = linker(dve, s.sem("dve_steps"))
            nx.dve(dve, link)
            dve.wait_ge(s.sem("br_in"), 16)
            dve.wait_ge(s.sem("router_ps"), 1)
            finish(dve, dve.tensor_tensor(sc[:, :], ps_y[0][:, 0:E], br[:, :], ALU.add), s.sem("router"))
            dve_first_max(dve, link, A, sc[:, :], E, m[:, 0:1], r[:, 3:4], oh[:, 0, :])
            link(dve.scalar_tensor_tensor(out=sc[:, :], in0=oh[:, 0, :], scalar=FAR, in1=sc[:, :], op0=ALU.mult, op1=ALU.add))
            dve_first_max(dve, link, A, sc[:, :], E, m[:, 1:2], r[:, 3:4], oh[:, 1, :])
            dve.tensor_tensor(r[:, 0:1], m[:, 1:2], m[:, 0:1], ALU.subtract).then_inc(s.sem("second"), 1)
            dve.wait_ge(s.sem("ratio"), 1)
            link(dve.tensor_scalar(r[:, 2:3], r[:, 1:2], 1.0, None, ALU.add))
            link(dve.reciprocal(r[:, 2:3], r[:, 2:3]))
            link(dve.tensor_tensor(r[:, 3:4], r[:, 1:2], r[:, 2:3], ALU.mult))
            link(dve.tensor_scalar(gate[:, :], oh[:, 0, :], r[:, 2:3], None, ALU.mult))
            link(dve.scalar_tensor_tensor(out=gate[:, :], in0=oh[:, 1, :], scalar=r[:, 3:4], in1=gate[:, :],
                                          op0=ALU.mult, op1=ALU.add))
            link(dve.memset(acc[:, :], 0.0))
            head_start(dve, s, "acc")

            def step(n, k):
                if exists(n + 1):
                    for j in range(2):
                        wait(dve, "freq_ps", n * 2 + 3 + j)
                        dve.tensor_scalar(pos[:, 1 - k, j, :], ps_f[j][:, :], 0.0, None, ALU.max).then_inc(s.sem("pos"), 1)
                    for j in range(2):
                        wait(dve, "pos", n * 2 + 3 + j)
                        dve.scalar_tensor_tensor(out=sp_[:, 1 - k, j, :], in0=pos[:, 1 - k, j, :], scalar=-2.0,
                                                 in1=ps_f[j][:, :], op0=ALU.mult, op1=ALU.add).then_inc(s.sem("negabs"), 1)
                if exists(n):
                    wait(dve, "log", n + 1)
                    wait(dve, "hid", n * 2)
                    for j in range(2):
                        dve.tensor_tensor(arg[:, j, :], sp_[:, k, j, :], pos[:, k, j, :], ALU.add).then_inc(s.sem("softplus"), 1)
                    for j in range(2):
                        dve.wait_ge(s.sem(f"phase_in{j}"), n * 16 + 16)
                        wait(dve, "softplus", n * 2 + 1 + j)
                        dve.scalar_tensor_tensor(out=arg[:, j, :], in0=arg[:, j, :], scalar=0.1, in1=ph[:, j, :],
                                                 op0=ALU.add, op1=ALU.add).then_inc(s.sem("y"), 1)
                    for j in range(2):
                        wait(dve, "y", n * 2 + 1 + j)
                        dve.tensor_scalar(turns[:, j, :], arg[:, j, :], 1 / TWO_PI, 0.25, ALU.mult, ALU.add).then_inc(s.sem("turns"), 1)
                    for j in range(2):
                        wait(dve, "turns", n * 2 + 1 + j)
                        dve.tensor_copy(whole[:, j, :], turns[:, j, :]).then_inc(s.sem("whole"), 1)
                    for j in range(2):
                        wait(dve, "whole", n * 2 + 1 + j)
                        dve.tensor_copy(turns[:, j, :], whole[:, j, :]).then_inc(s.sem("k"), 1)
                    for j in range(2):
                        wait(dve, "k", n * 2 + 1 + j)
                        dve.scalar_tensor_tensor(out=arg[:, j, :], in0=turns[:, j, :], scalar=-C1, in1=arg[:, j, :],
                                                 op0=ALU.mult, op1=ALU.add).then_inc(s.sem("less_c1"), 1)
                    for j in range(2):
                        wait(dve, "less_c1", n * 2 + 1 + j)
                        dve.scalar_tensor_tensor(out=arg[:, j, :], in0=turns[:, j, :], scalar=-C2, in1=arg[:, j, :],
                                                 op0=ALU.mult, op1=ALU.add).then_inc(s.sem("less_c2"), 1)
                    for j in range(2):
                        wait(dve, "less_c2", n * 2 + 1 + j)
                        dve.tensor_scalar(arg[:, j, :], arg[:, j, :], TWO_PI / 4, PI, ALU.add, ALU.min).then_inc(s.sem("below_pi"), 1)
                    for j in range(2):
                        wait(dve, "below_pi", n * 2 + 1 + j)
                        dve.tensor_scalar(arg[:, j, :], arg[:, j, :], -PI, None, ALU.max).then_inc(s.sem("angle"), 1)
                if exists(n - 1):
                    for j in range(2):
                        dve.wait_ge(s.sem("expert_ps"), n * 2 - 1 + j)
                        dve.wait_ge(s.sem("acc"), n * 2 - 1 + j)
                        dve.scalar_tensor_tensor(out=acc[:, :], in0=ps_y[j][:, 0:D], scalar=gate[:, bass.ds(n * 2 - 2 + j, 1)],
                                                 in1=acc[:, :], op0=ALU.mult, op1=ALU.add).then_inc(s.sem("acc"), 1)
                if exists(n):
                    for j in range(2):
                        wait(dve, "cos", n * 2 + 1 + j)
                        wait(dve, "tanh", n * 2 + 1 + j)
                        wait(dve, "hT_ps", n * 2)
                        dve.tensor_tensor(hid[:, j, :], mag[:, k, j, :], arg[:, j, :], ALU.mult).then_inc(s.sem("hid"), 1)

            steps(dve, step)
            dve.wait_ge(s.sem("acc"), E + 1)
            link = linker(dve, s.sem("dve_end"))
            link(dve.tensor_tensor(sq[:, :], acc[:, :], acc[:, :], ALU.mult))
            link(dve.tensor_reduce(r[:, 2:3], sq[:, :], AX.X, ALU.add))
            dve.tensor_scalar(r[:, 2:3], r[:, 2:3], 1 / D, 1e-6, ALU.mult, ALU.add).then_inc(s.sem("ms"), 1)
            dve.wait_ge(s.sem("rms"), 1)
            dve_rsqrt(dve, link, r[:, 0:1], r[:, 1:2], r[:, 2:3])
            dve.wait_ge(s.sem("nw_in"), 16)
            link(dve.scalar_tensor_tensor(out=acc[:, :], in0=acc[:, :], scalar=r[:, 0:1], in1=nw[:, :],
                                          op0=ALU.mult, op1=ALU.mult))
            link(dve.tensor_tensor(x[:, :], x[:, :], acc[:, :], ALU.add))


def stage_l1_attn(nc, A, x, ident):
    H, HD, I = 8, 64, 512
    IC = I // 128
    K = 4
    CAP = 15.0
    PFX = "L1_attn_"
    with Stage(nc, "mls") as s:
        wup = s.sb("wup", [128, DC, 2 * I])
        wts = {n: s.sb("w_" + n, [128, IC, I]) for n in ("skip", "q", "k", "v", "o")}
        wif, wdn = s.sb("wif", [128, IC, 16]), s.sb("wdn", [128, IC, D])
        rows = {n: s.sb("r_" + n, [128, w]) for n, w in (
            ("ln_g", D), ("ln_b", D), ("b_up_l", I), ("b_up_r", I), ("b_skip", I), ("b_v", I), ("b_o", I),
            ("mh_g", I), ("mh_b", I), ("b_down", D), ("conv_w", K), ("conv_b", 1))}
        bqk, bif = s.sb("bqk", [128, 2, IC]), s.sb("bif", [H, 2])
        xa, xaT = s.sb("xa", [128, D]), s.sb("xaT", [128, DC, T])
        xt, rt = s.sb("xt", [128, K - 1 + I]), s.sb("rt", [128, I])
        xc, sg, sr = s.sb("xc", [128, I]), s.sb("sg", [128, I]), s.sb("sr", [128, I])
        xtT, xcT = s.sb("xtT", [128, IC, T]), s.sb("xcT", [128, IC, T])
        skip, v, o = s.sb("skip", [128, I]), s.sb("v", [128, H, HD + 1]), s.sb("o", [128, I])
        qT, kT = s.sb("qT", [128, IC, T]), s.sb("kT", [128, IC, T])
        gi, gf, fs = s.sb("gi", [H, T]), s.sb("gf", [H, T]), s.sb("fs", [H, T])
        one8 = s.sb("one8", [H, T])
        b, mx, em = s.sb("b", [H, T]), s.sb("mx", [H, T]), s.sb("em", [H, T])
        hsel = s.sb("hsel", [H, H, T])
        halves = s.sb("halves", [128, 2])
        cb = s.sb("cb", [128, 16])
        dm, sd = s.sb("dm", [128, H, T]), s.sb("sd", [128, H, T])
        den, hh, hn = s.sb("den", [128, H]), s.sb("hh", [128, I]), s.sb("hn", [128, I])
        hst, hmv = s.sb("hst", [128, H, 6]), s.sb("hmv", [128, H, 2])
        hsd, hvar = s.sb("hsd", [128, H]), s.sb("hvar", [128, H])
        oT = s.sb("oT", [128, IC, T])
        P = [s.ps(f"P{n}") for n in range(8)]
        nx, n1 = NormX(s, x, ident, P[0]), RowNorm(s, "n1", 1e-6)
        block = s.block()

        @block.sync
        def _(sp):
            sp.dma_start(wup[:, :, :], A[PFX + "W_up"]).then_inc(s.sem("wup_in"), 16)
            for n in ("ln_g", "ln_b", "b_up_l", "b_up_r", "conv_w", "conv_b"):
                sp.dma_start(rows[n][:, :], A[PFX + n].partition_broadcast(128)).then_inc(s.sem("rows1_in"), 16)
            for n in ("skip", "v", "o", "q", "k"):
                sp.dma_start(wts[n][:, :, :], A[PFX + "W_" + n]).then_inc(s.sem(f"w_{n}_in"), 16)
            sp.dma_start(wif[:, :, :], A[PFX + "W_if"]).then_inc(s.sem("wif_in"), 16)
            for n in ("b_skip", "b_v", "b_o", "mh_g", "mh_b", "b_down"):
                sp.dma_start(rows[n][:, :], A[PFX + n].partition_broadcast(128)).then_inc(s.sem("rows2_in"), 16)
            sp.dma_start(bqk[:, :, :], A[PFX + "b_qk"]).then_inc(s.sem("rows2_in"), 16)
            sp.dma_start(bif[:, :], A[PFX + "b_if"]).then_inc(s.sem("rows2_in"), 16)
            sp.dma_start(wdn[:, :, :], A[PFX + "W_down"]).then_inc(s.sem("wdn_in"), 16)

        @block.gpsimd
        def _(pool):
            pool.memset(hsel[:, :, :], 0.0).then_inc(s.sem("hsel0"), 1)
            pool.wait_ge(s.sem("hsel0"), 1)
            pool.affine_select(out=hsel[:, :, :], in_=hsel[:, :, :], compare_op=ALU.not_equal, fill=1.0, base=0,
                               pattern=[[-1, H], [0, T]], channel_multiplier=1).then_inc(s.sem("hsel"), 1)
            pool.affine_select(out=halves[:, 0:1], in_=A["ones"][:, 0:1], compare_op=ALU.is_ge, fill=0.0, base=HD - 1,
                               pattern=[[0, 1]], channel_multiplier=-1).then_inc(s.sem("half0"), 1)
            pool.affine_select(out=halves[:, 1:2], in_=A["ones"][:, 0:1], compare_op=ALU.is_ge, fill=0.0, base=-HD,
                               pattern=[[0, 1]], channel_multiplier=1).then_inc(s.sem("half1"), 1)
            pool.wait_ge(s.sem("half0"), 1)
            pool.wait_ge(s.sem("half1"), 1)
            pool.sem_inc(s.sem("halves"), 1)
            for g in range(2):
                pool.wait_ge(s.sem("decay_all"), g + 1)
                pool.tensor_tensor(dm[:, 4 * g:4 * g + 4, :], dm[:, 4 * g:4 * g + 4, :],
                                   A["causal"][:, :].unsqueeze(1).to_broadcast([128, 4, T]), ALU.mult).then_inc(s.sem("decay"), 1)

        @block.tensor
        def _(pe):
            def dense(out, aT, w, n=IC):
                return pe_dense(pe, out, lambda c: aT[:, c, :], lambda c: w[:, c, :], n)

            nx.pe(pe)
            pe.wait_ge(s.sem("xa"), 1)
            pe.wait_ge(s.sem("xnT"), 1)
            pe_transposes(pe, P[0], xa, ident).then_inc(s.sem("xaT_ps"), 1)
            pe.wait_ge(s.sem("wup_in"), 16)
            pe.wait_ge(s.sem("xaT"), 1)
            pe_dense(pe, P[1][:, :], lambda c: xaT[:, c, :], lambda c: wup[:, c, 0:I]).then_inc(s.sem("up_ps"), 1)
            pe_dense(pe, P[2][:, :], lambda c: xaT[:, c, :], lambda c: wup[:, c, I:2 * I]).then_inc(s.sem("up_ps"), 1)
            pe.wait_ge(s.sem("xt"), 1)
            for c in range(IC):
                mm = pe.transpose(P[3][:, c * T:(c + 1) * T], xt[:, K - 1 + c * 128:K - 1 + (c + 1) * 128], ident[:, :])
            mm.then_inc(s.sem("xtT_ps"), 1)
            pe.wait_ge(s.sem("w_v_in"), 16)
            pe.wait_ge(s.sem("xtT"), 1)
            dense(P[6][:, :], xtT, wts["v"]).then_inc(s.sem("v_ps"), 1)
            pe.wait_ge(s.sem("w_o_in"), 16)
            dense(P[7][:, :], xtT, wts["o"]).then_inc(s.sem("o_ps"), 1)
            pe.wait_ge(s.sem("xc"), 1)
            pe_transposes(pe, P[4], xc, ident, IC).then_inc(s.sem("xcT_ps"), 1)
            pe.wait_ge(s.sem("wif_in"), 16)
            pe.wait_ge(s.sem("xcT"), 1)
            pe.wait_ge(s.sem("rt"), 1)
            for g in range(2):
                mm = pe_dense(pe, P[2][0:H, g * T:(g + 1) * T], lambda c: wif[:, c, g * H:(g + 1) * H],
                              lambda c: xcT[:, c, :], IC)
            mm.then_inc(s.sem("if_ps"), 1)
            for n, ps in (("q", P[0]), ("k", P[1])):
                pe.wait_ge(s.sem(f"w_{n}_in"), 16)
                for e in range(IC):
                    mm = pe_dense(pe, ps[:, e * T:(e + 1) * T], lambda c: wts[n][:, c, e * 128:(e + 1) * 128],
                                  lambda c: xcT[:, c, :], IC)
                mm.then_inc(s.sem(f"{n}_ps"), 1)
            pe.wait_ge(s.sem("w_skip_in"), 16)
            dense(P[5][:, :], xcT, wts["skip"]).then_inc(s.sem("skip_ps"), 1)
            pe.wait_ge(s.sem("em"), 1)
            pe.matmul(P[3][:, 0:H], b[:, :], ident[0:H, 0:H], start=True, stop=True)
            pe.matmul(P[3][:, H:2 * H], em[:, :], ident[0:H, 0:H], start=True, stop=True).then_inc(s.sem("cb_ps"), 1)
            pe.wait_ge(s.sem("hsel"), 1)
            pe.wait_ge(s.sem("skip"), 1)
            for h in range(H):
                mm = pe.matmul(P[4 + h // 4][:, (h % 4) * T:(h % 4 + 1) * T], hsel[:, h, :], mx[:, :], start=True, stop=True)
                if h % 4 == 3:
                    mm.then_inc(s.sem("mx_ps"), 1)
            pe.wait_ge(s.sem("qT"), 1)
            pe.wait_ge(s.sem("kT"), 1)
            pe.wait_ge(s.sem("v"), 1)
            pe.wait_ge(s.sem("o"), 1)
            for c in range(IC):
                for odd in range(2):
                    lo = HD * odd
                    mm = pe.matmul(P[6 + odd][:, c * T:(c + 1) * T], kT[lo:lo + HD, c, :], qT[lo:lo + HD, c, :],
                                   start=True, stop=True)
                    if c == IC - 1:
                        mm.then_inc(s.sem(f"scores{odd}"), 1)
            pe.wait_ge(s.sem("halves"), 1)
            for c in range(IC):
                mm = pe.matmul(P[2][:, 2 * c:2 * c + 2], qT[:, c, :], halves[:, :], start=True, stop=True)
            mm.then_inc(s.sem("qsum_ps"), 1)
            pe.wait_ge(s.sem("sd"), 2)
            for h in range(H):
                mm = pe.matmul(P[h // 4][:, (h % 4) * 65:(h % 4 + 1) * 65], sd[:, h, :], v[:, h, :], start=True, stop=True)
                if h % 4 == 3:
                    mm.then_inc(s.sem("num_ps"), 1)
            pe.wait_ge(s.sem("hn"), 1)
            pe_transposes(pe, P[3], hn, ident, IC).then_inc(s.sem("oT_ps"), 1)
            pe.wait_ge(s.sem("wdn_in"), 16)
            pe.wait_ge(s.sem("oT"), 1)
            dense(P[4][:, 0:D], oT, wdn).then_inc(s.sem("down_ps"), 1)

        @block.scalar
        def _(act):
            nx.act(act)
            n1.act(act)
            for name, tile in (("c", sg), ("r", sr), ("o", o)):
                act.wait_ge(s.sem(name + "_neg"), 1)
                act.activation(tile[:, :], tile[:, :], ACT.Exp).then_inc(s.sem(name + "_exp"), 1)
            act.wait_ge(s.sem("if_pre"), 1)
            act.activation(gi[:, :], gi[:, :], ACT.Tanh).then_inc(s.sem("tanh"), 1)
            act.activation(gf[:, :], gf[:, :], ACT.Tanh).then_inc(s.sem("tanh"), 1)
            act.wait_ge(s.sem("mx"), 1)
            act.activation(em[:, :], mx[:, :], ACT.Exp, scale=-1.0).then_inc(s.sem("em"), 1)
            for g in range(2):
                act.wait_ge(s.sem("dm"), 4 * g + 4)
                act.activation(dm[:, 4 * g:4 * g + 4, :], dm[:, 4 * g:4 * g + 4, :], ACT.Exp,
                               scale=-1.0).then_inc(s.sem("decay_all"), 1)
            act.wait_ge(s.sem("h_var"), 1)
            act.activation(hsd[:, :], hvar[:, :], ACT.Sqrt).then_inc(s.sem("h_std"), 1)

        @block.vector
        def _(dve):
            def sigmoid_in(name, tile, z):
                dve.tensor_scalar(tile[:, :], z[:, :], -1.0, 87.0, ALU.mult, ALU.min).then_inc(s.sem(name + "_neg"), 1)

            def sigmoid_out(link, name, tile):
                dve.wait_ge(s.sem(name + "_exp"), 1)
                link(dve.tensor_scalar(tile[:, :], tile[:, :], 1.0, None, ALU.add))
                link(dve.reciprocal(tile[:, :], tile[:, :]))

            link = linker(dve, s.sem("dve_steps"))
            link(dve.memset(xt[:, 0:K - 1], 0.0))
            link(dve.memset(v[:, :, HD:HD + 1], 1.0))
            link(dve.memset(one8[:, :], 1.0))
            nx.dve(dve, link)
            n1.dve(dve, link, xa[:, :], nx.xn[:, :])
            dve.wait_ge(s.sem("rows1_in"), 6 * 16)
            link(dve.tensor_tensor(xa[:, :], xa[:, :], rows["ln_g"][:, :], ALU.mult))
            dve.tensor_tensor(xa[:, :], xa[:, :], rows["ln_b"][:, :], ALU.add).then_inc(s.sem("xa"), 1)
            dve.wait_ge(s.sem("xaT_ps"), 1)
            dve.tensor_copy(xaT[:, :, :], cols(P[0])).then_inc(s.sem("xaT"), 1)
            dve.wait_ge(s.sem("up_ps"), 1)
            finish(dve, dve.tensor_tensor(xt[:, K - 1:], P[1][:, :], rows["b_up_l"][:, :], ALU.add), s.sem("xt"))
            link(dve.tensor_scalar(xc[:, :], xt[:, 0:I], rows["conv_w"][:, 0:1], rows["conv_b"][:, 0:1], ALU.mult, ALU.add))
            for m in range(1, K):
                ins = dve.scalar_tensor_tensor(out=xc[:, :], in0=xt[:, m:m + I], scalar=rows["conv_w"][:, m:m + 1],
                                               in1=xc[:, :], op0=ALU.mult, op1=ALU.add)
                if m < K - 1:
                    link(ins)
                else:
                    finish(dve, ins, s.sem("conv"))
            sigmoid_in("c", sg, xc)
            dve.wait_ge(s.sem("up_ps"), 2)
            finish(dve, dve.tensor_tensor(rt[:, :], P[2][:, :], rows["b_up_r"][:, :], ALU.add), s.sem("rt"))
            sigmoid_in("r", sr, rt)
            dve.wait_ge(s.sem("xtT_ps"), 1)
            dve.tensor_copy(xtT[:, :, :], cols(P[3], IC)).then_inc(s.sem("xtT"), 1)
            sigmoid_out(link, "c", sg)
            dve.tensor_tensor(xc[:, :], xc[:, :], sg[:, :], ALU.mult).then_inc(s.sem("xc"), 1)
            sigmoid_out(link, "r", sr)
            link(dve.tensor_tensor(sr[:, :], sr[:, :], rt[:, :], ALU.mult))
            dve.wait_ge(s.sem("xcT_ps"), 1)
            dve.tensor_copy(xcT[:, :, :], cols(P[4], IC)).then_inc(s.sem("xcT"), 1)
            dve.wait_ge(s.sem("rows2_in"), 8 * 16)
            dve.wait_ge(s.sem("v_ps"), 1)
            heads = "p (h e) -> p h e"
            dve.tensor_tensor(v[:, :, 0:HD], P[6][:, :].rearrange(heads, h=H),
                              rows["b_v"][:, :].rearrange(heads, h=H), ALU.add).then_inc(s.sem("v"), 1)
            dve.wait_ge(s.sem("o_ps"), 1)
            finish(dve, dve.tensor_tensor(o[:, :], P[7][:, :], rows["b_o"][:, :], ALU.add), s.sem("o"))
            sigmoid_in("o", o, o)
            dve.wait_ge(s.sem("if_ps"), 1)
            link(dve.tensor_scalar(gi[:, :], P[2][0:H, 0:T], bif[:, 0:1], 1 / CAP, ALU.add, ALU.mult))
            dve.tensor_scalar(gf[:, :], P[2][0:H, T:2 * T], bif[:, 1:2], 1 / CAP, ALU.add, ALU.mult).then_inc(s.sem("if_pre"), 1)
            dve.wait_ge(s.sem("tanh"), 2)
            link(dve.tensor_scalar(gi[:, :], gi[:, :], CAP, None, ALU.mult))
            link(dve.tensor_scalar(gf[:, :], gf[:, :], CAP, None, ALU.mult))
            link(dve.tensor_tensor_scan(fs[:, :], one8[:, :], gf[:, :], 0.0, ALU.mult, ALU.add))
            link(dve.tensor_tensor(b[:, :], gi[:, :], fs[:, :], ALU.subtract))
            dve.tensor_tensor_scan(mx[:, :], b[:, :], b[:, :], 0.0, ALU.max, ALU.max).then_inc(s.sem("mx"), 1)
            dve.wait_ge(s.sem("q_ps"), 1)
            for c in range(IC):
                ins = dve.tensor_scalar(qT[:, c, :], P[0][:, c * T:(c + 1) * T], bqk[:, 0, c:c + 1], None, ALU.add)
            ins.then_inc(s.sem("qT"), 1)
            dve.wait_ge(s.sem("k_ps"), 1)
            for c in range(IC):
                ins = dve.tensor_scalar(kT[:, c, :], P[1][:, c * T:(c + 1) * T], bqk[:, 1, c:c + 1], HD ** -0.5,
                                        ALU.add, ALU.mult)
            ins.then_inc(s.sem("kT"), 1)
            dve.wait_ge(s.sem("skip_ps"), 1)
            dve.tensor_tensor(skip[:, :], P[5][:, :], rows["b_skip"][:, :], ALU.add).then_inc(s.sem("skip"), 1)
            dve.wait_ge(s.sem("cb_ps"), 1)
            link(dve.tensor_copy(cb[:, :], P[3][:, 0:2 * H]))
            for h in range(H):
                dve.wait_ge(s.sem("mx_ps"), h // 4 + 1)
                dve.tensor_scalar(dm[:, h, :], P[4 + h // 4][:, (h % 4) * T:(h % 4 + 1) * T], cb[:, h:h + 1], 0.0,
                                  ALU.subtract, ALU.max).then_inc(s.sem("dm"), 1)
            dve.wait_ge(s.sem("decay"), 2)
            for odd in range(2):
                dve.wait_ge(s.sem(f"scores{odd}"), 1)
                by_row = "p (c odd) t -> p odd c t"
                dve.tensor_tensor(sd[:, :, :].rearrange(by_row, odd=2)[:, odd], cols(P[6 + odd], 4),
                                  dm[:, :, :].rearrange(by_row, odd=2)[:, odd], ALU.mult).then_inc(s.sem("sd"), 1)
            dve.wait_ge(s.sem("qsum_ps"), 1)
            link(dve.tensor_tensor(den[:, :], P[2][:, 0:H], cb[:, H:2 * H], ALU.mult))
            for g in range(2):
                dve.wait_ge(s.sem("num_ps"), g + 1)
                num = P[g][:, 0:260].rearrange("p (h e) -> p h e", h=4)
                gs = slice(4 * g, 4 * g + 4)
                link(dve.tensor_tensor(den[:, gs], den[:, gs], num[:, :, 64], ALU.add))
                link(dve.tensor_scalar(den[:, gs], den[:, gs], 1.0, None, ALU.max))
                link(dve.reciprocal(den[:, gs], den[:, gs]))
                link(dve.tensor_tensor(hh[:, g * 256:(g + 1) * 256].rearrange("p (h e) -> p h e", h=4), num[:, :, 0:64],
                                       add_cols(den[:, gs], HD), ALU.mult))
            sigmoid_out(link, "o", o)
            link(dve.tensor_tensor(hh[:, :], hh[:, :], o[:, :], ALU.mult))
            for h in range(H):
                link(dve.bn_stats(hst[:, h, :], hh[:, h * HD:(h + 1) * HD]))
                link(dve.bn_aggr(hmv[:, h, :], hst[:, h, :]))
            dve.tensor_scalar(hvar[:, :], hmv[:, :, 1], 1e-6, None, ALU.add).then_inc(s.sem("h_var"), 1)
            h3 = hh[:, :].rearrange("p (h e) -> p h e", h=H)
            link(dve.tensor_tensor(h3, h3, hmv[:, :, 0:1].to_broadcast([128, H, HD]), ALU.subtract))
            dve.wait_ge(s.sem("h_std"), 1)
            dve_rsqrt(dve, link, den[:, :], hsd[:, :], hvar[:, :])
            link(dve.tensor_tensor(h3, h3, add_cols(den[:, :], HD), ALU.mult))
            link(dve.tensor_tensor(hh[:, :], hh[:, :], rows["mh_g"][:, :], ALU.mult))
            link(dve.tensor_tensor(hh[:, :], hh[:, :], rows["mh_b"][:, :], ALU.add))
            link(dve.tensor_tensor(hh[:, :], hh[:, :], skip[:, :], ALU.add))
            dve.tensor_tensor(hn[:, :], hh[:, :], sr[:, :], ALU.mult).then_inc(s.sem("hn"), 1)
            dve.wait_ge(s.sem("oT_ps"), 1)
            dve.tensor_copy(oT[:, :, :], cols(P[3], IC)).then_inc(s.sem("oT"), 1)
            dve.wait_ge(s.sem("down_ps"), 1)
            link(dve.tensor_tensor(xa[:, :], P[4][:, 0:D], rows["b_down"][:, :], ALU.add))
            link(dve.tensor_tensor(xa[:, :], xa[:, :], nx.xn[:, :], ALU.add))
            link(dve.tensor_tensor(x[:, :], x[:, :], xa[:, :], ALU.add))


def more_layouts(i, out):
    import numpy as np
    w = i["L1_xattn_Wkv"]
    out["L1_xattn_wq"] = chunked(i["L1_xattn_Wq"])
    out["L1_xattn_wkT"] = chunked(w[:, :512].T, 64)
    out["L1_xattn_wv"] = chunked(w[:, 512:])
    out["L1_xattn_wo"] = chunked(i["L1_xattn_Wo"], 64)
    for n in ("ln_x_g", "ln_x_b", "ln_l_g", "ln_l_b", "ln_o_g", "ln_o_b"):
        out["L1_xattn_" + n] = i["L1_xattn_" + n]
    out["mask_bk1"] = i["mask_BxS2_bk1"][0].astype(np.int32)
    out["mask_ff1"] = i["mask_BxS2_ff1"][0].reshape(-1, 128).T
    out["mask_ik1"] = i["mask_BxSxS2_ik1"][0]
    out["L2_xattn_wq"] = chunked(i["L2_xattn_wq"])
    out["L2_xattn_wkv"] = chunked(np.concatenate([i["L2_xattn_wk"], i["L2_xattn_wv"]], 1))
    out["L2_xattn_dense_w"] = chunked(i["L2_xattn_dense_w"])
    for n in ("ln_gamma", "ln_beta", "dense_b"):
        out["L2_xattn_" + n] = i["L2_xattn_" + n]
    out["L0_attn_decay_logit"] = i["L0_attn_decay_logit"].reshape(1)
    out["L0_attn_out_scale"] = i["L0_attn_out_scale"].reshape(1)
    out["L0_attn_q_scale"] = i["L0_attn_q_scale"].reshape(DC, 128).T
    out["L0_attn_k_scale"] = i["L0_attn_k_scale"].reshape(DC, 128).T
    out["L2_attn_W_qkv"] = chunked(i["L2_attn_W_qkv"])
    out["L2_attn_W_o"] = chunked(i["L2_attn_W_o"])
    out["L3_attn_W_qkv"] = chunked(np.concatenate([i["L3_attn_W" + n].T for n in "qkv"], 1))
    out["L3_attn_b_qkv"] = np.concatenate([i["L3_attn_b" + n] for n in "qkv"])
    out["L3_attn_Wo"] = chunked(i["L3_attn_Wo"].T)
    out["L3_attn_bo"] = i["L3_attn_bo"]
    w = i["L3_ffn_W_qkv"]
    out["L3_ffn_W_kqv"] = chunked(np.concatenate([w[:, D:2 * D], w[:, :D], w[:, 2 * D:]], 1))
    out["L3_ffn_guide"] = i["L3_ffn_g_info"][0, 0]
    out["L3_ffn_W_proj"] = chunked(i["L3_ffn_W_proj"])
    out["L3_ffn_b_proj"] = i["L3_ffn_b_proj"]
    for p, w1, b1, w2, b2 in (("L1_ffn_", i["L1_ffn_W1"], i["L1_ffn_b1"], i["L1_ffn_W2"], i["L1_ffn_b2"]),
                              ("L2_ffn_", i["L2_ffn_fc1_w"].transpose(0, 2, 1), i["L2_ffn_fc1_b"][:, 0],
                               i["L2_ffn_fc2_w"], i["L2_ffn_fc2_b"][:, 0])):
        out[p + "W1"] = np.stack([chunked(w) for w in w1])
        out[p + "W2"] = np.stack([chunked(w) for w in w2])
        out[p + "b1"] = b1.reshape(-1, 128).T
        out[p + "b2"] = b2
    out["L1_ffn_wr"] = i["L1_ffn_wr"].reshape(DC, 128).T
    out["L1_ffn_br"] = i["L1_ffn_br"].reshape(1)
    out["L2_ffn_gate_w"] = chunked(i["L2_ffn_gate_w"].T)
    out["L0_ffn_router_w"] = chunked(i["L0_ffn_router_w"].T)
    for n in ("router_bias", "norm_w", "bank_phase"):
        out["L0_ffn_" + n] = i["L0_ffn_" + n]
    for n in ("mag", "freq", "down"):
        out["L0_ffn_bank_" + n] = np.stack([chunked(w) for w in i["L0_ffn_bank_" + n]])
    p = "L1_attn_"
    out[p + "W_up"] = chunked(np.concatenate([i[p + "W_up_l"].T, i[p + "W_up_r"].T], 1))
    for n in ("skip", "q", "k", "v", "o", "down"):
        out[p + "W_" + n] = chunked(i[p + "W_" + n].T)
    out[p + "W_if"] = chunked(np.concatenate([i[p + "W_i"].T, i[p + "W_f"].T], 1))
    for n in ("ln_g", "ln_b", "b_up_l", "b_up_r", "b_skip", "b_v", "b_o", "mh_g", "mh_b", "b_down", "conv_w", "conv_b"):
        out[p + n] = i[p + n].reshape(-1)
    out[p + "b_qk"] = np.stack([i[p + "b_q"].reshape(-1, 128).T, i[p + "b_k"].reshape(-1, 128).T], 1)
    out[p + "b_if"] = np.stack([i[p + "b_i"], i[p + "b_f"]], 1)


def stage_load(nc, A, x, ident):
    with Stage(nc, "load") as s:
        block = s.block()

        @block.sync
        def _(sp):
            sp.dma_start(x[:, :], A["x"]).then_inc(s.sem("x_in"), 16)
            sp.wait_ge(s.sem("x_in"), 16)

        @block.gpsimd
        def _(pool):
            pool.memset(ident[:, :], 0.0).then_inc(s.sem("zero"), 1)
            pool.wait_ge(s.sem("zero"), 1)
            pool.affine_select(out=ident[:, :], in_=ident[:, :], compare_op=ALU.not_equal, fill=1.0, base=0,
                               pattern=[[-1, 128]], channel_multiplier=1).then_inc(s.sem("ident"), 1)
            pool.wait_ge(s.sem("ident"), 1)
            hm = A["head_mask"]
            pool.memset(hm[:, :], 1.0).then_inc(s.sem("ones"), 1)
            pool.wait_ge(s.sem("ones"), 1)
            pool.affine_select(out=hm[:, :], in_=hm[:, :], compare_op=ALU.is_ge, fill=0.0, base=0,
                               pattern=[[-16, 8]], channel_multiplier=1).then_inc(s.sem("from"), 1)
            pool.wait_ge(s.sem("from"), 1)
            pool.affine_select(out=hm[:, :], in_=hm[:, :], compare_op=ALU.is_ge, fill=0.0, base=15,
                               pattern=[[16, 8]], channel_multiplier=-1).then_inc(s.sem("head_mask"), 1)
            pool.wait_ge(s.sem("head_mask"), 1)
            cm = A["causal"]
            pool.memset(cm[:, :], 1.0).then_inc(s.sem("ones2"), 1)
            pool.wait_ge(s.sem("ones2"), 1)
            pool.affine_select(out=cm[:, :], in_=cm[:, :], compare_op=ALU.is_ge, fill=0.0, base=0,
                               pattern=[[1, 128]], channel_multiplier=-1).then_inc(s.sem("causal"), 1)
            pool.iota(A["iota16"][:, :], [[1, 16]], base=0, channel_multiplier=0,
                      allow_small_or_imprecise_dtypes=True).then_inc(s.sem("iota16"), 1)
            pool.memset(A["ones"][:, :], 1.0).then_inc(s.sem("ones3"), 1)
            pool.wait_ge(s.sem("causal"), 1)
            pool.wait_ge(s.sem("iota16"), 1)
            pool.wait_ge(s.sem("ones3"), 1)


def stage_store(nc, A, x, ident):
    with Stage(nc, "store") as s:
        block = s.block()

        @block.sync
        def _(sp):
            sp.dma_start(A["out"], x[:, :]).then_inc(s.sem("x_out"), 16)
            sp.wait_ge(s.sem("x_out"), 16)


STAGES = [stage_prepare, stage_l0_xattn, stage_l0_attn, stage_l0_ffn, stage_l1_xattn, stage_l1_attn, stage_l1_ffn,
          stage_l2_xattn, stage_l2_attn, stage_l2_ffn, stage_l3_xattn, stage_l3_attn, stage_l3_ffn]


def program(nc, A, stages):
    with ExitStack() as ctx:
        x = ctx.enter_context(nc.sbuf_tensor("x", [T, D], F32))
        ident = ctx.enter_context(nc.sbuf_tensor("ident", [128, 128], F32))
        A["head_mask"] = ctx.enter_context(nc.sbuf_tensor("head_mask", [128, 8], F32))
        A["causal"] = ctx.enter_context(nc.sbuf_tensor("causal", [128, 128], F32))
        A["iota16"] = ctx.enter_context(nc.sbuf_tensor("iota16", [128, 16], F32))
        A["ones"] = ctx.enter_context(nc.sbuf_tensor("ones", [128, 128], F32))
        A["kv_sum"] = ctx.enter_context(nc.sbuf_tensor("kv_sum", [128, DC, 129], F32))
        A["xn_rows"] = nc.dram_tensor("xn_rows", (128, S2 // 128, D), F32, kind="Internal").ap()
        A["att_order"] = nc.dram_tensor("att_order", (16, T, 16), F32, kind="Internal").ap()
        A["xnT"] = nc.dram_tensor("xnT", (128, DC, S2), F32, kind="Internal").ap()
        for stage in [stage_load, *stages, stage_store]:
            stage(nc, A, x, ident)


def chunked(a, p=128):
    import numpy as np
    a = np.asarray(a)
    return np.ascontiguousarray(a.reshape(-1, p, a.shape[-1]).transpose(1, 0, 2))


def layouts(i):
    import numpy as np
    i = {k: np.asarray(v) for k, v in i.items()}
    ctx = i["ctx_1024"][0]
    out = {"x": i["x"][0], "ctx_rows": chunked(ctx), "ctxT": chunked(ctx.T)}
    w = i["L0_xattn_w_kv"]
    out["L0_xattn_wq"] = chunked(i["L0_xattn_w_q"])
    out["L0_xattn_wkT"] = chunked(w[:, :1024].T, 64)
    out["L0_xattn_wv"] = chunked(w[:, 1024:])
    out["L0_xattn_wo"] = chunked(i["L0_xattn_w_out1"], 64)
    out["L0_xattn_w_out2"] = chunked(i["L0_xattn_w_out2"])
    out["L0_xattn_gamma"] = i["L0_xattn_gamma"]
    more_layouts(i, out)
    return {k: np.ascontiguousarray(v) for k, v in out.items()}


def kernel(**inputs):
    import numpy as np
    import concourse.bacc as bacc
    from concourse.bass_utils import run_bass_kernel_spmd

    nc = bacc.Bacc("TRN2", target_bir_lowering=False, num_devices=1)
    arrays, A = {}, {}
    for name, a in layouts(inputs).items():
        arrays[f"in_{name}"] = a
        A[name] = nc.dram_tensor(f"in_{name}", a.shape, mybir.dt.from_np(a.dtype), kind="ExternalInput").ap()
    A["out"] = nc.dram_tensor("out_0", (T, D), F32, kind="ExternalOutput").ap()
    program(nc, A, STAGES)
    r = run_bass_kernel_spmd(nc, [arrays], core_ids=[0])
    return r.results[0]["out_0"].reshape(1, T, D)
```
